# Optimizing a Trainium2 kernel written in Bass

```python
import numpy as np
import jax
import jax.numpy as jnp

def _softmax(x, axis=-1):
    return jax.nn.softmax(x, axis=axis)

def _gelu(x):
    return jax.nn.gelu(x, approximate=True)

def _silu(x):
    return jax.nn.silu(x)

def _sigmoid(x):
    return jax.nn.sigmoid(x)

def _layernorm(x, axis=-1, eps=1e-05):
    m = jnp.mean(x, axis=axis, keepdims=True)
    v = jnp.var(x, axis=axis, keepdims=True)
    return (x - m) / jnp.sqrt(v + eps)

def _scatter_add(tgt, idx, src, axis=0):
    return tgt.at[idx].add(src)

def _segment_sum(src, seg, n):
    return jax.ops.segment_sum(src, seg, n)
kernel_name = 'mk_perceiver_d2_seqx_r8_356990'

def setup_inputs(seed: int=0):
    np.random.seed(seed)
    _w = jnp.asarray

    def _rec_inputs():
        import jax
        import jax.numpy as jnp
        _rk = jax.random.key(seed)
        x = 0.002226 + 0.9996 * jax.random.normal(jax.random.fold_in(_rk, 1), (128, 32, 128), jnp.float32)
        _lenS = 32 - jax.random.randint(jax.random.fold_in(_rk, 7), (128,), 0, max(1, 32 // 4) + 1, jnp.int32)
        _lenS2 = 257 - jax.random.randint(jax.random.fold_in(_rk, 8), (128,), 0, max(1, 257 // 4) + 1, jnp.int32)
        _ctx_1024P = jax.random.normal(jax.random.fold_in(_rk, 11), (128, 16, 128), jnp.float32)
        _ctx_1024c = jax.random.dirichlet(jax.random.fold_in(_rk, 511), 0.3 * jnp.ones((16,), jnp.float32), (128, 257))
        _ctx_1024t = jnp.einsum('bsk,bkd->bsd', _ctx_1024c, _ctx_1024P)
        _ctx_1024t = _ctx_1024t * jax.lax.rsqrt(jnp.mean(jnp.square(_ctx_1024t)) + 1e-12) * 0.953939
        ctx_1024 = -0.000125008 + 0.999885 * (_ctx_1024t + 0.3 * jax.random.normal(jax.random.fold_in(_rk, 611), (128, 257, 128), jnp.float32))
        _validS = jnp.arange(32)[None, :] < _lenS[:, None]
        _validS2 = jnp.arange(257)[None, :] < _lenS2[:, None]
        _causal = jnp.tril(jnp.ones((32, 32), dtype=bool))
        mask_BxS2_bk0 = jnp.logical_not(jnp.broadcast_to(_validS2[:, :], (128, 257)))
        mask_Bx1x1xS2_if1 = jnp.where(jnp.ones((128, 1, 1, 257), dtype=bool), 1, 0).astype(jnp.int32)
        return (x, ctx_1024, mask_BxS2_bk0, mask_Bx1x1xS2_if1)
    x, ctx_1024, mask_BxS2_bk0, mask_Bx1x1xS2_if1 = _rec_inputs()

    def _L0_xattn_setup():
        import jax, jax.numpy as jnp
        import numpy as np
        EPS = 1e-05

        def layer_norm(x, g, b):
            mu = jnp.mean(x, axis=-1, keepdims=True)
            var = jnp.mean((x - mu) ** 2, axis=-1, keepdims=True)
            return (x - mu) * jax.lax.rsqrt(var + EPS) * g + b
        key = jax.random.key(seed)
        ks = jax.random.split(key, 8)
        b, n, l, D = (8, 512, 64, 128)
        heads, dim_head = (16, 64)
        inner = heads * dim_head
        x = jax.random.normal(ks[0], (b, n, D), dtype=jnp.float32)
        latents = jax.random.normal(ks[1], (b, l, D), dtype=jnp.float32)
        mask = jax.random.randint(ks[2], (b, n), 0, 2) > 0
        Wq = jax.random.normal(ks[3], (D, inner), dtype=jnp.float32) * D ** (-0.5)
        Wkv = jax.random.normal(ks[4], (D, 2 * inner), dtype=jnp.float32) * D ** (-0.5)
        Wout = jax.random.normal(ks[5], (inner, D), dtype=jnp.float32) * inner ** (-0.5)
        g1 = jnp.ones((D,), jnp.float32)
        b1 = jnp.zeros((D,), jnp.float32)
        g2 = jnp.ones((D,), jnp.float32)
        b2 = jnp.zeros((D,), jnp.float32)
        return {'x': x, 'latents': latents, 'mask': mask, 'g1': g1, 'b1': b1, 'g2': g2, 'b2': b2, 'Wq': Wq, 'Wkv': Wkv, 'Wout': Wout}
    _L0_xattn_all = _L0_xattn_setup()
    _L0_xattn_in = {k: v for k, v in _L0_xattn_all.items() if k in ('g1', 'b1', 'g2', 'b2', 'Wq', 'Wkv', 'Wout')}
    del _L0_xattn_all

    def _L0_attn_setup():
        import jax, jax.numpy as jnp
        import numpy as np
        B, T, D = (4, 1024, 128)
        C = 8.0

        def _combine(c1, c2):
            a1, b1 = c1
            a2, b2 = c2
            return (a1 * a2, a2 * b1 + b2)
        key = jax.random.key(seed)
        k1, k2, k3 = jax.random.split(key, 3)
        init_std = D ** (-0.5)
        x = jax.random.normal(k1, (B, T, D), dtype=jnp.float32)
        W_in = jax.random.truncated_normal(k2, -3.0, 3.0, (D, D), dtype=jnp.float32) * init_std
        W_gate = jax.random.truncated_normal(k3, -3.0, 3.0, (D, D), dtype=jnp.float32) * init_std
        b_in = jnp.zeros((D,), dtype=jnp.float32)
        b_gate = jnp.zeros((D,), dtype=jnp.float32)
        forget_lambda = jnp.linspace(-4.323, -9.0, D, dtype=jnp.float32)
        return {'x': x, 'W_in': W_in, 'b_in': b_in, 'W_gate': W_gate, 'b_gate': b_gate, 'forget_lambda': forget_lambda}
    _L0_attn_all = _L0_attn_setup()
    _L0_attn_in = {k: v for k, v in _L0_attn_all.items() if k in ('W_in', 'b_in', 'W_gate', 'b_gate', 'forget_lambda')}
    del _L0_attn_all

    def _L0_ffn_setup():
        import jax, jax.numpy as jnp
        import numpy as np
        BLOCK = 32
        W_BITS = 4
        ACT_BITS = 16

        def act_qdq(x):
            qmax = 2.0 ** (ACT_BITS - 1) - 1.0
            scale = jnp.maximum(jnp.max(jnp.abs(x)) / qmax, 1e-12)
            return jnp.clip(jnp.round(x / scale), -qmax - 1.0, qmax) * scale

        def fixed_qdq_u16(x):
            scale = 1.0 / 65536.0
            return jnp.clip(jnp.round(x / scale), 0.0, 65535.0) * scale

        def lpbq_dequant(w):
            O, I = w.shape
            qmax = 2.0 ** (W_BITS - 1) - 1.0
            wb = w.reshape(O, I // BLOCK, BLOCK)
            s = jnp.maximum(jnp.max(jnp.abs(wb), axis=-1, keepdims=True) / qmax, 1e-12)
            wq = jnp.clip(jnp.round(wb / s), -qmax - 1.0, qmax) * s
            return wq.reshape(O, I)
        key = jax.random.key(seed)
        k1, k2, k3, k4 = jax.random.split(key, 4)
        B, S, H, I = (2, 512, 128, 384)
        x = jax.random.normal(k1, (B, S, H), jnp.float32)
        w_gate = jax.random.normal(k2, (I, H), jnp.float32) * 0.02
        w_up = jax.random.normal(k3, (I, H), jnp.float32) * 0.02
        w_down = jax.random.normal(k4, (H, I), jnp.float32) * 0.02
        return {'x': x, 'w_gate': w_gate, 'w_up': w_up, 'w_down': w_down}
    _L0_ffn_all = _L0_ffn_setup()
    _L0_ffn_in = {k: v for k, v in _L0_ffn_all.items() if k in ('w_gate', 'w_up', 'w_down')}
    del _L0_ffn_all

    def _L1_xattn_setup():
        import jax, jax.numpy as jnp
        import numpy as np
        D_MODEL = 128
        NUM_HEADS = 16
        D_K = D_MODEL // NUM_HEADS
        B, S = (2, 256)

        def _split_heads(x):
            b, s, _ = x.shape
            return x.reshape(b, s, NUM_HEADS, D_K).transpose(0, 2, 1, 3)
        key = jax.random.key(seed)
        ks = jax.random.split(key, 12)
        sc = 1.0 / np.sqrt(D_MODEL)
        return {'x_q': jax.random.normal(ks[0], (B, S, D_MODEL), jnp.float32), 'x_k': jax.random.normal(ks[1], (B, S, D_MODEL), jnp.float32), 'x_v': jax.random.normal(ks[2], (B, S, D_MODEL), jnp.float32), 'mask': jnp.ones((B, 1, 1, S), jnp.int32), 'W_q': jax.random.normal(ks[3], (D_MODEL, D_MODEL), jnp.float32) * sc, 'b_q': jax.random.normal(ks[4], (D_MODEL,), jnp.float32) * 0.01, 'W_k': jax.random.normal(ks[5], (D_MODEL, D_MODEL), jnp.float32) * sc, 'b_k': jax.random.normal(ks[6], (D_MODEL,), jnp.float32) * 0.01, 'W_v': jax.random.normal(ks[7], (D_MODEL, D_MODEL), jnp.float32) * sc, 'b_v': jax.random.normal(ks[8], (D_MODEL,), jnp.float32) * 0.01, 'W_o': jax.random.normal(ks[9], (D_MODEL, D_MODEL), jnp.float32) * sc, 'b_o': jax.random.normal(ks[10], (D_MODEL,), jnp.float32) * 0.01}
    _L1_xattn_all = _L1_xattn_setup()
    _L1_xattn_in = {k: v for k, v in _L1_xattn_all.items() if k in ('W_q', 'b_q', 'W_k', 'b_k', 'W_v', 'b_v', 'W_o', 'b_o')}
    del _L1_xattn_all

    def _L1_attn_setup():
        import jax, jax.numpy as jnp
        import numpy as np
        HEADS = 16

        def fenwick_mask(T):
            m = np.zeros((T, T), dtype=bool)
            for i in range(T):
                j = i + 1
                while j <= T:
                    m[i, j - 1] = True
                    j += j & -j
                step = 1
                while i - step >= 0:
                    m[i, i - step] = True
                    step *= 2
            m &= np.tril(np.ones((T, T), dtype=bool))
            return jnp.asarray(m)
        key = jax.random.key(seed)
        ks = jax.random.split(key, 4)
        B, T, C = (2, 256, 128)
        x = jax.random.normal(ks[0], (B, T, C), dtype=jnp.float32)
        W_qkv = jax.random.normal(ks[1], (C, 3 * C), dtype=jnp.float32) * C ** (-0.5)
        b_qkv = jnp.zeros((3 * C,), dtype=jnp.float32)
        W_proj = jax.random.normal(ks[2], (C, C), dtype=jnp.float32) * C ** (-0.5)
        b_proj = jnp.zeros((C,), dtype=jnp.float32)
        return {'x': x, 'W_qkv': W_qkv, 'b_qkv': b_qkv, 'W_proj': W_proj, 'b_proj': b_proj}
    _L1_attn_all = _L1_attn_setup()
    _L1_attn_in = {k: v for k, v in _L1_attn_all.items() if k in ('W_qkv', 'b_qkv', 'W_proj', 'b_proj')}
    del _L1_attn_all

    def _L1_ffn_setup():
        import jax, jax.numpy as jnp
        import numpy as np
        HIDDEN = 128
        MOE_FF = 64
        SHARED_FF = 352
        NUM_EXPERTS = 16
        TOP_K = 2
        NORM_TOPK = True
        key = jax.random.key(seed)
        ks = jax.random.split(key, 8)
        s = 0.02
        return {'layer_input': jax.random.normal(ks[0], (1, 256, HIDDEN), dtype=jnp.float32), 'gate_w': jax.random.normal(ks[1], (NUM_EXPERTS, HIDDEN), dtype=jnp.float32) * s, 'w_gate_up': jax.random.normal(ks[2], (NUM_EXPERTS, HIDDEN, 2 * MOE_FF), dtype=jnp.float32) * s, 'w_down': jax.random.normal(ks[3], (NUM_EXPERTS, MOE_FF, HIDDEN), dtype=jnp.float32) * s, 'shared_w_gate': jax.random.normal(ks[4], (SHARED_FF, HIDDEN), dtype=jnp.float32) * s, 'shared_w_up': jax.random.normal(ks[5], (SHARED_FF, HIDDEN), dtype=jnp.float32) * s, 'shared_w_down': jax.random.normal(ks[6], (HIDDEN, SHARED_FF), dtype=jnp.float32) * s, 'shared_gate_w': jax.random.normal(ks[7], (1, HIDDEN), dtype=jnp.float32) * s}
    _L1_ffn_all = _L1_ffn_setup()
    _L1_ffn_in = {k: v for k, v in _L1_ffn_all.items() if k in ('gate_w', 'w_gate_up', 'w_down', 'shared_w_gate', 'shared_w_up', 'shared_w_down', 'shared_gate_w')}
    del _L1_ffn_all
    return {'x': x, 'ctx_1024': ctx_1024, 'mask_BxS2_bk0': mask_BxS2_bk0, 'mask_Bx1x1xS2_if1': mask_Bx1x1xS2_if1, 'L0_xattn_g1': _L0_xattn_in['g1'], 'L0_xattn_b1': _L0_xattn_in['b1'], 'L0_xattn_g2': _L0_xattn_in['g2'], 'L0_xattn_b2': _L0_xattn_in['b2'], 'L0_xattn_Wq': _L0_xattn_in['Wq'], 'L0_xattn_Wkv': _L0_xattn_in['Wkv'], 'L0_xattn_Wout': _L0_xattn_in['Wout'], 'L0_attn_W_in': _L0_attn_in['W_in'], 'L0_attn_b_in': _L0_attn_in['b_in'], 'L0_attn_W_gate': _L0_attn_in['W_gate'], 'L0_attn_b_gate': _L0_attn_in['b_gate'], 'L0_attn_forget_lambda': _L0_attn_in['forget_lambda'], 'L0_ffn_w_gate': _L0_ffn_in['w_gate'], 'L0_ffn_w_up': _L0_ffn_in['w_up'], 'L0_ffn_w_down': _L0_ffn_in['w_down'], 'L1_xattn_W_q': _L1_xattn_in['W_q'], 'L1_xattn_b_q': _L1_xattn_in['b_q'], 'L1_xattn_W_k': _L1_xattn_in['W_k'], 'L1_xattn_b_k': _L1_xattn_in['b_k'], 'L1_xattn_W_v': _L1_xattn_in['W_v'], 'L1_xattn_b_v': _L1_xattn_in['b_v'], 'L1_xattn_W_o': _L1_xattn_in['W_o'], 'L1_xattn_b_o': _L1_xattn_in['b_o'], 'L1_attn_W_qkv': _L1_attn_in['W_qkv'], 'L1_attn_b_qkv': _L1_attn_in['b_qkv'], 'L1_attn_W_proj': _L1_attn_in['W_proj'], 'L1_attn_b_proj': _L1_attn_in['b_proj'], 'L1_ffn_gate_w': _L1_ffn_in['gate_w'], 'L1_ffn_w_gate_up': _L1_ffn_in['w_gate_up'], 'L1_ffn_w_down': _L1_ffn_in['w_down'], 'L1_ffn_shared_w_gate': _L1_ffn_in['shared_w_gate'], 'L1_ffn_shared_w_up': _L1_ffn_in['shared_w_up'], 'L1_ffn_shared_w_down': _L1_ffn_in['shared_w_down'], 'L1_ffn_shared_gate_w': _L1_ffn_in['shared_gate_w']}

def reference(x, ctx_1024, mask_BxS2_bk0, mask_Bx1x1xS2_if1, L0_xattn_g1, L0_xattn_b1, L0_xattn_g2, L0_xattn_b2, L0_xattn_Wq, L0_xattn_Wkv, L0_xattn_Wout, L0_attn_W_in, L0_attn_b_in, L0_attn_W_gate, L0_attn_b_gate, L0_attn_forget_lambda, L0_ffn_w_gate, L0_ffn_w_up, L0_ffn_w_down, L1_xattn_W_q, L1_xattn_b_q, L1_xattn_W_k, L1_xattn_b_k, L1_xattn_W_v, L1_xattn_b_v, L1_xattn_W_o, L1_xattn_b_o, L1_attn_W_qkv, L1_attn_b_qkv, L1_attn_W_proj, L1_attn_b_proj, L1_ffn_gate_w, L1_ffn_w_gate_up, L1_ffn_w_down, L1_ffn_shared_w_gate, L1_ffn_shared_w_up, L1_ffn_shared_w_down, L1_ffn_shared_gate_w):
    import jax
    import jax.numpy as jnp

    def _L0_xattn_ref(x, latents, mask, g1, b1, g2, b2, Wq, Wkv, Wout):
        import jax, jax.numpy as jnp
        import numpy as np
        EPS = 1e-05

        def layer_norm(x, g, b):
            mu = jnp.mean(x, axis=-1, keepdims=True)
            var = jnp.mean((x - mu) ** 2, axis=-1, keepdims=True)
            return (x - mu) * jax.lax.rsqrt(var + EPS) * g + b
        heads, dim_head = (16, 64)
        b, n, D = x.shape
        l = latents.shape[1]
        xn = layer_norm(x, g1, b1)
        ln_lat = layer_norm(latents, g2, b2)
        q = ln_lat @ Wq
        kv = jnp.concatenate([xn, ln_lat], axis=1) @ Wkv
        k, v = jnp.split(kv, 2, axis=-1)

        def to_heads(t):
            return t.reshape(t.shape[0], t.shape[1], heads, dim_head).transpose(0, 2, 1, 3)
        q, k, v = (to_heads(q), to_heads(k), to_heads(v))
        scale = 1.0 / np.sqrt(np.sqrt(dim_head)).astype(np.float32)
        weight = jnp.einsum('bhld,bhnd->bhln', q * scale, k * scale)
        full_mask = jnp.concatenate([mask, jnp.ones((b, l), dtype=bool)], axis=1)
        neg = -jnp.finfo(weight.dtype).max
        weight = jnp.where(full_mask[:, None, None, :], weight, neg)
        weight = jax.nn.softmax(weight.astype(jnp.float32), axis=-1).astype(q.dtype)
        out = jnp.einsum('bhln,bhnd->bhld', weight, v)
        out = out.transpose(0, 2, 1, 3).reshape(b, l, heads * dim_head)
        return out @ Wout

    def _L0_attn_ref(x, W_in, b_in, W_gate, b_gate, forget_lambda):
        import jax, jax.numpy as jnp
        import numpy as np
        B, T, D = (4, 1024, 128)
        C = 8.0

        def _combine(c1, c2):
            a1, b1 = c1
            a2, b2 = c2
            return (a1 * a2, a2 * b1 + b2)
        input_gate = x @ W_in.T + b_in
        recurrence_gate = x @ W_gate.T + b_gate
        alpha = jnp.exp(-C * jax.nn.softplus(forget_lambda) * jax.nn.sigmoid(recurrence_gate))
        beta = jnp.sqrt(1.0 - alpha ** 2 + 1e-06)
        xbeta = beta * jax.nn.sigmoid(input_gate) * x
        _, h = jax.lax.associative_scan(_combine, (alpha, xbeta), axis=1)
        return h

    def _L0_ffn_ref(x, w_gate, w_up, w_down):
        import jax, jax.numpy as jnp
        import numpy as np
        BLOCK = 32
        W_BITS = 4
        ACT_BITS = 16

        def act_qdq(x):
            qmax = 2.0 ** (ACT_BITS - 1) - 1.0
            scale = jnp.maximum(jnp.max(jnp.abs(x)) / qmax, 1e-12)
            return jnp.clip(jnp.round(x / scale), -qmax - 1.0, qmax) * scale

        def fixed_qdq_u16(x):
            scale = 1.0 / 65536.0
            return jnp.clip(jnp.round(x / scale), 0.0, 65535.0) * scale

        def lpbq_dequant(w):
            O, I = w.shape
            qmax = 2.0 ** (W_BITS - 1) - 1.0
            wb = w.reshape(O, I // BLOCK, BLOCK)
            s = jnp.maximum(jnp.max(jnp.abs(wb), axis=-1, keepdims=True) / qmax, 1e-12)
            wq = jnp.clip(jnp.round(wb / s), -qmax - 1.0, qmax) * s
            return wq.reshape(O, I)
        x = act_qdq(x)
        up = act_qdq(x @ lpbq_dequant(w_up).T)
        gate = act_qdq(x @ lpbq_dequant(w_gate).T)
        sig = fixed_qdq_u16(jax.nn.sigmoid(gate))
        gate = act_qdq(gate * sig)
        o = act_qdq(gate * up)
        return o @ lpbq_dequant(w_down).T

    def _L1_xattn_ref(x_q, x_k, x_v, mask, W_q, b_q, W_k, b_k, W_v, b_v, W_o, b_o):
        import jax, jax.numpy as jnp
        import numpy as np
        D_MODEL = 128
        NUM_HEADS = 16
        D_K = D_MODEL // NUM_HEADS
        B, S = (2, 256)

        def _split_heads(x):
            b, s, _ = x.shape
            return x.reshape(b, s, NUM_HEADS, D_K).transpose(0, 2, 1, 3)
        Q = _split_heads(x_q @ W_q.T + b_q)
        K = _split_heads(x_k @ W_k.T + b_k)
        V = _split_heads(x_v @ W_v.T + b_v)
        scores = jnp.einsum('bhqd,bhkd->bhqk', Q, K) / jnp.sqrt(jnp.float32(D_K))
        scores = jnp.where(mask == 0, jnp.float32(-1000000000.0), scores)
        attn = jax.nn.softmax(scores, axis=-1)
        out = jnp.einsum('bhqk,bhkd->bhqd', attn, V)
        out = out.transpose(0, 2, 1, 3).reshape(x_q.shape[0], x_q.shape[1], D_MODEL)
        return out @ W_o.T + b_o

    def _L1_attn_ref(x, W_qkv, b_qkv, W_proj, b_proj):
        import jax, jax.numpy as jnp
        import numpy as np
        HEADS = 16

        def fenwick_mask(T):
            m = np.zeros((T, T), dtype=bool)
            for i in range(T):
                j = i + 1
                while j <= T:
                    m[i, j - 1] = True
                    j += j & -j
                step = 1
                while i - step >= 0:
                    m[i, i - step] = True
                    step *= 2
            m &= np.tril(np.ones((T, T), dtype=bool))
            return jnp.asarray(m)
        B, T, C = x.shape
        H = HEADS
        Dh = C // H
        scale = Dh ** (-0.5)
        qkv = (x @ W_qkv + b_qkv).reshape(B, T, 3, H, Dh)
        qkv = jnp.transpose(qkv, (2, 0, 3, 1, 4))
        q, k, v = (qkv[0], qkv[1], qkv[2])
        attn = jnp.einsum('bhtd,bhsd->bhts', q, k) * scale
        mask = fenwick_mask(T)
        attn = jnp.where(mask[None, None], attn, -jnp.inf)
        attn = jax.nn.softmax(attn, axis=-1)
        out = jnp.einsum('bhts,bhsd->bhtd', attn, v)
        out = jnp.transpose(out, (0, 2, 1, 3)).reshape(B, T, C)
        return out @ W_proj + b_proj

    def _L1_ffn_ref(layer_input, gate_w, w_gate_up, w_down, shared_w_gate, shared_w_up, shared_w_down, shared_gate_w):
        import jax, jax.numpy as jnp
        import numpy as np
        HIDDEN = 128
        MOE_FF = 64
        SHARED_FF = 352
        NUM_EXPERTS = 16
        TOP_K = 2
        NORM_TOPK = True
        B, S, D = layer_input.shape
        x = layer_input.reshape(-1, D)
        N = x.shape[0]
        shared = jax.nn.silu(x @ shared_w_gate.T) * (x @ shared_w_up.T) @ shared_w_down.T
        shared = shared * jax.nn.sigmoid(x @ shared_gate_w.T)
        logits = x @ gate_w.T
        probs = jax.nn.softmax(logits.astype(jnp.float32), axis=-1)
        rw, sel = jax.lax.top_k(probs, TOP_K)
        if NORM_TOPK:
            rw = rw / rw.sum(axis=-1, keepdims=True)
        rw = rw.astype(x.dtype)
        combine = jnp.zeros((N, NUM_EXPERTS), x.dtype).at[jnp.arange(N)[:, None], sel].set(rw)
        gu = jnp.einsum('nd,edf->nef', x, w_gate_up)
        g, h = jnp.split(gu, 2, axis=-1)
        h = jax.nn.silu(g) * h
        expert_out = jnp.einsum('nef,efd,ne->nd', h, w_down, combine)
        out = expert_out + shared
        return out.reshape(B, S, D)
    x = x + _L0_xattn_ref(ctx_1024, _layernorm(x, axis=-1), mask_BxS2_bk0, L0_xattn_g1, L0_xattn_b1, L0_xattn_g2, L0_xattn_b2, L0_xattn_Wq, L0_xattn_Wkv, L0_xattn_Wout)
    x = x + _L0_attn_ref(_layernorm(x, axis=-1), L0_attn_W_in, L0_attn_b_in, L0_attn_W_gate, L0_attn_b_gate, L0_attn_forget_lambda)
    x = x + _L0_ffn_ref(_layernorm(x, axis=-1), L0_ffn_w_gate, L0_ffn_w_up, L0_ffn_w_down)
    x = x + _L1_xattn_ref(_layernorm(x, axis=-1), ctx_1024, ctx_1024, mask_Bx1x1xS2_if1, L1_xattn_W_q, L1_xattn_b_q, L1_xattn_W_k, L1_xattn_b_k, L1_xattn_W_v, L1_xattn_b_v, L1_xattn_W_o, L1_xattn_b_o)
    x = x + _L1_attn_ref(_layernorm(x, axis=-1), L1_attn_W_qkv, L1_attn_b_qkv, L1_attn_W_proj, L1_attn_b_proj)
    x = x + _L1_ffn_ref(_layernorm(x, axis=-1), L1_ffn_gate_w, L1_ffn_w_gate_up, L1_ffn_w_down, L1_ffn_shared_w_gate, L1_ffn_shared_w_up, L1_ffn_shared_w_down, L1_ffn_shared_gate_w)
    return x

_drawn_inputs = setup_inputs


def setup_inputs(seed=0):
    import zlib

    import numpy as np

    out = dict(_drawn_inputs(seed))
    spreads = {'L0_xattn_g1': (1.0, 0.2),
     'L0_xattn_b1': (0.0, 0.1),
     'L0_xattn_g2': (1.0, 0.2),
     'L0_xattn_b2': (0.0, 0.1),
     'L0_attn_b_in': (0.0, 0.75),
     'L0_attn_b_gate': (0.0, 0.8),
     'L1_attn_b_qkv': (0.0, 0.1),
     'L1_attn_b_proj': (0.0, 0.1)}
    factors = {'L0_ffn_w_gate': 7.164,
     'L0_ffn_w_up': 6.935,
     'L0_ffn_w_down': 7.005,
     'L1_xattn_b_q': 37.877,
     'L1_xattn_b_k': 64.0,
     'L1_xattn_b_v': 6.228,
     'L1_xattn_b_o': 5.688,
     'L1_ffn_gate_w': 8.0,
     'L1_ffn_w_gate_up': 8.0,
     'L1_ffn_w_down': 8.0,
     'L1_ffn_shared_w_gate': 8.0,
     'L1_ffn_shared_w_up': 8.0,
     'L1_ffn_shared_w_down': 8.0,
     'L1_ffn_shared_gate_w': 8.0}
    for name, (base, spread) in spreads.items():
        noise = np.random.default_rng([zlib.crc32(name.encode()), seed]).standard_normal(out[name].shape)
        drawn = base * np.exp(spread * noise) if base else spread * noise
        out[name] = jnp.asarray(drawn.astype(out[name].dtype))
    for name, factor in factors.items():
        out[name] = (out[name] * factor).astype(out[name].dtype)
    return out
```

```python
from contextlib import ExitStack

import numpy as np
import concourse.bass as bass
from concourse import mybir

F32 = mybir.dt.float32
BF16 = mybir.dt.bfloat16
U8 = mybir.dt.uint8
I32 = mybir.dt.int32
ALU = mybir.AluOpType
ACT = mybir.ActivationFunctionType
AX = mybir.AxisListType
ABSMAX = bass.bass_isa.ReduceOp.absmax
ds = bass.ds

P = 128
B, L, D = 128, 32, 128
N_CTX = 257
TOK = B * L
TILES = TOK // P
BPT = P // L
CH = 512
CHUNKS = TOK // CH
H = 16
DH0 = 64
DH1 = D // H
GROUPS = 4
HG = H // GROUPS
KEYS0 = N_CTX + L
TAIL0 = L + 1
EPS = 1e-5
NEG0 = 3e38
NEG1 = 1e9
RNE = 12582912.0
QMAX = 32767.0
FF0 = 384
FB0 = FF0 // P
WBLK = 32
E_N, E_FF = 16, 64
PAIRS = E_N // 2
SH_FF = 352
SH_BLOCKS = [(0, 128), (128, 128), (256, 96)]


class Core:
    pass


def ln_stats(k, stack, name, eng_src, n_tiles):
    nc = k.nc
    stats = stack.enter_context(nc.sbuf_tensor(f"{name}_stats", [P, TILES, 6], F32))
    mean = stack.enter_context(nc.sbuf_tensor(f"{name}_mean", [P, TILES], F32))
    rstd = stack.enter_context(nc.sbuf_tensor(f"{name}_rstd", [P, TILES], F32))
    tmp = stack.enter_context(nc.sbuf_tensor(f"{name}_tmp", [P, 3, TILES], F32))
    chain, var_ready, rstd_ready = k.sem(f"{name}_chain"), k.sem(f"{name}_var_ready"), k.sem(f"{name}_rstd_ready")
    n = n_tiles
    with nc.Block() as block:

        @block.vector
        def _(dve):
            if n == 1:
                nc.vector.bn_stats(stats[:, 0, :], eng_src(0)).then_inc(chain, 8)
            else:
                with dve.Fori(0, n // 4) as g:
                    t = g * 4
                    for j in range(4):
                        last = nc.vector.bn_stats(stats[:, ds(t + j, 1), :], eng_src(t + j))
                    last.then_inc(chain, 1)
            dve.wait_ge(chain, 8)
            nc.vector.tensor_tensor(tmp[:, 0, 0:n], stats[:, 0:n, 1], stats[:, 0:n, 4], ALU.subtract).then_inc(chain, 1)
            nc.vector.tensor_tensor(tmp[:, 1, 0:n], stats[:, 0:n, 2], stats[:, 0:n, 5], ALU.add).then_inc(chain, 1)
            nc.vector.tensor_tensor(tmp[:, 2, 0:n], stats[:, 0:n, 1], stats[:, 0:n, 4], ALU.add).then_inc(chain, 1)
            dve.wait_ge(chain, 11)
            nc.vector.tensor_scalar(mean[:, 0:n], tmp[:, 2, 0:n], 0.5, None, ALU.mult).then_inc(chain, 1)
            nc.vector.scalar_tensor_tensor(tmp[:, 0, 0:n], tmp[:, 0, 0:n], 0.25, tmp[:, 0, 0:n], ALU.mult, ALU.mult).then_inc(chain, 1)
            nc.vector.tensor_scalar(tmp[:, 1, 0:n], tmp[:, 1, 0:n], 1.0 / D, EPS, ALU.mult, ALU.add).then_inc(chain, 1)
            dve.wait_ge(chain, 14)
            nc.vector.tensor_tensor(tmp[:, 1, 0:n], tmp[:, 1, 0:n], tmp[:, 0, 0:n], ALU.add).then_inc(var_ready, 1)

        @block.gpsimd
        def _(pool):
            pool.wait_ge(var_ready, 1)
            nc.gpsimd.tensor_tensor(rstd[:, 0:n], tmp[:, 1, 0:n], k.minus_half[:, 0:n], ALU.pow).then_inc(rstd_ready, 1)
            pool.wait_ge(rstd_ready, 1)
    return mean, rstd


def layer_norm_T(k, name, yT):
    nc = k.nc
    with ExitStack() as stack:
        mean, rstd = ln_stats(k, stack, name, lambda t: k.x[:, ds(t * D, D)], TILES)
        z = stack.enter_context(nc.sbuf_tensor(f"{name}_z", [P, 2, 4, D], F32))
        bank = [stack.enter_context(nc.psum_tensor(f"{name}_ps{u}", [P, CH], F32)) for u in range(2)]
        z_ready, turned, copied = k.sem(f"{name}_z_ready"), k.sem(f"{name}_turned"), k.sem(f"{name}_copied")
        with nc.Block() as block:

            @block.vector
            def _(dve):
                with dve.Fori(0, CHUNKS // 2) as g:
                    c = g * 2
                    for u in range(2):
                        dve.wait_ge(turned, c + (u + 1))
                        for j in range(4):
                            t = c * 4 + (4 * u + j)
                            last = nc.vector.tensor_scalar(z[:, u, j, :], k.x[:, ds(t * D, D)], mean[:, ds(t, 1)],
                                                           rstd[:, ds(t, 1)], ALU.subtract, ALU.mult)
                        last.then_inc(z_ready, 1)

            @block.tensor
            def _(pe):
                pe.sem_inc(turned, 2)
                with pe.Fori(0, CHUNKS // 2) as g:
                    c = g * 2
                    for u in range(2):
                        pe.wait_ge(z_ready, c + (u + 1))
                        pe.wait_ge(copied, c + (u + 1))
                        for j in range(4):
                            last = nc.tensor.transpose(bank[u][:, j * P:(j + 1) * P], z[:, u, j, :], k.ident[:])
                        last.then_inc(turned, 1)

            @block.scalar
            def _(act):
                act.sem_inc(copied, 2)
                with act.Fori(0, CHUNKS // 2) as g:
                    c = g * 2
                    for u in range(2):
                        act.wait_ge(turned, c + (u + 3))
                        nc.scalar.activation(yT[:, ds((c + u) * CH, CH)], bank[u][:], ACT.Copy).then_inc(copied, 1)
                act.wait_ge(copied, CHUNKS + 2)


def setup(k, io):
    nc = k.nc
    keep = k.keep
    sb = lambda name, shape, dt=F32: keep.enter_context(nc.sbuf_tensor(name, shape, dt))
    k.x = sb("x", [P, TILES * D])
    k.ident = sb("ident", [P, P])
    k.minus_half = sb("minus_half", [P, TILES])
    k.rne = sb("rne", [P, 1])
    k.tiny = sb("tiny", [P, 1])
    k.zero = sb("zero", [P, 1])
    k.head_of_feature = sb("head_of_feature", [P, H])
    k.head_in_group4 = sb("head_in_group4", [P, BPT * HG])
    k.group_of_feature = sb("group_of_feature", [GROUPS, P])
    k.batch_in_tile = sb("batch_in_tile", [P, BPT])
    k.fenwick = sb("fenwick", [P, L])
    k.pair_select = sb("pair_select", [E_N, PAIRS, P])
    k.rank = sb("rank", [P, E_N])
    k.own_value = sb("own_value", [P, D])
    k.A = sb("A", [P, H, P])
    k.U = sb("U", [P, H, P])
    k.g1, k.b1, k.g2, k.b2 = (sb(n, [P, D]) for n in ("g1", "b1", "g2", "b2"))
    k.bo, k.bproj = sb("bo", [P, D]), sb("bproj", [P, D])
    k.w_in, k.w_gate = sb("w_inT", [P, P]), sb("w_gateT", [P, P])
    k.wq1, k.wk1, k.wv1, k.wo1 = (sb(n, [P, P]) for n in ("wq1T", "wk1T", "wv1T", "wo1T"))
    k.wqkv, k.wproj = sb("wqkv", [P, 3 * D]), sb("wproj", [P, D])
    k.f_gate, k.f_up, k.f_down = sb("f_gateT", [P, FF0]), sb("f_upT", [P, FF0]), sb("f_downT", [P, FB0, P])
    k.router = sb("router", [P, E_N])
    k.sh_gate_row = sb("sh_gate_row", [P, P])
    k.w_gu = sb("w_gu", [P, 2, E_N, E_FF])
    k.w_dn = sb("w_dn", [P, PAIRS, D])
    k.sh_gate, k.sh_up, k.sh_down = sb("sh_gateT", [P, SH_FF]), sb("sh_upT", [P, SH_FF]), sb("sh_downT", [P, 3, D])
    ROWS = 12
    k.cols = sb("cols", [P, ROWS])
    (k.b_in, k.b_gate, k.lam, k.bq1, k.bk1, k.bv1, k.bq2, k.bk2, k.bv2, k.g2c, k.b2c, k.shg) = (
        k.cols[:, j:j + 1] for j in range(ROWS))
    with ExitStack() as stack:
        tb = lambda name, shape, dt=F32: stack.enter_context(nc.sbuf_tensor(name, shape, dt))
        rows = tb("rows", [ROWS, D])
        wq0, wkv0, wout0 = tb("wq0", [P, H * DH0]), tb("wkv0", [P, 2 * H * DH0]), tb("wout0", [P, H // 2, D])
        wqT, wkT, wvT = (tb(n, [P, H // 2, P]) for n in ("wq0T", "wk0T", "wv0T"))
        sq = tb("square_weights", [P, 6, P])
        fg, fu, fd = tb("fg", [P, FB0, D]), tb("fu", [P, FB0, D]), tb("fd", [P, FB0, P])
        shg, shu, shd = tb("shg", [P, 3, D]), tb("shu", [P, 3, D]), tb("shd", [P, SH_FF])
        rt = tb("rt", [E_N, D])
        shrow = tb("shrow", [P, P])
        m0, m1 = tb("m0", [B, N_CTX], U8), tb("m1", [B, N_CTX], I32)
        m0b, m1b = tb("m0b", [B, N_CTX], BF16), tb("m1b", [B, N_CTX], BF16)
        qs = tb("qs", [P, 3, 2, FB0 * D // WBLK])
        qt = tb("qt", [P, 3, FB0 * D])
        ps = [stack.enter_context(nc.psum_tensor(f"setup_ps{j}", [P, CH], F32)) for j in range(4)]
        loaded, x_loaded = k.sem("weights_loaded"), k.sem("x_loaded")
        ident_ready, consts_ready = k.sem("ident_ready"), k.sem("consts_ready")
        quant, quant_ready = k.sem("quant_chain"), k.sem("weights_quantised")
        turned, copied = k.sem("weights_turned"), k.sem("weights_copied")
        rows_ready, mask_ready, mask_stored = k.sem("shared_gate_row"), k.sem("mask_ready"), k.sem("mask_stored")
        loads = [
            (k.head_of_feature[:], io["c_head_of_feature"]), (k.head_in_group4[:], io["c_head_in_group4"]),
            (k.group_of_feature[:], io["c_group_of_feature"]),
            (k.batch_in_tile[:], io["c_batch_in_tile"]), (k.fenwick[:], io["c_fenwick"]),
            (k.pair_select[:], io["c_pair_select"]), (k.rank[:], io["c_rank"]),
            (k.own_value[:], io["c_own_value"]),
            (wq0[:], io["L0_xattn_Wq"]), (wkv0[:], io["L0_xattn_Wkv"]),
            (wout0[:], io["L0_xattn_Wout"].rearrange("(p r) d -> r p d", r=P)),
            (k.wqkv[:], io["L1_attn_W_qkv"]), (k.wproj[:], io["L1_attn_W_proj"]),
            (k.w_gu[:, 0], io["L1_ffn_w_gate_up"].rearrange("e d f -> d e f")[:, :, 0:E_FF]),
            (k.w_gu[:, 1], io["L1_ffn_w_gate_up"].rearrange("e d f -> d e f")[:, :, E_FF:2 * E_FF]),
            (k.w_dn[:], io["L1_ffn_w_down"].rearrange("(p e) f d -> (e f) p d", e=2)),
            (fg[:], io["L0_ffn_w_gate"].rearrange("(j p) d -> p j d", p=P)),
            (fu[:], io["L0_ffn_w_up"].rearrange("(j p) d -> p j d", p=P)),
            (fd[:].rearrange("p j d -> p (j d)"), io["L0_ffn_w_down"]),
            (shd[:], io["L1_ffn_shared_w_down"]), (rt[:], io["L1_ffn_gate_w"]),
            (m0[:], io["mask_BxS2_bk0"].bitcast(U8).rearrange("(b s) -> b s", b=B)), (m1[:], io["mask_Bx1x1xS2_if1"].rearrange("b o u s -> b (o u s)")),
        ]
        for j, n in enumerate(("L0_attn_W_in", "L0_attn_W_gate", "L1_xattn_W_q", "L1_xattn_W_k", "L1_xattn_W_v", "L1_xattn_W_o")):
            loads.append((sq[:, j, :], io[n]))
        for a, n in ((shg, "L1_ffn_shared_w_gate"), (shu, "L1_ffn_shared_w_up")):
            for j, (r, m) in enumerate(SH_BLOCKS):
                loads.append((a[0:m, j, :], io[n][r:r + m, :]))
        row = lambda ap: ap.rearrange("(a d) -> a d", a=1)
        for n, a in (("L0_xattn_g1", k.g1), ("L0_xattn_b1", k.b1), ("L0_xattn_g2", k.g2), ("L0_xattn_b2", k.b2),
                     ("L1_xattn_b_o", k.bo), ("L1_attn_b_proj", k.bproj)):
            loads.append((a[:], row(io[n]).broadcast_to([P, D])))
        for j, n in enumerate(("L0_attn_b_in", "L0_attn_b_gate", "L0_attn_forget_lambda", "L1_xattn_b_q", "L1_xattn_b_k", "L1_xattn_b_v")):
            loads.append((rows[j:j + 1, :], row(io[n])))
        loads.append((rows[6:9, :], io["L1_attn_b_qkv"].rearrange("(a d) -> a d", a=3)))
        loads.append((rows[9:10, :], row(io["L0_xattn_g2"])))
        loads.append((rows[10:11, :], row(io["L0_xattn_b2"])))
        loads.append((rows[11:12, :], io["L1_ffn_shared_gate_w"]))
        turns = [(k.cols[:].unsqueeze(1), [rows[:]])]
        for w, base, t in ((wq0, 0, wqT), (wkv0, 0, wkT), (wkv0, H * DH0, wvT)):
            for h in range(0, H // 2, 4):
                turns.append((t[:, h:h + 4, :], [w[:, base + (h + j) * P:base + (h + j + 1) * P] for j in range(4)]))
        for j, a in enumerate((k.w_in, k.w_gate, k.wq1, k.wk1, k.wv1, k.wo1)):
            turns.append((a[:].unsqueeze(1), [sq[:, j, :]]))
        turns.append((k.router[:].unsqueeze(1), [rt[:]]))
        for a, t in ((shg, k.sh_gate), (shu, k.sh_up)):
            for j, (r, m) in enumerate(SH_BLOCKS):
                turns.append((t[:, r:r + m].unsqueeze(1), [a[0:m, j, :]]))
        for j, (r, m) in enumerate(SH_BLOCKS):
            turns.append((k.sh_down[0:m, j:j + 1, :], [shd[:, r:r + m]]))
        quant_from = len(turns)
        turns.append((k.f_gate[:].rearrange("p (j o) -> p j o", j=FB0), [fg[:, j, :] for j in range(FB0)]))
        turns.append((k.f_up[:].rearrange("p (j o) -> p j o", j=FB0), [fu[:, j, :] for j in range(FB0)]))
        turns.append((k.f_down[:], [fd[:, j, :] for j in range(FB0)]))
        half = lambda t, h: t[DH0 * (h % 2):DH0 * (h % 2 + 1), h // 2, :]
        products = []
        for h in (0, 1, 8, 9):
            heads = range(h, h + 8, 2)
            products.append((k.A[:, h:h + 7:2, :], [(half(wqT, i), half(wkT, i)) for i in heads]))
            products.append((k.U[:, h:h + 7:2, :], [(half(wvT, i), half(wout0, i)) for i in heads]))

        with nc.Block() as block:

            @block.sync
            def _(sp):
                for dst, src in loads:
                    sp.dma_start(dst, src).then_inc(loaded, 16)
                sp.dma_start(k.x[:].rearrange("p (t d) -> p t d", d=D),
                             io["x"].rearrange("(t b) l d -> (b l) t d", b=BPT)).then_inc(x_loaded, 16)
                sp.wait_ge(mask_ready, 2)
                sp.dma_start(k.keep0, m0b[:]).then_inc(mask_stored, 16)
                sp.dma_start(k.keep1, m1b[:]).then_inc(mask_stored, 16)
                sp.wait_ge(mask_stored, 32)
                sp.wait_ge(x_loaded, 16)

            @block.gpsimd
            def _(pool):
                nc.gpsimd.memset(k.ident[:], 0.0).then_inc(ident_ready, 1)
                nc.gpsimd.memset(k.minus_half[:], -0.5)
                nc.gpsimd.memset(k.rne[:], RNE)
                nc.gpsimd.memset(k.zero[:], 0.0)
                nc.gpsimd.memset(k.tiny[:], 1e-6).then_inc(consts_ready, 1)
                pool.wait_ge(ident_ready, 1)
                nc.gpsimd.affine_select(out=k.ident[:], in_=k.ident[:], compare_op=ALU.not_equal, fill=1.0, base=0,
                                        pattern=[[-1, P]], channel_multiplier=1).then_inc(ident_ready, 1)
                pool.wait_ge(ident_ready, 2)
                pool.wait_ge(consts_ready, 1)

            @block.vector
            def _(dve):
                dve.wait_ge(loaded, 16 * len(loads))
                nc.vector.tensor_copy(m0b[:], m0[:]).then_inc(mask_ready, 1)
                nc.vector.tensor_scalar(m1b[:], m1[:], 0.0, None, ALU.not_equal).then_inc(mask_ready, 1)
                blocks = lambda a: a.rearrange("p j (n e) -> p (j n) e", e=WBLK)
                spread = lambda a: a.unsqueeze(2).broadcast_to([P, FB0 * D // WBLK, WBLK])
                for j, w in enumerate((fg, fu, fd)):
                    nc.vector.tensor_reduce(qs[:, j, 0, :], blocks(w[:]), AX.X, ALU.max, apply_absolute_value=True)\
                        .then_inc(quant, 1)
                dve.wait_ge(quant, 3)
                nc.vector.tensor_scalar(qs[:, :, 0, :], qs[:, :, 0, :], 1.0 / 7.0, 1e-12, ALU.mult, ALU.max).then_inc(quant, 1)
                dve.wait_ge(quant, 4)
                nc.vector.reciprocal(qs[:, :, 1, :], qs[:, :, 0, :]).then_inc(quant, 1)
                dve.wait_ge(quant, 5)
                flat = lambda a, j: a[:, j, :].rearrange("p (n e) -> p n e", e=WBLK)
                for j, w in enumerate((fg, fu, fd)):
                    nc.vector.tensor_tensor(flat(qt, j), blocks(w[:]), spread(qs[:, j, 1, :]), ALU.mult).then_inc(quant, 1)
                dve.wait_ge(quant, 8)
                nc.vector.tensor_scalar(qt[:], qt[:], RNE, -RNE, ALU.add, ALU.add).then_inc(quant, 1)
                dve.wait_ge(quant, 9)
                for j, w in enumerate((fg, fu, fd)):
                    nc.vector.tensor_tensor(blocks(w[:]), flat(qt, j), spread(qs[:, j, 0, :]), ALU.mult).then_inc(quant_ready, 1)
                for n, (dst, srcs) in enumerate(turns):
                    dve.wait_ge(turned, n + 1)
                    m, r = srcs[0].shape[1], srcs[0].shape[0]
                    src = ps[n % 4][0:m, 0:len(srcs) * r].rearrange("p (n r) -> p n r", r=r)
                    nc.vector.tensor_copy(dst, src).then_inc(copied, 1)
                for n, (dst, mms) in enumerate(products):
                    dve.wait_ge(turned, len(turns) + n + 1)
                    src = ps[(len(turns) + n) % 4][:].rearrange("p (n r) -> p n r", r=P)
                    nc.vector.tensor_copy(dst, src).then_inc(copied, 1)
                dve.wait_ge(copied, len(turns) + len(products))
                nc.vector.tensor_copy(k.sh_gate_row[:], k.shg.broadcast_to([P, P])).then_inc(rows_ready, 1)
                dve.wait_ge(rows_ready, 1)

            @block.tensor
            def _(pe):
                pe.wait_ge(loaded, 16 * len(loads))
                pe.wait_ge(ident_ready, 2)
                for n, (dst, srcs) in enumerate(turns):
                    if n == quant_from:
                        pe.wait_ge(quant_ready, 3)
                    if n >= 4:
                        pe.wait_ge(copied, n - 3)
                    m, r = srcs[0].shape[1], srcs[0].shape[0]
                    for j, s in enumerate(srcs):
                        last = nc.tensor.transpose(ps[n % 4][0:m, j * r:(j + 1) * r], s, k.ident[0:r, 0:r])
                    last.then_inc(turned, 1)
                for n, (dst, mms) in enumerate(products):
                    n += len(turns)
                    pe.wait_ge(copied, n - 3)
                    for j, (lhsT, rhs) in enumerate(mms):
                        last = nc.tensor.matmul(ps[n % 4][:, j * P:(j + 1) * P], lhsT, rhs, start=True, stop=True)
                    last.then_inc(turned, 1)


def wait(eng, sem, count):
    if not isinstance(count, int) or count > 0:
        eng.wait_ge(sem, count)


def wait_apart(k, eng, sem, count):
    eng.wait_ge(sem, count)
    eng.sem_inc(k.passed, 1)


def run_steps(eng, step, lead, lag=0):
    for s in range(-lead, 8):
        step(s // 8, s % 8)
    with eng.Fori(1, B // 8 - 1) as g:
        for j in range(8):
            step(g, j)
    for s in range(B - 8, B + lag):
        step(s // 8, s % 8)


def live(g, j, ahead, n=B):
    return not isinstance(g, int) or 0 <= 8 * g + j + ahead < n


def xattn0_inputs(k, io, stack):
    nc = k.nc
    k.latT = stack.enter_context(nc.sbuf_tensor("latT", [P, TOK], F32))
    k.tailT = stack.enter_context(nc.sbuf_tensor("tailT", [P, B], F32))
    with ExitStack() as st:
        z1 = st.enter_context(nc.sbuf_tensor("lat_z1", [P, TILES * D], F32))
        z2 = st.enter_context(nc.sbuf_tensor("lat_z2", [P, 2, 4, D], F32))
        lat = st.enter_context(nc.sbuf_tensor("lat_affine", [P, 2, 4, D], F32))
        tail = st.enter_context(nc.sbuf_tensor("ctx_tail", [P, 3, D], F32))
        bank = [st.enter_context(nc.psum_tensor(f"lat_ps{u}", [P, CH], F32)) for u in range(2)]
        tail_ps = st.enter_context(nc.psum_tensor("lat_ps_tail", [P, P], F32))
        tail_loaded, z1_ready = k.sem("ctx_tail_loaded"), k.sem("lat_z1_ready")
        z2_ready, turned, copied = k.sem("lat_z2_ready"), k.sem("lat_turned"), k.sem("lat_copied")
        scaled, affine_ready, stored = k.sem("lat_scaled"), k.sem("lat_affine_ready"), [k.sem(f"lat_stored{u}") for u in range(2)]
        tail_z, tail_scaled, tail_turned, tail_stored = (k.sem(f"ctx_tail_{n}") for n in ("z", "scaled", "turned", "stored"))
        mean1, rstd1 = ln_stats(k, st, "lat_ln1", lambda t: k.x[:, ds(t * D, D)], TILES)
        with nc.Block() as block:

            @block.vector
            def _(dve):
                with dve.Fori(0, CHUNKS) as c:
                    for j in range(4):
                        t = c * 4 + j
                        last = nc.vector.tensor_scalar(z1[:, ds(t * D, D)], k.x[:, ds(t * D, D)], mean1[:, ds(t, 1)],
                                                       rstd1[:, ds(t, 1)], ALU.subtract, ALU.mult)
                    last.then_inc(z1_ready, 1)
                dve.wait_ge(z1_ready, CHUNKS)

            @block.sync
            def _(sp):
                sp.dma_start(tail[:, 0, :], io["ctx_1024"][:, N_CTX - 1, :]).then_inc(tail_loaded, 16)
                sp.wait_ge(tail_loaded, 16)
        mean2, rstd2 = ln_stats(k, st, "lat_ln2", lambda t: z1[:, ds(t * D, D)], TILES)
        mean3, rstd3 = ln_stats(k, st, "ctx_tail_ln", lambda t: tail[:, 0, :], 1)
        with nc.Block() as block:

            @block.vector
            def _(dve):
                nc.vector.tensor_scalar(tail[:, 1, :], tail[:, 0, :], mean3[:, 0:1], rstd3[:, 0:1], ALU.subtract,
                                        ALU.mult).then_inc(tail_z, 1)
                with dve.Fori(0, CHUNKS // 2) as g:
                    c = g * 2
                    for u in range(2):
                        dve.wait_ge(turned, c + (u + 1))
                        dve.wait_ge(affine_ready, c + (u + 1))
                        for j in range(4):
                            t = c * 4 + (4 * u + j)
                            last = nc.vector.tensor_scalar(z2[:, u, j, :], z1[:, ds(t * D, D)], mean2[:, ds(t, 1)],
                                                           rstd2[:, ds(t, 1)], ALU.subtract, ALU.mult)
                        last.then_inc(z2_ready, 1)
                dve.wait_ge(tail_turned, 1)
                nc.vector.tensor_copy(k.tailT[:], tail_ps[:]).then_inc(tail_turned, 1)
                dve.wait_ge(tail_turned, 2)

            @block.gpsimd
            def _(pool):
                pool.wait_ge(tail_z, 1)
                nc.gpsimd.tensor_tensor(tail[:, 1, :], tail[:, 1, :], k.g1[:], ALU.mult).then_inc(tail_scaled, 1)
                pool.wait_ge(tail_scaled, 1)
                nc.gpsimd.tensor_tensor(tail[:, 2, :], tail[:, 1, :], k.b1[:], ALU.add).then_inc(tail_scaled, 1)
                pool.sem_inc(affine_ready, 2)
                spread = lambda a: a[:].unsqueeze(1).broadcast_to([P, 4, D])
                with pool.Fori(0, CHUNKS // 2) as g:
                    c = g * 2
                    for u in range(2):
                        pool.wait_ge(z2_ready, c + (u + 1))
                        pool.wait_ge(stored[u], g * 16 + 16)
                        nc.gpsimd.tensor_tensor(lat[:, u], z2[:, u], spread(k.g2), ALU.mult).then_inc(scaled, 1)
                        pool.wait_ge(scaled, c + (u + 1))
                        nc.gpsimd.tensor_tensor(lat[:, u], lat[:, u], spread(k.b2), ALU.add).then_inc(affine_ready, 1)

            @block.tensor
            def _(pe):
                pe.sem_inc(turned, 2)
                with pe.Fori(0, CHUNKS // 2) as g:
                    c = g * 2
                    for u in range(2):
                        pe.wait_ge(z2_ready, c + (u + 1))
                        pe.wait_ge(copied, c + (u + 1))
                        for j in range(4):
                            last = nc.tensor.transpose(bank[u][:, j * P:(j + 1) * P], z2[:, u, j, :], k.ident[:])
                        last.then_inc(turned, 1)
                pe.wait_ge(tail_scaled, 2)
                nc.tensor.transpose(tail_ps[:], tail[:, 2, :], k.ident[:]).then_inc(tail_turned, 1)

            @block.scalar
            def _(act):
                act.sem_inc(copied, 2)
                with act.Fori(0, CHUNKS // 2) as g:
                    c = g * 2
                    for u in range(2):
                        act.wait_ge(turned, c + (u + 3))
                        nc.scalar.activation(k.latT[:, ds((c + u) * CH, CH)], bank[u][:], ACT.Identity, bias=k.b2c,
                                             scale=k.g2c).then_inc(copied, 1)
                act.wait_ge(copied, CHUNKS + 2)

            @block.sync
            def _(sp):
                for u in range(2):
                    sp.sem_inc(stored[u], 16)
                with sp.Fori(0, CHUNKS // 2) as g:
                    c = g * 2
                    for u in range(2):
                        sp.wait_ge(affine_ready, c + (u + 3))
                        sp.dma_start(k.lat_dram[ds((c + u) * CH, CH), :].rearrange("(t p) d -> p t d", p=P),
                                     lat[:, u]).then_inc(stored[u], 16)
                sp.wait_ge(tail_scaled, 2)
                sp.dma_start(k.ctx_tail_dram, tail[:, 2, :]).then_inc(tail_stored, 16)
                sp.wait_ge(tail_stored, 16)
                for u in range(2):
                    sp.wait_ge(stored[u], 16 * CHUNKS // 2 + 16)


def xattn0(k, io):
    nc = k.nc
    with ExitStack() as stack:
        xattn0_inputs(k, io, stack)
        sb = lambda name, shape, dt=F32: stack.enter_context(nc.sbuf_tensor(name, shape, dt))
        psum = lambda name: stack.enter_context(nc.psum_tensor(name, [P, CH], F32))
        sem = k.sem
        raw = sb("a_raw", [P, 8, 2, D])
        stats, mv = sb("a_stats", [P, 2, 2, 6]), sb("a_mv", [P, 2, 2, 2])
        var, rstd = sb("a_var", [P, 2, 2]), sb("a_rstd", [P, 2, 2])
        z = sb("a_z", [P, 2, 2, D])
        xn = sb("a_xn", [P, 8, 2, D])
        tail = sb("a_tail", [TAIL0, 8, D])
        xnT = sb("a_xnT", [P, 8, KEYS0])
        kept = sb("a_kept", [P, 2, BPT, N_CTX], BF16)
        bias = sb("a_bias", [P, 8, KEYS0])
        qT = sb("a_qT", [P, 2, BPT, H, L])
        neg = sb("a_neg", [P, GROUPS, KEYS0])
        nmax = sb("a_nmax", [P, 2, GROUPS])
        prob = sb("a_prob", [P, 2, GROUPS, KEYS0])
        rsum, rinv = sb("a_rsum", [P, 2, GROUPS]), sb("a_rinv", [P, 2, GROUPS])
        probT = sb("a_probT", [P, 3, CH])
        oT = sb("a_oT", [P, 2, H, P])
        score_ps, turn_ps = [psum("a_score0"), psum("a_score1")], [psum("a_turn0"), psum("a_turn1")]
        out_ps, ctx_ps, q_ps, proj_ps = psum("a_out"), psum("a_ctx"), psum("a_q"), psum("a_proj")
        raw_loaded = [sem(f"a_raw_loaded{j}") for j in range(8)]
        kept_loaded = [sem(f"a_kept_loaded{u}") for u in range(2)]
        tail_loaded = [sem(f"a_tail_loaded{u}") for u in range(2)]
        stats_ready, mv_ready, var_ready, rstd_ready = sem("a_stats_ready"), sem("a_mv_ready"), sem("a_var_ready"), sem("a_rstd_ready")
        z_ready, scaled, xn_ready = sem("a_z_ready"), sem("a_scaled"), sem("a_xn_ready")
        ctx_turned, xnT_ready, keys_ready = sem("a_ctx_turned"), sem("a_xnT_ready"), sem("a_tile_keys_ready")
        q_ready, q_copied = sem("a_q_ready"), sem("a_q_copied")
        scored, masked, exped, rinv_ready, prob_ready = (sem(f"a_{n}") for n in ("scored", "masked", "exped", "rinv_ready", "prob_ready"))
        turned, probT_ready = [sem(f"a_turned{n}") for n in range(3)], [sem(f"a_probT_ready{n}") for n in range(3)]
        out_ready, oT_ready, proj_ready, x_added = (sem(f"a_{n}") for n in ("out_ready", "oT_ready", "proj_ready", "x_added"))
        zeroed = sem("a_zeroed")
        LEAD, LAG = 5, 1
        TKEYS = (P, P, TAIL0)

        def tile_of(g, j, ahead=0):
            return g * 2 + (j + ahead) // 4

        def quarter(b):
            return (1, b + 1) if b < 3 else (2, 0)

        with nc.Block() as block:

            @block.sync
            def _(sp):
                def load_raw(g, j):
                    sp.dma_start(raw[:, j % 8], io["ctx_1024"][ds(g * 8 + j, 1), 0:2 * P, :].rearrange(
                        "b (t p) d -> p (b t) d", p=P)).then_inc(raw_loaded[j % 8], 16)

                def load_kept(t, u):
                    sp.dma_start(kept[:, u], k.keep0[ds(t * BPT, BPT), :].unsqueeze(0).broadcast_to([P, BPT, N_CTX]))\
                        .then_inc(kept_loaded[u], 16)

                def step(g, j):
                    s, t, u, b = g * 8 + j, tile_of(g, j), j // 4, j % 4
                    if live(g, j, 8):
                        wait(sp, z_ready, s + 1)
                        load_raw(g + 1, j)
                    if b == 0 and live(g, j, 8):
                        wait(sp, keys_ready, t + 1)
                        load_kept(t + 2, u)
                    if b == 3 and live(g, j, 8):
                        wait(sp, out_ready, s + 1)
                        rows = slice(4 * u, 4 * u + 4)
                        sp.dma_start(tail[0:L, rows, :], k.lat_dram[ds((t + 2) * P, P), :].rearrange(
                            "(b l) d -> l b d", l=L)).then_inc(tail_loaded[u], 16)
                        sp.dma_start(tail[L:L + 1, rows, :], k.ctx_tail_dram[ds((t + 2) * BPT, BPT), :].unsqueeze(0))\
                            .then_inc(tail_loaded[u], 16)

                for j in range(3):
                    load_raw(0, j)
                load_kept(0, 0)
                run_steps(sp, step, LEAD)

            @block.gpsimd
            def _(pool):
                nc.gpsimd.memset(bias[:, :, 2 * P:2 * P + L], 0.0).then_inc(zeroed, 1)
                spread = lambda a: a[:].unsqueeze(1).broadcast_to([P, 2, D])

                def step(g, j):
                    s, t, u, b = g * 8 + j, tile_of(g, j), j // 4, j % 4
                    if live(g, j, 4):
                        n, par = (j + 4) % 8, j % 2
                        pool.wait_ge(z_ready, s + 5)
                        nc.gpsimd.tensor_tensor(xn[:, n], z[:, par], spread(k.g1), ALU.mult).then_inc(scaled, 1)
                        pool.wait_ge(scaled, s + 5)
                        nc.gpsimd.tensor_tensor(xn[:, n], xn[:, n], spread(k.b1), ALU.add).then_inc(xn_ready, 1)
                    if live(g, j, 5):
                        par = (j + 5) % 2
                        wait_apart(k, pool, mv_ready, s + 6)
                        nc.gpsimd.tensor_scalar(var[:, par], mv[:, par, :, 1], EPS, None, ALU.add).then_inc(var_ready, 1)
                        pool.wait_ge(var_ready, s + 6)
                        nc.gpsimd.tensor_tensor(rstd[:, par], var[:, par], k.minus_half[:, 0:2], ALU.pow).then_inc(rstd_ready, 1)
                    if b == 3 and live(g, j, 8):
                        slots = slice(4 * u, 4 * u + 4)
                        wait(pool, masked, s * 4 + 8 - 4)
                        nc.gpsimd.tensor_copy(xnT[:, slots, 2 * P:2 * P + L],
                                              k.latT[:, ds((t + 2) * P, P)].rearrange("p (b l) -> p b l", l=L))
                        nc.gpsimd.tensor_copy(xnT[:, slots, KEYS0 - 1:KEYS0], k.tailT[:, ds((t + 2) * BPT, BPT)].unsqueeze(2))
                        wait_apart(k, pool, kept_loaded[u], (g + 2) * 16)
                        nc.gpsimd.tensor_scalar(bias[:, slots, 0:2 * P], kept[:, u, :, 0:2 * P], NEG0, -NEG0, ALU.mult, ALU.add)
                        nc.gpsimd.tensor_scalar(bias[:, slots, KEYS0 - 1:KEYS0], kept[:, u, :, 2 * P:N_CTX], NEG0, -NEG0,
                                                ALU.mult, ALU.add).then_inc(keys_ready, 1)

                run_steps(pool, step, LEAD)

            @block.vector
            def _(dve):
                def mask(g, j, grp):
                    s, n, par = g * 8 + j, (j + 1) % 8, (j + 1) % 2
                    if n % 4 == 0 and grp == 0:
                        dve.wait_ge(keys_ready, tile_of(g, j, 1) + 1)
                    wait_apart(k, dve, scored, s * 4 + (5 + grp))
                    nc.vector.tensor_tensor_reduce(
                        out=neg[:, grp, :], in0=score_ps[grp % 2][:, 0:KEYS0], in1=bias[:, n, :], scale=-DH0 ** -0.5,
                        scalar=3.4e38, op0=ALU.add, op1=ALU.min, accum_out=nmax[:, par, grp:grp + 1]).then_inc(masked, 1)

                def step(g, j):
                    s, t, u, b = g * 8 + j, tile_of(g, j), j // 4, j % 4
                    if live(g, j, 1):
                        mask(g, j, 0)
                        mask(g, j, 1)
                    if live(g, j, 0):
                        dve.wait_ge(turned[0], s + 1)
                        nc.vector.tensor_copy(probT[:, 0, :], turn_ps[0][:]).then_inc(probT_ready[0], 1)
                    if live(g, j, 1):
                        mask(g, j, 2)
                        mask(g, j, 3)
                    if live(g, j, 5):
                        n, par = (j + 5) % 8, (j + 5) % 2
                        dve.wait_ge(raw_loaded[n], (g + (j + 5) // 8 + 1) * 16)
                        for kt in range(2):
                            last = nc.vector.bn_stats(stats[:, par, kt, :], raw[:, n, kt, :])
                        last.then_inc(stats_ready, 1)
                    if live(g, j, 4):
                        n, par = (j + 4) % 8, j % 2
                        dve.wait_ge(rstd_ready, s + 5)
                        wait(dve, xn_ready, s + 3)
                        for kt in range(2):
                            last = nc.vector.tensor_scalar(z[:, par, kt, :], raw[:, n, kt, :], mv[:, par, kt, 0:1],
                                                           rstd[:, par, kt:kt + 1], ALU.subtract, ALU.mult)
                        last.then_inc(z_ready, 1)
                    if live(g, j, 5):
                        par = (j + 5) % 2
                        wait_apart(k, dve, stats_ready, s + 6)
                        for kt in range(2):
                            last = nc.vector.bn_aggr(mv[:, par, kt, :], stats[:, par, kt, :])
                        last.then_inc(mv_ready, 1)
                    if live(g, j, 1):
                        par = (j + 1) % 2
                        dve.wait_ge(exped, s * 4 + 8)
                        nc.vector.reciprocal(rinv[:, par, :], rsum[:, par, :]).then_inc(rinv_ready, 1)
                        dve.wait_ge(rinv_ready, s + 2)
                        for grp in range(GROUPS):
                            last = nc.vector.tensor_scalar(prob[:, par, grp, :], prob[:, par, grp, :],
                                                           rinv[:, par, grp:grp + 1], None, ALU.mult)
                        last.then_inc(prob_ready, 1)
                    if live(g, j, 3):
                        dve.wait_ge(ctx_turned, s + 4)
                        nc.vector.tensor_copy(xnT[:, (j + 3) % 8, 0:2 * P], ctx_ps[:, 0:2 * P]).then_inc(xnT_ready, 1)
                    if b == 0 and live(g, j, -1):
                        dve.wait_ge(proj_ready, t)
                        xt = k.x[:, ds((t - 1) * D, D)]
                        nc.vector.tensor_tensor(xt, proj_ps[:, 0:D], xt, ALU.add).then_inc(x_added, 1)

                dve.wait_ge(zeroed, 1)
                run_steps(dve, step, LEAD, LAG)
                dve.wait_ge(x_added, TILES)

            @block.scalar
            def _(act):
                def exp(g, j, grp):
                    s, par = g * 8 + j, (j + 1) % 2
                    act.wait_ge(masked, s * 4 + (5 + grp))
                    nc.scalar.activation(prob[:, par, grp, :], neg[:, grp, :], ACT.Exp, bias=nmax[:, par, grp:grp + 1],
                                         scale=-1.0, accum_out=rsum[:, par, grp:grp + 1]).then_inc(exped, 1)

                def step(g, j):
                    s, t, u, b = g * 8 + j, tile_of(g, j), j // 4, j % 4
                    if live(g, j, 1):
                        exp(g, j, 0)
                        exp(g, j, 1)
                    if live(g, j, 0):
                        act.wait_ge(turned[1], s + 1)
                        nc.scalar.activation(probT[:, 1, :], turn_ps[1][:], ACT.Copy).then_inc(probT_ready[1], 1)
                    if live(g, j, 1):
                        exp(g, j, 2)
                        exp(g, j, 3)
                    if live(g, j, 0):
                        act.wait_ge(turned[2], s + 1)
                        nc.scalar.activation(probT[0:TAIL0, 2, :], turn_ps[0][0:TAIL0, :], ACT.Copy).then_inc(probT_ready[2], 1)
                    ahead, hg = quarter(b)
                    if live(g, j, 4 * ahead - b):
                        act.wait_ge(q_ready, (t + ahead) * 4 + (hg + 1))
                        nc.scalar.activation(
                            qT[:, (u + ahead) % 2, :, 4 * hg:4 * hg + 4, :].rearrange("p b h l -> p h b l"),
                            q_ps[:].rearrange("p (h b l) -> p h b l", h=4, l=L), ACT.Copy).then_inc(q_copied, 1)
                    if live(g, j, 0):
                        act.wait_ge(out_ready, s + 1)
                        nc.scalar.activation(oT[:, u, :, b * L:(b + 1) * L], out_ps[:].rearrange("p (h l) -> p h l", l=L),
                                             ACT.Copy).then_inc(oT_ready, 1)

                run_steps(act, step, LEAD, LAG)

            @block.tensor
            def _(pe):
                def score(g, j, grp):
                    s, n, un, bn = g * 8 + j, (j + 1) % 8, (j + 1) // 4 % 2, (j + 1) % 4
                    if grp == 0:
                        pe.wait_ge(xnT_ready, s + 2)
                        if bn == 0:
                            pe.wait_ge(keys_ready, tile_of(g, j, 1) + 1)
                            pe.wait_ge(q_copied, tile_of(g, j, 1) * 4 + 4)
                    wait(pe, masked, s * 4 + (3 + grp))
                    nc.tensor.matmul(score_ps[grp % 2][:, 0:KEYS0], qT[:, un, bn, 4 * grp:4 * grp + 4, :], xnT[:, n, :],
                                     start=True, stop=True).then_inc(scored, 1)

                def turn(g, j, kt):
                    s, m = g * 8 + j, TKEYS[kt]
                    if kt == 0:
                        pe.wait_ge(prob_ready, s + 1)
                        wait(pe, probT_ready[2], s)
                    if kt == 2:
                        wait_apart(k, pe, probT_ready[0], s + 1)
                    for grp in range(GROUPS):
                        last = nc.tensor.transpose(turn_ps[kt % 2][0:m, grp * P:(grp + 1) * P],
                                                   prob[:, j % 2, grp, kt * P:kt * P + m], k.ident[:])
                    last.then_inc(turned[kt], 1)

                def values(g, j, kt):
                    s, m = g * 8 + j, TKEYS[kt]
                    pe.wait_ge(probT_ready[kt], s + 1)
                    if kt == 0:
                        wait(pe, oT_ready, s)
                    if kt == 2 and j % 4 == 0:
                        pe.wait_ge(tail_loaded[j // 4], (g + 1) * 32)
                    lhsT = xn[:, j, kt, :] if kt < 2 else tail[:, j, :]
                    last = nc.tensor.matmul(out_ps[:], lhsT, probT[0:m, kt, :], start=(kt == 0), stop=(kt == 2))
                    if kt == 2:
                        last.then_inc(out_ready, 1)

                def query(g, j):
                    ahead, hg = quarter(j % 4)
                    t = tile_of(g, j)
                    wait(pe, q_copied, (t + ahead) * 4 + hg)
                    for h in range(4):
                        last = nc.tensor.matmul(q_ps[:, h * P:(h + 1) * P], k.A[:, 4 * hg + h, :],
                                                k.latT[:, ds((t + ahead) * P, P)], start=True, stop=True)
                    last.then_inc(q_ready, 1)

                def step(g, j):
                    s, t, u, b = g * 8 + j, tile_of(g, j), j // 4, j % 4
                    here, ahead = live(g, j, 0), live(g, j, 1)
                    if ahead:
                        score(g, j, 0)
                        score(g, j, 1)
                    if here:
                        turn(g, j, 0)
                        turn(g, j, 1)
                    if ahead:
                        score(g, j, 2)
                        score(g, j, 3)
                    if b == 0 and live(g, j, -1):
                        pe.wait_ge(oT_ready, s)
                        wait(pe, x_added, t - 1)
                        for h in range(H):
                            last = nc.tensor.matmul(proj_ps[:, 0:D], oT[:, 1 - u, h, :], k.U[:, h, :], start=(h == 0),
                                                    stop=(h == H - 1))
                        last.then_inc(proj_ready, 1)
                    if here:
                        values(g, j, 0)
                        turn(g, j, 2)
                    if live(g, j, 4 * quarter(b)[0] - b):
                        query(g, j)
                    if here:
                        values(g, j, 1)
                        values(g, j, 2)
                    if live(g, j, 3):
                        n = (j + 3) % 8
                        pe.wait_ge(xn_ready, s + 4)
                        wait(pe, xnT_ready, s + 3)
                        for kt in range(2):
                            last = nc.tensor.transpose(ctx_ps[:, kt * P:(kt + 1) * P], xn[:, n, kt, :], k.ident[:])
                        last.then_inc(ctx_turned, 1)

                run_steps(pe, step, LEAD, LAG)


def rglru0(k, io):
    nc = k.nc
    with ExitStack() as stack:
        sb = lambda name, shape: stack.enter_context(nc.sbuf_tensor(name, shape, F32))
        psum = lambda name: stack.enter_context(nc.psum_tensor(name, [P, CH], F32))
        sem = k.sem
        yT = sb("r_yT", [P, TOK])
        layer_norm_T(k, "r_ln", yT)
        gate_in, alpha = sb("r_gate_in", [P, TOK]), sb("r_alpha", [P, TOK])
        sp_ = sb("r_softplus", [P, 6])
        beta, square, drive, h = (sb(f"r_{n}", [P, 2, CH]) for n in ("beta", "square", "drive", "h"))
        in_ps, rec_ps = [psum("r_in0"), psum("r_in1")], [psum("r_rec0"), psum("r_rec1")]
        hT_ps = [psum("r_hT0"), psum("r_hT1")]
        gates_done, gates_read, chain = sem("r_gates_done"), sem("r_gates_read"), sem("r_softplus_chain")
        with nc.Block() as block:

            @block.tensor
            def _(pe):
                with pe.Fori(0, CHUNKS // 2) as g:
                    c = g * 2
                    for u in range(2):
                        pe.wait_ge(gates_read, c + (u + 1))
                        y = yT[:, ds((c + u) * CH, CH)]
                        nc.tensor.matmul(in_ps[u][:], k.w_in[:], y, start=True, stop=True)
                        nc.tensor.matmul(rec_ps[u][:], k.w_gate[:], y, start=True, stop=True).then_inc(gates_done, 1)

            @block.scalar
            def _(act):
                act.wait_ge(chain, 1)
                nc.scalar.activation(sp_[:, 1:2], sp_[:, 0:1], ACT.Exp, scale=-1.0).then_inc(chain, 1)
                act.sem_inc(gates_read, 2)
                with act.Fori(0, CHUNKS // 2) as g:
                    c = g * 2
                    for u in range(2):
                        act.wait_ge(gates_done, c + (u + 1))
                        cols = ds((c + u) * CH, CH)
                        nc.scalar.activation(gate_in[:, cols], in_ps[u][:], ACT.Sigmoid, bias=k.b_in)
                        nc.scalar.activation(alpha[:, cols], rec_ps[u][:], ACT.Sigmoid, bias=k.b_gate).then_inc(gates_read, 1)
                act.wait_ge(gates_read, CHUNKS + 2)
                act.wait_ge(chain, 17)
                nc.scalar.activation(alpha[:], alpha[:], ACT.Exp, scale=sp_[:, 5:6]).then_inc(gates_read, 1)
                act.wait_ge(gates_read, CHUNKS + 3)

            @block.vector
            def _(dve):
                size, e, q, q2, t, rate = (sp_[:, j:j + 1] for j in range(6))
                nc.vector.scalar_tensor_tensor(size, k.lam, -1.0, k.lam, ALU.mult, ALU.max).then_inc(chain, 1)
                dve.wait_ge(chain, 2)
                nc.vector.tensor_scalar(q, e, 2.0, None, ALU.add).then_inc(chain, 1)
                dve.wait_ge(chain, 3)
                nc.vector.reciprocal(q, q).then_inc(chain, 1)
                dve.wait_ge(chain, 4)
                nc.vector.tensor_tensor(q, q, e, ALU.mult).then_inc(chain, 1)
                dve.wait_ge(chain, 5)
                nc.vector.tensor_tensor(q2, q, q, ALU.mult).then_inc(chain, 1)
                dve.wait_ge(chain, 6)
                nc.vector.tensor_scalar(t, q2, 1.0 / 17, None, ALU.mult).then_inc(chain, 1)
                for n, odd in enumerate((15, 13, 11, 9, 7, 5, 3)):
                    dve.wait_ge(chain, 7 + n)
                    nc.vector.scalar_tensor_tensor(t, t, 1.0 / odd, q2, ALU.add, ALU.mult).then_inc(chain, 1)
                dve.wait_ge(chain, 14)
                nc.vector.scalar_tensor_tensor(t, t, 1.0, q, ALU.add, ALU.mult).then_inc(chain, 1)
                nc.vector.tensor_scalar(q2, k.lam, 0.0, -8.0, ALU.max, ALU.mult).then_inc(chain, 1)
                dve.wait_ge(chain, 16)
                nc.vector.scalar_tensor_tensor(rate, t, -16.0, q2, ALU.mult, ALU.add).then_inc(chain, 1)
                dve.wait_ge(chain, 17)
        squared, rooted, driven, cleared, scanned, turned, added = (
            sem(f"r_{n}") for n in ("squared", "rooted", "driven", "cleared", "scanned", "turned", "added"))
        half_driven = sem("r_half_driven")
        with nc.Block() as block:

            @block.gpsimd
            def _(pool):
                pool.sem_inc(rooted, 2)
                with pool.Fori(0, CHUNKS // 2) as g:
                    c = g * 2
                    for u in range(2):
                        a = alpha[:, ds((c + u) * CH, CH)]
                        pool.wait_ge(rooted, c + (u + 1))
                        nc.gpsimd.tensor_tensor(square[:, u], a, a, ALU.mult).then_inc(squared, 1)

            @block.scalar
            def _(act):
                with act.Fori(0, CHUNKS // 2) as g:
                    c = g * 2
                    for u in range(2):
                        act.wait_ge(driven, c * 2 + (2 * u + 1))
                        nc.scalar.activation(beta[:, u], beta[:, u], ACT.Sqrt, bias=k.tiny[:]).then_inc(rooted, 1)

            @block.vector
            def _(dve):
                def start(g, u):
                    c = g * 2
                    cols = ds((c + u) * CH, CH)
                    dve.wait_ge(squared, c + (u + 1))
                    nc.vector.tensor_scalar(beta[:, u], square[:, u], -1.0, 1.0, ALU.mult, ALU.add).then_inc(driven, 1)
                    nc.vector.tensor_tensor(drive[:, u], gate_in[:, cols], yT[:, cols], ALU.mult).then_inc(driven, 1)

                def finish(g, u):
                    c = g * 2
                    cols = ds((c + u) * CH, CH)
                    nc.vector.tensor_copy(alpha[:, ds((c + u) * CH, CH)].rearrange("p (b l) -> p b l", l=L)[:, :, 0:1],
                                          k.zero[:].unsqueeze(1).broadcast_to([P, CH // L, 1])).then_inc(cleared, 1)
                    dve.wait_ge(rooted, c + (u + 3))
                    dve.wait_ge(driven, c * 2 + (2 * u + 2))
                    nc.vector.tensor_tensor(drive[:, u], drive[:, u], beta[:, u], ALU.mult).then_inc(half_driven, 1)
                    dve.wait_ge(half_driven, c + (u + 1))
                    dve.wait_ge(cleared, c + (u + 1))
                    dve.wait_ge(turned, c + (u + 1))
                    nc.vector.tensor_tensor_scan(h[:, u], alpha[:, cols], drive[:, u], 0.0, ALU.mult, ALU.add)\
                        .then_inc(scanned, 1)

                def add(g, u):
                    c = g * 2
                    dve.wait_ge(turned, c + (u + 3))
                    xc = k.x[:, ds((c + u) * CH, CH)]
                    nc.vector.tensor_tensor(xc, hT_ps[u][:], xc, ALU.add).then_inc(added, 1)

                dve.sem_inc(added, 1)
                with dve.Fori(0, CHUNKS // 2) as g:
                    start(g, 0)
                    start(g, 1)
                    finish(g, 0)
                    finish(g, 1)
                    add(g, 0)
                    add(g, 1)
                dve.wait_ge(added, CHUNKS + 1)

            @block.tensor
            def _(pe):
                pe.sem_inc(turned, 2)
                with pe.Fori(0, CHUNKS // 2) as g:
                    c = g * 2
                    for u in range(2):
                        pe.wait_ge(scanned, c + (u + 1))
                        pe.wait_ge(added, c + 1)
                        for j in range(4):
                            last = nc.tensor.transpose(hT_ps[u][:, j * P:(j + 1) * P], h[:, u, j * P:(j + 1) * P], k.ident[:])
                        last.then_inc(turned, 1)


def tensor_scale(k, name, stack, eng_max):
    nc = k.nc
    q = stack.enter_context(nc.sbuf_tensor(f"{name}_scale", [P, 4], F32))
    chain, reduced = k.sem(f"{name}_chain"), k.sem(f"{name}_reduced")
    with nc.Block() as block:

        @block.vector
        def _(dve):
            nc.vector.tensor_reduce(q[:, 0:1], eng_max, AX.X, ALU.max, apply_absolute_value=True).then_inc(chain, 1)
            dve.wait_ge(reduced, 1)
            nc.vector.tensor_scalar(q[:, 2:3], q[:, 1:2], 1.0 / QMAX, 1e-12, ALU.mult, ALU.max).then_inc(chain, 1)
            dve.wait_ge(chain, 2)
            nc.vector.reciprocal(q[:, 3:4], q[:, 2:3]).then_inc(chain, 1)
            dve.wait_ge(chain, 3)

        @block.gpsimd
        def _(pool):
            pool.wait_ge(chain, 1)
            nc.gpsimd.partition_all_reduce(q[:, 1:2], q[:, 0:1], P, ABSMAX).then_inc(reduced, 1)
            pool.wait_ge(reduced, 1)
    return q[:, 2:3], q[:, 3:4]


def ffn0(k, io):
    nc = k.nc
    with ExitStack() as stack:
        sb = lambda name, shape: stack.enter_context(nc.sbuf_tensor(name, shape, F32))
        sem = k.sem
        yT = sb("f_yT", [P, TOK])
        layer_norm_T(k, "f_ln", yT)
        up, gate = sb("f_up", [P, FB0, TOK]), sb("f_gate", [P, FB0, TOK])
        maxima = sb("f_max", [P, 2, CHUNKS, FB0])
        W = 2 * CH
        STEPS = TOK // W
        part = sb("f_part", [P, 4, W])
        gs_max, o_max = sb("f_gs_max", [P, STEPS * FB0]), sb("f_o_max", [P, STEPS * FB0])
        step, inv = tensor_scale(k, "f_y", stack, yT[:])
        with ExitStack() as st:
            up_ps, gate_ps = ([st.enter_context(nc.psum_tensor(f"f_{n}{j}", [P, CH], F32)) for j in range(FB0)] for n in ("up", "gate"))
            scaled, y_ready = sem("f_y_scaled"), sem("f_y_ready")
            done = {"up": sem("f_up_done"), "gate": sem("f_gate_done")}
            copied = {"up": sem("f_up_copied"), "gate": sem("f_gate_copied")}
            maxed = {"up": sem("f_up_maxed"), "gate": sem("f_gate_maxed")}
            sides = (("up", up, up_ps, k.f_up), ("gate", gate, gate_ps, k.f_gate))
            with nc.Block() as block:

                @block.scalar
                def _(act):
                    with act.Fori(0, CHUNKS) as c:
                        cols = ds(c * CH, CH)
                        nc.scalar.activation(yT[:, cols], yT[:, cols], ACT.Identity, bias=k.rne[:], scale=inv).then_inc(scaled, 1)
                    act.sem_inc(copied["gate"], 1)
                    act.sem_inc(copied["up"], 1)
                    with act.Fori(0, CHUNKS) as c:
                        for n, t, ps, w in sides:
                            act.wait_ge(done[n], c + 1)
                            for j in range(FB0):
                                last = nc.scalar.activation(t[:, j, ds(c * CH, CH)], ps[j][:], ACT.Copy)
                            last.then_inc(copied[n], 1)
                    act.wait_ge(copied["gate"], CHUNKS + 1)
                    act.wait_ge(copied["up"], CHUNKS + 1)

                @block.vector
                def _(dve):
                    def quantise(c):
                        cols = ds(c * CH, CH)
                        dve.wait_ge(scaled, c + 1)
                        nc.vector.tensor_scalar(yT[:, cols], yT[:, cols], -RNE, step, ALU.add, ALU.mult).then_inc(y_ready, 1)

                    def chunk(c, more):
                        for i, (n, t, ps, w) in enumerate(sides):
                            dve.wait_ge(copied[n], c + 2)
                            nc.vector.tensor_reduce(maxima[:, i, ds(c, 1), :], t[:, :, ds(c * CH, CH)], AX.X, ALU.max,
                                                    apply_absolute_value=True).then_inc(maxed[n], 1)
                            if i == 0 and more:
                                quantise(c + 1)

                    quantise(0)
                    with dve.Fori(0, CHUNKS - 1) as c:
                        chunk(c, True)
                    chunk(CHUNKS - 1, False)
                    dve.wait_ge(maxed["gate"], CHUNKS)
                    dve.wait_ge(maxed["up"], CHUNKS)

                @block.tensor
                def _(pe):
                    with pe.Fori(0, CHUNKS) as c:
                        pe.wait_ge(y_ready, c + 1)
                        for n, t, ps, w in sides:
                            pe.wait_ge(copied[n], c + 1)
                            for j in range(FB0):
                                last = nc.tensor.matmul(ps[j][:], w[:, j * P:(j + 1) * P], yT[:, ds(c * CH, CH)],
                                                        start=True, stop=True)
                            last.then_inc(done[n], 1)
        up_step, up_inv = tensor_scale(k, "f_u", stack, maxima[:, 0].rearrange("p c j -> p (c j)"))
        gate_step, gate_inv = tensor_scale(k, "f_g", stack, maxima[:, 1].rearrange("p c j -> p (c j)"))
        up_scaled, up_ready = sem("f_u_scaled"), sem("f_u_ready")
        g_scaled, g_ready, sig_ready, sig_rounded, sig_used, gs_ready = (
            sem(f"f_{n}") for n in ("g_scaled", "g_ready", "sig_ready", "sig_rounded", "sig_used", "gs_ready"))
        maxed = sem("f_gs_maxed")
        with nc.Block() as block:

            @block.scalar
            def _(act):
                act.sem_inc(sig_used, 2)
                with act.Fori(0, STEPS) as c:
                    cols = ds(c * W, W)
                    for j in range(FB0):
                        n, u = c * FB0 + j, j % 2
                        nc.scalar.activation(gate[:, j, cols], gate[:, j, cols], ACT.Identity, bias=k.rne[:], scale=gate_inv)\
                            .then_inc(g_scaled, 1)
                        nc.scalar.activation(up[:, j, cols], up[:, j, cols], ACT.Identity, bias=k.rne[:], scale=up_inv)\
                            .then_inc(up_scaled, 1)
                        act.wait_ge(sig_used, n + 1)
                        wait_apart(k, act, g_ready, n + 1)
                        nc.scalar.activation(part[:, j, :], gate[:, j, cols], ACT.Sigmoid).then_inc(sig_ready, 1)
                        act.wait_ge(sig_ready, n + 1)
                        nc.scalar.activation(part[:, j, :], part[:, j, :], ACT.Identity, bias=k.rne[:], scale=65536.0)\
                            .then_inc(sig_rounded, 1)

            @block.vector
            def _(dve):
                with dve.Fori(0, STEPS) as c:
                    cols = ds(c * W, W)
                    for j in range(FB0):
                        n = c * FB0 + j
                        g, s = gate[:, j, cols], part[:, j, :]
                        dve.wait_ge(g_scaled, n + 1)
                        nc.vector.tensor_scalar(g, g, -RNE, gate_step, ALU.add, ALU.mult).then_inc(g_ready, 1)
                        dve.wait_ge(up_scaled, n + 1)
                        nc.vector.tensor_scalar(up[:, j, cols], up[:, j, cols], -RNE, up_step, ALU.add, ALU.mult).then_inc(up_ready, 1)
                        dve.wait_ge(sig_rounded, n + 1)
                        nc.vector.tensor_scalar(s, s, -RNE, 65535.0, ALU.add, ALU.min).then_inc(gs_ready, 1)
                        dve.wait_ge(gs_ready, n * 2 + 1)
                        nc.vector.scalar_tensor_tensor(g, s, 1.0 / 65536, g, ALU.mult, ALU.mult).then_inc(gs_ready, 1)
                        dve.wait_ge(gs_ready, n * 2 + 2)
                        nc.vector.tensor_reduce(gs_max[:, ds(n, 1)], g, AX.X, ALU.max, apply_absolute_value=True).then_inc(maxed, 1)
                        dve.sem_inc(sig_used, 1)
                dve.wait_ge(maxed, STEPS * FB0)
                dve.wait_ge(up_ready, STEPS * FB0)
        gs_step, gs_inv = tensor_scale(k, "f_gs", stack, gs_max[:])
        gs_scaled, gs_quantised, o_ready, o_maxed = (sem(f"f_{n}") for n in ("gs_scaled", "gs_quantised", "o_ready", "o_maxed"))
        with nc.Block() as block:

            @block.scalar
            def _(act):
                with act.Fori(0, STEPS) as c:
                    for j in range(FB0):
                        g = gate[:, j, ds(c * W, W)]
                        nc.scalar.activation(g, g, ACT.Identity, bias=k.rne[:], scale=gs_inv).then_inc(gs_scaled, 1)

            @block.vector
            def _(dve):
                with dve.Fori(0, STEPS) as c:
                    for j in range(FB0):
                        n = c * FB0 + j
                        g, o = gate[:, j, ds(c * W, W)], up[:, j, ds(c * W, W)]
                        dve.wait_ge(gs_scaled, n + 1)
                        nc.vector.tensor_scalar(g, g, -RNE, gs_step, ALU.add, ALU.mult).then_inc(gs_quantised, 1)
                        dve.wait_ge(gs_quantised, n + 1)
                        nc.vector.tensor_tensor(o, g, o, ALU.mult).then_inc(o_ready, 1)
                        dve.wait_ge(o_ready, n + 1)
                        nc.vector.tensor_reduce(o_max[:, ds(n, 1)], o, AX.X, ALU.max, apply_absolute_value=True).then_inc(o_maxed, 1)
                dve.wait_ge(o_maxed, STEPS * FB0)
        o_step, o_inv = tensor_scale(k, "f_o", stack, o_max[:])
        down_ps, turn_ps = ([stack.enter_context(nc.psum_tensor(f"f_{n}{u}", [P, CH], F32)) for u in range(2)] for n in ("down", "turn"))
        o_scaled, o_quantised, down_done, down_copied, turned, added = (
            sem(f"f_{n}") for n in ("o_scaled", "o_quantised", "down_done", "down_copied", "turned", "added"))
        with nc.Block() as block:

            @block.scalar
            def _(act):
                def scale_o(c):
                    o = up[:, :, ds(c * CH, CH)]
                    nc.scalar.activation(o, o, ACT.Identity, bias=k.rne[:], scale=o_inv).then_inc(o_scaled, 1)

                def two_chunks(c, more):
                    for u in range(2):
                        if more:
                            scale_o(c + (2 + u))
                        act.wait_ge(down_done, c + (u + 1))
                        act.wait_ge(turned, c + (u + 1))
                        nc.scalar.activation(part[:, u, 0:CH], down_ps[u][:], ACT.Copy).then_inc(down_copied, 1)

                scale_o(0)
                scale_o(1)
                act.sem_inc(down_copied, 1)
                act.sem_inc(turned, 2)
                with act.Fori(0, CHUNKS // 2 - 1) as g:
                    two_chunks(g * 2, True)
                two_chunks(CHUNKS - 2, False)

            @block.vector
            def _(dve):
                def quantise(c):
                    o = up[:, :, ds(c * CH, CH)]
                    dve.wait_ge(o_scaled, c + 1)
                    nc.vector.tensor_scalar(o, o, -RNE, o_step, ALU.add, ALU.mult).then_inc(o_quantised, 1)

                def two_chunks(c, more):
                    for u in range(2):
                        if more:
                            quantise(c + (2 + u))
                        dve.wait_ge(turned, c + (u + 3))
                        xc = k.x[:, ds((c + u) * CH, CH)]
                        nc.vector.tensor_tensor(xc, turn_ps[u][:], xc, ALU.add).then_inc(added, 1)

                dve.sem_inc(added, 1)
                quantise(0)
                quantise(1)
                with dve.Fori(0, CHUNKS // 2 - 1) as g:
                    two_chunks(g * 2, True)
                two_chunks(CHUNKS - 2, False)
                dve.wait_ge(added, CHUNKS + 1)

            @block.tensor
            def _(pe):
                def down(c, u):
                    pe.wait_ge(o_quantised, c + (u + 1))
                    pe.wait_ge(down_copied, c + 1)
                    for j in range(FB0):
                        last = nc.tensor.matmul(down_ps[u][:], k.f_down[:, j, :], up[:, j, ds((c + u) * CH, CH)],
                                                start=(j == 0), stop=(j == FB0 - 1))
                    last.then_inc(down_done, 1)

                with pe.Fori(0, CHUNKS // 2) as g:
                    c = g * 2
                    down(c, 0)
                    down(c, 1)
                    for u in range(2):
                        pe.wait_ge(down_copied, c + (u + 2))
                        pe.wait_ge(added, c + 1)
                        for j in range(4):
                            last = nc.tensor.transpose(turn_ps[u][:, j * P:(j + 1) * P], part[:, u, j * P:(j + 1) * P], k.ident[:])
                        last.then_inc(turned, 1)


def xattn1(k, io):
    nc = k.nc
    sem = k.sem
    with ExitStack() as stack:
        sb = lambda name, shape, dt=F32: stack.enter_context(nc.sbuf_tensor(name, shape, dt))
        q_all = sb("b_q", [P, TOK])
        tailT = sb("b_tailT", [P, B])
        with ExitStack() as st:
            yT = st.enter_context(nc.sbuf_tensor("b_yT", [P, TOK], F32))
            layer_norm_T(k, "b_ln", yT)
            tail, v_tail = (st.enter_context(nc.sbuf_tensor(n, [B, D], F32)) for n in ("b_tail", "b_v_tail"))
            q_ps = [st.enter_context(nc.psum_tensor(f"b_q_ps{u}", [P, CH], F32)) for u in range(2)]
            tail_ps, v_ps = (st.enter_context(nc.psum_tensor(n, [P, P], F32)) for n in ("b_tail_ps", "b_v_tail_ps"))
            projected, copied, tail_loaded, tail_turned, tail_ready, v_done, v_copied, v_stored, biased = (
                sem(f"b_pre_{n}") for n in ("projected", "copied", "tail_loaded", "tail_turned", "tail_ready", "v_done",
                                            "v_copied", "v_stored", "biased"))
            with nc.Block() as block:

                @block.sync
                def _(sp):
                    sp.dma_start(tail[:], io["ctx_1024"][:, N_CTX - 1, :]).then_inc(tail_loaded, 16)
                    sp.wait_ge(v_copied, 1)
                    sp.dma_start(k.v_tail_dram, v_tail[:]).then_inc(v_stored, 16)
                    sp.wait_ge(v_stored, 16)

                @block.tensor
                def _(pe):
                    with pe.Fori(0, CHUNKS // 2) as g:
                        c = g * 2
                        for u in range(2):
                            pe.wait_ge(copied, c + (u + 1))
                            nc.tensor.matmul(q_ps[u][:], k.wq1[:], yT[:, ds((c + u) * CH, CH)], start=True, stop=True)\
                                .then_inc(projected, 1)
                    pe.wait_ge(tail_loaded, 16)
                    nc.tensor.transpose(tail_ps[:], tail[:], k.ident[:]).then_inc(tail_turned, 1)
                    pe.wait_ge(tail_ready, 1)
                    nc.tensor.matmul(v_ps[:], tailT[:], k.wv1[:], start=True, stop=True).then_inc(v_done, 1)

                @block.scalar
                def _(act):
                    act.sem_inc(copied, 2)
                    with act.Fori(0, CHUNKS // 2) as g:
                        c = g * 2
                        for u in range(2):
                            act.wait_ge(projected, c + (u + 1))
                            nc.scalar.activation(q_all[:, ds((c + u) * CH, CH)], q_ps[u][:], ACT.Identity, bias=k.bq1)\
                                .then_inc(copied, 1)
                    act.wait_ge(copied, CHUNKS + 2)

                @block.vector
                def _(dve):
                    xt = k.x[:].rearrange("p (t d) -> p t d", d=D)
                    nc.vector.tensor_tensor(xt, xt, k.bo[:].unsqueeze(1).broadcast_to([P, TILES, D]), ALU.add).then_inc(biased, 1)
                    dve.wait_ge(tail_turned, 1)
                    nc.vector.tensor_copy(tailT[:], tail_ps[:]).then_inc(tail_ready, 1)
                    dve.wait_ge(v_done, 1)
                    nc.vector.tensor_copy(v_tail[:], v_ps[:]).then_inc(v_copied, 1)
                    dve.wait_ge(biased, 1)

        raw = sb("b_raw", [P, 8, 2, D])
        ctxT = sb("b_ctxT", [P, 8, N_CTX])
        kept = sb("b_kept", [P, 2, BPT, N_CTX], BF16)
        bias = sb("b_bias", [P, 8, N_CTX])
        v_row = sb("b_v_row", [GROUPS, 2, BPT, D])
        v_last = sb("b_v_last", [GROUPS, 8, D])
        qbd = sb("b_qbd", [P, 4, H, L])
        kT = sb("b_kT", [P, 4, N_CTX])
        v = sb("b_v", [P, 4, 2, D])
        neg = sb("b_neg", [P, GROUPS, N_CTX])
        nmax = sb("b_nmax", [P, 2, GROUPS])
        prob = sb("b_prob", [P, 2, GROUPS, N_CTX])
        rsum, rinv = sb("b_rsum", [P, 2, GROUPS]), sb("b_rinv", [P, 2, GROUPS])
        probT, lastT = sb("b_probT", [P, 2, CH]), sb("b_lastT", [GROUPS, P])
        weight = sb("b_weight", [P, 2, D])
        weightT = sb("b_weightT", [P, P])
        own = sb("b_own", [P, BPT, HG, L])
        oT_sum, oT = sb("b_oT_sum", [P, P]), sb("b_oT", [P, P])
        psum = lambda name: stack.enter_context(nc.psum_tensor(name, [P, CH], F32))
        score_ps, turn_ps = [psum("b_score0"), psum("b_score1")], [psum("b_turn0"), psum("b_turn1")]
        out_ps, ctx_ps, k_ps, v_ps = psum("b_out"), psum("b_ctx"), psum("b_k"), psum("b_v_ps")
        weight_ps, proj_ps = ctx_ps[:, 2 * P:3 * P], out_ps[:, P:2 * P]
        raw_loaded = [sem(f"b_raw_loaded{j}") for j in range(8)]
        kept_loaded, v_row_loaded = ([sem(f"b_{n}_loaded{u}") for u in range(2)] for n in ("kept", "v_row"))
        ctx_turned, ctxT_ready, keys_ready, q_ready = sem("b_ctx_turned"), sem("b_ctxT_ready"), sem("b_tile_keys_ready"), sem("b_q_ready")
        k_done, k_ready, v_done, v_ready = sem("b_k_done"), sem("b_k_ready"), sem("b_v_done"), sem("b_v_ready")
        scored, masked, exped, rinv_ready = (sem(f"b_{n}") for n in ("scored", "masked", "exped", "rinv_ready"))
        turned, probT_ready = [sem(f"b_turned{n}") for n in range(3)], [sem(f"b_probT_ready{n}") for n in range(3)]
        out_ready, weight_ready, weight_turned, weightT_ready, own_ready, sum_ready, oT_ready, proj_ready, x_added = (
            sem(f"b_{n}") for n in ("out_ready", "weight_ready", "weight_turned", "weightT_ready", "own_ready", "sum_ready", "oT_ready",
                                    "proj_ready", "x_added"))
        LEAD, LAG = 5, 1

        def tile_of(g, j, ahead=0):
            return g * 2 + (j + ahead) // 4

        with nc.Block() as block:

            @block.sync
            def _(sp):
                def load_raw(g, j):
                    sp.dma_start(raw[:, j % 8], io["ctx_1024"][ds(g * 8 + j, 1), 0:2 * P, :].rearrange(
                        "b (t p) d -> p (b t) d", p=P)).then_inc(raw_loaded[j % 8], 16)

                def load_rows(t, u):
                    batches = ds(t * BPT, BPT)
                    sp.dma_start(kept[:, u], k.keep1[batches, :].unsqueeze(0).broadcast_to([P, BPT, N_CTX])).then_inc(kept_loaded[u], 16)
                    sp.dma_start(v_row[:, u], k.v_tail_dram[batches, :].unsqueeze(0).broadcast_to([GROUPS, BPT, D]))\
                        .then_inc(v_row_loaded[u], 16)

                def step(g, j):
                    s, t, u, b = g * 8 + j, tile_of(g, j), j // 4, j % 4
                    if live(g, j, 8):
                        wait(sp, ctx_turned, s + 1)
                        load_raw(g + 1, j)
                    if b == 1 and live(g, j, 8):
                        wait(sp, k_ready, s + 3)
                        wait(sp, keys_ready, t + 1)
                        load_rows(t + 2, u)

                for j in range(3):
                    load_raw(0, j)
                load_rows(0, 0)
                run_steps(sp, step, LEAD)

            @block.gpsimd
            def _(pool):
                def step(g, j):
                    s, t, u, b = g * 8 + j, tile_of(g, j), j // 4, j % 4
                    if live(g, j, 3):
                        wait(pool, scored, s * 4)
                        nc.gpsimd.tensor_tensor(
                            qbd[:, (j + 3) % 4], q_all[:, ds((s + 3) * L, L)].unsqueeze(1).broadcast_to([P, H, L]),
                            k.head_of_feature[:].unsqueeze(2).broadcast_to([P, H, L]), ALU.mult).then_inc(q_ready, 1)
                    if live(g, j, 1):
                        par = (j + 1) % 2
                        pool.wait_ge(rinv_ready, s + 2)
                        wait(pool, weight_turned, s)
                        nc.gpsimd.tensor_tensor(weight[:, par].rearrange("p (g f) -> p g f", g=GROUPS),
                                                k.own_value[:].rearrange("p (g f) -> p g f", g=GROUPS),
                                                rinv[:, par, :].unsqueeze(2).broadcast_to([P, GROUPS, L]), ALU.mult).then_inc(weight_ready, 1)
                    if b == 3 and live(g, j, 8):
                        slots = slice(4 * u, 4 * u + 4)
                        wait(pool, out_ready, s + 1)
                        nc.gpsimd.tensor_copy(ctxT[:, slots, N_CTX - 1:N_CTX], tailT[:, ds((t + 2) * BPT, BPT)].unsqueeze(2))
                        pool.wait_ge(v_row_loaded[u], (g + 2) * 16)
                        nc.gpsimd.tensor_tensor(v_last[:, slots, :], v_row[:, u],
                                                k.group_of_feature[:].unsqueeze(1).broadcast_to([GROUPS, BPT, D]), ALU.mult)
                        wait_apart(k, pool, kept_loaded[u], (g + 2) * 16)
                        nc.gpsimd.tensor_scalar(bias[:, slots, :], kept[:, u], NEG1, -NEG1, ALU.mult, ALU.add).then_inc(keys_ready, 1)

                run_steps(pool, step, LEAD)

            @block.vector
            def _(dve):
                def mask(g, j, grp):
                    s, n, par = g * 8 + j, (j + 1) % 8, (j + 1) % 2
                    if n % 4 == 0 and grp == 0:
                        dve.wait_ge(keys_ready, tile_of(g, j, 1) + 1)
                    wait_apart(k, dve, scored, s * 4 + (5 + grp))
                    nc.vector.tensor_tensor_reduce(
                        out=neg[:, grp, :], in0=score_ps[grp % 2][:, 0:N_CTX], in1=bias[:, n, :], scale=-DH1 ** -0.5,
                        scalar=3.4e38, op0=ALU.add, op1=ALU.min, accum_out=nmax[:, par, grp:grp + 1]).then_inc(masked, 1)

                def step(g, j):
                    s, t, u, b = g * 8 + j, tile_of(g, j), j // 4, j % 4
                    if live(g, j, 1):
                        mask(g, j, 0)
                        mask(g, j, 1)
                    if live(g, j, 0):
                        dve.wait_ge(turned[0], s + 1)
                        nc.vector.tensor_copy(probT[:, 0, :], turn_ps[0][:]).then_inc(probT_ready[0], 1)
                    if live(g, j, 1):
                        mask(g, j, 2)
                        mask(g, j, 3)
                    if live(g, j, 3):
                        dve.wait_ge(k_done, s + 4)
                        dve.wait_ge(kept_loaded[(j + 3) // 4 % 2], (g + (j + 3) // 8 + 1) * 16)
                        nc.vector.scalar_tensor_tensor(kT[:, (j + 3) % 4, :], k_ps[:, 0:N_CTX], k.bk1,
                                                       kept[:, (j + 3) // 4 % 2, (j + 3) % 4, :], ALU.add, ALU.mult).then_inc(k_ready, 1)
                    if live(g, j, 1):
                        par = (j + 1) % 2
                        dve.wait_ge(exped, s * 4 + 8)
                        wait(dve, weight_ready, s)
                        nc.vector.reciprocal(rinv[:, par, :], rsum[:, par, :]).then_inc(rinv_ready, 1)
                    if live(g, j, 0):
                        dve.wait_ge(out_ready, s + 1)
                        dve.wait_ge(weightT_ready, s + 1)
                        nc.vector.tensor_tensor(own[:, b].rearrange("p h l -> p (h l)"), out_ps[:, 0:P], weightT[:], ALU.mult)\
                            .then_inc(own_ready, 1)
                    if b == 0 and live(g, j, -1):
                        dve.wait_ge(proj_ready, t)
                        xt = k.x[:, ds((t - 1) * D, D)]
                        nc.vector.tensor_tensor(xt, proj_ps, xt, ALU.add).then_inc(x_added, 1)
                    if b == 3 and live(g, j, 0):
                        dve.wait_ge(own_ready, s + 1)
                        nc.vector.tensor_reduce(oT_sum[:], own[:].rearrange("p b h l -> p b l h"), AX.X, ALU.add).then_inc(sum_ready, 1)
                    if live(g, j, 4):
                        dve.wait_ge(ctx_turned, s + 5)
                        nc.vector.tensor_copy(ctxT[:, (j + 4) % 8, 0:2 * P], ctx_ps[:, 0:2 * P]).then_inc(ctxT_ready, 1)

                run_steps(dve, step, LEAD, LAG)
                dve.wait_ge(x_added, TILES)

            @block.scalar
            def _(act):
                def exp(g, j, grp):
                    s, par = g * 8 + j, (j + 1) % 2
                    act.wait_ge(masked, s * 4 + (5 + grp))
                    nc.scalar.activation(prob[:, par, grp, :], neg[:, grp, :], ACT.Exp, bias=nmax[:, par, grp:grp + 1],
                                         scale=-1.0, accum_out=rsum[:, par, grp:grp + 1]).then_inc(exped, 1)

                def step(g, j):
                    s, t, u, b = g * 8 + j, tile_of(g, j), j // 4, j % 4
                    if live(g, j, 1):
                        exp(g, j, 0)
                        exp(g, j, 1)
                    if b == 0 and live(g, j, -1):
                        act.wait_ge(sum_ready, t)
                        nc.scalar.activation(oT[:], oT_sum[:], ACT.Identity, bias=k.bv1).then_inc(oT_ready, 1)
                    if live(g, j, 0):
                        act.wait_ge(turned[1], s + 1)
                        nc.scalar.activation(probT[:, 1, :], turn_ps[1][:], ACT.Copy).then_inc(probT_ready[1], 1)
                        act.wait_ge(weight_turned, s + 1)
                        wait(act, own_ready, s)
                        nc.scalar.activation(weightT[:], weight_ps, ACT.Copy).then_inc(weightT_ready, 1)
                    if live(g, j, 1):
                        exp(g, j, 2)
                        exp(g, j, 3)
                    if live(g, j, 0):
                        act.wait_ge(turned[2], s + 1)
                        nc.scalar.activation(lastT[:], turn_ps[0][0:GROUPS, 0:P], ACT.Copy).then_inc(probT_ready[2], 1)
                    if live(g, j, 3):
                        act.wait_ge(v_done, s + 4)
                        nc.scalar.activation(v[:, (j + 3) % 4], v_ps[:, 0:2 * P].rearrange("p (t d) -> p t d", d=D), ACT.Copy)\
                            .then_inc(v_ready, 1)

                run_steps(act, step, LEAD, LAG)

            @block.tensor
            def _(pe):
                def score(g, j, grp):
                    s, n = g * 8 + j, (j + 1) % 4
                    if grp == 0:
                        pe.wait_ge(k_ready, s + 2)
                        pe.wait_ge(q_ready, s + 2)
                    wait(pe, masked, s * 4 + (3 + grp))
                    nc.tensor.matmul(score_ps[grp % 2][:, 0:N_CTX], qbd[:, n, 4 * grp:4 * grp + 4, :], kT[:, n, :],
                                     start=True, stop=True).then_inc(scored, 1)

                def turn(g, j, kt):
                    s = g * 8 + j
                    if kt == 0:
                        pe.wait_ge(exped, s * 4 + 4)
                        wait(pe, probT_ready[2], s)
                    if kt < 2:
                        for grp in range(GROUPS):
                            last = nc.tensor.transpose(turn_ps[kt][:, grp * P:(grp + 1) * P],
                                                       prob[:, j % 2, grp, kt * P:(kt + 1) * P], k.ident[:])
                    else:
                        pe.wait_ge(probT_ready[0], s + 1)
                        last = nc.tensor.transpose(turn_ps[0][0:GROUPS, 0:P], prob[:, j % 2, :, N_CTX - 1], k.ident[:])
                    last.then_inc(turned[kt], 1)

                def values(g, j, kt):
                    s, b = g * 8 + j, j % 4
                    pe.wait_ge(probT_ready[kt], s + 1)
                    if kt == 0:
                        pe.wait_ge(v_ready, s + 1)
                        wait(pe, own_ready, s)
                        if b == 1 and live(g, j, -4):
                            pe.wait_ge(x_added, tile_of(g, j))
                    if kt < 2:
                        for grp in range(GROUPS):
                            rows = slice(grp * 32, grp * 32 + 32)
                            nc.tensor.matmul(out_ps[rows, 0:P], v[:, j % 4, kt, rows], probT[:, kt, grp * P:(grp + 1) * P],
                                             start=(kt == 0), stop=False, skip_group_check=True)
                    else:
                        nc.tensor.matmul(out_ps[:, 0:P], v_last[:, j, :], lastT[:], start=False, stop=True,
                                         skip_group_check=True).then_inc(out_ready, 1)

                def step(g, j):
                    s, t, u, b = g * 8 + j, tile_of(g, j), j // 4, j % 4
                    here, ahead = live(g, j, 0), live(g, j, 1)
                    if ahead:
                        score(g, j, 0)
                        score(g, j, 1)
                    if here:
                        turn(g, j, 0)
                        turn(g, j, 1)
                    if here:
                        pe.wait_ge(weight_ready, s + 1)
                        pe.wait_ge(ctxT_ready, s + 4 if live(g, j, 3) else B)
                        nc.tensor.transpose(weight_ps, weight[:, j % 2], k.ident[:]).then_inc(weight_turned, 1)
                    if ahead:
                        score(g, j, 2)
                        score(g, j, 3)
                    if live(g, j, 3):
                        n = (j + 3) % 8
                        pe.wait_ge(ctxT_ready, s + 4)
                        if n % 4 == 0:
                            pe.wait_ge(keys_ready, tile_of(g, j, 3) + 1)
                        wait(pe, k_ready, s + 3)
                        nc.tensor.matmul(k_ps[:, 0:N_CTX], k.wk1[:], ctxT[:, n, :], start=True, stop=True).then_inc(k_done, 1)
                    if here:
                        values(g, j, 0)
                        turn(g, j, 2)
                    if live(g, j, 3):
                        n = (j + 3) % 8
                        wait(pe, v_ready, s + 3)
                        for kt in range(2):
                            last = nc.tensor.matmul(v_ps[:, kt * D:(kt + 1) * D], ctxT[:, n, kt * P:(kt + 1) * P], k.wv1[:],
                                                    start=True, stop=True)
                        last.then_inc(v_done, 1)
                    if here:
                        values(g, j, 1)
                    if b == 0 and live(g, j, -1):
                        pe.wait_ge(oT_ready, t)
                        nc.tensor.matmul(proj_ps, oT[:], k.wo1[:], start=not here, stop=True, skip_group_check=True).then_inc(proj_ready, 1)
                    if here:
                        values(g, j, 2)
                    if live(g, j, 4):
                        n = (j + 4) % 8
                        pe.wait_ge(raw_loaded[n], (g + (j + 4) // 8 + 1) * 16)
                        wait(pe, ctxT_ready, s + 4)
                        if here:
                            pe.wait_ge(weightT_ready, s + 1)
                        for kt in range(2):
                            last = nc.tensor.transpose(ctx_ps[:, kt * P:(kt + 1) * P], raw[:, n, kt, :], k.ident[:])
                        last.then_inc(ctx_turned, 1)

                run_steps(pe, step, LEAD, LAG)


def run_tiles(eng, step, lead, lag):
    for t in range(-lead, 4):
        step(t // 4, t % 4)
    with eng.Fori(1, TILES // 4 - 2) as g:
        for u in range(4):
            step(g, u)
    for t in range(TILES - 8, TILES + lag):
        step(t // 4, t % 4)


def live_tile(g, u, ahead):
    return not isinstance(g, int) or 0 <= 4 * g + u + ahead < TILES


def attn1(k, io):
    nc = k.nc
    sem = k.sem
    POOL_HEADS = 12
    with ExitStack() as stack:
        sb = lambda name, shape, dt=F32: stack.enter_context(nc.sbuf_tensor(name, shape, dt))
        psum = lambda name: stack.enter_context(nc.psum_tensor(name, [P, CH], F32))
        mean, rstd = ln_stats(k, stack, "s_ln", lambda t: k.x[:, ds(t * D, D)], TILES)
        z, y = sb("s_z", [P, 2, D]), sb("s_y", [P, 4, BPT, HG, L])
        q, keys = sb("s_q", [P, 2, P]), sb("s_keys", [P, 2, P])
        spread = sb("s_spread", [P, 2, BPT, H, L])
        v = sb("s_v", [P, 4, BPT, D])
        shifted, expd = sb("s_shifted", [P, 2, H, L]), sb("s_expd", [P, 2, H, L])
        rmax, rsum, rinv = sb("s_rmax", [P, H]), sb("s_rsum", [P, H]), sb("s_rinv", [P, 2, H])
        probT, out, oT = sb("s_probT", [P, GROUPS, P]), sb("s_out", [P, 2, D]), sb("s_oT", [P, P])
        query_row, mask_row = sb("s_query_row", [L, P], BF16), sb("s_mask_row", [L, H, L], BF16)
        y_ps, qk_ps, v_ps, turn_ps, out_ps, proj_ps = (psum(f"s_{n}_ps") for n in ("y", "qk", "v", "turn", "out", "proj"))
        score_ps = [psum("s_score0"), psum("s_score1")]
        rows_ready, z_ready, y_turned, y_ready, qk_done, q_ready, keys_ready, spread_pool, spread_act, v_done, v_ready, biased = (
            sem(f"s_{n}") for n in ("rows_ready", "z_ready", "y_turned", "y_ready", "qk_done", "q_ready", "keys_ready", "spread_pool",
                                    "spread_act", "v_done", "v_ready", "biased"))
        scored, max_ready, shift_ready, exped, sum_ready, rinv_ready, turned, probT_ready = (
            sem(f"s_{n}") for n in ("scored", "max_ready", "shift_ready", "exped", "sum_ready", "rinv_ready", "turned", "probT_ready"))
        out_done, out_ready, out_turned, oT_ready, proj_done, x_added = (
            sem(f"s_{n}") for n in ("out_done", "out_ready", "out_turned", "oT_ready", "proj_done", "x_added"))
        LEAD, LAG = 5, 1
        row_wide = lambda a, n: a.unsqueeze(2).broadcast_to([P, H, n])
        with nc.Block() as block:

            @block.gpsimd
            def _(pool):
                def step(g, u):
                    t = g * 4 + u
                    if live_tile(g, u, 2):
                        n = u % 2
                        wait(pool, keys_ready, t + 3)
                        wait(pool, scored, t + 1)
                        nc.gpsimd.tensor_tensor(
                            spread[:, n, :, 0:POOL_HEADS, :],
                            keys[:, n].rearrange("p (b l) -> p b l", l=L).unsqueeze(2).broadcast_to([P, BPT, POOL_HEADS, L]),
                            k.head_of_feature[:, 0:POOL_HEADS].unsqueeze(1).unsqueeze(3).broadcast_to([P, BPT, POOL_HEADS, L]),
                            ALU.mult).then_inc(spread_pool, 1)
                    if live_tile(g, u, 4):
                        xt = k.x[:, ds((t + 4) * D, D)]
                        wait(pool, z_ready, t + 5)
                        nc.gpsimd.tensor_tensor(xt, xt, k.bproj[:], ALU.add).then_inc(biased, 1)

                run_tiles(pool, step, LEAD, LAG)

            @block.vector
            def _(dve):
                def step(g, u):
                    t = g * 4 + u
                    if live_tile(g, u, 1):
                        n = (u + 1) % 2
                        dve.wait_ge(scored, t + 2)
                        scores = score_ps[n][:].rearrange("p (h l) -> p h l", l=L)
                        nc.vector.tensor_reduce(rmax[:], scores, AX.X, ALU.max).then_inc(max_ready, 1)
                        dve.wait_ge(max_ready, t + 2)
                        wait(dve, exped, t)
                        nc.vector.tensor_tensor(shifted[:, n], scores, row_wide(rmax[:], L), ALU.subtract).then_inc(shift_ready, 1)
                    if live_tile(g, u, 5):
                        wait(dve, y_turned, t + 4)
                        nc.vector.tensor_scalar(z[:, (u + 1) % 2], k.x[:, ds((t + 5) * D, D)], mean[:, ds(t + 5, 1)],
                                                rstd[:, ds(t + 5, 1)], ALU.subtract, ALU.mult).then_inc(z_ready, 1)
                    if live_tile(g, u, 3):
                        dve.wait_ge(v_done, t + 4)
                        nc.vector.tensor_tensor(v[:, (u + 3) % 4], v_ps[:].rearrange("p (b d) -> p b d", d=D),
                                                k.own_value[:].unsqueeze(1).broadcast_to([P, BPT, D]), ALU.mult).then_inc(v_ready, 1)
                    if live_tile(g, u, 1):
                        n = (u + 1) % 2
                        dve.wait_ge(exped, t + 2)
                        nc.vector.tensor_reduce(rsum[:], expd[:, n], AX.X, ALU.add).then_inc(sum_ready, 1)
                        dve.wait_ge(sum_ready, t + 2)
                        nc.vector.reciprocal(rinv[:, n], rsum[:]).then_inc(rinv_ready, 1)
                    if live_tile(g, u, 0):
                        dve.wait_ge(out_done, t + 1)
                        dve.wait_ge(rinv_ready, t + 1)
                        wait(dve, out_turned, t - 1)
                        nc.vector.tensor_tensor(out[:, u % 2].rearrange("p (h e) -> p h e", e=DH1),
                                                out_ps[:, 0:D].rearrange("p (h e) -> p h e", e=DH1),
                                                row_wide(rinv[:, u % 2], DH1), ALU.mult).then_inc(out_ready, 1)
                    if live_tile(g, u, -1):
                        dve.wait_ge(proj_done, t)
                        dve.wait_ge(biased, t)
                        xt = k.x[:, ds((t - 1) * D, D)]
                        nc.vector.tensor_tensor(xt, proj_ps[:, D:2 * D], xt, ALU.add).then_inc(x_added, 1)

                nc.vector.tensor_copy(query_row[:].rearrange("p (b l) -> p b l", l=L),
                                      k.ident[0:L, 0:L].unsqueeze(1).broadcast_to([L, BPT, L])).then_inc(rows_ready, 1)
                nc.vector.tensor_copy(mask_row[:], k.fenwick[0:L, :].unsqueeze(1).broadcast_to([L, H, L])).then_inc(rows_ready, 1)
                run_tiles(dve, step, LEAD, LAG)
                dve.wait_ge(x_added, TILES)

            @block.scalar
            def _(act):
                def step(g, u):
                    t = g * 4 + u
                    if live_tile(g, u, 4):
                        act.wait_ge(y_turned, t + 5)
                        nc.scalar.activation(y[:, u], y_ps[:, 0:P].rearrange("p (b l) -> p b l", l=L).unsqueeze(2).broadcast_to([P, BPT, HG, L]),
                                             ACT.Copy).then_inc(y_ready, 1)
                    if live_tile(g, u, 2):
                        n = u % 2
                        act.wait_ge(keys_ready, t + 3)
                        wait(act, scored, t + 1)
                        for h in range(POOL_HEADS, H):
                            last = nc.scalar.activation(spread[:, n, :, h, :], keys[:, n].rearrange("p (b l) -> p b l", l=L), ACT.Copy,
                                                        scale=k.head_of_feature[:, h:h + 1])
                        last.then_inc(spread_act, 1)
                    if live_tile(g, u, 0):
                        act.wait_ge(turned, t + 1)
                        nc.scalar.activation(probT[:].rearrange("p g q -> p (g q)"), turn_ps[:], ACT.Copy).then_inc(probT_ready, 1)
                    if live_tile(g, u, 1):
                        n = (u + 1) % 2
                        act.wait_ge(shift_ready, t + 2)
                        wait(act, turned, t)
                        nc.scalar.activation(expd[:, n], shifted[:, n], ACT.Exp, scale=DH1 ** -0.5).then_inc(exped, 1)
                    if live_tile(g, u, 3):
                        n = (u + 3) % 2
                        act.wait_ge(qk_done, t + 4)
                        wait(act, scored, t + 2)
                        wait(act, spread_pool, t + 2)
                        nc.scalar.activation(q[:, n], qk_ps[:, 0:P], ACT.Identity, bias=k.bq2).then_inc(q_ready, 1)
                        nc.scalar.activation(keys[:, n], qk_ps[:, P:2 * P], ACT.Identity, bias=k.bk2).then_inc(keys_ready, 1)
                    if live_tile(g, u, -1):
                        act.wait_ge(out_turned, t)
                        nc.scalar.activation(oT[:], proj_ps[:, 0:P], ACT.Identity, bias=k.bv2).then_inc(oT_ready, 1)

                run_tiles(act, step, LEAD, LAG)

            @block.tensor
            def _(pe):
                def step(g, u):
                    t = g * 4 + u
                    if live_tile(g, u, 4):
                        pe.wait_ge(z_ready, t + 5)
                        wait(pe, y_ready, t + 4)
                        nc.tensor.transpose(y_ps[:, 0:P], z[:, u % 2], k.ident[:]).then_inc(y_turned, 1)
                    if live_tile(g, u, 1):
                        n = (u + 1) % 2
                        wait(pe, shift_ready, t)
                        pe.wait_ge(q_ready, t + 2)
                        pe.wait_ge(spread_pool, t + 2)
                        pe.wait_ge(spread_act, t + 2)
                        nc.tensor.matmul(score_ps[n][:], query_row[:], mask_row[:].rearrange("p h l -> p (h l)"), start=True, stop=False,
                                         skip_group_check=True)
                        for b in range(BPT):
                            rows = slice(b * L, (b + 1) * L)
                            last = nc.tensor.matmul(score_ps[n][rows, :], q[:, n, rows], spread[:, n, b].rearrange("p h l -> p (h l)"),
                                                    start=False, stop=True, skip_group_check=True)
                        last.then_inc(scored, 1)
                    if live_tile(g, u, 0):
                        pe.wait_ge(exped, t + 1)
                        wait(pe, probT_ready, t)
                        for grp in range(GROUPS):
                            last = nc.tensor.transpose(turn_ps[:, grp * P:(grp + 1) * P], expd[:, u % 2, 4 * grp:4 * grp + 4, :], k.ident[:])
                        last.then_inc(turned, 1)
                    if live_tile(g, u, 3):
                        n = (u + 3) % 4
                        pe.wait_ge(y_ready, t + 4)
                        wait(pe, keys_ready, t + 3)
                        nc.tensor.matmul(qk_ps[:, 0:P], k.wqkv[:, 0:D], y[:, n, :, 0, :], start=True, stop=True)
                        nc.tensor.matmul(qk_ps[:, P:2 * P], k.wqkv[:, D:2 * D], y[:, n, :, 0, :], start=True, stop=True).then_inc(qk_done, 1)
                        wait(pe, v_ready, t + 3)
                        for b in range(BPT):
                            last = nc.tensor.matmul(v_ps[:, b * D:(b + 1) * D], y[:, n, b].rearrange("p r l -> p (r l)"),
                                                    k.wqkv[:, 2 * D:3 * D], start=True, stop=True)
                        last.then_inc(v_done, 1)
                    if live_tile(g, u, -1):
                        pe.wait_ge(out_ready, t)
                        wait(pe, x_added, t - 1)
                        nc.tensor.transpose(proj_ps[:, 0:P], out[:, (u - 1) % 2], k.ident[:]).then_inc(out_turned, 1)
                    if live_tile(g, u, 0):
                        pe.wait_ge(probT_ready, t + 1)
                        pe.wait_ge(v_ready, t + 1)
                        wait(pe, out_ready, t)
                        for grp in range(GROUPS):
                            for b in range(BPT):
                                rows = slice(b * L, (b + 1) * L)
                                cols = slice(grp * HG * DH1, (grp + 1) * HG * DH1)
                                last = nc.tensor.matmul(out_ps[rows, cols], probT[:, grp, rows], v[:, u, b, cols], start=True, stop=True,
                                                        skip_group_check=True)
                        last.then_inc(out_done, 1)
                    if live_tile(g, u, -1):
                        pe.wait_ge(oT_ready, t)
                        nc.tensor.matmul(proj_ps[:, D:2 * D], oT[:], k.wproj[:], start=True, stop=True).then_inc(proj_done, 1)

                pe.wait_ge(rows_ready, 2)
                run_tiles(pe, step, LEAD, LAG)


def moe_routing(k, yT, combT):
    nc = k.nc
    sem = k.sem
    GRP = CH // P
    with ExitStack() as stack:
        sb = lambda name, shape: stack.enter_context(nc.sbuf_tensor(name, shape, F32))
        psum = lambda name: stack.enter_context(nc.psum_tensor(name, [P, CH], F32))
        logitT = sb("mr_logitT", [E_N, 2, CH])
        logits, rest, marked, first, second = (sb(f"mr_{n}", [P, TILES, E_N]) for n in ("logits", "rest", "marked", "first", "second"))
        best, next_best, best_rank, next_rank, ratio, w1, w2 = (
            sb(f"mr_{n}", [P, TILES]) for n in ("best", "next_best", "best_rank", "next_rank", "ratio", "w1", "w2"))
        comb = sb("mr_comb", [P, 2, GRP, E_N])
        logit_ps, comb_ps = ([psum(f"mr_{n}{u}") for u in range(2)] for n in ("logit", "comb_ps"))
        token_ps = [psum(f"mr_token{u}") for u in range(2)]
        routed, copied, turned, gathered = (sem(f"mr_{n}") for n in ("routed", "copied", "turned", "gathered"))
        wide = lambda a: a.unsqueeze(2).broadcast_to([P, TILES, E_N])
        ranks = k.rank[:].unsqueeze(1).broadcast_to([P, TILES, E_N])
        with nc.Block() as block:

            @block.tensor
            def _(pe):
                def turn(c, u):
                    pe.wait_ge(gathered, c + (u + 1))
                    wait_apart(k, pe, copied, c + (u + 3))
                    for j in range(GRP):
                        last = nc.tensor.transpose(token_ps[u][:, j * E_N:(j + 1) * E_N], logitT[:, u, j * P:(j + 1) * P],
                                                   k.ident[0:E_N, 0:E_N])
                    last.then_inc(turned, 1)

                with pe.Fori(0, CHUNKS // 2) as g:
                    c = g * 2
                    for u in range(2):
                        pe.wait_ge(copied, c + (u + 1))
                        nc.tensor.matmul(logit_ps[u][0:E_N, :], k.router[:], yT[:, ds((c + u) * CH, CH)],
                                         start=True, stop=True).then_inc(routed, 1)
                    for u in range(2):
                        turn(c, u)

            @block.scalar
            def _(act):
                act.sem_inc(copied, 2)
                act.sem_inc(turned, 2)
                with act.Fori(0, CHUNKS // 2) as g:
                    c = g * 2
                    for u in range(2):
                        act.wait_ge(routed, c + (u + 1))
                        act.wait_ge(turned, c + (u + 1))
                        nc.scalar.activation(logitT[:, u, :], logit_ps[u][0:E_N, :], ACT.Copy).then_inc(copied, 1)

            @block.vector
            def _(dve):
                dve.sem_inc(gathered, 2)
                with dve.Fori(0, CHUNKS // 2) as g:
                    c = g * 2
                    for u in range(2):
                        dve.wait_ge(turned, c + (u + 3))
                        nc.vector.tensor_copy(logits[:, ds((c + u) * GRP, GRP), :],
                                              token_ps[u][:, 0:GRP * E_N].rearrange("p (t e) -> p t e", e=E_N)).then_inc(gathered, 1)
                dve.wait_ge(gathered, CHUNKS + 2)
        chain, ratio_ready = sem("mr_chain"), sem("mr_ratio_ready")
        with nc.Block() as block:

            @block.vector
            def _(dve):
                def mark(n, x, top, top_rank, one):
                    nc.vector.tensor_reduce(top[:], x[:], AX.X, ALU.max).then_inc(chain, 1)
                    dve.wait_ge(chain, n + 1)
                    nc.vector.tensor_tensor(marked[:], x[:], wide(top[:]), ALU.is_ge).then_inc(chain, 1)
                    dve.wait_ge(chain, n + 2)
                    nc.vector.tensor_tensor(marked[:], marked[:], ranks, ALU.mult).then_inc(chain, 1)
                    dve.wait_ge(chain, n + 3)
                    nc.vector.tensor_reduce(top_rank[:], marked[:], AX.X, ALU.max).then_inc(chain, 1)
                    dve.wait_ge(chain, n + 4)
                    nc.vector.tensor_tensor(one[:], marked[:], wide(top_rank[:]), ALU.is_equal).then_inc(chain, 1)
                    dve.wait_ge(chain, n + 5)
                    return n + 5

                n = mark(0, logits, best, best_rank, first)
                nc.vector.scalar_tensor_tensor(rest[:], first[:], -NEG0, logits[:], ALU.mult, ALU.add).then_inc(chain, 1)
                dve.wait_ge(chain, n + 1)
                n = mark(n + 1, rest, next_best, next_rank, second)
                nc.vector.tensor_tensor(w2[:], next_best[:], best[:], ALU.subtract).then_inc(chain, 1)
                n += 1
                dve.wait_ge(ratio_ready, 1)
                nc.vector.tensor_scalar(w1[:], ratio[:], 1.0, None, ALU.add).then_inc(chain, 1)
                dve.wait_ge(chain, n + 1)
                nc.vector.reciprocal(w1[:], w1[:]).then_inc(chain, 1)
                dve.wait_ge(chain, n + 2)
                nc.vector.tensor_tensor(w2[:], w1[:], ratio[:], ALU.mult).then_inc(chain, 1)
                nc.vector.tensor_tensor(first[:], first[:], wide(w1[:]), ALU.mult).then_inc(chain, 1)
                dve.wait_ge(chain, n + 4)
                nc.vector.tensor_tensor(second[:], second[:], wide(w2[:]), ALU.mult).then_inc(chain, 1)
                dve.wait_ge(chain, n + 5)
                nc.vector.tensor_tensor(first[:], first[:], second[:], ALU.add).then_inc(chain, 1)
                dve.wait_ge(chain, n + 6)

            @block.scalar
            def _(act):
                act.wait_ge(chain, 12)
                nc.scalar.activation(ratio[:], w2[:], ACT.Exp).then_inc(ratio_ready, 1)
        staged, comb_turned, comb_copied = sem("mr_staged"), sem("mr_comb_turned"), sem("mr_comb_copied")
        with nc.Block() as block:

            @block.vector
            def _(dve):
                with dve.Fori(0, CHUNKS // 2) as g:
                    c = g * 2
                    for u in range(2):
                        dve.wait_ge(comb_turned, c + (u + 1))
                        nc.vector.tensor_copy(comb[:, u], first[:, ds((c + u) * GRP, GRP), :]).then_inc(staged, 1)

            @block.tensor
            def _(pe):
                pe.sem_inc(comb_turned, 2)
                with pe.Fori(0, CHUNKS // 2) as g:
                    c = g * 2
                    for u in range(2):
                        pe.wait_ge(staged, c + (u + 1))
                        pe.wait_ge(comb_copied, c + (u + 1))
                        for j in range(GRP):
                            last = nc.tensor.transpose(comb_ps[u][0:E_N, j * P:(j + 1) * P], comb[:, u, j, :], k.ident[:])
                        last.then_inc(comb_turned, 1)

            @block.scalar
            def _(act):
                act.sem_inc(comb_copied, 2)
                with act.Fori(0, CHUNKS // 2) as g:
                    c = g * 2
                    for u in range(2):
                        act.wait_ge(comb_turned, c + (u + 3))
                        nc.scalar.activation(combT[:, ds((c + u) * CH, CH)], comb_ps[u][0:E_N, :], ACT.Copy).then_inc(comb_copied, 1)
                act.wait_ge(comb_copied, CHUNKS + 2)


def moe1(k, io):
    nc = k.nc
    sem = k.sem
    ITEMS = PAIRS + len(SH_BLOCKS)
    USES = PAIRS + 1
    LAST = CHUNKS // 2
    with ExitStack() as stack:
        sb = lambda name, shape: stack.enter_context(nc.sbuf_tensor(name, shape, F32))
        yT = sb("m_yT", [P, TOK])
        layer_norm_T(k, "m_ln", yT)
        combT = sb("m_combT", [E_N, TOK])
        moe_routing(k, yT, combT)
        psum = lambda name: stack.enter_context(nc.psum_tensor(name, [P, CH], F32))
        act_in, mul_in = ([psum(f"m_{n}{u}") for u in range(2)] for n in ("g", "h"))
        wide_ps, expert_ps, shared_ps, turn_ps = (psum(f"m_{n}") for n in ("wide", "expert", "shared", "turn"))
        silu, gated, hidden = sb("m_silu", [P, 2, CH]), sb("m_gated", [P, CH]), sb("m_hidden", [P, 2, CH])
        experts, share, shared, total = (sb(f"m_{n}", [P, CH]) for n in ("experts", "share", "shared_out", "total"))
        g_done, h_done, wide_done, down_done, silu_ready, gated_ready, wide_used, hidden_ready = (
            sem(f"m_{n}") for n in ("g_done", "h_done", "wide_done", "down_done", "silu_ready", "gated_ready", "wide_used", "hidden_ready"))
        experts_copied, share_ready, shared_taken, total_ready, turned, x_added = (
            sem(f"m_{n}") for n in ("experts_copied", "share_ready", "shared_taken", "total_ready", "turned", "x_added"))
        rows = lambda j: P if j < PAIRS else SH_BLOCKS[j - PAIRS][1]

        def place(g, i):
            return g * (2 * ITEMS) + i, g * 2 + i // ITEMS, i % ITEMS

        def current(g):
            return not isinstance(g, int) or g < LAST

        def after(g, i, items):
            return not isinstance(g, int) or 0 <= g * 2 * ITEMS + i - items < CHUNKS * ITEMS

        def run(eng, step):
            for i in range(2 * ITEMS):
                step(0, i)
            with eng.Fori(1, LAST) as g:
                for i in range(2 * ITEMS):
                    step(g, i)
            for i in range(6):
                step(LAST, i)

        with nc.Block() as block:

            @block.tensor
            def _(pe):
                def step(g, i):
                    n, c, j = place(g, i)
                    u = i % 2
                    if current(g):
                        y = yT[:, ds(c * CH, CH)]
                        r = rows(j)
                        if j < PAIRS:
                            wg, wh = (k.w_gu[:, a, 2 * j:2 * j + 2, :] for a in range(2))
                        else:
                            first = SH_BLOCKS[j - PAIRS][0]
                            wg, wh = (w[:, first:first + r] for w in (k.sh_gate, k.sh_up))
                        wait(pe, silu_ready, n - 1)
                        nc.tensor.matmul(act_in[u][0:r, :], wg, y, start=True, stop=True).then_inc(g_done, 1)
                        if after(g, i, 2):
                            j2 = (j - 2) % ITEMS
                            if j2 < PAIRS:
                                pe.wait_ge(gated_ready, (c - (1 if j < 2 else 0)) * PAIRS + (j2 + 1))
                            else:
                                pe.wait_ge(hidden_ready, n - 1)
                        nc.tensor.matmul(mul_in[u][0:r, :], wh, y, start=True, stop=True).then_inc(h_done, 1)
                    if after(g, i, 1):
                        j1 = (j - 1) % ITEMS
                        pe.wait_ge(hidden_ready, n)
                        if j1 == 0:
                            wait(pe, experts_copied, c)
                        if j1 == PAIRS:
                            wait(pe, shared_taken, c)
                        if j1 < PAIRS:
                            nc.tensor.matmul(expert_ps[:], k.w_dn[:, j1, :], hidden[:, 1 - u, :],
                                             start=(j1 == 0), stop=(j1 == PAIRS - 1)).then_inc(down_done, 1)
                        else:
                            r = rows(j1)
                            nc.tensor.matmul(shared_ps[:], k.sh_down[0:r, j1 - PAIRS, :], hidden[0:r, 1 - u, :],
                                             start=(j1 == PAIRS), stop=(j1 == ITEMS - 1)).then_inc(down_done, 1)
                    if current(g) and j < USES:
                        if not isinstance(n, int) or c * USES + j > 0:
                            wait_apart(k, pe, wide_used, c * USES + j)
                        lhsT, rhs = (k.pair_select[:, j, :], combT) if j < PAIRS else (k.sh_gate_row[:], yT)
                        nc.tensor.matmul(wide_ps[:], lhsT, rhs[:, ds(c * CH, CH)], start=True, stop=True).then_inc(wide_done, 1)
                    if j == 3 and after(g, i, ITEMS):
                        pe.wait_ge(total_ready, c)
                        wait(pe, x_added, c - 1)
                        for t in range(CH // P):
                            last = nc.tensor.transpose(turn_ps[:, t * P:(t + 1) * P], total[:, t * P:(t + 1) * P], k.ident[:])
                        last.then_inc(turned, 1)

                run(pe, step)

            @block.scalar
            def _(act):
                def step(g, i):
                    if not current(g):
                        return
                    n, c, j = place(g, i)
                    u, r = i % 2, rows(j)
                    act.wait_ge(g_done, n + 1)
                    if after(g, i, 2):
                        j2 = (j - 2) % ITEMS
                        if j2 < PAIRS:
                            act.wait_ge(gated_ready, (c - (1 if j < 2 else 0)) * PAIRS + (j2 + 1))
                        else:
                            act.wait_ge(hidden_ready, n - 1)
                    nc.scalar.activation(silu[0:r, u, :], act_in[u][0:r, :], ACT.Silu).then_inc(silu_ready, 1)
                    if j == PAIRS:
                        act.wait_ge(wide_done, c * USES + USES)
                        wait(act, shared_taken, c)
                        nc.scalar.activation(share[:], wide_ps[:], ACT.Sigmoid).then_inc(share_ready, 1)
                        act.wait_ge(share_ready, c + 1)
                        act.sem_inc(wide_used, 1)
                    if j == PAIRS + 1:
                        act.wait_ge(down_done, c * ITEMS + PAIRS)
                        wait(act, total_ready, c)
                        nc.scalar.activation(experts[:], expert_ps[:], ACT.Copy).then_inc(experts_copied, 1)

                run(act, step)

            @block.vector
            def _(dve):
                def step(g, i):
                    n, c, j = place(g, i)
                    u = i % 2
                    if current(g):
                        r = rows(j)
                        dve.wait_ge(silu_ready, n + 1)
                        dve.wait_ge(h_done, n + 1)
                        if j < PAIRS:
                            wait(dve, hidden_ready, n)
                            nc.vector.tensor_tensor(gated[:], silu[:, u, :], mul_in[u][:], ALU.mult).then_inc(gated_ready, 1)
                            dve.wait_ge(gated_ready, c * PAIRS + (j + 1))
                            dve.wait_ge(wide_done, c * USES + (j + 1))
                            wait(dve, down_done, n - 1)
                            nc.vector.tensor_tensor(hidden[:, u, :], gated[:], wide_ps[:], ALU.mult).then_inc(hidden_ready, 1)
                            dve.wait_ge(hidden_ready, n + 1)
                            dve.sem_inc(wide_used, 1)
                        else:
                            wait(dve, down_done, n - 1)
                            nc.vector.tensor_tensor(hidden[0:r, u, :], silu[0:r, u, :], mul_in[u][0:r, :], ALU.mult).then_inc(hidden_ready, 1)
                    if j == 1 and after(g, i, ITEMS):
                        dve.wait_ge(down_done, c * ITEMS)
                        dve.wait_ge(share_ready, c)
                        nc.vector.tensor_tensor(shared[:], share[:], shared_ps[:], ALU.mult).then_inc(shared_taken, 1)
                        dve.wait_ge(shared_taken, c)
                        dve.wait_ge(experts_copied, c)
                        wait(dve, turned, c - 1)
                        nc.vector.tensor_tensor(total[:], shared[:], experts[:], ALU.add).then_inc(total_ready, 1)
                    if j == 4 and after(g, i, ITEMS):
                        dve.wait_ge(turned, c)
                        xc = k.x[:, ds((c - 1) * CH, CH)]
                        nc.vector.tensor_tensor(xc, turn_ps[:], xc, ALU.add).then_inc(x_added, 1)

                run(dve, step)
                dve.wait_ge(x_added, CHUNKS)


STAGES = [xattn0, rglru0, ffn0, xattn1, attn1, moe1]




def build(nc, io, out):
    k = Core()
    k.nc = nc
    k.keep = ExitStack()
    k.in_use = []

    def sem(name):
        k.in_use.append(nc.alloc_semaphore(name=name))
        return k.in_use[-1]

    k.sem = sem
    k.keep0 = nc.dram_tensor("keep0", [B, N_CTX], BF16, kind="Internal").ap()
    k.keep1 = nc.dram_tensor("keep1", [B, N_CTX], BF16, kind="Internal").ap()
    k.lat_dram = nc.dram_tensor("latents_normalised", [TOK, D], F32, kind="Internal").ap()
    k.ctx_tail_dram = nc.dram_tensor("ctx_tail_normalised", [B, D], F32, kind="Internal").ap()
    k.v_tail_dram = nc.dram_tensor("ctx_tail_values", [B, D], F32, kind="Internal").ap()
    with k.keep:
        setup(k, io)
        for stage in STAGES:
            k.passed = k.sem(f"passed_{stage.__name__}")
            stage(k, io)
            recycle(k)
        store(k, out)


def recycle(k):
    k.nc.clear_and_free_semaphores(k.in_use)
    k.nc.all_engine_barrier()
    k.in_use = []


def store(k, out):
    nc = k.nc
    stored = k.sem("out_stored")
    with nc.Block() as block:

        @block.sync
        def _(sp):
            sp.dma_start(out.rearrange("(t b) l d -> (b l) t d", b=BPT),
                         k.x[:].rearrange("p (t d) -> p t d", d=D)).then_inc(stored, 16)
            sp.wait_ge(stored, 16)


def constants():
    p = np.arange(P)
    c = {}
    c["c_head_of_feature"] = (p[:, None] // DH1 == np.arange(H)).astype(np.float32)
    c["c_head_in_group4"] = (p[:, None] % L // DH1 == np.arange(BPT * HG) % HG).astype(np.float32)
    c["c_group_of_feature"] = (np.arange(GROUPS)[:, None] == p // L).astype(np.float32)
    c["c_own_value"] = (p[:, None] // L == p % L // DH1).astype(np.float32)
    c["c_batch_in_tile"] = (p[:, None] // L == np.arange(BPT)).astype(np.float32)
    fenwick = np.zeros((L, L), bool)
    for i in range(L):
        j = i + 1
        while j <= L:
            fenwick[i, j - 1] = True
            j += j & -j
        step = 1
        while i - step >= 0:
            fenwick[i, i - step] = True
            step *= 2
    fenwick &= np.tril(np.ones((L, L), bool))
    c["c_fenwick"] = np.tile(np.where(fenwick, 0.0, -NEG0), (HG, 1)).astype(np.float32)
    e = np.arange(E_N)
    c["c_rank"] = np.tile(E_N - e, (P, 1)).astype(np.float32)
    c["c_pair_select"] = (e[:, None, None] == 2 * np.arange(PAIRS)[None, :, None] + p[None, None, :] // E_FF).astype(np.float32)
    return c


def kernel(**inputs):
    import numpy as _np
    import concourse.bacc as _bacc
    from concourse import mybir as _mybir
    from concourse.bass_utils import run_bass_kernel_spmd as _run

    nc = _bacc.Bacc("TRN2", target_bir_lowering=False, num_devices=1)
    arrays, io = {}, {}
    for name, a in {**inputs, **constants()}.items():
        a = _np.ascontiguousarray(a)
        if a.dtype == bool:
            a = a.reshape(-1).view(_np.int32)
        arrays[f"in_{name}"] = a
        io[name] = nc.dram_tensor(f"in_{name}", a.shape, _mybir.dt.from_np(a.dtype), kind="ExternalInput").ap()
    out = nc.dram_tensor("out_0", (B, L, D), F32, kind="ExternalOutput").ap()
    build(nc, io, out)
    r = _run(nc, [arrays], core_ids=[0])
    return r.results[0]["out_0"]
```

```python
from contextlib import ExitStack

import numpy as np
import concourse.bass as bass
from concourse import mybir

F32 = mybir.dt.float32
BF16 = mybir.dt.bfloat16
F32R = mybir.dt.float32r
U8 = mybir.dt.uint8
I32 = mybir.dt.int32
ALU = mybir.AluOpType
ACT = mybir.ActivationFunctionType
AX = mybir.AxisListType
ABSMAX = bass.bass_isa.ReduceOp.absmax
ds = bass.ds

P = 128
B, L, D = 128, 32, 128
N_CTX = 257
TOK = B * L
TILES = TOK // P
BPT = P // L
CH = 512
CHUNKS = TOK // CH
H = 16
DH0 = 64
DH1 = D // H
GROUPS = 4
HG = H // GROUPS
KEYS0 = N_CTX + L
TAIL0 = L + 1
EPS = 1e-5
NEG0 = 3e38
NEG1 = 1e9
RNE = 12582912.0
QMAX = 32767.0
FF0 = 384
FB0 = FF0 // P
WBLK = 32
E_N, E_FF = 16, 64
PAIRS = E_N // 2
PARTS = 3
SH_FF = 352
SH_BLOCKS = [(0, 128), (128, 128), (256, 96)]


HI, LO = 0, 1
PASSES = ((LO, HI), (HI, LO), (HI, HI))
even = lambda n: n + n % 2


class Core:
    pass


def ln_stats(k, stack, name, extra=None):
    nc = k.nc
    n = TILES + (extra is not None)
    tile = lambda part, w: stack.enter_context(nc.sbuf_tensor(f"{name}_{part}", [P, n] + w, F32))
    stats, mean, rstd, twice = tile("stats", [6]), tile("mean", []), tile("rstd", []), tile("twice", [])
    mean_sum, mean_diff, var, var_eps = (tile(part, []) for part in ("mean_sum", "mean_diff", "var", "var_eps"))
    chain, var_ready, rstd_ready = k.sem(f"{name}_chain"), k.sem(f"{name}_var_ready"), k.sem(f"{name}_rstd_ready")
    with nc.Block() as block:

        @block.vector
        def _(dve):
            if extra is not None:
                nc.vector.bn_stats(stats[:, TILES, :], extra)
            with dve.Fori(0, TILES // 4) as g:
                t = g * 4
                for j in range(4):
                    last = nc.vector.bn_stats(stats[:, ds(t + j, 1), :], k.x[:, ds((t + j) * D, D)])
                last.then_inc(chain, 1)
            dve.wait_ge(chain, 8)
            nc.vector.tensor_tensor(mean_diff[:], stats[:, :, 1], stats[:, :, 4], ALU.subtract).then_inc(chain, 1)
            nc.vector.tensor_tensor(var[:], stats[:, :, 2], stats[:, :, 5], ALU.add).then_inc(chain, 1)
            nc.vector.tensor_tensor(mean_sum[:], stats[:, :, 1], stats[:, :, 4], ALU.add).then_inc(chain, 1)
            dve.wait_ge(chain, 11)
            nc.vector.tensor_scalar(mean[:], mean_sum[:], 0.5, None, ALU.mult).then_inc(chain, 1)
            nc.vector.scalar_tensor_tensor(mean_diff[:], mean_diff[:], 0.25, mean_diff[:], ALU.mult, ALU.mult).then_inc(chain, 1)
            dve.wait_ge(chain, 13)
            nc.vector.scalar_tensor_tensor(var[:], var[:], 1.0 / D, mean_diff[:], ALU.mult, ALU.add).then_inc(chain, 1)
            dve.wait_ge(chain, 14)
            nc.vector.tensor_scalar(var_eps[:], var[:], EPS, None, ALU.add).then_inc(var_ready, 1)
            if extra is not None:
                dve.wait_ge(rstd_ready, 1)
                nc.vector.tensor_tensor(twice[:], rstd[:], rstd[:], ALU.mult).then_inc(chain, 1)
                dve.wait_ge(chain, 15)
                nc.vector.tensor_tensor(var[:], var[:], twice[:], ALU.mult).then_inc(chain, 1)
                dve.wait_ge(chain, 16)
                nc.vector.tensor_scalar(var_eps[:], var[:], EPS, None, ALU.add).then_inc(var_ready, 1)
                dve.wait_ge(rstd_ready, 2)
                nc.vector.tensor_tensor(twice[:], twice[:], rstd[:], ALU.mult).then_inc(chain, 1)
                dve.wait_ge(chain, 17)

        @block.gpsimd
        def _(pool):
            pool.wait_ge(var_ready, 1)
            nc.gpsimd.tensor_tensor(rstd[:], var_eps[:], k.minus_half[:, 0:n], ALU.pow).then_inc(rstd_ready, 1)
            if extra is not None:
                pool.wait_ge(var_ready, 2)
                nc.gpsimd.tensor_tensor(twice[:], var_eps[:], k.minus_half[:, 0:n], ALU.pow).then_inc(rstd_ready, 1)
            pool.wait_ge(rstd_ready, 1 + (extra is not None))
    return (mean, rstd) if extra is None else (mean, rstd, twice)


def layer_norm_T(k, name, yT):
    nc = k.nc
    with ExitStack() as stack:
        mean, rstd = ln_stats(k, stack, name)
        z = stack.enter_context(nc.sbuf_tensor(f"{name}_z", [P, 2, 4, D], F32))
        bank = [stack.enter_context(nc.psum_tensor(f"{name}_ps{u}", [P, CH], F32)) for u in range(2)]
        z_ready, turned, copied = k.sem(f"{name}_z_ready"), k.sem(f"{name}_turned"), k.sem(f"{name}_copied")
        with nc.Block() as block:

            @block.vector
            def _(dve):
                with dve.Fori(0, CHUNKS // 2) as g:
                    c = g * 2
                    for u in range(2):
                        dve.wait_ge(turned, c + (u + 1))
                        for j in range(4):
                            t = c * 4 + (4 * u + j)
                            last = nc.vector.tensor_scalar(z[:, u, j, :], k.x[:, ds(t * D, D)], mean[:, ds(t, 1)],
                                                           rstd[:, ds(t, 1)], ALU.subtract, ALU.mult)
                        last.then_inc(z_ready, 1)

            @block.tensor
            def _(pe):
                pe.sem_inc(turned, 2)
                with pe.Fori(0, CHUNKS // 2) as g:
                    c = g * 2
                    for u in range(2):
                        pe.wait_ge(z_ready, c + (u + 1))
                        pe.wait_ge(copied, c + (u + 1))
                        for j in range(4):
                            last = nc.tensor.transpose(bank[u][:, j * P:(j + 1) * P], z[:, u, j, :], k.ident[:])
                        last.then_inc(turned, 1)

            @block.scalar
            def _(act):
                act.sem_inc(copied, 2)
                with act.Fori(0, CHUNKS // 2) as g:
                    c = g * 2
                    for u in range(2):
                        act.wait_ge(turned, c + (u + 3))
                        nc.scalar.activation(yT[:, ds((c + u) * CH, CH)], bank[u][:], ACT.Copy).then_inc(copied, 1)
                act.wait_ge(copied, CHUNKS + 2)


def setup(k, io):
    nc = k.nc
    keep = k.keep
    sb = lambda name, shape, dt=F32: keep.enter_context(nc.sbuf_tensor(name, shape, dt))
    k.x = sb("x", [P, TILES * D])
    k.ident = sb("ident", [P, P])
    k.minus_half = sb("minus_half", [P, TILES + 1])
    k.rne, k.minus_rne = sb("rne", [P, 1]), sb("minus_rne", [P, 1])
    k.tiny = sb("tiny", [P, 1])
    k.zero = sb("zero", [P, 1])
    k.head_of_feature = sb("head_of_feature", [P, H])
    k.head_in_group4 = sb("head_in_group4", [P, BPT * HG])
    k.group_of_feature = sb("group_of_feature", [GROUPS, P])
    k.batch_in_tile = sb("batch_in_tile", [P, BPT])
    k.fenwick = sb("fenwick", [P, L])
    k.pair_select = sb("pair_select", [PARTS * E_N, PAIRS, P], BF16)
    k.rank = sb("rank", [P, E_N])
    k.own_value = sb("own_value", [P, D])
    k.ctx_tail = sb("ctx_tail", [B, D])
    k.A = sb("A", [P, H, P])
    k.U = sb("U", [P, H, P])
    k.g1, k.b1, k.g2, k.b2 = (sb(n, [P, D]) for n in ("g1", "b1", "g2", "b2"))
    k.bo, k.bproj = sb("bo", [P, D]), sb("bproj", [P, D])
    k.w_in, k.w_gate = sb("w_inT", [P, P]), sb("w_gateT", [P, P])
    k.wq1, k.wk1, k.wv1, k.wo1 = (sb(n, [P, P]) for n in ("wq1T", "wk1T", "wv1T", "wo1T"))
    k.wqkv, k.wproj = sb("wqkv", [P, 3 * D]), sb("wproj", [P, D])
    k.f_gate, k.f_up, k.f_down = sb("f_gateT", [P, FF0]), sb("f_upT", [P, FF0]), sb("f_downT", [P, FB0, P])
    k.router = sb("router", [P, E_N])
    k.sh_gate_row = sb("sh_gate_row", [P, P])
    k.sh_gate, k.sh_up, k.sh_down = sb("sh_gateT", [P, SH_FF]), sb("sh_upT", [P, SH_FF]), sb("sh_downT", [P, 3, D])
    ROWS = 12
    k.cols = sb("cols", [P, ROWS])
    (k.b_in, k.b_gate, k.lam, k.bq1, k.bk1, k.bv1, k.bq2, k.bk2, k.bv2, k.g2c, k.b2c, k.shg) = (
        k.cols[:, j:j + 1] for j in range(ROWS))
    with ExitStack() as stack:
        tb = lambda name, shape, dt=F32: stack.enter_context(nc.sbuf_tensor(name, shape, dt))
        rows = tb("rows", [ROWS, D])
        wq0, wkv0, wout0 = tb("wq0", [P, H * DH0]), tb("wkv0", [P, 2 * H * DH0]), tb("wout0", [P, H // 2, D])
        wqT, wkT, wvT = (tb(n, [P, H // 2, P]) for n in ("wq0T", "wk0T", "wv0T"))
        sq = tb("square_weights", [P, 6, P])
        fg, fu, fd = tb("fg", [P, FB0, D]), tb("fu", [P, FB0, D]), tb("fd", [P, FB0, P])
        shg, shu, shd = tb("shg", [P, 3, D]), tb("shu", [P, 3, D]), tb("shd", [P, SH_FF])
        rt = tb("rt", [E_N, D])
        pair_select = tb("pair_select_f32", [PARTS * E_N, PAIRS, P])
        shrow = tb("shrow", [P, P])
        m0, m1 = tb("m0", [B, N_CTX], U8), tb("m1", [B, N_CTX], I32)
        m0b, m1b = tb("m0b", [B, N_CTX], BF16), tb("m1b", [B, N_CTX], BF16)
        qs = tb("qs", [P, 3, 2, FB0 * D // WBLK])
        qt = tb("qt", [P, 3, FB0 * D])
        ps = [stack.enter_context(nc.psum_tensor(f"setup_ps{j}", [P, CH], F32)) for j in range(4)]
        loaded, pool_loaded, x_loaded = k.sem("weights_loaded"), k.sem("weights_loaded_pool"), k.sem("x_loaded")
        ident_ready, consts_ready = k.sem("ident_ready"), k.sem("consts_ready")
        quant, quant_ready = k.sem("quant_chain"), k.sem("weights_quantised")
        turned, copied = k.sem("weights_turned"), [k.sem("weights_copied_dve"), k.sem("weights_copied_act")]
        rows_ready, mask_ready, mask_stored = k.sem("shared_gate_row"), k.sem("mask_ready"), k.sem("mask_stored")
        loads = [
            (k.head_of_feature[:], io["c_head_of_feature"]), (k.head_in_group4[:], io["c_head_in_group4"]),
            (k.group_of_feature[:], io["c_group_of_feature"]),
            (k.batch_in_tile[:], io["c_batch_in_tile"]), (k.fenwick[:], io["c_fenwick"]),
            (pair_select[:], io["c_pair_select"]), (k.rank[:], io["c_rank"]),
            (k.own_value[:], io["c_own_value"]),
            (k.ctx_tail[:], io["ctx_1024"][:, N_CTX - 1, :]), (wq0[:], io["L0_xattn_Wq"]), (wkv0[:], io["L0_xattn_Wkv"]),
            (wout0[:], io["L0_xattn_Wout"].rearrange("(p r) d -> r p d", r=P)),
            (k.wqkv[:], io["L1_attn_W_qkv"]), (k.wproj[:], io["L1_attn_W_proj"]),
            (fg[:], io["L0_ffn_w_gate"].rearrange("(j p) d -> p j d", p=P)),
            (fu[:], io["L0_ffn_w_up"].rearrange("(j p) d -> p j d", p=P)),
            (fd[:].rearrange("p j d -> p (j d)"), io["L0_ffn_w_down"]),
            (shd[:], io["L1_ffn_shared_w_down"]), (rt[:], io["L1_ffn_gate_w"]),
            (m0[:], io["mask_BxS2_bk0"].bitcast(U8).rearrange("(b s) -> b s", b=B)), (m1[:], io["mask_Bx1x1xS2_if1"].rearrange("b o u s -> b (o u s)")),
        ]
        for j, n in enumerate(("L0_attn_W_in", "L0_attn_W_gate", "L1_xattn_W_q", "L1_xattn_W_k", "L1_xattn_W_v", "L1_xattn_W_o")):
            loads.append((sq[:, j, :], io[n]))
        for a, n in ((shg, "L1_ffn_shared_w_gate"), (shu, "L1_ffn_shared_w_up")):
            for j, (r, m) in enumerate(SH_BLOCKS):
                loads.append((a[0:m, j, :], io[n][r:r + m, :]))
        row = lambda ap: ap.rearrange("(a d) -> a d", a=1)
        for n, a in (("L0_xattn_g1", k.g1), ("L0_xattn_b1", k.b1), ("L0_xattn_g2", k.g2), ("L0_xattn_b2", k.b2),
                     ("L1_xattn_b_o", k.bo), ("L1_attn_b_proj", k.bproj)):
            loads.append((a[:], row(io[n]).broadcast_to([P, D])))
        for j, n in enumerate(("L0_attn_b_in", "L0_attn_b_gate", "L0_attn_forget_lambda", "L1_xattn_b_q", "L1_xattn_b_k", "L1_xattn_b_v")):
            loads.append((rows[j:j + 1, :], row(io[n])))
        loads.append((rows[6:9, :], io["L1_attn_b_qkv"].rearrange("(a d) -> a d", a=3)))
        loads.append((rows[9:10, :], row(io["L0_xattn_g2"])))
        loads.append((rows[10:11, :], row(io["L0_xattn_b2"])))
        loads.append((rows[11:12, :], io["L1_ffn_shared_gate_w"]))
        by_sync, by_scalar, by_pool = loads[0::5] + loads[1::5], loads[2::5] + loads[3::5], loads[4::5]
        turns = [(k.cols[:].unsqueeze(1), [rows[:]])]
        for w, base, t in ((wq0, 0, wqT), (wkv0, 0, wkT), (wkv0, H * DH0, wvT)):
            for h in range(0, H // 2, 4):
                turns.append((t[:, h:h + 4, :], [w[:, base + (h + j) * P:base + (h + j + 1) * P] for j in range(4)]))
        for j, a in enumerate((k.w_in, k.w_gate, k.wq1, k.wk1, k.wv1, k.wo1)):
            turns.append((a[:].unsqueeze(1), [sq[:, j, :]]))
        turns.append((k.router[:].unsqueeze(1), [rt[:]]))
        for a, t in ((shg, k.sh_gate), (shu, k.sh_up)):
            for j, (r, m) in enumerate(SH_BLOCKS):
                turns.append((t[:, r:r + m].unsqueeze(1), [a[0:m, j, :]]))
        for j, (r, m) in enumerate(SH_BLOCKS):
            turns.append((k.sh_down[0:m, j:j + 1, :], [shd[:, r:r + m]]))
        quant_from = len(turns)
        turns.append((k.f_gate[:].rearrange("p (j o) -> p j o", j=FB0), [fg[:, j, :] for j in range(FB0)]))
        turns.append((k.f_up[:].rearrange("p (j o) -> p j o", j=FB0), [fu[:, j, :] for j in range(FB0)]))
        turns.append((k.f_down[:], [fd[:, j, :] for j in range(FB0)]))
        half = lambda t, h: t[DH0 * (h % 2):DH0 * (h % 2 + 1), h // 2, :]
        products = []
        for h in (0, 1, 8, 9):
            heads = range(h, h + 8, 2)
            products.append((k.A[:, h:h + 7:2, :], [(half(wqT, i), half(wkT, i)) for i in heads]))
            products.append((k.U[:, h:h + 7:2, :], [(half(wvT, i), half(wout0, i)) for i in heads]))

        VECTOR, SCALAR = 0, 1
        count = len(turns) + len(products)
        groups = [[n for n in range(quant_from, count) if n % 2], [n for n in range(count) if n < quant_from or n % 2 == 0]]

        def filled(n):
            if n < len(turns):
                dst, srcs = turns[n]
                m, r = srcs[0].shape[1], srcs[0].shape[0]
            else:
                dst, srcs = products[n - len(turns)]
                m = r = P
            return dst, ps[n % 4][0:m, 0:len(srcs) * r].rearrange("p (n r) -> p n r", r=r)

        with nc.Block() as block:

            @block.sync
            def _(sp):
                for dst, src in by_sync:
                    sp.dma_start(dst, src).then_inc(loaded, 16)
                sp.dma_start(k.x[:].rearrange("p (t d) -> p t d", d=D),
                             io["x"].rearrange("(t b) l d -> (b l) t d", b=BPT)).then_inc(x_loaded, 16)
                sp.wait_ge(mask_ready, 2)
                sp.dma_start(k.keep0, m0b[:]).then_inc(mask_stored, 16)
                sp.dma_start(k.keep1, m1b[:]).then_inc(mask_stored, 16)
                sp.wait_ge(mask_stored, 32)
                sp.wait_ge(x_loaded, 16)

            @block.gpsimd
            def _(pool):
                for dst, src in by_pool:
                    pool.dma_start(dst, src).then_inc(pool_loaded, 16)
                nc.gpsimd.memset(k.ident[:], 0.0).then_inc(ident_ready, 1)
                nc.gpsimd.memset(k.minus_half[:], -0.5)
                nc.gpsimd.memset(k.rne[:], RNE)
                nc.gpsimd.memset(k.minus_rne[:], -RNE)
                nc.gpsimd.memset(k.zero[:], 0.0)
                nc.gpsimd.memset(k.tiny[:], 1e-6).then_inc(consts_ready, 1)
                pool.wait_ge(ident_ready, 1)
                nc.gpsimd.affine_select(out=k.ident[:], in_=k.ident[:], compare_op=ALU.not_equal, fill=1.0, base=0,
                                        pattern=[[-1, P]], channel_multiplier=1).then_inc(ident_ready, 1)
                pool.wait_ge(ident_ready, 2)
                pool.wait_ge(consts_ready, 1)

            @block.vector
            def _(dve):
                dve.wait_ge(loaded, 16 * len(by_sync + by_scalar))
                dve.wait_ge(pool_loaded, 16 * len(by_pool))
                nc.vector.tensor_copy(k.pair_select[:], pair_select[:])
                nc.vector.tensor_copy(m0b[:], m0[:]).then_inc(mask_ready, 1)
                nc.vector.tensor_scalar(m1b[:], m1[:], 0.0, None, ALU.not_equal).then_inc(mask_ready, 1)
                blocks = lambda a: a.rearrange("p j (n e) -> p (j n) e", e=WBLK)
                spread = lambda a: a.unsqueeze(2).broadcast_to([P, FB0 * D // WBLK, WBLK])
                for j, w in enumerate((fg, fu, fd)):
                    nc.vector.tensor_reduce(qs[:, j, 0, :], blocks(w[:]), AX.X, ALU.max, apply_absolute_value=True)\
                        .then_inc(quant, 1)
                dve.wait_ge(quant, 3)
                nc.vector.tensor_scalar(qs[:, :, 0, :], qs[:, :, 0, :], 1.0 / 7.0, 1e-12, ALU.mult, ALU.max).then_inc(quant, 1)
                dve.wait_ge(quant, 4)
                nc.vector.reciprocal(qs[:, :, 1, :], qs[:, :, 0, :]).then_inc(quant, 1)
                dve.wait_ge(quant, 5)
                flat = lambda a, j: a[:, j, :].rearrange("p (n e) -> p n e", e=WBLK)
                for j, w in enumerate((fg, fu, fd)):
                    nc.vector.tensor_tensor(flat(qt, j), blocks(w[:]), spread(qs[:, j, 1, :]), ALU.mult).then_inc(quant, 1)
                dve.wait_ge(quant, 8)
                nc.vector.tensor_scalar(qt[:], qt[:], RNE, -RNE, ALU.add, ALU.add).then_inc(quant, 1)
                dve.wait_ge(quant, 9)
                for j, w in enumerate((fg, fu, fd)):
                    nc.vector.tensor_tensor(blocks(w[:]), flat(qt, j), spread(qs[:, j, 0, :]), ALU.mult).then_inc(quant_ready, 1)
                for n in groups[VECTOR]:
                    dve.wait_ge(turned, n + 1)
                    nc.vector.tensor_copy(*filled(n)).then_inc(copied[VECTOR], 1)
                dve.wait_ge(copied[VECTOR], len(groups[VECTOR]))
                dve.wait_ge(copied[SCALAR], 1)
                nc.vector.tensor_copy(k.sh_gate_row[:], k.shg.broadcast_to([P, P])).then_inc(rows_ready, 1)
                dve.wait_ge(rows_ready, 1)

            @block.scalar
            def _(act):
                for dst, src in by_scalar:
                    act.dma_start(dst, src).then_inc(loaded, 16)
                for n in groups[SCALAR]:
                    act.wait_ge(turned, n + 1)
                    nc.scalar.activation(*filled(n), ACT.Copy).then_inc(copied[SCALAR], 1)
                act.wait_ge(copied[SCALAR], len(groups[SCALAR]))

            @block.tensor
            def _(pe):
                def wait_copied(n):
                    who = 0 if n in groups[0] else 1
                    pe.wait_ge(copied[who], groups[who].index(n) + 1)

                pe.wait_ge(loaded, 16 * len(by_sync + by_scalar))
                pe.wait_ge(pool_loaded, 16 * len(by_pool))
                pe.wait_ge(ident_ready, 2)
                for n, (dst, srcs) in enumerate(turns):
                    if n == quant_from:
                        pe.wait_ge(quant_ready, 3)
                    if n >= 4:
                        wait_copied(n - 4)
                    m, r = srcs[0].shape[1], srcs[0].shape[0]
                    for j, s in enumerate(srcs):
                        last = nc.tensor.transpose(ps[n % 4][0:m, j * r:(j + 1) * r], s, k.ident[0:r, 0:r])
                    last.then_inc(turned, 1)
                wait_copied(6)
                for n, (dst, mms) in enumerate(products):
                    n += len(turns)
                    wait_copied(n - 4)
                    for j, (lhsT, rhs) in enumerate(mms):
                        last = nc.tensor.matmul(ps[n % 4][:, j * P:(j + 1) * P], lhsT, rhs, start=True, stop=True)
                    last.then_inc(turned, 1)


def wait(eng, sem, count):
    if not isinstance(count, int) or count > 0:
        eng.wait_ge(sem, count)


def wait_apart(k, eng, sem, count):
    eng.wait_ge(sem, count)
    eng.sem_inc(k.passed, 1)


def run_steps(eng, step, lead, lag=0):
    for s in range(-lead, 8):
        step(s // 8, s % 8)
    with eng.Fori(1, B // 8 - 1) as g:
        for j in range(8):
            step(g, j)
    for s in range(B - 8, B + lag):
        step(s // 8, s % 8)


def live(g, j, ahead, n=B):
    return not isinstance(g, int) or 0 <= 8 * g + j + ahead < n


def xattn0_inputs(k, io, stack):
    nc = k.nc
    k.latT = stack.enter_context(nc.sbuf_tensor("latT", [P, TOK], F32))
    k.tailT = stack.enter_context(nc.sbuf_tensor("tailT", [P, B], F32))
    with ExitStack() as st:
        z2 = st.enter_context(nc.sbuf_tensor("lat_z2", [P, 2, 4, D], F32))
        lat = st.enter_context(nc.sbuf_tensor("lat_affine", [P, 2, 4, D], F32))
        tail = st.enter_context(nc.sbuf_tensor("ctx_tail_affine", [P, 2, D], F32))
        bank = [st.enter_context(nc.psum_tensor(f"lat_ps{u}", [P, CH], F32)) for u in range(2)]
        tail_ps = st.enter_context(nc.psum_tensor("lat_ps_tail", [P, P], F32))
        z2_ready, turned, copied = k.sem("lat_z2_ready"), k.sem("lat_turned"), k.sem("lat_copied")
        scaled, affine_ready, stored = k.sem("lat_scaled"), k.sem("lat_affine_ready"), [k.sem(f"lat_stored{u}") for u in range(2)]
        tail_z, tail_scaled, tail_turned, tail_stored = (k.sem(f"ctx_tail_{n}") for n in ("z", "scaled", "turned", "stored"))
        mean, rstd, twice = ln_stats(k, st, "lat_ln", k.ctx_tail[:])
        with nc.Block() as block:

            @block.vector
            def _(dve):
                nc.vector.tensor_scalar(tail[:, 0, :], k.ctx_tail[:], mean[:, TILES:TILES + 1], rstd[:, TILES:TILES + 1],
                                        ALU.subtract, ALU.mult).then_inc(tail_z, 1)
                with dve.Fori(0, CHUNKS // 2) as g:
                    c = g * 2
                    for u in range(2):
                        dve.wait_ge(turned, c + (u + 1))
                        dve.wait_ge(affine_ready, c + (u + 1))
                        for j in range(4):
                            t = c * 4 + (4 * u + j)
                            last = nc.vector.tensor_scalar(z2[:, u, j, :], k.x[:, ds(t * D, D)], mean[:, ds(t, 1)],
                                                           twice[:, ds(t, 1)], ALU.subtract, ALU.mult)
                        last.then_inc(z2_ready, 1)
                dve.wait_ge(tail_turned, 1)
                nc.vector.tensor_copy(k.tailT[:], tail_ps[:]).then_inc(tail_turned, 1)
                dve.wait_ge(tail_turned, 2)

            @block.gpsimd
            def _(pool):
                pool.wait_ge(tail_z, 1)
                nc.gpsimd.tensor_tensor(tail[:, 0, :], tail[:, 0, :], k.g1[:], ALU.mult).then_inc(tail_scaled, 1)
                pool.wait_ge(tail_scaled, 1)
                nc.gpsimd.tensor_tensor(tail[:, 1, :], tail[:, 0, :], k.b1[:], ALU.add).then_inc(tail_scaled, 1)
                pool.sem_inc(affine_ready, 2)
                spread = lambda a: a[:].unsqueeze(1).broadcast_to([P, 4, D])
                with pool.Fori(0, CHUNKS // 2) as g:
                    c = g * 2
                    for u in range(2):
                        pool.wait_ge(z2_ready, c + (u + 1))
                        pool.wait_ge(stored[u], g * 16 + 16)
                        nc.gpsimd.tensor_tensor(lat[:, u], z2[:, u], spread(k.g2), ALU.mult).then_inc(scaled, 1)
                        pool.wait_ge(scaled, c + (u + 1))
                        nc.gpsimd.tensor_tensor(lat[:, u], lat[:, u], spread(k.b2), ALU.add).then_inc(affine_ready, 1)

            @block.tensor
            def _(pe):
                pe.sem_inc(turned, 2)
                with pe.Fori(0, CHUNKS // 2) as g:
                    c = g * 2
                    for u in range(2):
                        pe.wait_ge(z2_ready, c + (u + 1))
                        pe.wait_ge(copied, c + (u + 1))
                        for j in range(4):
                            last = nc.tensor.transpose(bank[u][:, j * P:(j + 1) * P], z2[:, u, j, :], k.ident[:])
                        last.then_inc(turned, 1)
                pe.wait_ge(tail_scaled, 2)
                nc.tensor.transpose(tail_ps[:], tail[:, 1, :], k.ident[:]).then_inc(tail_turned, 1)

            @block.scalar
            def _(act):
                act.sem_inc(copied, 2)
                with act.Fori(0, CHUNKS // 2) as g:
                    c = g * 2
                    for u in range(2):
                        act.wait_ge(turned, c + (u + 3))
                        nc.scalar.activation(k.latT[:, ds((c + u) * CH, CH)], bank[u][:], ACT.Identity, bias=k.b2c,
                                             scale=k.g2c).then_inc(copied, 1)
                act.wait_ge(copied, CHUNKS + 2)

            @block.sync
            def _(sp):
                for u in range(2):
                    sp.sem_inc(stored[u], 16)
                with sp.Fori(0, CHUNKS // 2) as g:
                    c = g * 2
                    for u in range(2):
                        sp.wait_ge(affine_ready, c + (u + 3))
                        sp.dma_start(k.lat_dram[ds((c + u) * CH, CH), :].rearrange("(t p) d -> p t d", p=P),
                                     lat[:, u]).then_inc(stored[u], 16)
                sp.wait_ge(tail_scaled, 2)
                sp.dma_start(k.ctx_tail_dram, tail[:, 1, :]).then_inc(tail_stored, 16)
                sp.wait_ge(tail_stored, 16)
                for u in range(2):
                    sp.wait_ge(stored[u], 16 * CHUNKS // 2 + 16)


def xattn0(k, io):
    nc = k.nc
    with ExitStack() as stack:
        xattn0_inputs(k, io, stack)
        sb = lambda name, shape, dt=F32: stack.enter_context(nc.sbuf_tensor(name, shape, dt))
        psum = lambda name: stack.enter_context(nc.psum_tensor(name, [P, CH], F32))
        sem = k.sem
        raw = sb("a_raw", [P, 8, 2, D])
        stats, mv = sb("a_stats", [P, 2, 2, 6]), sb("a_mv", [P, 2, 2, 2])
        var, rstd = sb("a_var", [P, 2, 2]), sb("a_rstd", [P, 2, 2])
        z = sb("a_z", [P, 2, 2, D])
        xn = sb("a_xn", [P, 8, 2, D])
        tail = sb("a_tail", [TAIL0, 8, D])
        xnT = sb("a_xnT", [P, 2, 8, even(KEYS0)], F32R)
        kept = sb("a_kept", [P, 2, BPT, N_CTX], BF16)
        bias = sb("a_bias", [P, 8, KEYS0])
        qT = sb("a_qT", [P, 2, 2, BPT, H, L], F32R)
        neg = sb("a_neg", [P, GROUPS, KEYS0])
        nmax = sb("a_nmax", [P, 2, GROUPS])
        prob = sb("a_prob", [P, 2, GROUPS, KEYS0])
        rsum, rinv = sb("a_rsum", [P, 2, GROUPS]), sb("a_rinv", [P, 2, GROUPS])
        probT = sb("a_probT", [P, 3, CH])
        oT = sb("a_oT", [P, H, P])
        score_ps, turn_ps = [psum("a_score0"), psum("a_score1")], [psum("a_turn0"), psum("a_turn1")]
        out_ps, ctx_ps, q_ps, proj_ps = psum("a_out"), psum("a_ctx"), psum("a_q"), psum("a_proj")
        raw_loaded = [sem(f"a_raw_loaded{j}") for j in range(8)]
        kept_loaded = [sem(f"a_kept_loaded{u}") for u in range(2)]
        tail_loaded = [sem(f"a_tail_loaded{u}") for u in range(2)]
        stats_ready, mv_ready, var_ready, rstd_ready = sem("a_stats_ready"), sem("a_mv_ready"), sem("a_var_ready"), sem("a_rstd_ready")
        z_ready, scaled, xn_ready = sem("a_z_ready"), sem("a_scaled"), sem("a_xn_ready")
        ctx_turned, xnT_hi, xnT_ready, keys_hi, keys_ready = (sem(f"a_{n}") for n in ("ctx_turned", "xnT_hi", "xnT_ready", "tile_keys_hi", "tile_keys_ready"))
        q_ready, q_hi, q_copied = sem("a_q_ready"), sem("a_q_hi"), sem("a_q_copied")
        scored, masked, exped, rinv_ready, prob_ready = (sem(f"a_{n}") for n in ("scored", "masked", "exped", "rinv_ready", "prob_ready"))
        turned, probT_ready = [sem(f"a_turned{n}") for n in range(3)], [sem(f"a_probT_ready{n}") for n in range(3)]
        out_ready, oT_ready, proj_ready, x_added = (sem(f"a_{n}") for n in ("out_ready", "oT_ready", "proj_ready", "x_added"))
        zeroed = sem("a_zeroed")
        LEAD, LAG = 5, 1
        TKEYS = (P, P, TAIL0)

        def tile_of(g, j, ahead=0):
            return g * 2 + (j + ahead) // 4

        def quarter(b):
            return (1, b + 1) if b < 3 else (2, 0)

        def q_half(g, j, half):
            ahead, hg = quarter(j % 4)
            return qT[:, half, (j // 4 + ahead) % 2, :, 4 * hg:4 * hg + 4, :].rearrange("p b h l -> p h b l")

        with nc.Block() as block:

            @block.sync
            def _(sp):
                def load_raw(g, j):
                    sp.dma_start(raw[:, j % 8], io["ctx_1024"][ds(g * 8 + j, 1), 0:2 * P, :].rearrange(
                        "b (t p) d -> p (b t) d", p=P)).then_inc(raw_loaded[j % 8], 16)

                def load_kept(t, u):
                    sp.dma_start(kept[:, u], k.keep0[ds(t * BPT, BPT), :].unsqueeze(0).broadcast_to([P, BPT, N_CTX]))\
                        .then_inc(kept_loaded[u], 16)

                def step(g, j):
                    s, t, u, b = g * 8 + j, tile_of(g, j), j // 4, j % 4
                    if live(g, j, 8):
                        wait(sp, z_ready, s + 1)
                        load_raw(g + 1, j)
                    if b == 0 and live(g, j, 8):
                        wait(sp, keys_ready, t + 1)
                        load_kept(t + 2, u)
                    if b == 3 and live(g, j, 8):
                        wait(sp, out_ready, s + 1)
                        rows = slice(4 * u, 4 * u + 4)
                        sp.dma_start(tail[0:L, rows, :], k.lat_dram[ds((t + 2) * P, P), :].rearrange(
                            "(b l) d -> l b d", l=L)).then_inc(tail_loaded[u], 16)
                        sp.dma_start(tail[L:L + 1, rows, :], k.ctx_tail_dram[ds((t + 2) * BPT, BPT), :].unsqueeze(0))\
                            .then_inc(tail_loaded[u], 16)

                for j in range(3):
                    load_raw(0, j)
                load_kept(0, 0)
                run_steps(sp, step, LEAD)

            @block.gpsimd
            def _(pool):
                for half in (HI, LO):
                    nc.gpsimd.tensor_copy(xnT[:, half, :, KEYS0:], k.zero[:].unsqueeze(1).broadcast_to([P, 8, even(KEYS0) - KEYS0]))
                nc.gpsimd.memset(bias[:, :, 2 * P:2 * P + L], 0.0).then_inc(zeroed, 1)
                spread = lambda a: a[:].unsqueeze(1).broadcast_to([P, 2, D])

                def step(g, j):
                    s, t, u, b = g * 8 + j, tile_of(g, j), j // 4, j % 4
                    if live(g, j, 4):
                        n, par = (j + 4) % 8, j % 2
                        pool.wait_ge(z_ready, s + 5)
                        nc.gpsimd.tensor_tensor(xn[:, n], z[:, par], spread(k.g1), ALU.mult).then_inc(scaled, 1)
                        pool.wait_ge(scaled, s + 5)
                        nc.gpsimd.tensor_tensor(xn[:, n], xn[:, n], spread(k.b1), ALU.add).then_inc(xn_ready, 1)
                    if live(g, j, 5):
                        par = (j + 5) % 2
                        wait_apart(k, pool, mv_ready, s + 6)
                        nc.gpsimd.tensor_scalar(var[:, par], mv[:, par, :, 1], EPS, None, ALU.add).then_inc(var_ready, 1)
                        pool.wait_ge(var_ready, s + 6)
                        nc.gpsimd.tensor_tensor(rstd[:, par], var[:, par], k.minus_half[:, 0:2], ALU.pow).then_inc(rstd_ready, 1)
                    if b == 3 and live(g, j, 8):
                        slots = slice(4 * u, 4 * u + 4)
                        wait(pool, masked, s * 4 + 8 - 4)
                        lat = k.latT[:, ds((t + 2) * P, P)].rearrange("p (b l) -> p b l", l=L)
                        last = k.tailT[:, ds((t + 2) * BPT, BPT)].unsqueeze(2)
                        lat_half, last_half = ((lambda half, r=r: xnT[:, half, slots, r]) for r in (slice(2 * P, 2 * P + L), slice(KEYS0 - 1, KEYS0)))
                        nc.gpsimd.tensor_copy(lat_half(HI), lat)
                        nc.gpsimd.tensor_copy(last_half(HI), last).then_inc(keys_hi, 1)
                        wait_apart(k, pool, keys_hi, t + 3)
                        nc.gpsimd.tensor_tensor(lat_half(LO), lat, lat_half(HI), ALU.subtract)
                        nc.gpsimd.tensor_tensor(last_half(LO), last, last_half(HI), ALU.subtract)
                        wait_apart(k, pool, kept_loaded[u], (g + 2) * 16)
                        nc.gpsimd.tensor_scalar(bias[:, slots, 0:2 * P], kept[:, u, :, 0:2 * P], NEG0, -NEG0, ALU.mult, ALU.add)
                        nc.gpsimd.tensor_scalar(bias[:, slots, KEYS0 - 1:KEYS0], kept[:, u, :, 2 * P:N_CTX], NEG0, -NEG0,
                                                ALU.mult, ALU.add).then_inc(keys_ready, 1)

                run_steps(pool, step, LEAD)

            @block.vector
            def _(dve):
                def mask(g, j, grp):
                    s, n, par = g * 8 + j, (j + 1) % 8, (j + 1) % 2
                    if n % 4 == 0 and grp == 0:
                        dve.wait_ge(keys_ready, tile_of(g, j, 1) + 1)
                    wait_apart(k, dve, scored, s * 4 + (5 + grp))
                    nc.vector.tensor_tensor_reduce(
                        out=neg[:, grp, :], in0=score_ps[grp % 2][:, 0:KEYS0], in1=bias[:, n, :], scale=-DH0 ** -0.5,
                        scalar=3.4e38, op0=ALU.add, op1=ALU.min, accum_out=nmax[:, par, grp:grp + 1]).then_inc(masked, 1)

                def step(g, j):
                    s, t, u, b = g * 8 + j, tile_of(g, j), j // 4, j % 4
                    if live(g, j, 1):
                        mask(g, j, 0)
                        mask(g, j, 1)
                    if live(g, j, 0):
                        dve.wait_ge(turned[0], s + 1)
                        nc.vector.tensor_copy(probT[:, 0, :], turn_ps[0][:]).then_inc(probT_ready[0], 1)
                    if live(g, j, 1):
                        mask(g, j, 2)
                        mask(g, j, 3)
                    if live(g, j, 5):
                        n, par = (j + 5) % 8, (j + 5) % 2
                        dve.wait_ge(raw_loaded[n], (g + (j + 5) // 8 + 1) * 16)
                        for kt in range(2):
                            last = nc.vector.bn_stats(stats[:, par, kt, :], raw[:, n, kt, :])
                        last.then_inc(stats_ready, 1)
                    if live(g, j, 4):
                        n, par = (j + 4) % 8, j % 2
                        dve.wait_ge(rstd_ready, s + 5)
                        wait(dve, xn_ready, s + 3)
                        for kt in range(2):
                            last = nc.vector.tensor_scalar(z[:, par, kt, :], raw[:, n, kt, :], mv[:, par, kt, 0:1],
                                                           rstd[:, par, kt:kt + 1], ALU.subtract, ALU.mult)
                        last.then_inc(z_ready, 1)
                    if live(g, j, 5):
                        par = (j + 5) % 2
                        wait_apart(k, dve, stats_ready, s + 6)
                        for kt in range(2):
                            last = nc.vector.bn_aggr(mv[:, par, kt, :], stats[:, par, kt, :])
                        last.then_inc(mv_ready, 1)
                    if live(g, j, 1):
                        par = (j + 1) % 2
                        dve.wait_ge(exped, s * 4 + 8)
                        nc.vector.reciprocal(rinv[:, par, :], rsum[:, par, :]).then_inc(rinv_ready, 1)
                        dve.wait_ge(rinv_ready, s + 2)
                        for grp in range(GROUPS):
                            last = nc.vector.tensor_scalar(prob[:, par, grp, :], prob[:, par, grp, :],
                                                           rinv[:, par, grp:grp + 1], None, ALU.mult)
                        last.then_inc(prob_ready, 1)
                    if live(g, j, 4 * quarter(b)[0] - b):
                        dve.wait_ge(q_hi, (t + quarter(b)[0]) * 4 + (quarter(b)[1] + 1))
                        nc.vector.tensor_tensor(q_half(g, j, LO), q_ps[:].rearrange("p (h b l) -> p h b l", h=4, l=L),
                                                q_half(g, j, HI), ALU.subtract).then_inc(q_copied, 1)
                    if live(g, j, 3):
                        dve.wait_ge(xnT_hi, s + 4)
                        n = (j + 3) % 8
                        nc.vector.tensor_tensor(xnT[:, LO, n, 0:2 * P], ctx_ps[:, 0:2 * P], xnT[:, HI, n, 0:2 * P],
                                                ALU.subtract).then_inc(xnT_ready, 1)
                    if b == 0 and live(g, j, -1):
                        dve.wait_ge(proj_ready, t)
                        xt = k.x[:, ds((t - 1) * D, D)]
                        nc.vector.tensor_tensor(xt, proj_ps[:, 0:D], xt, ALU.add).then_inc(x_added, 1)

                dve.wait_ge(zeroed, 1)
                run_steps(dve, step, LEAD, LAG)
                dve.wait_ge(x_added, TILES)

            @block.scalar
            def _(act):
                def exp(g, j, grp):
                    s, par = g * 8 + j, (j + 1) % 2
                    act.wait_ge(masked, s * 4 + (5 + grp))
                    nc.scalar.activation(prob[:, par, grp, :], neg[:, grp, :], ACT.Exp, bias=nmax[:, par, grp:grp + 1],
                                         scale=-1.0, accum_out=rsum[:, par, grp:grp + 1]).then_inc(exped, 1)

                def step(g, j):
                    s, t, u, b = g * 8 + j, tile_of(g, j), j // 4, j % 4
                    if live(g, j, 1):
                        exp(g, j, 0)
                        exp(g, j, 1)
                    if live(g, j, 0):
                        act.wait_ge(turned[1], s + 1)
                        nc.scalar.activation(probT[:, 1, :], turn_ps[1][:], ACT.Copy).then_inc(probT_ready[1], 1)
                    if live(g, j, 1):
                        exp(g, j, 2)
                        exp(g, j, 3)
                    if live(g, j, 3):
                        act.wait_ge(ctx_turned, s + 4)
                        nc.scalar.activation(xnT[:, HI, (j + 3) % 8, 0:2 * P], ctx_ps[:, 0:2 * P], ACT.Copy).then_inc(xnT_hi, 1)
                    if live(g, j, 0):
                        act.wait_ge(turned[2], s + 1)
                        nc.scalar.activation(probT[0:TAIL0, 2, :], turn_ps[0][0:TAIL0, :], ACT.Copy).then_inc(probT_ready[2], 1)
                    ahead, hg = quarter(b)
                    if live(g, j, 4 * ahead - b):
                        act.wait_ge(q_ready, (t + ahead) * 4 + (hg + 1))
                        nc.scalar.activation(q_half(g, j, HI), q_ps[:].rearrange("p (h b l) -> p h b l", h=4, l=L),
                                             ACT.Copy).then_inc(q_hi, 1)
                    if live(g, j, 0):
                        act.wait_ge(out_ready, s + 1)
                        if b == 0:
                            wait(act, proj_ready, t)
                        nc.scalar.activation(oT[:, :, b * L:(b + 1) * L], out_ps[:].rearrange("p (h l) -> p h l", l=L),
                                             ACT.Copy).then_inc(oT_ready, 1)

                run_steps(act, step, LEAD, LAG)

            @block.tensor
            def _(pe):
                def score(g, j, grp):
                    s, n, un, bn = g * 8 + j, (j + 1) % 8, (j + 1) // 4 % 2, (j + 1) % 4
                    if grp == 0:
                        pe.wait_ge(xnT_ready, s + 2)
                        if bn == 0:
                            pe.wait_ge(keys_ready, tile_of(g, j, 1) + 1)
                            pe.wait_ge(q_copied, tile_of(g, j, 1) * 4 + 4)
                    wait(pe, masked, s * 4 + (3 + grp))
                    for p, (a, c) in enumerate(PASSES):
                        last = nc.tensor.matmul(score_ps[grp % 2][:, 0:even(KEYS0)], qT[:, a, un, bn, 4 * grp:4 * grp + 4, :],
                                                xnT[:, c, n, :], start=(p == 0), stop=(p == len(PASSES) - 1))
                    last.then_inc(scored, 1)

                def turn(g, j, kt):
                    s, m = g * 8 + j, TKEYS[kt]
                    if kt == 0:
                        pe.wait_ge(prob_ready, s + 1)
                        wait(pe, probT_ready[2], s)
                    if kt == 2:
                        wait_apart(k, pe, probT_ready[0], s + 1)
                    for grp in range(GROUPS):
                        last = nc.tensor.transpose(turn_ps[kt % 2][0:m, grp * P:(grp + 1) * P],
                                                   prob[:, j % 2, grp, kt * P:kt * P + m], k.ident[:])
                    last.then_inc(turned[kt], 1)

                def values(g, j, kt):
                    s, m = g * 8 + j, TKEYS[kt]
                    pe.wait_ge(probT_ready[kt], s + 1)
                    if kt == 0:
                        wait(pe, oT_ready, s)
                    if kt == 2 and j % 4 == 0:
                        pe.wait_ge(tail_loaded[j // 4], (g + 1) * 32)
                    lhsT = xn[:, j, kt, :] if kt < 2 else tail[:, j, :]
                    last = nc.tensor.matmul(out_ps[:], lhsT, probT[0:m, kt, :], start=(kt == 0), stop=(kt == 2))
                    if kt == 2:
                        last.then_inc(out_ready, 1)

                def query(g, j):
                    ahead, hg = quarter(j % 4)
                    t = tile_of(g, j)
                    wait(pe, q_copied, (t + ahead) * 4 + hg)
                    for h in range(4):
                        last = nc.tensor.matmul(q_ps[:, h * P:(h + 1) * P], k.A[:, 4 * hg + h, :],
                                                k.latT[:, ds((t + ahead) * P, P)], start=True, stop=True)
                    last.then_inc(q_ready, 1)

                def step(g, j):
                    s, t, u, b = g * 8 + j, tile_of(g, j), j // 4, j % 4
                    here, ahead = live(g, j, 0), live(g, j, 1)
                    if ahead:
                        score(g, j, 0)
                        score(g, j, 1)
                    if here:
                        turn(g, j, 0)
                        turn(g, j, 1)
                    if live(g, j, 3):
                        n = (j + 3) % 8
                        pe.wait_ge(xn_ready, s + 4)
                        wait(pe, xnT_ready, s + 3)
                        for kt in range(2):
                            last = nc.tensor.transpose(ctx_ps[:, kt * P:(kt + 1) * P], xn[:, n, kt, :], k.ident[:])
                        last.then_inc(ctx_turned, 1)
                    if ahead:
                        score(g, j, 2)
                        score(g, j, 3)
                    if b == 0 and live(g, j, -1):
                        pe.wait_ge(oT_ready, s)
                        wait(pe, x_added, t - 1)
                        for h in range(H):
                            last = nc.tensor.matmul(proj_ps[:, 0:D], oT[:, h, :], k.U[:, h, :], start=(h == 0),
                                                    stop=(h == H - 1))
                        last.then_inc(proj_ready, 1)
                    if here:
                        values(g, j, 0)
                        turn(g, j, 2)
                    if live(g, j, 4 * quarter(b)[0] - b):
                        query(g, j)
                    if here:
                        values(g, j, 1)
                        values(g, j, 2)

                run_steps(pe, step, LEAD, LAG)


def rglru0(k, io):
    nc = k.nc
    with ExitStack() as stack:
        sb = lambda name, shape: stack.enter_context(nc.sbuf_tensor(name, shape, F32))
        psum = lambda name: stack.enter_context(nc.psum_tensor(name, [P, CH], F32))
        sem = k.sem
        yT = sb("r_yT", [P, TOK])
        layer_norm_T(k, "r_ln", yT)
        gate_in, alpha = sb("r_gate_in", [P, TOK]), sb("r_alpha", [P, TOK])
        sp_ = sb("r_softplus", [P, 6])
        beta, square, drive, h = (sb(f"r_{n}", [P, 2, CH]) for n in ("beta", "square", "drive", "h"))
        in_ps, rec_ps = [psum("r_in0"), psum("r_in1")], [psum("r_rec0"), psum("r_rec1")]
        hT_ps = [psum("r_hT0"), psum("r_hT1")]
        gates_done, gates_read, chain = sem("r_gates_done"), sem("r_gates_read"), sem("r_softplus_chain")
        with nc.Block() as block:

            @block.tensor
            def _(pe):
                with pe.Fori(0, CHUNKS // 2) as g:
                    c = g * 2
                    for u in range(2):
                        pe.wait_ge(gates_read, c + (u + 1))
                        y = yT[:, ds((c + u) * CH, CH)]
                        nc.tensor.matmul(in_ps[u][:], k.w_in[:], y, start=True, stop=True)
                        nc.tensor.matmul(rec_ps[u][:], k.w_gate[:], y, start=True, stop=True).then_inc(gates_done, 1)

            @block.scalar
            def _(act):
                act.wait_ge(chain, 1)
                nc.scalar.activation(sp_[:, 1:2], sp_[:, 0:1], ACT.Exp, scale=-1.0).then_inc(chain, 1)
                act.sem_inc(gates_read, 2)
                with act.Fori(0, CHUNKS // 2) as g:
                    c = g * 2
                    for u in range(2):
                        act.wait_ge(gates_done, c + (u + 1))
                        cols = ds((c + u) * CH, CH)
                        nc.scalar.activation(gate_in[:, cols], in_ps[u][:], ACT.Sigmoid, bias=k.b_in)
                        nc.scalar.activation(alpha[:, cols], rec_ps[u][:], ACT.Sigmoid, bias=k.b_gate).then_inc(gates_read, 1)
                act.wait_ge(gates_read, CHUNKS + 2)
                act.wait_ge(chain, 17)
                nc.scalar.activation(alpha[:], alpha[:], ACT.Exp, scale=sp_[:, 5:6]).then_inc(gates_read, 1)
                act.wait_ge(gates_read, CHUNKS + 3)

            @block.vector
            def _(dve):
                size, e, q, q2, t, rate = (sp_[:, j:j + 1] for j in range(6))
                nc.vector.scalar_tensor_tensor(size, k.lam, -1.0, k.lam, ALU.mult, ALU.max).then_inc(chain, 1)
                dve.wait_ge(chain, 2)
                nc.vector.tensor_scalar(q, e, 2.0, None, ALU.add).then_inc(chain, 1)
                dve.wait_ge(chain, 3)
                nc.vector.reciprocal(q, q).then_inc(chain, 1)
                dve.wait_ge(chain, 4)
                nc.vector.tensor_tensor(q, q, e, ALU.mult).then_inc(chain, 1)
                dve.wait_ge(chain, 5)
                nc.vector.tensor_tensor(q2, q, q, ALU.mult).then_inc(chain, 1)
                dve.wait_ge(chain, 6)
                nc.vector.tensor_scalar(t, q2, 1.0 / 17, None, ALU.mult).then_inc(chain, 1)
                for n, odd in enumerate((15, 13, 11, 9, 7, 5, 3)):
                    dve.wait_ge(chain, 7 + n)
                    nc.vector.scalar_tensor_tensor(t, t, 1.0 / odd, q2, ALU.add, ALU.mult).then_inc(chain, 1)
                dve.wait_ge(chain, 14)
                nc.vector.scalar_tensor_tensor(t, t, 1.0, q, ALU.add, ALU.mult).then_inc(chain, 1)
                nc.vector.tensor_scalar(q2, k.lam, 0.0, -8.0, ALU.max, ALU.mult).then_inc(chain, 1)
                dve.wait_ge(chain, 16)
                nc.vector.scalar_tensor_tensor(rate, t, -16.0, q2, ALU.mult, ALU.add).then_inc(chain, 1)
                dve.wait_ge(chain, 17)
        squared, rooted, driven, cleared, scanned, turned, added = (
            sem(f"r_{n}") for n in ("squared", "rooted", "driven", "cleared", "scanned", "turned", "added"))
        half_driven = sem("r_half_driven")
        with nc.Block() as block:

            @block.gpsimd
            def _(pool):
                pool.sem_inc(rooted, 2)
                with pool.Fori(0, CHUNKS // 2) as g:
                    c = g * 2
                    for u in range(2):
                        a = alpha[:, ds((c + u) * CH, CH)]
                        pool.wait_ge(rooted, c + (u + 1))
                        nc.gpsimd.tensor_tensor(square[:, u], a, a, ALU.mult).then_inc(squared, 1)

            @block.scalar
            def _(act):
                with act.Fori(0, CHUNKS // 2) as g:
                    c = g * 2
                    for u in range(2):
                        act.wait_ge(driven, c * 2 + (2 * u + 1))
                        nc.scalar.activation(beta[:, u], beta[:, u], ACT.Sqrt, bias=k.tiny[:]).then_inc(rooted, 1)

            @block.vector
            def _(dve):
                def start(g, u):
                    c = g * 2
                    cols = ds((c + u) * CH, CH)
                    dve.wait_ge(squared, c + (u + 1))
                    nc.vector.tensor_scalar(beta[:, u], square[:, u], -1.0, 1.0, ALU.mult, ALU.add).then_inc(driven, 1)
                    nc.vector.tensor_tensor(drive[:, u], gate_in[:, cols], yT[:, cols], ALU.mult).then_inc(driven, 1)

                def finish(g, u):
                    c = g * 2
                    cols = ds((c + u) * CH, CH)
                    nc.vector.tensor_copy(alpha[:, ds((c + u) * CH, CH)].rearrange("p (b l) -> p b l", l=L)[:, :, 0:1],
                                          k.zero[:].unsqueeze(1).broadcast_to([P, CH // L, 1])).then_inc(cleared, 1)
                    dve.wait_ge(rooted, c + (u + 3))
                    dve.wait_ge(driven, c * 2 + (2 * u + 2))
                    nc.vector.tensor_tensor(drive[:, u], drive[:, u], beta[:, u], ALU.mult).then_inc(half_driven, 1)
                    dve.wait_ge(half_driven, c + (u + 1))
                    dve.wait_ge(cleared, c + (u + 1))
                    dve.wait_ge(turned, c + (u + 1))
                    nc.vector.tensor_tensor_scan(h[:, u], alpha[:, cols], drive[:, u], 0.0, ALU.mult, ALU.add)\
                        .then_inc(scanned, 1)

                def add(g, u):
                    c = g * 2
                    dve.wait_ge(turned, c + (u + 3))
                    xc = k.x[:, ds((c + u) * CH, CH)]
                    nc.vector.tensor_tensor(xc, hT_ps[u][:], xc, ALU.add).then_inc(added, 1)

                dve.sem_inc(added, 1)
                with dve.Fori(0, CHUNKS // 2) as g:
                    start(g, 0)
                    start(g, 1)
                    finish(g, 0)
                    finish(g, 1)
                    add(g, 0)
                    add(g, 1)
                dve.wait_ge(added, CHUNKS + 1)

            @block.tensor
            def _(pe):
                pe.sem_inc(turned, 2)
                with pe.Fori(0, CHUNKS // 2) as g:
                    c = g * 2
                    for u in range(2):
                        pe.wait_ge(scanned, c + (u + 1))
                        pe.wait_ge(added, c + 1)
                        for j in range(4):
                            last = nc.tensor.transpose(hT_ps[u][:, j * P:(j + 1) * P], h[:, u, j * P:(j + 1) * P], k.ident[:])
                        last.then_inc(turned, 1)


def tensor_scale(k, name, stack, maxima, factor=None):
    nc = k.nc
    n = maxima.shape[1]
    q = stack.enter_context(nc.sbuf_tensor(f"{name}_scale", [P, 4, n], F32))
    chain, reduced = k.sem(f"{name}_chain"), k.sem(f"{name}_reduced")
    with nc.Block() as block:

        @block.vector
        def _(dve):
            nc.vector.tensor_reduce(q[:, 0], maxima, AX.X, ALU.max, apply_absolute_value=True).then_inc(chain, 1)
            dve.wait_ge(reduced, 1)
            scaled = 1
            if factor is not None:
                nc.vector.tensor_scalar(q[:, 1], q[:, 1], factor, None, ALU.mult).then_inc(chain, 1)
                scaled = 2
                dve.wait_ge(chain, scaled)
            nc.vector.tensor_scalar(q[:, 2], q[:, 1], 1.0 / QMAX, 1e-12, ALU.mult, ALU.max).then_inc(chain, 1)
            dve.wait_ge(chain, scaled + 1)
            nc.vector.reciprocal(q[:, 3], q[:, 2]).then_inc(chain, 1)
            dve.wait_ge(chain, scaled + 2)
            if factor is not None:
                nc.vector.tensor_scalar(q[:, 3], q[:, 3], factor, None, ALU.mult).then_inc(chain, 1)
                dve.wait_ge(chain, scaled + 3)

        @block.gpsimd
        def _(pool):
            pool.wait_ge(chain, 1)
            nc.gpsimd.partition_all_reduce(q[:, 1], q[:, 0], P, ABSMAX).then_inc(reduced, 1)
            pool.wait_ge(reduced, 1)
    return [(q[:, 2, t:t + 1], q[:, 3, t:t + 1]) for t in range(n)]


def ffn0(k, io):
    nc = k.nc
    with ExitStack() as stack:
        sb = lambda name, shape: stack.enter_context(nc.sbuf_tensor(name, shape, F32))
        sem = k.sem
        yT = sb("f_yT", [P, TOK])
        layer_norm_T(k, "f_ln", yT)
        up, gate = sb("f_up", [P, FB0, TOK]), sb("f_gate", [P, FB0, TOK])
        maxima = sb("f_max", [P, 2, CHUNKS, FB0])
        W = 2 * CH
        ITEMS = FB0 * TOK // W
        part = sb("f_part", [P, 3, W])
        gs_max, o_max = sb("f_gs_max", [P, 1, ITEMS]), sb("f_o_max", [P, 1, ITEMS])
        [(step, inv)] = tensor_scale(k, "f_y", stack, yT[:].unsqueeze(1))
        with ExitStack() as st:
            up_ps, gate_ps = ([st.enter_context(nc.psum_tensor(f"f_{n}{j}", [P, CH], F32)) for j in range(FB0)] for n in ("up", "gate"))
            scaled, y_ready = sem("f_y_scaled"), sem("f_y_ready")
            done = {"up": sem("f_up_done"), "gate": sem("f_gate_done")}
            copied = {"up": sem("f_up_copied"), "gate": sem("f_gate_copied")}
            maxed = {"up": sem("f_up_maxed"), "gate": sem("f_gate_maxed")}
            sides = (("up", up, up_ps, k.f_up), ("gate", gate, gate_ps, k.f_gate))
            with nc.Block() as block:

                @block.scalar
                def _(act):
                    with act.Fori(0, CHUNKS) as c:
                        cols = ds(c * CH, CH)
                        nc.scalar.activation(yT[:, cols], yT[:, cols], ACT.Identity, bias=k.rne[:], scale=inv).then_inc(scaled, 1)
                    act.sem_inc(copied["gate"], FB0)
                    act.sem_inc(copied["up"], FB0)
                    with act.Fori(0, CHUNKS) as c:
                        for n, t, ps, w in sides:
                            for j in range(FB0):
                                act.wait_ge(done[n], c * FB0 + (j + 1))
                                nc.scalar.activation(t[:, j, ds(c * CH, CH)], ps[j][:], ACT.Copy).then_inc(copied[n], 1)
                    act.wait_ge(copied["gate"], FB0 * CHUNKS + FB0)
                    act.wait_ge(copied["up"], FB0 * CHUNKS + FB0)

                @block.vector
                def _(dve):
                    def quantise(c):
                        cols = ds(c * CH, CH)
                        dve.wait_ge(scaled, c + 1)
                        nc.vector.tensor_scalar(yT[:, cols], yT[:, cols], -RNE, step, ALU.add, ALU.mult).then_inc(y_ready, 1)

                    def chunk(c, more):
                        for i, (n, t, ps, w) in enumerate(sides):
                            dve.wait_ge(copied[n], c * FB0 + 2 * FB0)
                            nc.vector.tensor_reduce(maxima[:, i, ds(c, 1), :], t[:, :, ds(c * CH, CH)], AX.X, ALU.max,
                                                    apply_absolute_value=True).then_inc(maxed[n], 1)
                            if i == 0 and more:
                                quantise(c + 1)

                    quantise(0)
                    with dve.Fori(0, CHUNKS - 1) as c:
                        chunk(c, True)
                    chunk(CHUNKS - 1, False)
                    dve.wait_ge(maxed["gate"], CHUNKS)
                    dve.wait_ge(maxed["up"], CHUNKS)

                @block.tensor
                def _(pe):
                    with pe.Fori(0, CHUNKS) as c:
                        pe.wait_ge(y_ready, c + 1)
                        for n, t, ps, w in sides:
                            for j in range(FB0):
                                pe.wait_ge(copied[n], c * FB0 + (j + 1))
                                nc.tensor.matmul(ps[j][:], w[:, j * P:(j + 1) * P], yT[:, ds(c * CH, CH)],
                                                 start=True, stop=True).then_inc(done[n], 1)
        (up_step, up_inv), (gate_step, gate_inv) = tensor_scale(k, "f_ug", stack, maxima[:].rearrange("p t c j -> p t (c j)"))
        all_gate, all_up = (t[:].rearrange("p j n -> p (j n)") for t in (gate, up))
        item = lambda a, n: a[:, ds(n * W, W)]
        g_scaled, g_ready, sig_ready, sig_rounded, gs_ready, maxed = (
            sem(f"f_{n}") for n in ("g_scaled", "g_ready", "sig_ready", "sig_rounded", "gs_ready", "gs_maxed"))
        SIG = 192.0
        SIG_MAX = SIG + 65535.0 / 65536
        pool_rounded = sem("f_pool_rounded")
        with nc.Block() as block:

            @block.scalar
            def _(act):
                def step(n, u):
                    static = isinstance(n, int)
                    if not static or n + 2 < ITEMS:
                        nc.scalar.activation(item(all_gate, n + 2), item(all_gate, n + 2), ACT.Identity, bias=k.rne[:], scale=gate_inv)\
                            .then_inc(g_scaled, 1)
                    if not static or 0 <= n + 1 < ITEMS:
                        wait_apart(k, act, g_scaled, n + 2)
                        nc.scalar.activation(item(all_gate, n + 1), item(all_gate, n + 1), ACT.Identity, bias=k.minus_rne[:])\
                            .then_inc(g_ready, 1)
                    if not static or n >= 0:
                        if not static or n >= 3:
                            act.wait_ge(gs_ready, n - 2)
                        wait_apart(k, act, g_ready, n + 1)
                        nc.scalar.activation(part[:, u, :], item(all_gate, n), ACT.Sigmoid, scale=gate_step).then_inc(sig_ready, 1)

                for n in range(-2, 3):
                    step(n, n % 3)
                with act.Fori(1, ITEMS // 3 - 1) as g:
                    for u in range(3):
                        step(g * 3 + u, u)
                for n in range(ITEMS - 3, ITEMS):
                    step(n, n % 3)

            @block.gpsimd
            def _(pool):
                with pool.Fori(0, ITEMS // 3) as g:
                    wait_apart(k, pool, sig_ready, g * 3 + 3)
                    nc.gpsimd.tensor_scalar(part[:, 2, :], part[:, 2, :], SIG, SIG_MAX, ALU.add, ALU.min).then_inc(pool_rounded, 1)

            @block.vector
            def _(dve):
                with dve.Fori(0, ITEMS // 3) as g:
                    for u in range(3):
                        n = g * 3 + u
                        if u < 2:
                            dve.wait_ge(sig_ready, n + 1)
                            nc.vector.tensor_scalar(part[:, u, :], part[:, u, :], SIG, SIG_MAX, ALU.add, ALU.min).then_inc(sig_rounded, 1)
                            dve.wait_ge(sig_rounded, g * 2 + (u + 1))
                        else:
                            dve.wait_ge(pool_rounded, g + 1)
                        dve.wait_ge(g_ready, n + 1)
                        nc.vector.scalar_tensor_tensor(item(all_gate, n), part[:, u, :], -SIG, item(all_gate, n), ALU.add, ALU.mult)\
                            .then_inc(gs_ready, 1)
                        dve.wait_ge(gs_ready, n + 1)
                        nc.vector.tensor_reduce(gs_max[:, 0, ds(n, 1)], item(all_gate, n), AX.X, ALU.max, apply_absolute_value=True)\
                            .then_inc(maxed, 1)
                dve.wait_ge(maxed, ITEMS)
        [(gs_step, gs_inv)] = tensor_scale(k, "f_gs", stack, gs_max[:], gate_step)
        up_scaled, up_even, up_odd, gs_scaled, o_ready, o_maxed = (
            sem(f"f_{n}") for n in ("u_scaled", "u_even", "u_odd", "gs_scaled", "o_ready", "o_maxed"))
        product = stack.enter_context(nc.sbuf_tensor("f_product_step", [P, 1], F32))
        with nc.Block() as block:

            @block.scalar
            def _(act):
                with act.Fori(0, ITEMS // 2) as g:
                    for u in range(2):
                        n = g * 2 + (1 - u)
                        nc.scalar.activation(item(all_up, n), item(all_up, n), ACT.Identity, bias=k.rne[:], scale=up_inv).then_inc(up_scaled, 1)
                        nc.scalar.activation(item(all_gate, n), item(all_gate, n), ACT.Identity, bias=k.rne[:], scale=gs_inv)\
                            .then_inc(gs_scaled, 1)
                    wait_apart(k, act, up_scaled, g * 2 + 2)
                    nc.scalar.activation(item(all_up, g * 2), item(all_up, g * 2), ACT.Identity, bias=k.minus_rne[:]).then_inc(up_even, 1)

            @block.gpsimd
            def _(pool):
                with pool.Fori(0, ITEMS // 2) as g:
                    wait_apart(k, pool, up_scaled, g * 2 + 1)
                    nc.gpsimd.tensor_tensor(item(all_up, g * 2 + 1), item(all_up, g * 2 + 1), k.minus_rne[:].broadcast_to([P, W]), ALU.add)\
                        .then_inc(up_odd, 1)

            @block.vector
            def _(dve):
                nc.vector.tensor_tensor(product[:], gs_step, up_step, ALU.mult)
                with dve.Fori(0, ITEMS // 2) as g:
                    dve.wait_ge(gs_scaled, g * 2 + 2)
                    for u in range(2):
                        n = g * 2 + u
                        dve.wait_ge((up_even, up_odd)[u], g + 1)
                        nc.vector.scalar_tensor_tensor(item(all_up, n), item(all_gate, n), -RNE, item(all_up, n), ALU.add, ALU.mult)\
                            .then_inc(o_ready, 1)
                        dve.wait_ge(o_ready, n + 1)
                        nc.vector.tensor_reduce(o_max[:, 0, ds(n, 1)], item(all_up, n), AX.X, ALU.max, apply_absolute_value=True)\
                            .then_inc(o_maxed, 1)
                dve.wait_ge(o_maxed, ITEMS)
        [(o_step, o_inv)] = tensor_scale(k, "f_o", stack, o_max[:], product[:])
        down_ps, turn_ps = ([stack.enter_context(nc.psum_tensor(f"f_{n}{u}", [P, CH], F32)) for u in range(2)] for n in ("down", "turn"))
        o_scaled, o_quantised, down_done, down_copied, turned, added = (
            sem(f"f_{n}") for n in ("o_scaled", "o_quantised", "down_done", "down_copied", "turned", "added"))
        with nc.Block() as block:

            @block.scalar
            def _(act):
                def scale_o(c):
                    o = up[:, :, ds(c * CH, CH)]
                    nc.scalar.activation(o, o, ACT.Identity, bias=k.rne[:], scale=o_inv).then_inc(o_scaled, 1)

                def two_chunks(c, more):
                    for u in range(2):
                        if more:
                            scale_o(c + (2 + u))
                        act.wait_ge(down_done, c + (u + 1))
                        act.wait_ge(turned, c + (u + 1))
                        nc.scalar.activation(part[:, u, 0:CH], down_ps[u][:], ACT.Copy).then_inc(down_copied, 1)

                scale_o(0)
                scale_o(1)
                act.sem_inc(down_copied, 1)
                act.sem_inc(turned, 2)
                with act.Fori(0, CHUNKS // 2 - 1) as g:
                    two_chunks(g * 2, True)
                two_chunks(CHUNKS - 2, False)

            @block.vector
            def _(dve):
                def quantise(c):
                    o = up[:, :, ds(c * CH, CH)]
                    dve.wait_ge(o_scaled, c + 1)
                    nc.vector.tensor_scalar(o, o, -RNE, o_step, ALU.add, ALU.mult).then_inc(o_quantised, 1)

                def two_chunks(c, more):
                    for u in range(2):
                        if more:
                            quantise(c + (2 + u))
                        dve.wait_ge(turned, c + (u + 3))
                        xc = k.x[:, ds((c + u) * CH, CH)]
                        nc.vector.tensor_tensor(xc, turn_ps[u][:], xc, ALU.add).then_inc(added, 1)

                dve.sem_inc(added, 1)
                quantise(0)
                quantise(1)
                with dve.Fori(0, CHUNKS // 2 - 1) as g:
                    two_chunks(g * 2, True)
                two_chunks(CHUNKS - 2, False)
                dve.wait_ge(added, CHUNKS + 1)

            @block.tensor
            def _(pe):
                def down(c, u):
                    pe.wait_ge(o_quantised, c + (u + 1))
                    pe.wait_ge(down_copied, c + 1)
                    for j in range(FB0):
                        last = nc.tensor.matmul(down_ps[u][:], k.f_down[:, j, :], up[:, j, ds((c + u) * CH, CH)],
                                                start=(j == 0), stop=(j == FB0 - 1))
                    last.then_inc(down_done, 1)

                with pe.Fori(0, CHUNKS // 2) as g:
                    c = g * 2
                    down(c, 0)
                    down(c, 1)
                    for u in range(2):
                        pe.wait_ge(down_copied, c + (u + 2))
                        pe.wait_ge(added, c + 1)
                        for j in range(4):
                            last = nc.tensor.transpose(turn_ps[u][:, j * P:(j + 1) * P], part[:, u, j * P:(j + 1) * P], k.ident[:])
                        last.then_inc(turned, 1)


def xattn1(k, io):
    nc = k.nc
    sem = k.sem
    with ExitStack() as stack:
        sb = lambda name, shape, dt=F32: stack.enter_context(nc.sbuf_tensor(name, shape, dt))
        q_all = sb("b_q", [P, 2, TOK], F32R)
        tailT = sb("b_tailT", [P, B])
        with ExitStack() as st:
            yT = st.enter_context(nc.sbuf_tensor("b_yT", [P, TOK], F32))
            layer_norm_T(k, "b_ln", yT)
            tail, v_tail = (st.enter_context(nc.sbuf_tensor(n, [B, D], F32)) for n in ("b_tail", "b_v_tail"))
            q_ps = [st.enter_context(nc.psum_tensor(f"b_q_ps{u}", [P, CH], F32)) for u in range(2)]
            tail_ps, v_ps = (st.enter_context(nc.psum_tensor(n, [P, P], F32)) for n in ("b_tail_ps", "b_v_tail_ps"))
            projected, copied, split, tail_loaded, tail_turned, tail_ready, v_done, v_copied, v_stored, biased = (
                sem(f"b_pre_{n}") for n in ("projected", "copied", "split", "tail_loaded", "tail_turned", "tail_ready", "v_done",
                                            "v_copied", "v_stored", "biased"))
            with nc.Block() as block:

                @block.sync
                def _(sp):
                    sp.dma_start(tail[:], io["ctx_1024"][:, N_CTX - 1, :]).then_inc(tail_loaded, 16)
                    sp.wait_ge(v_copied, 1)
                    sp.dma_start(k.v_tail_dram, v_tail[:]).then_inc(v_stored, 16)
                    sp.wait_ge(v_stored, 16)

                @block.tensor
                def _(pe):
                    with pe.Fori(0, CHUNKS // 2) as g:
                        c = g * 2
                        for u in range(2):
                            pe.wait_ge(copied, c + (u + 1))
                            nc.tensor.matmul(q_ps[u][:], k.wq1[:], yT[:, ds((c + u) * CH, CH)], start=True, stop=True)\
                                .then_inc(projected, 1)
                    pe.wait_ge(tail_loaded, 16)
                    nc.tensor.transpose(tail_ps[:], tail[:], k.ident[:]).then_inc(tail_turned, 1)
                    pe.wait_ge(tail_ready, 1)
                    nc.tensor.matmul(v_ps[:], tailT[:], k.wv1[:], start=True, stop=True).then_inc(v_done, 1)

                @block.scalar
                def _(act):
                    act.sem_inc(copied, 2)
                    with act.Fori(0, CHUNKS // 2) as g:
                        c = g * 2
                        for u in range(2):
                            act.wait_ge(projected, c + (u + 1))
                            cols = ds((c + u) * CH, CH)
                            for target in (q_all[:, HI, cols], yT[:, cols]):
                                last = nc.scalar.activation(target, q_ps[u][:], ACT.Identity, bias=k.bq1)
                            last.then_inc(copied, 1)
                    act.wait_ge(copied, CHUNKS + 2)

                @block.vector
                def _(dve):
                    xt = k.x[:].rearrange("p (t d) -> p t d", d=D)
                    nc.vector.tensor_tensor(xt, xt, k.bo[:].unsqueeze(1).broadcast_to([P, TILES, D]), ALU.add).then_inc(biased, 1)
                    with dve.Fori(0, CHUNKS // 2) as g:
                        c = g * 2
                        for u in range(2):
                            cols = ds((c + u) * CH, CH)
                            dve.wait_ge(copied, c + (u + 3))
                            nc.vector.tensor_tensor(q_all[:, LO, cols], yT[:, cols], q_all[:, HI, cols], ALU.subtract).then_inc(split, 1)
                    dve.wait_ge(split, CHUNKS)
                    dve.wait_ge(tail_turned, 1)
                    nc.vector.tensor_copy(tailT[:], tail_ps[:]).then_inc(tail_ready, 1)
                    dve.wait_ge(v_done, 1)
                    nc.vector.tensor_copy(v_tail[:], v_ps[:]).then_inc(v_copied, 1)
                    dve.wait_ge(biased, 1)

        raw = sb("b_raw", [P, 8, 2, D])
        ctxT = sb("b_ctxT", [P, 8, N_CTX])
        kept = sb("b_kept", [P, 2, BPT, N_CTX], BF16)
        bias = sb("b_bias", [P, 8, N_CTX])
        v_row = sb("b_v_row", [GROUPS, 2, BPT, D])
        v_last = sb("b_v_last", [GROUPS, 8, D])
        qbd = sb("b_qbd", [P, 2, 4, H, L], F32R)
        k_whole = sb("b_k_whole", [P, 2, N_CTX])
        kT = sb("b_kT", [P, 2, 4, even(N_CTX)], F32R)
        v = sb("b_v", [P, 4, 2, D])
        neg = sb("b_neg", [P, GROUPS, N_CTX])
        nmax = sb("b_nmax", [P, 2, GROUPS])
        prob = sb("b_prob", [P, 2, GROUPS, N_CTX])
        rsum, rinv = sb("b_rsum", [P, 2, GROUPS]), sb("b_rinv", [P, 2, GROUPS])
        probT, lastT = sb("b_probT", [P, 2, CH]), sb("b_lastT", [GROUPS, P])
        weight = sb("b_weight", [P, 2, D])
        weightT = sb("b_weightT", [P, P])
        own = sb("b_own", [P, BPT, HG, L])
        oT_sum, oT = sb("b_oT_sum", [P, P]), sb("b_oT", [P, P])
        psum = lambda name: stack.enter_context(nc.psum_tensor(name, [P, CH], F32))
        score_ps, turn_ps = [psum("b_score0"), psum("b_score1")], [psum("b_turn0"), psum("b_turn1")]
        out_ps, ctx_ps, k_ps, v_ps = psum("b_out"), psum("b_ctx"), psum("b_k"), psum("b_v_ps")
        weight_ps, last_ps, proj_ps = ctx_ps[:, 2 * P:3 * P], ctx_ps[0:GROUPS, 3 * P:4 * P], out_ps[:, P:2 * P]
        raw_loaded = [sem(f"b_raw_loaded{j}") for j in range(8)]
        kept_loaded, v_row_loaded = ([sem(f"b_{n}_loaded{u}") for u in range(2)] for n in ("kept", "v_row"))
        ctx_turned, ctxT_ready, keys_ready, q_ready = sem("b_ctx_turned"), sem("b_ctxT_ready"), sem("b_tile_keys_ready"), sem("b_q_ready")
        k_done, k_taken, k_hi, k_ready, v_done, v_ready = (sem(f"b_{n}") for n in ("k_done", "k_taken", "k_hi", "k_ready", "v_done", "v_ready"))
        scored, masked, exped, rinv_ready = (sem(f"b_{n}") for n in ("scored", "masked", "exped", "rinv_ready"))
        turned, probT_ready = [sem(f"b_turned{n}") for n in range(3)], [sem(f"b_probT_ready{n}") for n in range(3)]
        out_ready, weight_ready, weight_turned, weightT_ready, own_ready, sum_ready, oT_ready, proj_ready, x_added = (
            sem(f"b_{n}") for n in ("out_ready", "weight_ready", "weight_turned", "weightT_ready", "own_ready", "sum_ready", "oT_ready",
                                    "proj_ready", "x_added"))
        LEAD, LAG = 5, 1

        def tile_of(g, j, ahead=0):
            return g * 2 + (j + ahead) // 4

        with nc.Block() as block:

            @block.sync
            def _(sp):
                def load_raw(g, j):
                    sp.dma_start(raw[:, j % 8], io["ctx_1024"][ds(g * 8 + j, 1), 0:2 * P, :].rearrange(
                        "b (t p) d -> p (b t) d", p=P)).then_inc(raw_loaded[j % 8], 16)

                def load_rows(t, u):
                    batches = ds(t * BPT, BPT)
                    sp.dma_start(kept[:, u], k.keep1[batches, :].unsqueeze(0).broadcast_to([P, BPT, N_CTX])).then_inc(kept_loaded[u], 16)
                    sp.dma_start(v_row[:, u], k.v_tail_dram[batches, :].unsqueeze(0).broadcast_to([GROUPS, BPT, D]))\
                        .then_inc(v_row_loaded[u], 16)

                def step(g, j):
                    s, t, u, b = g * 8 + j, tile_of(g, j), j // 4, j % 4
                    if live(g, j, 8):
                        wait(sp, ctx_turned, s + 1)
                        load_raw(g + 1, j)
                    if b == 1 and live(g, j, 8):
                        wait(sp, k_taken, s + 3)
                        wait(sp, keys_ready, t + 1)
                        load_rows(t + 2, u)

                for j in range(3):
                    load_raw(0, j)
                load_rows(0, 0)
                run_steps(sp, step, LEAD)

            @block.gpsimd
            def _(pool):
                def step(g, j):
                    s, t, u, b = g * 8 + j, tile_of(g, j), j // 4, j % 4
                    if live(g, j, 3):
                        wait(pool, scored, s * 4)
                        for half in (HI, LO):
                            last = nc.gpsimd.tensor_tensor(
                                qbd[:, half, (j + 3) % 4], q_all[:, half, ds((s + 3) * L, L)].unsqueeze(1).broadcast_to([P, H, L]),
                                k.head_of_feature[:].unsqueeze(2).broadcast_to([P, H, L]), ALU.mult)
                        last.then_inc(q_ready, 1)
                    if live(g, j, 3):
                        n = (j + 3) % 4
                        pool.wait_ge(k_hi, s + 4)
                        nc.gpsimd.tensor_tensor(kT[:, LO, n, 0:N_CTX], k_whole[:, n % 2, :], kT[:, HI, n, 0:N_CTX], ALU.subtract).then_inc(k_ready, 1)
                    if live(g, j, 1):
                        par = (j + 1) % 2
                        pool.wait_ge(rinv_ready, s + 2)
                        wait(pool, weight_turned, s)
                        nc.gpsimd.tensor_tensor(weight[:, par].rearrange("p (g f) -> p g f", g=GROUPS),
                                                k.own_value[:].rearrange("p (g f) -> p g f", g=GROUPS),
                                                rinv[:, par, :].unsqueeze(2).broadcast_to([P, GROUPS, L]), ALU.mult).then_inc(weight_ready, 1)
                    if b == 3 and live(g, j, 8):
                        slots = slice(4 * u, 4 * u + 4)
                        wait(pool, out_ready, s + 1)
                        nc.gpsimd.tensor_copy(ctxT[:, slots, N_CTX - 1:N_CTX], tailT[:, ds((t + 2) * BPT, BPT)].unsqueeze(2))
                        pool.wait_ge(v_row_loaded[u], (g + 2) * 16)
                        nc.gpsimd.tensor_tensor(v_last[:, slots, :], v_row[:, u],
                                                k.group_of_feature[:].unsqueeze(1).broadcast_to([GROUPS, BPT, D]), ALU.mult)
                        wait_apart(k, pool, kept_loaded[u], (g + 2) * 16)
                        nc.gpsimd.tensor_scalar(bias[:, slots, :], kept[:, u], NEG1, -NEG1, ALU.mult, ALU.add).then_inc(keys_ready, 1)

                for half in (HI, LO):
                    nc.gpsimd.tensor_copy(kT[:, half, :, N_CTX:], k.zero[:].unsqueeze(1).broadcast_to([P, 4, even(N_CTX) - N_CTX]))
                run_steps(pool, step, LEAD)

            @block.vector
            def _(dve):
                def mask(g, j, grp):
                    s, n, par = g * 8 + j, (j + 1) % 8, (j + 1) % 2
                    if n % 4 == 0 and grp == 0:
                        dve.wait_ge(keys_ready, tile_of(g, j, 1) + 1)
                    wait_apart(k, dve, scored, s * 4 + (5 + grp))
                    nc.vector.tensor_tensor_reduce(
                        out=neg[:, grp, :], in0=score_ps[grp % 2][:, 0:N_CTX], in1=bias[:, n, :], scale=-DH1 ** -0.5,
                        scalar=3.4e38, op0=ALU.add, op1=ALU.min, accum_out=nmax[:, par, grp:grp + 1]).then_inc(masked, 1)

                def step(g, j):
                    s, t, u, b = g * 8 + j, tile_of(g, j), j // 4, j % 4
                    if live(g, j, 1):
                        mask(g, j, 0)
                        mask(g, j, 1)
                    if live(g, j, 0):
                        dve.wait_ge(turned[0], s + 1)
                        nc.vector.tensor_copy(probT[:, 0, :], turn_ps[0][:]).then_inc(probT_ready[0], 1)
                    if live(g, j, 1):
                        mask(g, j, 2)
                        mask(g, j, 3)
                    if live(g, j, 3):
                        dve.wait_ge(k_done, s + 4)
                        dve.wait_ge(kept_loaded[(j + 3) // 4 % 2], (g + (j + 3) // 8 + 1) * 16)
                        wait(dve, k_ready, s + 2)
                        nc.vector.scalar_tensor_tensor(k_whole[:, (j + 3) % 2, :], k_ps[:, 0:N_CTX], k.bk1,
                                                       kept[:, (j + 3) // 4 % 2, (j + 3) % 4, :], ALU.add, ALU.mult).then_inc(k_taken, 1)
                    if live(g, j, 0):
                        dve.wait_ge(out_ready, s + 1)
                        dve.wait_ge(weightT_ready, s + 1)
                        nc.vector.tensor_tensor(own[:, b].rearrange("p h l -> p (h l)"), out_ps[:, 0:P], weightT[:], ALU.mult)\
                            .then_inc(own_ready, 1)
                    if live(g, j, 1):
                        par = (j + 1) % 2
                        dve.wait_ge(exped, s * 4 + 8)
                        wait(dve, weight_ready, s)
                        nc.vector.reciprocal(rinv[:, par, :], rsum[:, par, :]).then_inc(rinv_ready, 1)
                    if live(g, j, 4):
                        dve.wait_ge(ctx_turned, s + 5)
                        nc.vector.tensor_copy(ctxT[:, (j + 4) % 8, 0:2 * P], ctx_ps[:, 0:2 * P]).then_inc(ctxT_ready, 1)
                    if b == 0 and live(g, j, -1):
                        dve.wait_ge(proj_ready, t)
                        xt = k.x[:, ds((t - 1) * D, D)]
                        nc.vector.tensor_tensor(xt, proj_ps, xt, ALU.add).then_inc(x_added, 1)
                    if b == 3 and live(g, j, 0):
                        dve.wait_ge(own_ready, s + 1)
                        nc.vector.tensor_reduce(oT_sum[:], own[:].rearrange("p b h l -> p b l h"), AX.X, ALU.add).then_inc(sum_ready, 1)

                run_steps(dve, step, LEAD, LAG)
                dve.wait_ge(x_added, TILES)

            @block.scalar
            def _(act):
                def exp(g, j, grp):
                    s, par = g * 8 + j, (j + 1) % 2
                    act.wait_ge(masked, s * 4 + (5 + grp))
                    nc.scalar.activation(prob[:, par, grp, :], neg[:, grp, :], ACT.Exp, bias=nmax[:, par, grp:grp + 1],
                                         scale=-1.0, accum_out=rsum[:, par, grp:grp + 1]).then_inc(exped, 1)

                def step(g, j):
                    s, t, u, b = g * 8 + j, tile_of(g, j), j // 4, j % 4
                    if live(g, j, 1):
                        exp(g, j, 0)
                        exp(g, j, 1)
                    if b == 0 and live(g, j, -1):
                        act.wait_ge(sum_ready, t)
                        nc.scalar.activation(oT[:], oT_sum[:], ACT.Identity, bias=k.bv1).then_inc(oT_ready, 1)
                    if live(g, j, 0):
                        act.wait_ge(turned[1], s + 1)
                        nc.scalar.activation(probT[:, 1, :], turn_ps[1][:], ACT.Copy).then_inc(probT_ready[1], 1)
                        act.wait_ge(weight_turned, s + 1)
                        wait(act, own_ready, s)
                        nc.scalar.activation(weightT[:], weight_ps, ACT.Copy).then_inc(weightT_ready, 1)
                        nc.scalar.activation(lastT[:], last_ps, ACT.Copy).then_inc(probT_ready[2], 1)
                    if live(g, j, 1):
                        exp(g, j, 2)
                        exp(g, j, 3)
                    if live(g, j, 3):
                        act.wait_ge(v_done, s + 4)
                        nc.scalar.activation(v[:, (j + 3) % 4], v_ps[:, 0:2 * P].rearrange("p (t d) -> p t d", d=D), ACT.Copy)\
                            .then_inc(v_ready, 1)
                        n = (j + 3) % 4
                        act.wait_ge(k_taken, s + 4)
                        nc.scalar.activation(kT[:, HI, n, 0:N_CTX], k_whole[:, n % 2, :], ACT.Copy).then_inc(k_hi, 1)

                run_steps(act, step, LEAD, LAG)

            @block.tensor
            def _(pe):
                def score(g, j, grp):
                    s, n = g * 8 + j, (j + 1) % 4
                    if grp == 0:
                        pe.wait_ge(k_ready, s + 2)
                        pe.wait_ge(q_ready, s + 2)
                    wait(pe, masked, s * 4 + (3 + grp))
                    for p, (a, c) in enumerate(PASSES):
                        last = nc.tensor.matmul(score_ps[grp % 2][:, 0:even(N_CTX)], qbd[:, a, n, 4 * grp:4 * grp + 4, :], kT[:, c, n, :],
                                                start=(p == 0), stop=(p == len(PASSES) - 1))
                    last.then_inc(scored, 1)

                def turn(g, j, kt):
                    s = g * 8 + j
                    if kt == 0:
                        pe.wait_ge(exped, s * 4 + 4)
                    if kt < 2:
                        for grp in range(GROUPS):
                            last = nc.tensor.transpose(turn_ps[kt][:, grp * P:(grp + 1) * P],
                                                       prob[:, j % 2, grp, kt * P:(kt + 1) * P], k.ident[:])
                    else:
                        last = nc.tensor.transpose(last_ps, prob[:, j % 2, :, N_CTX - 1], k.ident[:])
                    last.then_inc(turned[kt], 1)

                def values(g, j, kt):
                    s, b = g * 8 + j, j % 4
                    pe.wait_ge(probT_ready[kt], s + 1)
                    if kt == 0:
                        pe.wait_ge(v_ready, s + 1)
                        wait(pe, own_ready, s)
                        if b == 1 and live(g, j, -4):
                            pe.wait_ge(x_added, tile_of(g, j))
                    if kt < 2:
                        for grp in range(GROUPS):
                            rows = slice(grp * 32, grp * 32 + 32)
                            nc.tensor.matmul(out_ps[rows, 0:P], v[:, j % 4, kt, rows], probT[:, kt, grp * P:(grp + 1) * P],
                                             start=(kt == 0), stop=False, skip_group_check=True)
                    else:
                        nc.tensor.matmul(out_ps[:, 0:P], v_last[:, j, :], lastT[:], start=False, stop=True,
                                         skip_group_check=True).then_inc(out_ready, 1)

                def step(g, j):
                    s, t, u, b = g * 8 + j, tile_of(g, j), j // 4, j % 4
                    here, ahead = live(g, j, 0), live(g, j, 1)
                    if ahead:
                        score(g, j, 0)
                        score(g, j, 1)
                    if here:
                        turn(g, j, 0)
                        turn(g, j, 1)
                    if here:
                        pe.wait_ge(ctxT_ready, s + 4 if live(g, j, 3) else B)
                        turn(g, j, 2)
                        pe.wait_ge(weight_ready, s + 1)
                        nc.tensor.transpose(weight_ps, weight[:, j % 2], k.ident[:]).then_inc(weight_turned, 1)
                    if ahead:
                        score(g, j, 2)
                        score(g, j, 3)
                    if live(g, j, 3):
                        n = (j + 3) % 8
                        pe.wait_ge(ctxT_ready, s + 4)
                        if n % 4 == 0:
                            pe.wait_ge(keys_ready, tile_of(g, j, 3) + 1)
                        wait(pe, k_taken, s + 3)
                        nc.tensor.matmul(k_ps[:, 0:N_CTX], k.wk1[:], ctxT[:, n, :], start=True, stop=True).then_inc(k_done, 1)
                    if here:
                        values(g, j, 0)
                    if live(g, j, 3):
                        n = (j + 3) % 8
                        wait(pe, v_ready, s + 3)
                        for kt in range(2):
                            last = nc.tensor.matmul(v_ps[:, kt * D:(kt + 1) * D], ctxT[:, n, kt * P:(kt + 1) * P], k.wv1[:],
                                                    start=True, stop=True)
                        last.then_inc(v_done, 1)
                    if here:
                        values(g, j, 1)
                    if b == 0 and live(g, j, -1):
                        pe.wait_ge(oT_ready, t)
                        nc.tensor.matmul(proj_ps, oT[:], k.wo1[:], start=not here, stop=True, skip_group_check=True).then_inc(proj_ready, 1)
                    if here:
                        values(g, j, 2)
                    if live(g, j, 4):
                        n = (j + 4) % 8
                        pe.wait_ge(raw_loaded[n], (g + (j + 4) // 8 + 1) * 16)
                        wait(pe, ctxT_ready, s + 4)
                        if here:
                            pe.wait_ge(weightT_ready, s + 1)
                        for kt in range(2):
                            last = nc.tensor.transpose(ctx_ps[:, kt * P:(kt + 1) * P], raw[:, n, kt, :], k.ident[:])
                        last.then_inc(ctx_turned, 1)

                run_steps(pe, step, LEAD, LAG)


def run_tiles(eng, step, lead, lag):
    for t in range(-lead, 4):
        step(t // 4, t % 4)
    with eng.Fori(1, TILES // 4 - 2) as g:
        for u in range(4):
            step(g, u)
    for t in range(TILES - 8, TILES + lag):
        step(t // 4, t % 4)


def live_tile(g, u, ahead):
    return not isinstance(g, int) or 0 <= 4 * g + u + ahead < TILES


def attn1(k, io):
    nc = k.nc
    sem = k.sem
    POOL_HEADS = 12
    with ExitStack() as stack:
        sb = lambda name, shape, dt=F32: stack.enter_context(nc.sbuf_tensor(name, shape, dt))
        psum = lambda name: stack.enter_context(nc.psum_tensor(name, [P, CH], F32))
        mean, rstd = ln_stats(k, stack, "s_ln")
        z, y = sb("s_z", [P, 2, D]), sb("s_y", [P, 4, BPT, HG, L])
        q, keys = sb("s_q", [P, 2, P]), sb("s_keys", [P, 2, P])
        spread = sb("s_spread", [P, 2, BPT, H, L])
        v = sb("s_v", [P, 4, BPT, D])
        shifted, expd = sb("s_shifted", [P, 2, H, L]), sb("s_expd", [P, 2, H, L])
        rmax, rsum, rinv = sb("s_rmax", [P, H]), sb("s_rsum", [P, H]), sb("s_rinv", [P, 2, H])
        probT, out, oT = sb("s_probT", [P, GROUPS, P]), sb("s_out", [P, 2, D]), sb("s_oT", [P, P])
        query_row, mask_row = sb("s_query_row", [L, P], BF16), sb("s_mask_row", [L, H, L], BF16)
        y_ps, qk_ps, v_ps, turn_ps, out_ps, proj_ps = (psum(f"s_{n}_ps") for n in ("y", "qk", "v", "turn", "out", "proj"))
        score_ps = [psum("s_score0"), psum("s_score1")]
        rows_ready, z_ready, y_turned, y_ready, qk_done, q_ready, keys_ready, spread_pool, spread_act, v_done, v_ready, biased = (
            sem(f"s_{n}") for n in ("rows_ready", "z_ready", "y_turned", "y_ready", "qk_done", "q_ready", "keys_ready", "spread_pool",
                                    "spread_act", "v_done", "v_ready", "biased"))
        scored, max_ready, shift_ready, exped, sum_ready, rinv_ready, turned, probT_ready = (
            sem(f"s_{n}") for n in ("scored", "max_ready", "shift_ready", "exped", "sum_ready", "rinv_ready", "turned", "probT_ready"))
        out_done, out_ready, out_turned, oT_ready, proj_done, x_added = (
            sem(f"s_{n}") for n in ("out_done", "out_ready", "out_turned", "oT_ready", "proj_done", "x_added"))
        LEAD, LAG = 5, 2
        row_wide = lambda a, n: a.unsqueeze(2).broadcast_to([P, H, n])
        with nc.Block() as block:

            @block.gpsimd
            def _(pool):
                def step(g, u):
                    t = g * 4 + u
                    if live_tile(g, u, 2):
                        n = u % 2
                        wait(pool, keys_ready, t + 3)
                        wait(pool, scored, t + 1)
                        nc.gpsimd.tensor_tensor(
                            spread[:, n, :, 0:POOL_HEADS, :],
                            keys[:, n].rearrange("p (b l) -> p b l", l=L).unsqueeze(2).broadcast_to([P, BPT, POOL_HEADS, L]),
                            k.head_of_feature[:, 0:POOL_HEADS].unsqueeze(1).unsqueeze(3).broadcast_to([P, BPT, POOL_HEADS, L]),
                            ALU.mult).then_inc(spread_pool, 1)
                    if live_tile(g, u, 4):
                        xt = k.x[:, ds((t + 4) * D, D)]
                        wait(pool, z_ready, t + 5)
                        nc.gpsimd.tensor_tensor(xt, xt, k.bproj[:], ALU.add).then_inc(biased, 1)

                run_tiles(pool, step, LEAD, LAG)

            @block.vector
            def _(dve):
                def step(g, u):
                    t = g * 4 + u
                    if live_tile(g, u, 1):
                        n = (u + 1) % 2
                        dve.wait_ge(scored, t + 2)
                        scores = score_ps[n][:].rearrange("p (h l) -> p h l", l=L)
                        nc.vector.tensor_reduce(rmax[:], scores, AX.X, ALU.max).then_inc(max_ready, 1)
                        dve.wait_ge(max_ready, t + 2)
                        wait(dve, exped, t)
                        nc.vector.tensor_tensor(shifted[:, n], scores, row_wide(rmax[:], L), ALU.subtract).then_inc(shift_ready, 1)
                    if live_tile(g, u, -2):
                        dve.wait_ge(proj_done, t - 1)
                        dve.wait_ge(biased, t - 1)
                        xt = k.x[:, ds((t - 2) * D, D)]
                        nc.vector.tensor_tensor(xt, proj_ps[:, D:2 * D], xt, ALU.add).then_inc(x_added, 1)
                    if live_tile(g, u, 5):
                        wait(dve, y_turned, t + 4)
                        nc.vector.tensor_scalar(z[:, (u + 1) % 2], k.x[:, ds((t + 5) * D, D)], mean[:, ds(t + 5, 1)],
                                                rstd[:, ds(t + 5, 1)], ALU.subtract, ALU.mult).then_inc(z_ready, 1)
                    if live_tile(g, u, 3):
                        dve.wait_ge(v_done, t + 4)
                        nc.vector.tensor_tensor(v[:, (u + 3) % 4], v_ps[:].rearrange("p (b d) -> p b d", d=D),
                                                k.own_value[:].unsqueeze(1).broadcast_to([P, BPT, D]), ALU.mult).then_inc(v_ready, 1)
                    if live_tile(g, u, 1):
                        n = (u + 1) % 2
                        dve.wait_ge(exped, t + 2)
                        nc.vector.tensor_reduce(rsum[:], expd[:, n], AX.X, ALU.add).then_inc(sum_ready, 1)
                        dve.wait_ge(sum_ready, t + 2)
                        nc.vector.reciprocal(rinv[:, n], rsum[:]).then_inc(rinv_ready, 1)
                    if live_tile(g, u, 0):
                        dve.wait_ge(out_done, t + 1)
                        dve.wait_ge(rinv_ready, t + 1)
                        wait(dve, out_turned, t - 1)
                        nc.vector.tensor_tensor(out[:, u % 2].rearrange("p (h e) -> p h e", e=DH1),
                                                out_ps[:, 0:D].rearrange("p (h e) -> p h e", e=DH1),
                                                row_wide(rinv[:, u % 2], DH1), ALU.mult).then_inc(out_ready, 1)

                nc.vector.tensor_copy(query_row[:].rearrange("p (b l) -> p b l", l=L),
                                      k.ident[0:L, 0:L].unsqueeze(1).broadcast_to([L, BPT, L])).then_inc(rows_ready, 1)
                nc.vector.tensor_copy(mask_row[:], k.fenwick[0:L, :].unsqueeze(1).broadcast_to([L, H, L])).then_inc(rows_ready, 1)
                run_tiles(dve, step, LEAD, LAG)
                dve.wait_ge(x_added, TILES)

            @block.scalar
            def _(act):
                def step(g, u):
                    t = g * 4 + u
                    if live_tile(g, u, 4):
                        act.wait_ge(y_turned, t + 5)
                        nc.scalar.activation(y[:, u], y_ps[:, 0:P].rearrange("p (b l) -> p b l", l=L).unsqueeze(2).broadcast_to([P, BPT, HG, L]),
                                             ACT.Copy).then_inc(y_ready, 1)
                    if live_tile(g, u, 2):
                        n = u % 2
                        act.wait_ge(keys_ready, t + 3)
                        wait(act, scored, t + 1)
                        for h in range(POOL_HEADS, H):
                            last = nc.scalar.activation(spread[:, n, :, h, :], keys[:, n].rearrange("p (b l) -> p b l", l=L), ACT.Copy,
                                                        scale=k.head_of_feature[:, h:h + 1])
                        last.then_inc(spread_act, 1)
                    if live_tile(g, u, 0):
                        act.wait_ge(turned, t + 1)
                        nc.scalar.activation(probT[:].rearrange("p g q -> p (g q)"), turn_ps[:], ACT.Copy).then_inc(probT_ready, 1)
                    if live_tile(g, u, 1):
                        n = (u + 1) % 2
                        act.wait_ge(shift_ready, t + 2)
                        wait(act, turned, t)
                        nc.scalar.activation(expd[:, n], shifted[:, n], ACT.Exp, scale=DH1 ** -0.5).then_inc(exped, 1)
                    if live_tile(g, u, 3):
                        n = (u + 3) % 2
                        act.wait_ge(qk_done, t + 4)
                        wait(act, scored, t + 2)
                        wait(act, spread_pool, t + 2)
                        nc.scalar.activation(q[:, n], qk_ps[:, 0:P], ACT.Identity, bias=k.bq2).then_inc(q_ready, 1)
                        nc.scalar.activation(keys[:, n], qk_ps[:, P:2 * P], ACT.Identity, bias=k.bk2).then_inc(keys_ready, 1)
                    if live_tile(g, u, -1):
                        act.wait_ge(out_turned, t)
                        nc.scalar.activation(oT[:], proj_ps[:, 0:P], ACT.Identity, bias=k.bv2).then_inc(oT_ready, 1)

                run_tiles(act, step, LEAD, LAG)

            @block.tensor
            def _(pe):
                def step(g, u):
                    t = g * 4 + u
                    if live_tile(g, u, 4):
                        pe.wait_ge(z_ready, t + 5)
                        wait(pe, y_ready, t + 4)
                        nc.tensor.transpose(y_ps[:, 0:P], z[:, u % 2], k.ident[:]).then_inc(y_turned, 1)
                    if live_tile(g, u, 1):
                        n = (u + 1) % 2
                        wait(pe, shift_ready, t)
                        pe.wait_ge(q_ready, t + 2)
                        pe.wait_ge(spread_pool, t + 2)
                        pe.wait_ge(spread_act, t + 2)
                        nc.tensor.matmul(score_ps[n][:], query_row[:], mask_row[:].rearrange("p h l -> p (h l)"), start=True, stop=False,
                                         skip_group_check=True)
                        for b in range(BPT):
                            rows = slice(b * L, (b + 1) * L)
                            last = nc.tensor.matmul(score_ps[n][rows, :], q[:, n, rows], spread[:, n, b].rearrange("p h l -> p (h l)"),
                                                    start=False, stop=True, skip_group_check=True)
                        last.then_inc(scored, 1)
                    if live_tile(g, u, -2):
                        pe.wait_ge(oT_ready, t - 1)
                        nc.tensor.matmul(proj_ps[:, D:2 * D], oT[:], k.wproj[:], start=True, stop=True).then_inc(proj_done, 1)
                    if live_tile(g, u, 0):
                        pe.wait_ge(exped, t + 1)
                        wait(pe, probT_ready, t)
                        for grp in range(GROUPS):
                            last = nc.tensor.transpose(turn_ps[:, grp * P:(grp + 1) * P], expd[:, u % 2, 4 * grp:4 * grp + 4, :], k.ident[:])
                        last.then_inc(turned, 1)
                    if live_tile(g, u, 3):
                        n = (u + 3) % 4
                        pe.wait_ge(y_ready, t + 4)
                        wait(pe, keys_ready, t + 3)
                        nc.tensor.matmul(qk_ps[:, 0:P], k.wqkv[:, 0:D], y[:, n, :, 0, :], start=True, stop=True)
                        nc.tensor.matmul(qk_ps[:, P:2 * P], k.wqkv[:, D:2 * D], y[:, n, :, 0, :], start=True, stop=True).then_inc(qk_done, 1)
                        wait(pe, v_ready, t + 3)
                        for b in range(BPT):
                            last = nc.tensor.matmul(v_ps[:, b * D:(b + 1) * D], y[:, n, b].rearrange("p r l -> p (r l)"),
                                                    k.wqkv[:, 2 * D:3 * D], start=True, stop=True)
                        last.then_inc(v_done, 1)
                    if live_tile(g, u, -1):
                        pe.wait_ge(out_ready, t)
                        wait(pe, x_added, t - 1)
                        nc.tensor.transpose(proj_ps[:, 0:P], out[:, (u - 1) % 2], k.ident[:]).then_inc(out_turned, 1)
                    if live_tile(g, u, 0):
                        pe.wait_ge(probT_ready, t + 1)
                        pe.wait_ge(v_ready, t + 1)
                        wait(pe, out_ready, t)
                        for grp in range(GROUPS):
                            for b in range(BPT):
                                rows = slice(b * L, (b + 1) * L)
                                cols = slice(grp * HG * DH1, (grp + 1) * HG * DH1)
                                last = nc.tensor.matmul(out_ps[rows, cols], probT[:, grp, rows], v[:, u, b, cols], start=True, stop=True,
                                                        skip_group_check=True)
                        last.then_inc(out_done, 1)

                pe.wait_ge(rows_ready, 2)
                run_tiles(pe, step, LEAD, LAG)


def moe_routing(k, yT, y, combT, weights, loads):
    nc = k.nc
    sem = k.sem
    GRP = CH // P
    with ExitStack() as stack:
        sb = lambda name, shape, dt=F32: stack.enter_context(nc.sbuf_tensor(name, shape, dt))
        psum = lambda name: stack.enter_context(nc.psum_tensor(name, [P, CH], F32))
        logitT = sb("mr_logitT", [E_N, 2, CH])
        logits, rest, marked, first, second = (sb(f"mr_{n}", [P, TILES, E_N]) for n in ("logits", "rest", "marked", "first", "second"))
        best, next_best, best_rank, next_rank, ratio, w1, w2 = (
            sb(f"mr_{n}", [P, TILES]) for n in ("best", "next_best", "best_rank", "next_rank", "ratio", "w1", "w2"))
        parts = sb("mr_parts", [P, TILES, PARTS, E_N], BF16)
        comb = sb("mr_comb", [P, 2, GRP, PARTS * E_N])
        logit_ps, comb_ps = ([psum(f"mr_{n}{u}") for u in range(2)] for n in ("logit", "comb_ps"))
        token_ps = [psum(f"mr_token{u}") for u in range(2)]
        routed, copied, turned, gathered, y_hi, y_lo, loaded, w_hi, w_lo = (
            sem(f"mr_{n}") for n in ("routed", "copied", "turned", "gathered", "y_hi", "y_lo", "loaded", "w_hi", "w_lo"))
        wide = lambda a: a.unsqueeze(2).broadcast_to([P, TILES, E_N])
        ranks = k.rank[:].unsqueeze(1).broadcast_to([P, TILES, E_N])
        with nc.Block() as block:

            @block.sync
            def _(sp):
                for target, source in loads:
                    sp.dma_start(target, source).then_inc(loaded, 16)

            @block.tensor
            def _(pe):
                def turn(c, u):
                    pe.wait_ge(gathered, c + (u + 1))
                    wait_apart(k, pe, copied, c + (u + 3))
                    for j in range(GRP):
                        last = nc.tensor.transpose(token_ps[u][:, j * E_N:(j + 1) * E_N], logitT[:, u, j * P:(j + 1) * P],
                                                   k.ident[0:E_N, 0:E_N])
                    last.then_inc(turned, 1)

                with pe.Fori(0, CHUNKS // 2) as g:
                    c = g * 2
                    for u in range(2):
                        pe.wait_ge(copied, c + (u + 1))
                        nc.tensor.matmul(logit_ps[u][0:E_N, :], k.router[:], yT[:, ds((c + u) * CH, CH)],
                                         start=True, stop=True).then_inc(routed, 1)
                    for u in range(2):
                        turn(c, u)

            @block.scalar
            def _(act):
                act.sem_inc(copied, 2)
                act.sem_inc(turned, 2)
                with act.Fori(0, CHUNKS // 2) as g:
                    c = g * 2
                    for u in range(2):
                        act.wait_ge(routed, c + (u + 1))
                        act.wait_ge(turned, c + (u + 1))
                        nc.scalar.activation(logitT[:, u, :], logit_ps[u][0:E_N, :], ACT.Copy).then_inc(copied, 1)
                        cols = ds((c + u) * CH, CH)
                        nc.scalar.activation(y[:, HI, cols], yT[:, cols], ACT.Copy).then_inc(y_hi, 1)
                act.wait_ge(loaded, 16 * len(loads))
                for halves, w in weights:
                    nc.scalar.activation(halves[:, HI], w, ACT.Copy).then_inc(w_hi, 1)

            @block.vector
            def _(dve):
                dve.sem_inc(gathered, 2)
                with dve.Fori(0, CHUNKS // 2) as g:
                    c = g * 2
                    for u in range(2):
                        dve.wait_ge(turned, c + (u + 3))
                        nc.vector.tensor_copy(logits[:, ds((c + u) * GRP, GRP), :],
                                              token_ps[u][:, 0:GRP * E_N].rearrange("p (t e) -> p t e", e=E_N)).then_inc(gathered, 1)
                        cols = ds((c + u) * CH, CH)
                        dve.wait_ge(y_hi, c + (u + 1))
                        nc.vector.tensor_tensor(y[:, LO, cols], yT[:, cols], y[:, HI, cols], ALU.subtract).then_inc(y_lo, 1)
                for n, (halves, w) in enumerate(weights):
                    dve.wait_ge(w_hi, n + 1)
                    nc.vector.tensor_tensor(halves[:, LO], w, halves[:, HI], ALU.subtract).then_inc(w_lo, 1)
                dve.wait_ge(gathered, CHUNKS + 2)
                dve.wait_ge(y_lo, CHUNKS)
                dve.wait_ge(w_lo, len(weights))
        chain, ratio_ready = sem("mr_chain"), sem("mr_ratio_ready")
        with nc.Block() as block:

            @block.vector
            def _(dve):
                def mark(n, x, top, top_rank, one):
                    nc.vector.tensor_reduce(top[:], x[:], AX.X, ALU.max).then_inc(chain, 1)
                    dve.wait_ge(chain, n + 1)
                    nc.vector.tensor_tensor(marked[:], x[:], wide(top[:]), ALU.is_ge).then_inc(chain, 1)
                    dve.wait_ge(chain, n + 2)
                    nc.vector.tensor_tensor(marked[:], marked[:], ranks, ALU.mult).then_inc(chain, 1)
                    dve.wait_ge(chain, n + 3)
                    nc.vector.tensor_reduce(top_rank[:], marked[:], AX.X, ALU.max).then_inc(chain, 1)
                    dve.wait_ge(chain, n + 4)
                    nc.vector.tensor_tensor(one[:], marked[:], wide(top_rank[:]), ALU.is_equal).then_inc(chain, 1)
                    dve.wait_ge(chain, n + 5)
                    return n + 5

                n = mark(0, logits, best, best_rank, first)
                nc.vector.scalar_tensor_tensor(rest[:], first[:], -NEG0, logits[:], ALU.mult, ALU.add).then_inc(chain, 1)
                dve.wait_ge(chain, n + 1)
                n = mark(n + 1, rest, next_best, next_rank, second)
                nc.vector.tensor_tensor(w2[:], next_best[:], best[:], ALU.subtract).then_inc(chain, 1)
                n += 1
                dve.wait_ge(ratio_ready, 1)
                nc.vector.tensor_scalar(w1[:], ratio[:], 1.0, None, ALU.add).then_inc(chain, 1)
                dve.wait_ge(chain, n + 1)
                nc.vector.reciprocal(w1[:], w1[:]).then_inc(chain, 1)
                dve.wait_ge(chain, n + 2)
                nc.vector.tensor_tensor(w2[:], w1[:], ratio[:], ALU.mult).then_inc(chain, 1)
                nc.vector.tensor_tensor(first[:], first[:], wide(w1[:]), ALU.mult).then_inc(chain, 1)
                dve.wait_ge(chain, n + 4)
                nc.vector.tensor_tensor(second[:], second[:], wide(w2[:]), ALU.mult).then_inc(chain, 1)
                dve.wait_ge(chain, n + 5)
                nc.vector.tensor_tensor(first[:], first[:], second[:], ALU.add).then_inc(chain, 1)
                dve.wait_ge(chain, n + 6)
                n += 6
                for part in range(PARTS):
                    nc.vector.tensor_copy(parts[:, :, part, :], first[:]).then_inc(chain, 1)
                    dve.wait_ge(chain, n + 1)
                    if part < PARTS - 1:
                        nc.vector.tensor_tensor(first[:], first[:], parts[:, :, part, :], ALU.subtract).then_inc(chain, 1)
                        dve.wait_ge(chain, n + 2)
                    n += 2

            @block.scalar
            def _(act):
                act.wait_ge(chain, 12)
                nc.scalar.activation(ratio[:], w2[:], ACT.Exp).then_inc(ratio_ready, 1)
        staged, comb_turned, comb_copied = sem("mr_staged"), sem("mr_comb_turned"), sem("mr_comb_copied")
        with nc.Block() as block:

            @block.vector
            def _(dve):
                with dve.Fori(0, CHUNKS // 2) as g:
                    c = g * 2
                    for u in range(2):
                        dve.wait_ge(comb_turned, c + (u + 1))
                        nc.vector.tensor_copy(comb[:, u], parts[:, ds((c + u) * GRP, GRP), :, :].rearrange("p t n e -> p t (n e)"))\
                            .then_inc(staged, 1)

            @block.tensor
            def _(pe):
                pe.sem_inc(comb_turned, 2)
                with pe.Fori(0, CHUNKS // 2) as g:
                    c = g * 2
                    for u in range(2):
                        pe.wait_ge(comb_copied, c + (u + 1))
                        wait_apart(k, pe, staged, c + (u + 1))
                        for j in range(GRP):
                            last = nc.tensor.transpose(comb_ps[u][0:PARTS * E_N, j * P:(j + 1) * P], comb[:, u, j, :], k.ident[:])
                        last.then_inc(comb_turned, 1)

            @block.scalar
            def _(act):
                act.sem_inc(comb_copied, 2)
                with act.Fori(0, CHUNKS // 2) as g:
                    c = g * 2
                    for u in range(2):
                        act.wait_ge(comb_turned, c + (u + 3))
                        nc.scalar.activation(combT[:, ds((c + u) * CH, CH)], comb_ps[u][0:PARTS * E_N, :], ACT.Copy).then_inc(comb_copied, 1)
                act.wait_ge(comb_copied, CHUNKS + 2)


def moe1(k, io):
    nc = k.nc
    sem = k.sem
    ITEMS = PAIRS + len(SH_BLOCKS)
    USES = PAIRS + 1
    LAST = CHUNKS // 2
    with ExitStack() as stack:
        sb = lambda name, shape: stack.enter_context(nc.sbuf_tensor(name, shape, F32))
        yT = sb("m_yT", [P, TOK])
        layer_norm_T(k, "m_ln", yT)
        combT = stack.enter_context(nc.sbuf_tensor("m_combT", [PARTS * E_N, TOK], BF16))
        halves = lambda name, n, rows=P: stack.enter_context(nc.sbuf_tensor(f"m_{name}", [rows, 2, n], F32R))
        y = halves("y", TOK)
        w_gu, w_dn = halves("w_gu", 2 * E_N * E_FF), halves("w_dn", PAIRS * D)
        sh_gate, sh_up, sh_down, sh_row = halves("sh_gate", SH_FF), halves("sh_up", SH_FF), halves("sh_down", 3 * D), halves("sh_row", P)
        with ExitStack() as whole:
            w_gu_raw = whole.enter_context(nc.sbuf_tensor("m_w_gu_raw", [P, 2, E_N, E_FF], F32))
            w_dn_raw = whole.enter_context(nc.sbuf_tensor("m_w_dn_raw", [P, PAIRS, D], F32))
            gate_up = io["L1_ffn_w_gate_up"].rearrange("e d f -> d e f")
            moe_routing(k, yT, y, combT, [
                (w_gu, w_gu_raw[:].rearrange("p a e f -> p (a e f)")), (w_dn, w_dn_raw[:].rearrange("p n d -> p (n d)")),
                (sh_gate, k.sh_gate[:]), (sh_up, k.sh_up[:]), (sh_row, k.sh_gate_row[:]),
                (sh_down[:, :, 0:2 * D], k.sh_down[:, 0:2].rearrange("p j d -> p (j d)")),
                (sh_down[0:SH_BLOCKS[2][1], :, 2 * D:3 * D], k.sh_down[0:SH_BLOCKS[2][1], 2])], [
                (w_gu_raw[:, 0], gate_up[:, :, 0:E_FF]), (w_gu_raw[:, 1], gate_up[:, :, E_FF:2 * E_FF]),
                (w_dn_raw[:], io["L1_ffn_w_down"].rearrange("(p e) f d -> (e f) p d", e=2))])
        psum = lambda name: stack.enter_context(nc.psum_tensor(name, [P, CH], F32))
        act_in, mul_in = ([psum(f"m_{n}{u}") for u in range(2)] for n in ("g", "h"))
        wide_ps, expert_ps, shared_ps, turn_ps = (psum(f"m_{n}") for n in ("wide", "expert", "shared", "turn"))
        silu, gated, full = sb("m_silu", [P, 2, CH]), sb("m_gated", [P, CH]), sb("m_full", [P, 2, CH])
        hidden = [halves(f"hidden{n}", CH) for n in range(4)]
        experts, share, shared, total = (sb(f"m_{n}", [P, CH]) for n in ("experts", "share", "shared_out", "total"))
        g_done, h_done, wide_done, down_done, silu_ready, gated_ready, wide_used, full_ready, hi_ready, lo_ready = (
            sem(f"m_{n}") for n in ("g_done", "h_done", "wide_done", "down_done", "silu_ready", "gated_ready", "wide_used",
                                    "full_ready", "hi_ready", "lo_ready"))
        experts_copied, share_ready, shared_taken, total_ready, turned, x_added = (
            sem(f"m_{n}") for n in ("experts_copied", "share_ready", "shared_taken", "total_ready", "turned", "x_added"))
        rows = lambda j: P if j < PAIRS else SH_BLOCKS[j - PAIRS][1]

        def place(g, i):
            return g * (2 * ITEMS) + i, g * 2 + i // ITEMS, i % ITEMS

        def slot(i):
            i %= 2 * ITEMS
            return 3 if i == 2 * ITEMS - 1 else i % 3

        def current(g):
            return not isinstance(g, int) or g < LAST

        def after(g, i, items):
            return not isinstance(g, int) or 0 <= g * 2 * ITEMS + i - items < CHUNKS * ITEMS

        def run(eng, step):
            for i in range(2 * ITEMS):
                step(0, i)
            with eng.Fori(1, LAST) as g:
                for i in range(2 * ITEMS):
                    step(g, i)
            for i in range(6):
                step(LAST, i)

        with nc.Block() as block:

            @block.tensor
            def _(pe):
                def product(out, w, x, start=True, stop=True):
                    for n, (a, b) in enumerate(PASSES):
                        last = nc.tensor.matmul(out, w(a), x(b), start=(start and n == 0), stop=(stop and n == len(PASSES) - 1))
                    return last

                def step(g, i):
                    n, c, j = place(g, i)
                    u = i % 2
                    y_half = lambda half: y[:, half, ds(c * CH, CH)]
                    if current(g):
                        r = rows(j)
                        if j < PAIRS:
                            wg, wh = ((lambda half, a=a: w_gu[:, half, (a * E_N + 2 * j) * E_FF:(a * E_N + 2 * j + 2) * E_FF]) for a in range(2))
                        else:
                            first = SH_BLOCKS[j - PAIRS][0]
                            wg, wh = ((lambda half, w=w: w[:, half, first:first + r]) for w in (sh_gate, sh_up))
                        wait(pe, silu_ready, n - 1)
                        product(act_in[u][0:r, :], wg, y_half).then_inc(g_done, 1)
                        if after(g, i, 2):
                            j2 = (j - 2) % ITEMS
                            if j2 < PAIRS:
                                pe.wait_ge(gated_ready, (c - (1 if j < 2 else 0)) * PAIRS + (j2 + 1))
                            else:
                                pe.wait_ge(full_ready, n - 1)
                        product(mul_in[u][0:r, :], wh, y_half).then_inc(h_done, 1)
                    if current(g) and j < USES:
                        if not isinstance(n, int) or c * USES + j > 0:
                            wait_apart(k, pe, wide_used, c * USES + j)
                        if j < PAIRS:
                            nc.tensor.matmul(wide_ps[:], k.pair_select[:, j, :], combT[:, ds(c * CH, CH)], start=True, stop=True)\
                                .then_inc(wide_done, 1)
                        else:
                            product(wide_ps[:], lambda half: sh_row[:, half, :], y_half).then_inc(wide_done, 1)
                    if after(g, i, 2):
                        j2 = (j - 2) % ITEMS
                        pe.wait_ge(lo_ready, n - 1)
                        if j2 == 0:
                            wait(pe, experts_copied, c)
                        if j2 == PAIRS:
                            wait(pe, shared_taken, c)
                        h = hidden[slot(i - 2)]
                        if j2 < PAIRS:
                            product(expert_ps[:], lambda half: w_dn[:, half, j2 * D:(j2 + 1) * D], lambda half: h[:, half, :],
                                    start=(j2 == 0), stop=(j2 == PAIRS - 1)).then_inc(down_done, 1)
                        else:
                            r = rows(j2)
                            b = j2 - PAIRS
                            product(shared_ps[:], lambda half: sh_down[0:r, half, b * D:(b + 1) * D], lambda half: h[0:r, half, :],
                                    start=(j2 == PAIRS), stop=(j2 == ITEMS - 1)).then_inc(down_done, 1)
                    if j == 4 and after(g, i, ITEMS):
                        pe.wait_ge(total_ready, c)
                        wait(pe, x_added, c - 1)
                        for t in range(CH // P):
                            last = nc.tensor.transpose(turn_ps[:, t * P:(t + 1) * P], total[:, t * P:(t + 1) * P], k.ident[:])
                        last.then_inc(turned, 1)

                run(pe, step)

            @block.scalar
            def _(act):
                def step(g, i):
                    n, c, j = place(g, i)
                    if current(g):
                        u, r = i % 2, rows(j)
                        act.wait_ge(g_done, n + 1)
                        if after(g, i, 2):
                            j2 = (j - 2) % ITEMS
                            if j2 < PAIRS:
                                act.wait_ge(gated_ready, (c - (1 if j < 2 else 0)) * PAIRS + (j2 + 1))
                            else:
                                act.wait_ge(full_ready, n - 1)
                        nc.scalar.activation(silu[0:r, u, :], act_in[u][0:r, :], ACT.Silu).then_inc(silu_ready, 1)
                    if after(g, i, 1):
                        r1 = rows((j - 1) % ITEMS)
                        act.wait_ge(full_ready, n)
                        wait(act, down_done, n - 3)
                        nc.scalar.activation(hidden[slot(i - 1)][0:r1, HI, :], full[0:r1, (i - 1) % 2, :], ACT.Copy).then_inc(hi_ready, 1)
                    if not current(g):
                        return
                    if j == PAIRS:
                        act.wait_ge(wide_done, c * USES + USES)
                        wait(act, shared_taken, c)
                        nc.scalar.activation(share[:], wide_ps[:], ACT.Sigmoid).then_inc(share_ready, 1)
                        act.wait_ge(share_ready, c + 1)
                        act.sem_inc(wide_used, 1)
                    if j == ITEMS - 1:
                        act.wait_ge(down_done, c * ITEMS + PAIRS)
                        wait(act, total_ready, c)
                        nc.scalar.activation(experts[:], expert_ps[:], ACT.Copy).then_inc(experts_copied, 1)

                run(act, step)

            @block.gpsimd
            def _(pool):
                def step(g, i):
                    n, c, j = place(g, i)
                    u = i % 2
                    if after(g, i, 1):
                        r1 = rows((j - 1) % ITEMS)
                        h = hidden[slot(i - 1)]
                        pool.wait_ge(hi_ready, n)
                        nc.gpsimd.tensor_tensor(h[0:r1, LO, :], full[0:r1, 1 - u, :], h[0:r1, HI, :], ALU.subtract).then_inc(lo_ready, 1)

                run(pool, step)

            @block.vector
            def _(dve):
                def step(g, i):
                    n, c, j = place(g, i)
                    u = i % 2
                    if current(g):
                        r = rows(j)
                        dve.wait_ge(silu_ready, n + 1)
                        dve.wait_ge(h_done, n + 1)
                        if j < PAIRS:
                            wait(dve, full_ready, n)
                            nc.vector.tensor_tensor(gated[:], silu[:, u, :], mul_in[u][:], ALU.mult).then_inc(gated_ready, 1)
                            dve.wait_ge(gated_ready, c * PAIRS + (j + 1))
                            dve.wait_ge(wide_done, c * USES + (j + 1))
                            wait(dve, lo_ready, n - 1)
                            nc.vector.tensor_tensor(full[:, u, :], gated[:], wide_ps[:], ALU.mult).then_inc(full_ready, 1)
                            dve.wait_ge(full_ready, n + 1)
                            dve.sem_inc(wide_used, 1)
                        else:
                            wait(dve, lo_ready, n - 1)
                            nc.vector.tensor_tensor(full[0:r, u, :], silu[0:r, u, :], mul_in[u][0:r, :], ALU.mult).then_inc(full_ready, 1)
                    if j == 2 and after(g, i, ITEMS):
                        dve.wait_ge(down_done, c * ITEMS)
                        dve.wait_ge(share_ready, c)
                        nc.vector.tensor_tensor(shared[:], share[:], shared_ps[:], ALU.mult).then_inc(shared_taken, 1)
                        dve.wait_ge(shared_taken, c)
                        dve.wait_ge(experts_copied, c)
                        wait(dve, turned, c - 1)
                        nc.vector.tensor_tensor(total[:], shared[:], experts[:], ALU.add).then_inc(total_ready, 1)
                    if j == 5 and after(g, i, ITEMS):
                        dve.wait_ge(turned, c)
                        xc = k.x[:, ds((c - 1) * CH, CH)]
                        nc.vector.tensor_tensor(xc, turn_ps[:], xc, ALU.add).then_inc(x_added, 1)

                run(dve, step)
                dve.wait_ge(x_added, CHUNKS)


STAGES = [xattn0, rglru0, ffn0, xattn1, attn1, moe1]




def build(nc, io, out):
    k = Core()
    k.nc = nc
    k.keep = ExitStack()
    k.in_use = []

    def sem(name):
        k.in_use.append(nc.alloc_semaphore(name=name))
        return k.in_use[-1]

    k.sem = sem
    k.keep0 = nc.dram_tensor("keep0", [B, N_CTX], BF16, kind="Internal").ap()
    k.keep1 = nc.dram_tensor("keep1", [B, N_CTX], BF16, kind="Internal").ap()
    k.lat_dram = nc.dram_tensor("latents_normalised", [TOK, D], F32, kind="Internal").ap()
    k.ctx_tail_dram = nc.dram_tensor("ctx_tail_normalised", [B, D], F32, kind="Internal").ap()
    k.v_tail_dram = nc.dram_tensor("ctx_tail_values", [B, D], F32, kind="Internal").ap()
    with k.keep:
        setup(k, io)
        for stage in STAGES:
            k.passed = k.sem(f"passed_{stage.__name__}")
            stage(k, io)
            recycle(k)
        store(k, out)


def recycle(k):
    k.nc.clear_and_free_semaphores(k.in_use)
    k.nc.all_engine_barrier()
    k.in_use = []


def store(k, out):
    nc = k.nc
    stored = k.sem("out_stored")
    with nc.Block() as block:

        @block.sync
        def _(sp):
            sp.dma_start(out.rearrange("(t b) l d -> (b l) t d", b=BPT),
                         k.x[:].rearrange("p (t d) -> p t d", d=D)).then_inc(stored, 16)
            sp.wait_ge(stored, 16)


def constants():
    p = np.arange(P)
    c = {}
    c["c_head_of_feature"] = (p[:, None] // DH1 == np.arange(H)).astype(np.float32)
    c["c_head_in_group4"] = (p[:, None] % L // DH1 == np.arange(BPT * HG) % HG).astype(np.float32)
    c["c_group_of_feature"] = (np.arange(GROUPS)[:, None] == p // L).astype(np.float32)
    c["c_own_value"] = (p[:, None] // L == p % L // DH1).astype(np.float32)
    c["c_batch_in_tile"] = (p[:, None] // L == np.arange(BPT)).astype(np.float32)
    fenwick = np.zeros((L, L), bool)
    for i in range(L):
        j = i + 1
        while j <= L:
            fenwick[i, j - 1] = True
            j += j & -j
        step = 1
        while i - step >= 0:
            fenwick[i, i - step] = True
            step *= 2
    fenwick &= np.tril(np.ones((L, L), bool))
    c["c_fenwick"] = np.tile(np.where(fenwick, 0.0, -NEG0), (HG, 1)).astype(np.float32)
    e = np.tile(np.arange(E_N), PARTS)
    c["c_rank"] = np.tile(E_N - np.arange(E_N), (P, 1)).astype(np.float32)
    c["c_pair_select"] = (e[:, None, None] == 2 * np.arange(PAIRS)[None, :, None] + p[None, None, :] // E_FF).astype(np.float32)
    return c


def kernel(**inputs):
    import numpy as _np
    import concourse.bacc as _bacc
    from concourse import mybir as _mybir
    from concourse.bass_utils import run_bass_kernel_spmd as _run

    nc = _bacc.Bacc("TRN2", target_bir_lowering=False, num_devices=1)
    arrays, io = {}, {}
    for name, a in {**inputs, **constants()}.items():
        a = _np.ascontiguousarray(a)
        if a.dtype == bool:
            a = a.reshape(-1).view(_np.int32)
        arrays[f"in_{name}"] = a
        io[name] = nc.dram_tensor(f"in_{name}", a.shape, _mybir.dt.from_np(a.dtype), kind="ExternalInput").ap()
    out = nc.dram_tensor("out_0", (B, L, D), F32, kind="ExternalOutput").ap()
    build(nc, io, out)
    r = _run(nc, [arrays], core_ids=[0])
    return r.results[0]["out_0"]
```

```python
from contextlib import ExitStack

import numpy as np
import concourse.bass as bass
from concourse import mybir

F32 = mybir.dt.float32
BF16 = mybir.dt.bfloat16
F32R = mybir.dt.float32r
U8 = mybir.dt.uint8
I32 = mybir.dt.int32
ALU = mybir.AluOpType
ACT = mybir.ActivationFunctionType
AX = mybir.AxisListType
ABSMAX = bass.bass_isa.ReduceOp.absmax
ds = bass.ds

P = 128
B, L, D = 128, 32, 128
N_CTX = 257
TOK = B * L
TILES = TOK // P
BPT = P // L
CH = 512
CHUNKS = TOK // CH
H = 16
DH0 = 64
DH1 = D // H
GROUPS = 4
HG = H // GROUPS
KEYS0 = N_CTX + L
TAIL0 = L + 1
EPS = 1e-5
NEG0 = 3e38
NEG1 = 1e9
RNE = 12582912.0
QMAX = 32767.0
FF0 = 384
FB0 = FF0 // P
WBLK = 32
E_N, E_FF = 16, 64
PAIRS = E_N // 2
PARTS = 3
SH_FF = 352
SH_BLOCKS = [(0, 128), (128, 128), (256, 96)]


HI, LO = 0, 1
PASSES = ((LO, HI), (HI, LO), (HI, HI))
even = lambda n: n + n % 2


class Core:
    pass


def tile_stats(k, t):
    return k.nc.vector.bn_stats(k.stats[:, ds(t, 1), :], k.x[:, ds(t * D, D)])


def ln_stats(k, stack, name, extra=None):
    nc = k.nc
    n = TILES + (extra is not None)
    tile = lambda part: stack.enter_context(nc.sbuf_tensor(f"{name}_{part}", [P, n], F32))
    stats = k.stats[:, 0:n]
    mean, rstd, twice = tile("mean"), tile("rstd"), tile("twice")
    mean_sum, mean_diff, var, var_eps, inv, error, inner = (tile(part) for part in (
        "mean_sum", "mean_diff", "var", "var_eps", "inv", "error", "inner"))
    chain, inv_ready, root_ready = k.sem(f"{name}_chain"), k.sem(f"{name}_inv_ready"), k.sem(f"{name}_root_ready")
    with nc.Block() as block:

        @block.vector
        def _(dve):
            if extra is not None:
                nc.vector.bn_stats(stats[:, TILES, :], extra).then_inc(chain, 1)
                dve.wait_ge(chain, 1)
            first = int(extra is not None)
            nc.vector.tensor_tensor(mean_diff[:], stats[:, :, 1], stats[:, :, 4], ALU.subtract).then_inc(chain, 1)
            nc.vector.tensor_tensor(var[:], stats[:, :, 2], stats[:, :, 5], ALU.add).then_inc(chain, 1)
            nc.vector.tensor_tensor(mean_sum[:], stats[:, :, 1], stats[:, :, 4], ALU.add).then_inc(chain, 1)
            dve.wait_ge(chain, first + 3)
            nc.vector.tensor_scalar(mean[:], mean_sum[:], 0.5, None, ALU.mult).then_inc(chain, 1)
            nc.vector.scalar_tensor_tensor(mean_diff[:], mean_diff[:], 0.25, mean_diff[:], ALU.mult, ALU.mult).then_inc(chain, 1)
            dve.wait_ge(chain, first + 5)
            nc.vector.scalar_tensor_tensor(var[:], var[:], 1.0 / D, mean_diff[:], ALU.mult, ALU.add).then_inc(chain, 1)
            dve.wait_ge(chain, first + 6)
            def rsqrt(root, n, before):
                nc.vector.tensor_scalar(var_eps[:], var[:], EPS, None, ALU.add).then_inc(chain, 1)
                dve.wait_ge(chain, before + 1)
                nc.vector.reciprocal(inv[:], var_eps[:]).then_inc(inv_ready, 1)
                dve.wait_ge(root_ready, n)
                nc.vector.tensor_tensor(error[:], root[:], root[:], ALU.mult).then_inc(chain, 1)
                dve.wait_ge(chain, before + 2)
                nc.vector.scalar_tensor_tensor(error[:], error[:], -0.5, var_eps[:], ALU.mult, ALU.mult).then_inc(chain, 1)
                dve.wait_ge(chain, before + 3)
                nc.vector.scalar_tensor_tensor(root[:], error[:], 1.5, root[:], ALU.add, ALU.mult).then_inc(chain, 1)
                dve.wait_ge(chain, before + 4)

            rsqrt(rstd, 1, first + 6)
            if extra is not None:
                nc.vector.tensor_tensor(inner[:], rstd[:], rstd[:], ALU.mult).then_inc(chain, 1)
                dve.wait_ge(chain, first + 11)
                nc.vector.tensor_tensor(var[:], var[:], inner[:], ALU.mult).then_inc(chain, 1)
                dve.wait_ge(chain, first + 12)
                rsqrt(twice, 2, first + 12)
                nc.vector.tensor_tensor(twice[:], twice[:], rstd[:], ALU.mult).then_inc(chain, 1)
                dve.wait_ge(chain, first + 17)

        @block.scalar
        def _(act):
            for n, root in enumerate((rstd,) if extra is None else (rstd, twice)):
                act.wait_ge(inv_ready, n + 1)
                nc.scalar.activation(root[:], inv[:], ACT.Sqrt).then_inc(root_ready, 1)
    return (mean, rstd) if extra is None else (mean, rstd, twice)


def layer_norm_T(k, name, yT):
    nc = k.nc
    with ExitStack() as stack:
        mean, rstd = ln_stats(k, stack, name)
        z = stack.enter_context(nc.sbuf_tensor(f"{name}_z", [P, 2, 4, D], F32))
        bank = [stack.enter_context(nc.psum_tensor(f"{name}_ps{u}", [P, CH], F32)) for u in range(2)]
        z_ready, turned, copied = k.sem(f"{name}_z_ready"), k.sem(f"{name}_turned"), k.sem(f"{name}_copied")
        with nc.Block() as block:

            @block.vector
            def _(dve):
                with dve.Fori(0, CHUNKS // 4) as g:
                    for i in range(4):
                        c, u = g * 4 + i, i % 2
                        dve.wait_ge(turned, c + 1)
                        for j in range(4):
                            t = c * 4 + j
                            last = nc.vector.tensor_scalar(z[:, u, j, :], k.x[:, ds(t * D, D)], mean[:, ds(t, 1)],
                                                           rstd[:, ds(t, 1)], ALU.subtract, ALU.mult)
                        last.then_inc(z_ready, 1)

            @block.tensor
            def _(pe):
                pe.sem_inc(turned, 2)
                with pe.Fori(0, CHUNKS // 4) as g:
                    for i in range(4):
                        c, u = g * 4 + i, i % 2
                        pe.wait_ge(z_ready, c + 1)
                        pe.wait_ge(copied, c + 1)
                        for j in range(4):
                            last = nc.tensor.transpose(bank[u][:, j * P:(j + 1) * P], z[:, u, j, :], k.ident[:])
                        last.then_inc(turned, 1)

            @block.scalar
            def _(act):
                act.sem_inc(copied, 2)
                with act.Fori(0, CHUNKS // 4) as g:
                    for i in range(4):
                        c, u = g * 4 + i, i % 2
                        act.wait_ge(turned, c + 3)
                        nc.scalar.activation(yT[:, ds(c * CH, CH)], bank[u][:], ACT.Copy).then_inc(copied, 1)
                act.wait_ge(copied, CHUNKS + 2)


def setup(k, io):
    nc = k.nc
    keep = k.keep
    sb = lambda name, shape, dt=F32: keep.enter_context(nc.sbuf_tensor(name, shape, dt))
    k.x = sb("x", [P, TILES * D])
    k.stats = sb("stats", [P, TILES + 1, 6])
    k.ident = sb("ident", [P, P])
    k.minus_half = sb("minus_half", [P, 2])
    k.rne, k.minus_rne = sb("rne", [P, 1]), sb("minus_rne", [P, 1])
    k.tiny = sb("tiny", [P, 1])
    k.zero = sb("zero", [P, 1])
    k.head_of_feature = sb("head_of_feature", [P, H])
    k.head_in_group4 = sb("head_in_group4", [P, BPT * HG])
    k.group_of_feature = sb("group_of_feature", [GROUPS, P])
    k.batch_in_tile = sb("batch_in_tile", [P, BPT])
    k.fenwick = sb("fenwick", [P, L])
    k.pair_select = sb("pair_select", [PARTS * E_N, PAIRS, P], BF16)
    k.rank = sb("rank", [P, E_N])
    k.own_value = sb("own_value", [P, D])
    k.ctx_tail = sb("ctx_tail", [B, D])
    k.g1, k.b1, k.g2, k.b2 = (sb(n, [P, D]) for n in ("g1", "b1", "g2", "b2"))
    k.bo, k.bproj = sb("bo", [P, D]), sb("bproj", [P, D])
    k.w_in, k.w_gate = sb("w_inT", [P, P]), sb("w_gateT", [P, P])
    k.wq1, k.wk1, k.wv1, k.wo1 = (sb(n, [P, P]) for n in ("wq1T", "wk1T", "wv1T", "wo1T"))
    k.wqkv, k.wproj = sb("wqkv", [P, 3 * D]), sb("wproj", [P, D])
    k.f_gate, k.f_up, k.f_down = sb("f_gateT", [P, FF0]), sb("f_upT", [P, FF0]), sb("f_downT", [P, FB0, P])
    k.router = sb("router", [P, E_N])
    k.sh_gate_row = sb("sh_gate_row", [P, P])
    k.sh_gate, k.sh_up, k.sh_down = sb("sh_gateT", [P, SH_FF]), sb("sh_upT", [P, SH_FF]), sb("sh_downT", [P, 3, D])
    ROWS = 12
    k.cols = sb("cols", [P, ROWS])
    (k.b_in, k.b_gate, k.lam, k.bq1, k.bk1, k.bv1, k.bq2, k.bk2, k.bv2, k.g2c, k.b2c, k.shg) = (
        k.cols[:, j:j + 1] for j in range(ROWS))
    k.xattn0_weights = ExitStack()
    k.A, k.U = (k.xattn0_weights.enter_context(nc.sbuf_tensor(n, [P, H, P], F32)) for n in ("A", "U"))
    with ExitStack() as stack:
        tb = lambda name, shape, dt=F32: stack.enter_context(nc.sbuf_tensor(name, shape, dt))
        rows = tb("rows", [ROWS, D])
        wq0, wkv0, wout0 = tb("wq0", [P, H * DH0]), tb("wkv0", [P, 2 * H * DH0]), tb("wout0", [P, H // 2, D])
        wqT, wkT, wvT = (tb(n, [P, H // 2, P]) for n in ("wq0T", "wk0T", "wv0T"))
        sq = tb("square_weights", [P, 6, P])
        fg, fu, fd = tb("fg", [P, FB0, D]), tb("fu", [P, FB0, D]), tb("fd", [P, FB0, P])
        shg, shu, shd = tb("shg", [P, 3, D]), tb("shu", [P, 3, D]), tb("shd", [P, SH_FF])
        rt = tb("rt", [E_N, D])
        pair_select = tb("pair_select_f32", [PARTS * E_N, PAIRS, P])
        shrow = tb("shrow", [P, P])
        m0, m1 = tb("m0", [B, N_CTX], U8), tb("m1", [B, N_CTX], I32)
        m0b, m1b = tb("m0b", [B, N_CTX], BF16), tb("m1b", [B, N_CTX], BF16)
        qs = tb("qs", [P, 3, 2, FB0 * D // WBLK])
        qt = tb("qt", [P, 3, FB0 * D])
        ps = [stack.enter_context(nc.psum_tensor(f"setup_ps{j}", [P, CH], F32)) for j in range(4)]
        first_loaded, loaded, pool_loaded, x_loaded = k.sem("first_weights_loaded"), k.sem("weights_loaded"), k.sem("weights_loaded_pool"), k.sem("x_loaded")
        ident_ready, consts_ready = k.sem("ident_ready"), k.sem("consts_ready")
        quant, quant_ready = k.sem("quant_chain"), k.sem("weights_quantised")
        turned, copied = k.sem("weights_turned"), k.sem("weights_copied")
        stats_ready = k.sem("x_stats_ready")
        rows_ready, mask_ready, mask_stored = k.sem("shared_gate_row"), k.sem("mask_ready"), k.sem("mask_stored")
        first = [(wkv0[:], io["L0_xattn_Wkv"]), (wq0[:], io["L0_xattn_Wq"]),
                 (wout0[:], io["L0_xattn_Wout"].rearrange("(p r) d -> r p d", r=P))]
        loads = [
            (k.head_of_feature[:], io["c_head_of_feature"]), (k.head_in_group4[:], io["c_head_in_group4"]),
            (k.group_of_feature[:], io["c_group_of_feature"]),
            (k.batch_in_tile[:], io["c_batch_in_tile"]), (k.fenwick[:], io["c_fenwick"]),
            (pair_select[:], io["c_pair_select"]), (k.rank[:], io["c_rank"]),
            (k.own_value[:], io["c_own_value"]),
            (k.ctx_tail[:], io["ctx_1024"][:, N_CTX - 1, :]),
            (k.wqkv[:], io["L1_attn_W_qkv"]), (k.wproj[:], io["L1_attn_W_proj"]),
            (fg[:], io["L0_ffn_w_gate"].rearrange("(j p) d -> p j d", p=P)),
            (fu[:], io["L0_ffn_w_up"].rearrange("(j p) d -> p j d", p=P)),
            (fd[:].rearrange("p j d -> p (j d)"), io["L0_ffn_w_down"]),
            (shd[:], io["L1_ffn_shared_w_down"]), (rt[:], io["L1_ffn_gate_w"]),
            (m0[:], io["mask_BxS2_bk0"].bitcast(U8).rearrange("(b s) -> b s", b=B)), (m1[:], io["mask_Bx1x1xS2_if1"].rearrange("b o u s -> b (o u s)")),
        ]
        for j, n in enumerate(("L0_attn_W_in", "L0_attn_W_gate", "L1_xattn_W_q", "L1_xattn_W_k", "L1_xattn_W_v", "L1_xattn_W_o")):
            loads.append((sq[:, j, :], io[n]))
        for a, n in ((shg, "L1_ffn_shared_w_gate"), (shu, "L1_ffn_shared_w_up")):
            for j, (r, m) in enumerate(SH_BLOCKS):
                loads.append((a[0:m, j, :], io[n][r:r + m, :]))
        row = lambda ap: ap.rearrange("(a d) -> a d", a=1)
        for n, a in (("L0_xattn_g1", k.g1), ("L0_xattn_b1", k.b1), ("L0_xattn_g2", k.g2), ("L0_xattn_b2", k.b2),
                     ("L1_xattn_b_o", k.bo), ("L1_attn_b_proj", k.bproj)):
            loads.append((a[:], row(io[n]).broadcast_to([P, D])))
        for j, n in enumerate(("L0_attn_b_in", "L0_attn_b_gate", "L0_attn_forget_lambda", "L1_xattn_b_q", "L1_xattn_b_k", "L1_xattn_b_v")):
            first.append((rows[j:j + 1, :], row(io[n])))
        first.append((rows[6:9, :], io["L1_attn_b_qkv"].rearrange("(a d) -> a d", a=3)))
        first.append((rows[9:10, :], row(io["L0_xattn_g2"])))
        first.append((rows[10:11, :], row(io["L0_xattn_b2"])))
        first.append((rows[11:12, :], io["L1_ffn_shared_gate_w"]))
        by_sync, by_pool = loads[0::4] + loads[1::4] + loads[2::4], loads[3::4]
        turns = [(k.cols[:].unsqueeze(1), [rows[:]])]
        for w, base, t in ((wq0, 0, wqT), (wkv0, 0, wkT), (wkv0, H * DH0, wvT)):
            for h in range(0, H // 2, 4):
                turns.append((t[:, h:h + 4, :], [w[:, base + (h + j) * P:base + (h + j + 1) * P] for j in range(4)]))
        half = lambda t, h: t[DH0 * (h % 2):DH0 * (h % 2 + 1), h // 2, :]
        products = []
        for h in (0, 1, 8, 9):
            heads = range(h, h + 8, 2)
            products.append((k.A[:, h:h + 7:2, :], [(half(wqT, i), half(wkT, i)) for i in heads]))
            products.append((k.U[:, h:h + 7:2, :], [(half(wvT, i), half(wout0, i)) for i in heads]))
        later_turns = []
        for j, a in enumerate((k.w_in, k.w_gate, k.wq1, k.wk1, k.wv1, k.wo1)):
            later_turns.append((a[:].unsqueeze(1), [sq[:, j, :]]))
        later_turns.append((k.router[:].unsqueeze(1), [rt[:]]))
        for a, t in ((shg, k.sh_gate), (shu, k.sh_up)):
            for j, (r, m) in enumerate(SH_BLOCKS):
                later_turns.append((t[:, r:r + m].unsqueeze(1), [a[0:m, j, :]]))
        for j, (r, m) in enumerate(SH_BLOCKS):
            later_turns.append((k.sh_down[0:m, j:j + 1, :], [shd[:, r:r + m]]))
        first_product, first_later = len(turns), len(turns) + len(products)
        quant_from = first_later + len(later_turns)
        later_turns.append((k.f_gate[:].rearrange("p (j o) -> p j o", j=FB0), [fg[:, j, :] for j in range(FB0)]))
        later_turns.append((k.f_up[:].rearrange("p (j o) -> p j o", j=FB0), [fu[:, j, :] for j in range(FB0)]))
        later_turns.append((k.f_down[:], [fd[:, j, :] for j in range(FB0)]))
        groups = turns + products + later_turns

        def filled(n):
            dst, srcs = groups[n]
            m = r = P
            if not first_product <= n < first_later:
                m, r = srcs[0].shape[1], srcs[0].shape[0]
            return dst, ps[n % 4][0:m, 0:len(srcs) * r].rearrange("p (n r) -> p n r", r=r)

        with nc.Block() as block:

            @block.sync
            def _(sp):
                sp.dma_start(k.x[:].rearrange("p (t d) -> p t d", d=D),
                             io["x"].rearrange("(t b) l d -> (b l) t d", b=BPT)).then_inc(x_loaded, 16)
                for dst, src in first[1::2]:
                    sp.dma_start(dst, src).then_inc(first_loaded, 16)
                for dst, src in by_sync:
                    sp.dma_start(dst, src).then_inc(loaded, 16)
                sp.wait_ge(mask_ready, 2)
                sp.dma_start(k.keep0, m0b[:]).then_inc(mask_stored, 16)
                sp.dma_start(k.keep1, m1b[:]).then_inc(mask_stored, 16)
                sp.wait_ge(mask_stored, 32)

            @block.gpsimd
            def _(pool):
                for dst, src in by_pool:
                    pool.dma_start(dst, src).then_inc(pool_loaded, 16)
                nc.gpsimd.memset(k.ident[:], 0.0).then_inc(ident_ready, 1)
                nc.gpsimd.memset(k.minus_half[:], -0.5)
                nc.gpsimd.memset(k.rne[:], RNE)
                nc.gpsimd.memset(k.minus_rne[:], -RNE)
                nc.gpsimd.memset(k.zero[:], 0.0)
                nc.gpsimd.memset(k.tiny[:], 1e-6).then_inc(consts_ready, 1)
                pool.wait_ge(ident_ready, 1)
                nc.gpsimd.affine_select(out=k.ident[:], in_=k.ident[:], compare_op=ALU.not_equal, fill=1.0, base=0,
                                        pattern=[[-1, P]], channel_multiplier=1).then_inc(ident_ready, 1)
                pool.wait_ge(ident_ready, 2)
                pool.wait_ge(consts_ready, 1)

            @block.vector
            def _(dve):
                dve.wait_ge(x_loaded, 16)
                with dve.Fori(0, TILES // 4) as g:
                    for j in range(4):
                        last = tile_stats(k, g * 4 + j)
                    last.then_inc(stats_ready, 1)
                dve.wait_ge(stats_ready, TILES // 4)
                dve.wait_ge(loaded, 16 * len(by_sync))
                dve.wait_ge(pool_loaded, 16 * len(by_pool))
                nc.vector.tensor_copy(k.pair_select[:], pair_select[:])
                nc.vector.tensor_copy(m0b[:], m0[:]).then_inc(mask_ready, 1)
                nc.vector.tensor_scalar(m1b[:], m1[:], 0.0, None, ALU.not_equal).then_inc(mask_ready, 1)
                blocks = lambda a: a.rearrange("p j (n e) -> p (j n) e", e=WBLK)
                spread = lambda a: a.unsqueeze(2).broadcast_to([P, FB0 * D // WBLK, WBLK])
                for j, w in enumerate((fg, fu, fd)):
                    nc.vector.tensor_reduce(qs[:, j, 0, :], blocks(w[:]), AX.X, ALU.max, apply_absolute_value=True)\
                        .then_inc(quant, 1)
                dve.wait_ge(quant, 3)
                nc.vector.tensor_scalar(qs[:, :, 0, :], qs[:, :, 0, :], 1.0 / 7.0, 1e-12, ALU.mult, ALU.max).then_inc(quant, 1)
                dve.wait_ge(quant, 4)
                nc.vector.reciprocal(qs[:, :, 1, :], qs[:, :, 0, :]).then_inc(quant, 1)
                dve.wait_ge(quant, 5)
                flat = lambda a, j: a[:, j, :].rearrange("p (n e) -> p n e", e=WBLK)
                for j, w in enumerate((fg, fu, fd)):
                    nc.vector.tensor_tensor(flat(qt, j), blocks(w[:]), spread(qs[:, j, 1, :]), ALU.mult).then_inc(quant, 1)
                dve.wait_ge(quant, 8)
                nc.vector.tensor_scalar(qt[:], qt[:], RNE, -RNE, ALU.add, ALU.add).then_inc(quant, 1)
                dve.wait_ge(quant, 9)
                for j, w in enumerate((fg, fu, fd)):
                    nc.vector.tensor_tensor(blocks(w[:]), flat(qt, j), spread(qs[:, j, 0, :]), ALU.mult).then_inc(quant_ready, 1)
                dve.wait_ge(copied, 1)
                nc.vector.tensor_copy(k.sh_gate_row[:], k.shg.broadcast_to([P, P])).then_inc(rows_ready, 1)
                dve.wait_ge(rows_ready, 1)

            @block.scalar
            def _(act):
                for dst, src in first[0::2]:
                    act.dma_start(dst, src).then_inc(first_loaded, 16)
                for n in range(len(groups)):
                    act.wait_ge(turned, n + 1)
                    nc.scalar.activation(*filled(n), ACT.Copy).then_inc(copied, 1)
                act.wait_ge(copied, len(groups))

            @block.tensor
            def _(pe):
                pe.wait_ge(first_loaded, 16 * len(first))
                pe.wait_ge(ident_ready, 2)
                for n, (dst, srcs) in enumerate(groups):
                    if n == first_product:
                        pe.wait_ge(copied, first_product)
                    if n == first_later:
                        pe.wait_ge(loaded, 16 * len(by_sync))
                        pe.wait_ge(pool_loaded, 16 * len(by_pool))
                    if n == quant_from:
                        pe.wait_ge(quant_ready, 3)
                    if n >= 4:
                        pe.wait_ge(copied, n - 3)
                    if first_product <= n < first_later:
                        for j, (lhsT, rhs) in enumerate(srcs):
                            last = nc.tensor.matmul(ps[n % 4][:, j * P:(j + 1) * P], lhsT, rhs, start=True, stop=True)
                    else:
                        m, r = srcs[0].shape[1], srcs[0].shape[0]
                        for j, src in enumerate(srcs):
                            last = nc.tensor.transpose(ps[n % 4][0:m, j * r:(j + 1) * r], src, k.ident[0:r, 0:r])
                    last.then_inc(turned, 1)


def wait(eng, sem, count):
    if not isinstance(count, int) or count > 0:
        eng.wait_ge(sem, count)


def wait_apart(k, eng, sem, count):
    eng.wait_ge(sem, count)
    eng.sem_inc(k.passed, 1)


def run_steps(eng, step, lead, lag=0):
    for s in range(-lead, 8):
        step(s // 8, s % 8)
    with eng.Fori(1, B // 8 - 1) as g:
        for j in range(8):
            step(g, j)
    for s in range(B - 8, B + lag):
        step(s // 8, s % 8)


def live(g, j, ahead, n=B):
    return not isinstance(g, int) or 0 <= 8 * g + j + ahead < n


def xattn0_inputs(k, io, stack):
    nc = k.nc
    k.latT = stack.enter_context(nc.sbuf_tensor("latT", [P, TOK], F32))
    k.tailT = stack.enter_context(nc.sbuf_tensor("tailT", [P, B], F32))
    with ExitStack() as st:
        z2 = st.enter_context(nc.sbuf_tensor("lat_z2", [P, 2, 4, D], F32))
        lat = st.enter_context(nc.sbuf_tensor("lat_affine", [P, 2, 4, D], F32))
        tail = st.enter_context(nc.sbuf_tensor("ctx_tail_affine", [P, 2, D], F32))
        bank = [st.enter_context(nc.psum_tensor(f"lat_ps{u}", [P, CH], F32)) for u in range(2)]
        tail_ps = st.enter_context(nc.psum_tensor("lat_ps_tail", [P, P], F32))
        z2_ready, turned, copied = k.sem("lat_z2_ready"), k.sem("lat_turned"), k.sem("lat_copied")
        scaled, affine_ready, stored = k.sem("lat_scaled"), k.sem("lat_affine_ready"), [k.sem(f"lat_stored{u}") for u in range(2)]
        tail_z, tail_scaled, tail_turned, tail_stored = (k.sem(f"ctx_tail_{n}") for n in ("z", "scaled", "turned", "stored"))
        spread = lambda a: a[:].unsqueeze(1).broadcast_to([P, 4, D])
        k.latents_stored = [(tail_stored, 16)] + [(sem, 16 * CHUNKS // 2 + 16) for sem in stored]
        mean, rstd, twice = ln_stats(k, st, "lat_ln", k.ctx_tail[:])
        with nc.Block() as block:

            @block.vector
            def _(dve):
                nc.vector.tensor_scalar(tail[:, 0, :], k.ctx_tail[:], mean[:, TILES:TILES + 1], rstd[:, TILES:TILES + 1],
                                        ALU.subtract, ALU.mult).then_inc(tail_z, 1)
                with dve.Fori(0, CHUNKS // 2) as g:
                    c = g * 2
                    for u in range(2):
                        dve.wait_ge(turned, c + (u + 1))
                        for j in range(4):
                            t = c * 4 + (4 * u + j)
                            last = nc.vector.tensor_scalar(z2[:, u, j, :], k.x[:, ds(t * D, D)], mean[:, ds(t, 1)],
                                                           twice[:, ds(t, 1)], ALU.subtract, ALU.mult)
                        last.then_inc(z2_ready, 1)
                        dve.wait_ge(stored[u], g * 16 + 16)
                        dve.wait_ge(z2_ready, c + (u + 1))
                        nc.vector.tensor_tensor(lat[:, u], z2[:, u], spread(k.g2), ALU.mult).then_inc(scaled, 1)
                dve.wait_ge(tail_turned, 1)
                nc.vector.tensor_copy(k.tailT[:], tail_ps[:]).then_inc(tail_turned, 1)
                dve.wait_ge(tail_turned, 2)

            @block.gpsimd
            def _(pool):
                pool.wait_ge(tail_z, 1)
                nc.gpsimd.tensor_tensor(tail[:, 0, :], tail[:, 0, :], k.g1[:], ALU.mult).then_inc(tail_scaled, 1)
                pool.wait_ge(tail_scaled, 1)
                nc.gpsimd.tensor_tensor(tail[:, 1, :], tail[:, 0, :], k.b1[:], ALU.add).then_inc(tail_scaled, 1)
                with pool.Fori(0, CHUNKS // 2) as g:
                    c = g * 2
                    for u in range(2):
                        pool.wait_ge(scaled, c + (u + 1))
                        nc.gpsimd.tensor_tensor(lat[:, u], lat[:, u], spread(k.b2), ALU.add).then_inc(affine_ready, 1)

            @block.tensor
            def _(pe):
                pe.sem_inc(turned, 2)
                with pe.Fori(0, CHUNKS // 2) as g:
                    c = g * 2
                    for u in range(2):
                        pe.wait_ge(z2_ready, c + (u + 1))
                        pe.wait_ge(copied, c + (u + 1))
                        for j in range(4):
                            last = nc.tensor.transpose(bank[u][:, j * P:(j + 1) * P], z2[:, u, j, :], k.ident[:])
                        last.then_inc(turned, 1)
                pe.wait_ge(tail_scaled, 2)
                nc.tensor.transpose(tail_ps[:], tail[:, 1, :], k.ident[:]).then_inc(tail_turned, 1)

            @block.scalar
            def _(act):
                act.sem_inc(copied, 2)
                with act.Fori(0, CHUNKS // 2) as g:
                    c = g * 2
                    for u in range(2):
                        act.wait_ge(turned, c + (u + 3))
                        nc.scalar.activation(k.latT[:, ds((c + u) * CH, CH)], bank[u][:], ACT.Identity, bias=k.b2c,
                                             scale=k.g2c).then_inc(copied, 1)
                act.wait_ge(copied, CHUNKS + 2)

            @block.sync
            def _(sp):
                for u in range(2):
                    sp.sem_inc(stored[u], 16)
                with sp.Fori(0, CHUNKS // 2) as g:
                    c = g * 2
                    for u in range(2):
                        sp.wait_ge(affine_ready, c + (u + 1))
                        sp.dma_start(k.lat_dram[ds((c + u) * CH, CH), :].rearrange("(t p) d -> p t d", p=P),
                                     lat[:, u]).then_inc(stored[u], 16)
                sp.wait_ge(tail_scaled, 2)
                sp.dma_start(k.ctx_tail_dram, tail[:, 1, :]).then_inc(tail_stored, 16)


def xattn0(k, io):
    nc = k.nc
    with ExitStack() as stack:
        xattn0_inputs(k, io, stack)
        sb = lambda name, shape, dt=F32: stack.enter_context(nc.sbuf_tensor(name, shape, dt))
        psum = lambda name: stack.enter_context(nc.psum_tensor(name, [P, CH], F32))
        sem = k.sem
        raw = sb("a_raw", [P, 8, 2, D])
        stats, mv = sb("a_stats", [P, 2, 2, 6]), sb("a_mv", [P, 2, 2, 2])
        var, rstd = sb("a_var", [P, 2, 2]), sb("a_rstd", [P, 2, 2])
        z = sb("a_z", [P, 2, 2, D])
        xn = sb("a_xn", [P, 8, 2, D])
        tail = sb("a_tail", [TAIL0, 8, D])
        xnT = sb("a_xnT", [P, 2, 8, even(KEYS0)], F32R)
        kept = sb("a_kept", [P, 2, BPT, N_CTX], BF16)
        bias = sb("a_bias", [P, 8, KEYS0])
        qT = sb("a_qT", [P, 2, 2, BPT, H, L], F32R)
        neg = sb("a_neg", [P, GROUPS, KEYS0])
        nmax = sb("a_nmax", [P, 2, GROUPS])
        prob = sb("a_prob", [P, 2, GROUPS, KEYS0])
        rsum, rinv = sb("a_rsum", [P, 2, GROUPS]), sb("a_rinv", [P, 2, GROUPS])
        probT = sb("a_probT", [P, 3, CH])
        oT = sb("a_oT", [P, H, P])
        score_ps, turn_ps = [psum("a_score0"), psum("a_score1")], [psum("a_turn0"), psum("a_turn1")]
        out_ps, ctx_ps, q_ps, proj_ps = psum("a_out"), psum("a_ctx"), psum("a_q"), psum("a_proj")
        raw_loaded = [sem(f"a_raw_loaded{j}") for j in range(8)]
        kept_loaded = [sem(f"a_kept_loaded{u}") for u in range(2)]
        tail_loaded = [sem(f"a_tail_loaded{u}") for u in range(2)]
        stats_ready, mv_ready, var_ready, rstd_ready = sem("a_stats_ready"), sem("a_mv_ready"), sem("a_var_ready"), sem("a_rstd_ready")
        z_ready, scaled, xn_ready = sem("a_z_ready"), sem("a_scaled"), sem("a_xn_ready")
        ctx_turned, xnT_hi, xnT_ready, keys_hi, keys_ready = (sem(f"a_{n}") for n in ("ctx_turned", "xnT_hi", "xnT_ready", "tile_keys_hi", "tile_keys_ready"))
        q_ready, q_hi, q_copied = sem("a_q_ready"), sem("a_q_hi"), sem("a_q_copied")
        scored, masked, exped, rinv_ready, prob_ready = (sem(f"a_{n}") for n in ("scored", "masked", "exped", "rinv_ready", "prob_ready"))
        turned, probT_ready = [sem(f"a_turned{n}") for n in range(3)], [sem(f"a_probT_ready{n}") for n in range(3)]
        out_ready, oT_ready, proj_ready, x_added = (sem(f"a_{n}") for n in ("out_ready", "oT_ready", "proj_ready", "x_added"))
        zeroed = sem("a_zeroed")
        x_stats_ready = sem("a_x_stats_ready")
        LEAD, LAG = 5, 1
        TKEYS = (P, P, TAIL0)

        def tile_of(g, j, ahead=0):
            return g * 2 + (j + ahead) // 4

        def quarter(b):
            return (1, b + 1) if b < 3 else (2, 0)

        def q_half(g, j, half):
            ahead, hg = quarter(j % 4)
            return qT[:, half, (j // 4 + ahead) % 2, :, 4 * hg:4 * hg + 4, :].rearrange("p b h l -> p h b l")

        with nc.Block() as block:

            @block.sync
            def _(sp):
                def load_raw(g, j):
                    sp.dma_start(raw[:, j % 8], io["ctx_1024"][ds(g * 8 + j, 1), 0:2 * P, :].rearrange(
                        "b (t p) d -> p (b t) d", p=P)).then_inc(raw_loaded[j % 8], 16)

                def load_kept(t, u):
                    sp.dma_start(kept[:, u], k.keep0[ds(t * BPT, BPT), :].unsqueeze(0).broadcast_to([P, BPT, N_CTX]))\
                        .then_inc(kept_loaded[u], 16)

                def step(g, j):
                    s, t, u, b = g * 8 + j, tile_of(g, j), j // 4, j % 4
                    if live(g, j, 8):
                        wait(sp, z_ready, s + 1)
                        load_raw(g + 1, j)
                    if b == 0 and live(g, j, 8):
                        wait(sp, keys_ready, t + 1)
                        load_kept(t + 2, u)
                    if b == 3 and live(g, j, 8):
                        wait(sp, out_ready, s + 1)
                        rows = slice(4 * u, 4 * u + 4)
                        sp.dma_start(tail[0:L, rows, :], k.lat_dram[ds((t + 2) * P, P), :].rearrange(
                            "(b l) d -> l b d", l=L)).then_inc(tail_loaded[u], 16)
                        sp.dma_start(tail[L:L + 1, rows, :], k.ctx_tail_dram[ds((t + 2) * BPT, BPT), :].unsqueeze(0))\
                            .then_inc(tail_loaded[u], 16)

                for j in range(3):
                    load_raw(0, j)
                load_kept(0, 0)
                for stored, count in k.latents_stored:
                    sp.wait_ge(stored, count)
                run_steps(sp, step, LEAD)

            @block.gpsimd
            def _(pool):
                for half in (HI, LO):
                    nc.gpsimd.tensor_copy(xnT[:, half, :, KEYS0:], k.zero[:].unsqueeze(1).broadcast_to([P, 8, even(KEYS0) - KEYS0]))
                nc.gpsimd.memset(bias[:, :, 2 * P:2 * P + L], 0.0).then_inc(zeroed, 1)
                spread = lambda a: a[:].unsqueeze(1).broadcast_to([P, 2, D])

                def step(g, j):
                    s, t, u, b = g * 8 + j, tile_of(g, j), j // 4, j % 4
                    if live(g, j, 4):
                        n, par = (j + 4) % 8, j % 2
                        pool.wait_ge(z_ready, s + 5)
                        nc.gpsimd.tensor_tensor(xn[:, n], z[:, par], spread(k.g1), ALU.mult).then_inc(scaled, 1)
                        pool.wait_ge(scaled, s + 5)
                        nc.gpsimd.tensor_tensor(xn[:, n], xn[:, n], spread(k.b1), ALU.add).then_inc(xn_ready, 1)
                    if live(g, j, 5):
                        par = (j + 5) % 2
                        wait_apart(k, pool, mv_ready, s + 6)
                        nc.gpsimd.tensor_scalar(var[:, par], mv[:, par, :, 1], EPS, None, ALU.add).then_inc(var_ready, 1)
                        pool.wait_ge(var_ready, s + 6)
                        nc.gpsimd.tensor_tensor(rstd[:, par], var[:, par], k.minus_half[:, 0:2], ALU.pow).then_inc(rstd_ready, 1)
                    if b == 3 and live(g, j, 8):
                        slots = slice(4 * u, 4 * u + 4)
                        wait(pool, masked, s * 4 + 8 - 4)
                        lat = k.latT[:, ds((t + 2) * P, P)].rearrange("p (b l) -> p b l", l=L)
                        last = k.tailT[:, ds((t + 2) * BPT, BPT)].unsqueeze(2)
                        lat_half, last_half = ((lambda half, r=r: xnT[:, half, slots, r]) for r in (slice(2 * P, 2 * P + L), slice(KEYS0 - 1, KEYS0)))
                        nc.gpsimd.tensor_copy(lat_half(HI), lat)
                        nc.gpsimd.tensor_copy(last_half(HI), last).then_inc(keys_hi, 1)
                        wait_apart(k, pool, keys_hi, t + 3)
                        nc.gpsimd.tensor_tensor(lat_half(LO), lat, lat_half(HI), ALU.subtract)
                        nc.gpsimd.tensor_tensor(last_half(LO), last, last_half(HI), ALU.subtract)
                        wait_apart(k, pool, kept_loaded[u], (g + 2) * 16)
                        nc.gpsimd.tensor_scalar(bias[:, slots, 0:2 * P], kept[:, u, :, 0:2 * P], NEG0, -NEG0, ALU.mult, ALU.add)
                        nc.gpsimd.tensor_scalar(bias[:, slots, KEYS0 - 1:KEYS0], kept[:, u, :, 2 * P:N_CTX], NEG0, -NEG0,
                                                ALU.mult, ALU.add).then_inc(keys_ready, 1)

                run_steps(pool, step, LEAD)

            @block.vector
            def _(dve):
                def mask(g, j, grp):
                    s, n, par = g * 8 + j, (j + 1) % 8, (j + 1) % 2
                    if n % 4 == 0 and grp == 0:
                        dve.wait_ge(keys_ready, tile_of(g, j, 1) + 1)
                    wait_apart(k, dve, scored, s * 4 + (5 + grp))
                    nc.vector.tensor_tensor_reduce(
                        out=neg[:, grp, :], in0=score_ps[grp % 2][:, 0:KEYS0], in1=bias[:, n, :], scale=-DH0 ** -0.5,
                        scalar=3.4e38, op0=ALU.add, op1=ALU.min, accum_out=nmax[:, par, grp:grp + 1]).then_inc(masked, 1)

                def step(g, j):
                    s, t, u, b = g * 8 + j, tile_of(g, j), j // 4, j % 4
                    if live(g, j, 1):
                        mask(g, j, 0)
                        mask(g, j, 1)
                    if live(g, j, 0):
                        dve.wait_ge(turned[0], s + 1)
                        nc.vector.tensor_copy(probT[:, 0, :], turn_ps[0][:]).then_inc(probT_ready[0], 1)
                    if live(g, j, 1):
                        mask(g, j, 2)
                        mask(g, j, 3)
                    if live(g, j, 5):
                        n, par = (j + 5) % 8, (j + 5) % 2
                        dve.wait_ge(raw_loaded[n], (g + (j + 5) // 8 + 1) * 16)
                        for kt in range(2):
                            last = nc.vector.bn_stats(stats[:, par, kt, :], raw[:, n, kt, :])
                        last.then_inc(stats_ready, 1)
                    if live(g, j, 4):
                        n, par = (j + 4) % 8, j % 2
                        dve.wait_ge(rstd_ready, s + 5)
                        wait(dve, xn_ready, s + 3)
                        for kt in range(2):
                            last = nc.vector.tensor_scalar(z[:, par, kt, :], raw[:, n, kt, :], mv[:, par, kt, 0:1],
                                                           rstd[:, par, kt:kt + 1], ALU.subtract, ALU.mult)
                        last.then_inc(z_ready, 1)
                    if live(g, j, 5):
                        par = (j + 5) % 2
                        wait_apart(k, dve, stats_ready, s + 6)
                        for kt in range(2):
                            last = nc.vector.bn_aggr(mv[:, par, kt, :], stats[:, par, kt, :])
                        last.then_inc(mv_ready, 1)
                    if live(g, j, 1):
                        par = (j + 1) % 2
                        dve.wait_ge(exped, s * 4 + 8)
                        nc.vector.reciprocal(rinv[:, par, :], rsum[:, par, :]).then_inc(rinv_ready, 1)
                        dve.wait_ge(rinv_ready, s + 2)
                        for grp in range(GROUPS):
                            last = nc.vector.tensor_scalar(prob[:, par, grp, :], prob[:, par, grp, :],
                                                           rinv[:, par, grp:grp + 1], None, ALU.mult)
                        last.then_inc(prob_ready, 1)
                    if live(g, j, 4 * quarter(b)[0] - b):
                        dve.wait_ge(q_hi, (t + quarter(b)[0]) * 4 + (quarter(b)[1] + 1))
                        nc.vector.tensor_tensor(q_half(g, j, LO), q_ps[:].rearrange("p (h b l) -> p h b l", h=4, l=L),
                                                q_half(g, j, HI), ALU.subtract).then_inc(q_copied, 1)
                    if live(g, j, 3):
                        dve.wait_ge(xnT_hi, s + 4)
                        n = (j + 3) % 8
                        nc.vector.tensor_tensor(xnT[:, LO, n, 0:2 * P], ctx_ps[:, 0:2 * P], xnT[:, HI, n, 0:2 * P],
                                                ALU.subtract).then_inc(xnT_ready, 1)
                    if b == 0 and live(g, j, -1):
                        dve.wait_ge(proj_ready, t)
                        xt = k.x[:, ds((t - 1) * D, D)]
                        nc.vector.tensor_tensor(xt, proj_ps[:, 0:D], xt, ALU.add).then_inc(x_added, 1)
                        wait_apart(k, dve, x_added, t)
                        tile_stats(k, t - 1).then_inc(x_stats_ready, 1)

                dve.wait_ge(zeroed, 1)
                run_steps(dve, step, LEAD, LAG)
                dve.wait_ge(x_stats_ready, TILES)

            @block.scalar
            def _(act):
                def exp(g, j, grp):
                    s, par = g * 8 + j, (j + 1) % 2
                    act.wait_ge(masked, s * 4 + (5 + grp))
                    nc.scalar.activation(prob[:, par, grp, :], neg[:, grp, :], ACT.Exp, bias=nmax[:, par, grp:grp + 1],
                                         scale=-1.0, accum_out=rsum[:, par, grp:grp + 1]).then_inc(exped, 1)

                def step(g, j):
                    s, t, u, b = g * 8 + j, tile_of(g, j), j // 4, j % 4
                    if live(g, j, 1):
                        exp(g, j, 0)
                        exp(g, j, 1)
                    if live(g, j, 0):
                        act.wait_ge(turned[1], s + 1)
                        nc.scalar.activation(probT[:, 1, :], turn_ps[1][:], ACT.Copy).then_inc(probT_ready[1], 1)
                    if live(g, j, 1):
                        exp(g, j, 2)
                        exp(g, j, 3)
                    if live(g, j, 3):
                        act.wait_ge(ctx_turned, s + 4)
                        nc.scalar.activation(xnT[:, HI, (j + 3) % 8, 0:2 * P], ctx_ps[:, 0:2 * P], ACT.Copy).then_inc(xnT_hi, 1)
                    if live(g, j, 0):
                        act.wait_ge(turned[2], s + 1)
                        nc.scalar.activation(probT[0:TAIL0, 2, :], turn_ps[0][0:TAIL0, :], ACT.Copy).then_inc(probT_ready[2], 1)
                    ahead, hg = quarter(b)
                    if live(g, j, 4 * ahead - b):
                        act.wait_ge(q_ready, (t + ahead) * 4 + (hg + 1))
                        nc.scalar.activation(q_half(g, j, HI), q_ps[:].rearrange("p (h b l) -> p h b l", h=4, l=L),
                                             ACT.Copy).then_inc(q_hi, 1)
                    if live(g, j, 0):
                        act.wait_ge(out_ready, s + 1)
                        if b == 0:
                            wait(act, proj_ready, t)
                        nc.scalar.activation(oT[:, :, b * L:(b + 1) * L], out_ps[:].rearrange("p (h l) -> p h l", l=L),
                                             ACT.Copy).then_inc(oT_ready, 1)

                run_steps(act, step, LEAD, LAG)

            @block.tensor
            def _(pe):
                def score(g, j, grp):
                    s, n, un, bn = g * 8 + j, (j + 1) % 8, (j + 1) // 4 % 2, (j + 1) % 4
                    if grp == 0:
                        pe.wait_ge(xnT_ready, s + 2)
                        if bn == 0:
                            pe.wait_ge(keys_ready, tile_of(g, j, 1) + 1)
                            pe.wait_ge(q_copied, tile_of(g, j, 1) * 4 + 4)
                    wait(pe, masked, s * 4 + (3 + grp))
                    for p, (a, c) in enumerate(PASSES):
                        last = nc.tensor.matmul(score_ps[grp % 2][:, 0:even(KEYS0)], qT[:, a, un, bn, 4 * grp:4 * grp + 4, :],
                                                xnT[:, c, n, :], start=(p == 0), stop=(p == len(PASSES) - 1))
                    last.then_inc(scored, 1)

                def turn(g, j, kt):
                    s, m = g * 8 + j, TKEYS[kt]
                    if kt == 0:
                        pe.wait_ge(prob_ready, s + 1)
                        wait(pe, probT_ready[2], s)
                    if kt == 2:
                        wait_apart(k, pe, probT_ready[0], s + 1)
                    for grp in range(GROUPS):
                        last = nc.tensor.transpose(turn_ps[kt % 2][0:m, grp * P:(grp + 1) * P],
                                                   prob[:, j % 2, grp, kt * P:kt * P + m], k.ident[:])
                    last.then_inc(turned[kt], 1)

                def values(g, j, kt):
                    s, m = g * 8 + j, TKEYS[kt]
                    pe.wait_ge(probT_ready[kt], s + 1)
                    if kt == 0:
                        wait(pe, oT_ready, s)
                    if kt == 2 and j % 4 == 0:
                        pe.wait_ge(tail_loaded[j // 4], (g + 1) * 32)
                    lhsT = xn[:, j, kt, :] if kt < 2 else tail[:, j, :]
                    last = nc.tensor.matmul(out_ps[:], lhsT, probT[0:m, kt, :], start=(kt == 0), stop=(kt == 2))
                    if kt == 2:
                        last.then_inc(out_ready, 1)

                def query(g, j):
                    ahead, hg = quarter(j % 4)
                    t = tile_of(g, j)
                    wait(pe, q_copied, (t + ahead) * 4 + hg)
                    for h in range(4):
                        last = nc.tensor.matmul(q_ps[:, h * P:(h + 1) * P], k.A[:, 4 * hg + h, :],
                                                k.latT[:, ds((t + ahead) * P, P)], start=True, stop=True)
                    last.then_inc(q_ready, 1)

                def step(g, j):
                    s, t, u, b = g * 8 + j, tile_of(g, j), j // 4, j % 4
                    here, ahead = live(g, j, 0), live(g, j, 1)
                    if ahead:
                        score(g, j, 0)
                        score(g, j, 1)
                    if here:
                        turn(g, j, 0)
                        turn(g, j, 1)
                    if live(g, j, 3):
                        n = (j + 3) % 8
                        pe.wait_ge(xn_ready, s + 4)
                        wait(pe, xnT_ready, s + 3)
                        for kt in range(2):
                            last = nc.tensor.transpose(ctx_ps[:, kt * P:(kt + 1) * P], xn[:, n, kt, :], k.ident[:])
                        last.then_inc(ctx_turned, 1)
                    if ahead:
                        score(g, j, 2)
                        score(g, j, 3)
                    if b == 0 and live(g, j, -1):
                        pe.wait_ge(oT_ready, s)
                        wait(pe, x_added, t - 1)
                        for h in range(H):
                            last = nc.tensor.matmul(proj_ps[:, 0:D], oT[:, h, :], k.U[:, h, :], start=(h == 0),
                                                    stop=(h == H - 1))
                        last.then_inc(proj_ready, 1)
                    if here:
                        values(g, j, 0)
                        turn(g, j, 2)
                    if live(g, j, 4 * quarter(b)[0] - b):
                        query(g, j)
                    if here:
                        values(g, j, 1)
                        values(g, j, 2)

                run_steps(pe, step, LEAD, LAG)
    k.xattn0_weights.close()


def rglru0(k, io):
    nc = k.nc
    with ExitStack() as stack:
        sb = lambda name, shape: stack.enter_context(nc.sbuf_tensor(name, shape, F32))
        psum = lambda name: stack.enter_context(nc.psum_tensor(name, [P, CH], F32))
        sem = k.sem
        yT = sb("r_yT", [P, TOK])
        layer_norm_T(k, "r_ln", yT)
        gate_in, alpha = sb("r_gate_in", [P, TOK]), sb("r_alpha", [P, TOK])
        sp_ = sb("r_softplus", [P, 6])
        beta, square, drive, h = (sb(f"r_{n}", [P, 2, CH]) for n in ("beta", "square", "drive", "h"))
        in_ps, rec_ps = [psum("r_in0"), psum("r_in1")], [psum("r_rec0"), psum("r_rec1")]
        hT_ps = [psum("r_hT0"), psum("r_hT1")]
        gates_done, gates_read, chain = sem("r_gates_done"), sem("r_gates_read"), sem("r_softplus_chain")
        with nc.Block() as block:

            @block.tensor
            def _(pe):
                with pe.Fori(0, CHUNKS // 2) as g:
                    c = g * 2
                    for u in range(2):
                        pe.wait_ge(gates_read, c + (u + 1))
                        y = yT[:, ds((c + u) * CH, CH)]
                        nc.tensor.matmul(in_ps[u][:], k.w_in[:], y, start=True, stop=True)
                        nc.tensor.matmul(rec_ps[u][:], k.w_gate[:], y, start=True, stop=True).then_inc(gates_done, 1)

            @block.scalar
            def _(act):
                act.wait_ge(chain, 1)
                nc.scalar.activation(sp_[:, 1:2], sp_[:, 0:1], ACT.Exp, scale=-1.0).then_inc(chain, 1)
                act.sem_inc(gates_read, 2)

                def gates(c):
                    for u in range(2):
                        act.wait_ge(gates_done, c + (u + 1))
                        cols = ds((c + u) * CH, CH)
                        nc.scalar.activation(gate_in[:, cols], in_ps[u][:], ACT.Sigmoid, bias=k.b_in)
                        nc.scalar.activation(alpha[:, cols], rec_ps[u][:], ACT.Sigmoid, bias=k.b_gate).then_inc(gates_read, 1)

                gates(0)
                with act.Fori(1, CHUNKS // 2) as g:
                    gates(g * 2)
                act.wait_ge(gates_read, CHUNKS + 2)
                act.wait_ge(chain, 17)
                nc.scalar.activation(alpha[:], alpha[:], ACT.Exp, scale=sp_[:, 5:6]).then_inc(gates_read, 1)
                act.wait_ge(gates_read, CHUNKS + 3)

            @block.vector
            def _(dve):
                size, e, q, q2, t, rate = (sp_[:, j:j + 1] for j in range(6))
                nc.vector.scalar_tensor_tensor(size, k.lam, -1.0, k.lam, ALU.mult, ALU.max).then_inc(chain, 1)
                dve.wait_ge(chain, 2)
                nc.vector.tensor_scalar(q, e, 2.0, None, ALU.add).then_inc(chain, 1)
                dve.wait_ge(chain, 3)
                nc.vector.reciprocal(q, q).then_inc(chain, 1)
                dve.wait_ge(chain, 4)
                nc.vector.tensor_tensor(q, q, e, ALU.mult).then_inc(chain, 1)
                dve.wait_ge(chain, 5)
                nc.vector.tensor_tensor(q2, q, q, ALU.mult).then_inc(chain, 1)
                dve.wait_ge(chain, 6)
                nc.vector.tensor_scalar(t, q2, 1.0 / 17, None, ALU.mult).then_inc(chain, 1)
                for n, odd in enumerate((15, 13, 11, 9, 7, 5, 3)):
                    dve.wait_ge(chain, 7 + n)
                    nc.vector.scalar_tensor_tensor(t, t, 1.0 / odd, q2, ALU.add, ALU.mult).then_inc(chain, 1)
                dve.wait_ge(chain, 14)
                nc.vector.scalar_tensor_tensor(t, t, 1.0, q, ALU.add, ALU.mult).then_inc(chain, 1)
                nc.vector.tensor_scalar(q2, k.lam, 0.0, -8.0, ALU.max, ALU.mult).then_inc(chain, 1)
                dve.wait_ge(chain, 16)
                nc.vector.scalar_tensor_tensor(rate, t, -16.0, q2, ALU.mult, ALU.add).then_inc(chain, 1)
                dve.wait_ge(chain, 17)
        squared, rooted, beta_ready, drive_ready, cleared, scanned, turned, added = (
            sem(f"r_{n}") for n in ("squared", "rooted", "beta_ready", "drive_ready", "cleared", "scanned", "turned", "added"))
        half_driven, x_stats_ready = sem("r_half_driven"), sem("r_x_stats_ready")
        with nc.Block() as block:

            @block.gpsimd
            def _(pool):
                pool.sem_inc(rooted, 2)
                with pool.Fori(0, CHUNKS // 2) as g:
                    c = g * 2
                    for u in range(2):
                        a = alpha[:, ds((c + u) * CH, CH)]
                        pool.wait_ge(rooted, c + (u + 1))
                        nc.gpsimd.tensor_tensor(square[:, u], a, a, ALU.mult).then_inc(squared, 1)
                        pool.wait_ge(scanned, c + (u + 1))
                        nc.gpsimd.tensor_tensor(drive[:, u], gate_in[:, ds((c + u) * CH, CH)], yT[:, ds((c + u) * CH, CH)], ALU.mult)\
                            .then_inc(drive_ready, 1)

            @block.scalar
            def _(act):
                with act.Fori(0, CHUNKS // 2) as g:
                    c = g * 2
                    for u in range(2):
                        act.wait_ge(beta_ready, c + (u + 1))
                        nc.scalar.activation(beta[:, u], beta[:, u], ACT.Sqrt, bias=k.tiny[:]).then_inc(rooted, 1)

            @block.vector
            def _(dve):
                def start(g, u):
                    c = g * 2
                    dve.wait_ge(squared, c + (u + 1))
                    nc.vector.tensor_scalar(beta[:, u], square[:, u], -1.0, 1.0, ALU.mult, ALU.add).then_inc(beta_ready, 1)

                def finish(g, u):
                    c = g * 2
                    cols = ds((c + u) * CH, CH)
                    nc.vector.tensor_copy(alpha[:, ds((c + u) * CH, CH)].rearrange("p (b l) -> p b l", l=L)[:, :, 0:1],
                                          k.zero[:].unsqueeze(1).broadcast_to([P, CH // L, 1])).then_inc(cleared, 1)
                    dve.wait_ge(rooted, c + (u + 3))
                    dve.wait_ge(drive_ready, c + (u + 1))
                    nc.vector.tensor_tensor(drive[:, u], drive[:, u], beta[:, u], ALU.mult).then_inc(half_driven, 1)
                    dve.wait_ge(half_driven, c + (u + 1))
                    dve.wait_ge(cleared, c + (u + 1))
                    dve.wait_ge(turned, c + (u + 1))
                    nc.vector.tensor_tensor_scan(h[:, u], alpha[:, cols], drive[:, u], 0.0, ALU.mult, ALU.add)\
                        .then_inc(scanned, 1)

                def add(g, u):
                    c = g * 2
                    dve.wait_ge(turned, c + (u + 3))
                    xc = k.x[:, ds((c + u) * CH, CH)]
                    nc.vector.tensor_tensor(xc, hT_ps[u][:], xc, ALU.add).then_inc(added, 1)

                dve.sem_inc(added, 1)
                dve.sem_inc(scanned, 2)

                def two_chunks(g, more):
                    finish(g, 0)
                    finish(g, 1)
                    if more:
                        start(g + 1, 0)
                        start(g + 1, 1)
                    add(g, 0)
                    add(g, 1)
                    wait_apart(k, dve, added, g * 2 + 3)
                    for j in range(8):
                        last = tile_stats(k, g * 8 + j)
                    last.then_inc(x_stats_ready, 1)

                start(0, 0)
                start(0, 1)
                with dve.Fori(0, CHUNKS // 2 - 1) as g:
                    two_chunks(g, True)
                two_chunks(CHUNKS // 2 - 1, False)
                dve.wait_ge(x_stats_ready, CHUNKS // 2)

            @block.tensor
            def _(pe):
                pe.sem_inc(turned, 2)
                with pe.Fori(0, CHUNKS // 2) as g:
                    c = g * 2
                    for u in range(2):
                        pe.wait_ge(scanned, c + (u + 3))
                        pe.wait_ge(added, c + 1)
                        for j in range(4):
                            last = nc.tensor.transpose(hT_ps[u][:, j * P:(j + 1) * P], h[:, u, j * P:(j + 1) * P], k.ident[:])
                        last.then_inc(turned, 1)


def tensor_scale(k, name, stack, maxima, factor=None):
    nc = k.nc
    n = maxima.shape[1]
    q = stack.enter_context(nc.sbuf_tensor(f"{name}_scale", [P, 4, n], F32))
    chain, reduced = k.sem(f"{name}_chain"), k.sem(f"{name}_reduced")
    with nc.Block() as block:

        @block.vector
        def _(dve):
            nc.vector.tensor_reduce(q[:, 0], maxima, AX.X, ALU.max, apply_absolute_value=True).then_inc(chain, 1)
            dve.wait_ge(reduced, 1)
            scaled = 1
            if factor is not None:
                nc.vector.tensor_scalar(q[:, 1], q[:, 1], factor, None, ALU.mult).then_inc(chain, 1)
                scaled = 2
                dve.wait_ge(chain, scaled)
            nc.vector.tensor_scalar(q[:, 2], q[:, 1], 1.0 / QMAX, 1e-12, ALU.mult, ALU.max).then_inc(chain, 1)
            dve.wait_ge(chain, scaled + 1)
            nc.vector.reciprocal(q[:, 3], q[:, 2]).then_inc(chain, 1)
            dve.wait_ge(chain, scaled + 2)
            if factor is not None:
                nc.vector.tensor_scalar(q[:, 3], q[:, 3], factor, None, ALU.mult).then_inc(chain, 1)
                dve.wait_ge(chain, scaled + 3)

        @block.gpsimd
        def _(pool):
            pool.wait_ge(chain, 1)
            nc.gpsimd.partition_all_reduce(q[:, 1], q[:, 0], P, ABSMAX).then_inc(reduced, 1)
            pool.wait_ge(reduced, 1)
    return [(q[:, 2, t:t + 1], q[:, 3, t:t + 1]) for t in range(n)]


def ffn0(k, io):
    nc = k.nc
    with ExitStack() as stack:
        sb = lambda name, shape: stack.enter_context(nc.sbuf_tensor(name, shape, F32))
        sem = k.sem
        yT = sb("f_yT", [P, TOK])
        layer_norm_T(k, "f_ln", yT)
        up, gate = sb("f_up", [P, FB0, TOK]), sb("f_gate", [P, FB0, TOK])
        maxima = sb("f_max", [P, 2, CHUNKS, FB0])
        W = 2 * CH
        ITEMS = FB0 * TOK // W
        part = sb("f_part", [P, 3, W])
        gs_max, o_max = sb("f_gs_max", [P, 1, ITEMS]), sb("f_o_max", [P, 1, ITEMS])
        [(step, inv)] = tensor_scale(k, "f_y", stack, yT[:].unsqueeze(1))
        with ExitStack() as st:
            halves = lambda name, n: st.enter_context(nc.sbuf_tensor(f"f_{name}", [P, 2, n], F32R))
            y, w_up, w_gate = halves("y", TOK), halves("w_up", FF0), halves("w_gate", FF0)
            weights = ((w_up, k.f_up), (w_gate, k.f_gate))
            up_ps, gate_ps = ([st.enter_context(nc.psum_tensor(f"f_{n}{j}", [P, CH], F32)) for j in range(FB0)] for n in ("up", "gate"))
            scaled, y_ready, y_hi, y_lo, w_hi, w_lo = (sem(f"f_{n}") for n in ("y_scaled", "y_ready", "y_hi", "y_lo", "w_hi", "w_lo"))
            done = {"up": sem("f_up_done"), "gate": sem("f_gate_done")}
            copied = {"up": sem("f_up_copied"), "gate": sem("f_gate_copied")}
            maxed = {"up": sem("f_up_maxed"), "gate": sem("f_gate_maxed")}
            sides = (("up", up, up_ps, w_up), ("gate", gate, gate_ps, w_gate))
            with nc.Block() as block:

                @block.scalar
                def _(act):
                    def scale(c):
                        cols = ds(c * CH, CH)
                        nc.scalar.activation(yT[:, cols], yT[:, cols], ACT.Identity, bias=k.rne[:], scale=inv).then_inc(scaled, 1)

                    scale(0)
                    for w, whole in weights:
                        nc.scalar.activation(w[:, HI], whole[:], ACT.Copy).then_inc(w_hi, 1)
                    scale(1)
                    act.sem_inc(copied["gate"], FB0)
                    act.sem_inc(copied["up"], FB0)

                    def upper_half(c):
                        wait_apart(k, act, y_ready, c + 1)
                        nc.scalar.activation(y[:, HI, ds(c * CH, CH)], yT[:, ds(c * CH, CH)], ACT.Copy).then_inc(y_hi, 1)

                    def chunk(c, more):
                        if more:
                            upper_half(c + 1)
                        for n, t, ps, w in sides:
                            for j in range(FB0):
                                act.wait_ge(done[n], c * FB0 + (j + 1))
                                nc.scalar.activation(t[:, j, ds(c * CH, CH)], ps[j][:], ACT.Copy).then_inc(copied[n], 1)

                    upper_half(0)
                    with act.Fori(2, CHUNKS) as c:
                        scale(c)
                    with act.Fori(0, CHUNKS - 1) as c:
                        chunk(c, True)
                    chunk(CHUNKS - 1, False)
                    act.wait_ge(copied["gate"], FB0 * CHUNKS + FB0)
                    act.wait_ge(copied["up"], FB0 * CHUNKS + FB0)

                @block.vector
                def _(dve):
                    def quantise(c):
                        cols = ds(c * CH, CH)
                        dve.wait_ge(scaled, c + 1)
                        nc.vector.tensor_scalar(yT[:, cols], yT[:, cols], -RNE, step, ALU.add, ALU.mult).then_inc(y_ready, 1)

                    def chunk(c, more):
                        if more:
                            quantise(c + 2)
                        for i, (n, t, ps, w) in enumerate(sides):
                            dve.wait_ge(copied[n], c * FB0 + 2 * FB0)
                            nc.vector.tensor_reduce(maxima[:, i, ds(c, 1), :], t[:, :, ds(c * CH, CH)], AX.X, ALU.max,
                                                    apply_absolute_value=True).then_inc(maxed[n], 1)

                    quantise(0)
                    for n, (w, whole) in enumerate(weights):
                        dve.wait_ge(w_hi, n + 1)
                        nc.vector.tensor_tensor(w[:, LO], whole[:], w[:, HI], ALU.subtract).then_inc(w_lo, 1)
                    quantise(1)
                    with dve.Fori(0, CHUNKS - 2) as c:
                        chunk(c, True)
                    for c in range(CHUNKS - 2, CHUNKS):
                        chunk(c, False)
                    dve.wait_ge(maxed["gate"], CHUNKS)
                    dve.wait_ge(maxed["up"], CHUNKS)

                @block.gpsimd
                def _(pool):
                    with pool.Fori(0, CHUNKS) as c:
                        cols = ds(c * CH, CH)
                        wait_apart(k, pool, y_hi, c + 1)
                        nc.gpsimd.tensor_tensor(y[:, LO, cols], yT[:, cols], y[:, HI, cols], ALU.subtract).then_inc(y_lo, 1)

                @block.tensor
                def _(pe):
                    pe.wait_ge(w_lo, 2)
                    with pe.Fori(0, CHUNKS) as c:
                        pe.wait_ge(y_lo, c + 1)
                        for n, t, ps, w in sides:
                            for j in range(FB0):
                                pe.wait_ge(copied[n], c * FB0 + (j + 1))
                                for p, (a, b) in enumerate(PASSES):
                                    last = nc.tensor.matmul(ps[j][:], w[:, a, j * P:(j + 1) * P], y[:, b, ds(c * CH, CH)],
                                                            start=(p == 0), stop=(p == len(PASSES) - 1))
                                last.then_inc(done[n], 1)
        (up_step, up_inv), (gate_step, gate_inv) = tensor_scale(k, "f_ug", stack, maxima[:].rearrange("p t c j -> p t (c j)"))
        all_gate, all_up = (t[:].rearrange("p j n -> p (j n)") for t in (gate, up))
        item = lambda a, n: a[:, ds(n * W, W)]
        g_scaled, g_ready, sig_ready, sig_rounded, gs_ready, maxed = (
            sem(f"f_{n}") for n in ("g_scaled", "g_ready", "sig_ready", "sig_rounded", "gs_ready", "gs_maxed"))
        SIG = 192.0
        SIG_MAX = SIG + 65535.0 / 65536
        with nc.Block() as block:

            @block.scalar
            def _(act):
                def step(n, u):
                    static = isinstance(n, int)
                    if not static or n + 2 < ITEMS:
                        nc.scalar.activation(item(all_gate, n + 2), item(all_gate, n + 2), ACT.Identity, bias=k.rne[:], scale=gate_inv)\
                            .then_inc(g_scaled, 1)
                    if not static or n >= 0:
                        if not static or n >= 3:
                            act.wait_ge(gs_ready, n - 2)
                        wait_apart(k, act, g_ready, n + 1)
                        nc.scalar.activation(part[:, u, :], item(all_gate, n), ACT.Sigmoid, scale=gate_step).then_inc(sig_ready, 1)

                for n in range(-2, 3):
                    step(n, n % 3)
                with act.Fori(1, ITEMS // 3 - 1) as g:
                    for u in range(3):
                        step(g * 3 + u, u)
                for n in range(ITEMS - 3, ITEMS):
                    step(n, n % 3)

            @block.gpsimd
            def _(pool):
                with pool.Fori(0, ITEMS) as n:
                    wait_apart(k, pool, g_scaled, n + 1)
                    nc.gpsimd.tensor_tensor(item(all_gate, n), item(all_gate, n), k.minus_rne[:].broadcast_to([P, W]), ALU.add)\
                        .then_inc(g_ready, 1)

            @block.vector
            def _(dve):
                def step(n, u):
                    static = isinstance(n, int)
                    if not static or n + 1 < ITEMS:
                        sig = part[:, (u + 1) % 3, :]
                        dve.wait_ge(sig_ready, n + 2)
                        nc.vector.tensor_scalar(sig, sig, SIG, SIG_MAX, ALU.add, ALU.min).then_inc(sig_rounded, 1)
                    if not static or 0 <= n < ITEMS:
                        dve.wait_ge(sig_rounded, n + 1)
                        dve.wait_ge(g_ready, n + 1)
                        nc.vector.scalar_tensor_tensor(item(all_gate, n), part[:, u, :], -SIG, item(all_gate, n), ALU.add, ALU.mult)\
                            .then_inc(gs_ready, 1)
                    if not static or n >= 1:
                        dve.wait_ge(gs_ready, n)
                        nc.vector.tensor_reduce(gs_max[:, 0, ds(n - 1, 1)], item(all_gate, n - 1), AX.X, ALU.max,
                                                apply_absolute_value=True).then_inc(maxed, 1)

                for n in range(-1, 3):
                    step(n, n % 3)
                with dve.Fori(1, ITEMS // 3 - 1) as g:
                    for u in range(3):
                        step(g * 3 + u, u)
                for n in range(ITEMS - 3, ITEMS + 1):
                    step(n, n % 3)
                dve.wait_ge(maxed, ITEMS)
        [(gs_step, gs_inv)] = tensor_scale(k, "f_gs", stack, gs_max[:], gate_step)
        up_scaled, up_ready, gs_scaled, o_ready, o_maxed = (
            sem(f"f_{n}") for n in ("u_scaled", "u_ready", "gs_scaled", "o_ready", "o_maxed"))
        product = stack.enter_context(nc.sbuf_tensor("f_product_step", [P, 1], F32))
        with nc.Block() as block:

            @block.scalar
            def _(act):
                with act.Fori(0, ITEMS // 2) as g:
                    for u in range(2):
                        n = g * 2 + u
                        nc.scalar.activation(item(all_up, n), item(all_up, n), ACT.Identity, bias=k.rne[:], scale=up_inv).then_inc(up_scaled, 1)
                        nc.scalar.activation(item(all_gate, n), item(all_gate, n), ACT.Identity, bias=k.rne[:], scale=gs_inv)\
                            .then_inc(gs_scaled, 1)

            @block.gpsimd
            def _(pool):
                with pool.Fori(0, ITEMS // 2) as g:
                    for u in range(2):
                        n = g * 2 + u
                        wait_apart(k, pool, up_scaled, n + 1)
                        nc.gpsimd.tensor_tensor(item(all_up, n), item(all_up, n), k.minus_rne[:].broadcast_to([P, W]), ALU.add)\
                            .then_inc(up_ready, 1)

            @block.vector
            def _(dve):
                def multiply(n):
                    dve.wait_ge(gs_scaled, n + 1)
                    dve.wait_ge(up_ready, n + 1)
                    nc.vector.scalar_tensor_tensor(item(all_up, n), item(all_gate, n), -RNE, item(all_up, n), ALU.add, ALU.mult)\
                        .then_inc(o_ready, 1)

                def maximum(n):
                    dve.wait_ge(o_ready, n + 1)
                    nc.vector.tensor_reduce(o_max[:, 0, ds(n, 1)], item(all_up, n), AX.X, ALU.max, apply_absolute_value=True)\
                        .then_inc(o_maxed, 1)

                nc.vector.tensor_tensor(product[:], gs_step, up_step, ALU.mult)
                multiply(0)
                with dve.Fori(0, ITEMS // 2 - 1) as g:
                    for u in range(2):
                        multiply(g * 2 + (u + 1))
                        maximum(g * 2 + u)
                multiply(ITEMS - 1)
                maximum(ITEMS - 2)
                maximum(ITEMS - 1)
                dve.wait_ge(o_maxed, ITEMS)
        [(o_step, o_inv)] = tensor_scale(k, "f_o", stack, o_max[:], product[:])
        down_ps, turn_ps = ([stack.enter_context(nc.psum_tensor(f"f_{n}{u}", [P, CH], F32)) for u in range(2)] for n in ("down", "turn"))
        x_stats_ready, o_scaled, o_quantised, down_done, down_copied, turned, added = (
            sem(f"f_{n}") for n in ("x_stats_ready", "o_scaled", "o_quantised", "down_done", "down_copied", "turned", "added"))
        with nc.Block() as block:

            @block.scalar
            def _(act):
                def scale_o(c):
                    o = up[:, :, ds(c * CH, CH)]
                    nc.scalar.activation(o, o, ACT.Identity, bias=k.rne[:], scale=o_inv).then_inc(o_scaled, 1)

                def two_chunks(c, more):
                    for u in range(2):
                        if more:
                            scale_o(c + (2 + u))
                        act.wait_ge(down_done, c + (u + 1))
                        act.wait_ge(turned, c + (u + 1))
                        nc.scalar.activation(part[:, u, 0:CH], down_ps[u][:], ACT.Copy).then_inc(down_copied, 1)

                scale_o(0)
                scale_o(1)
                act.sem_inc(down_copied, 1)
                act.sem_inc(turned, 2)
                with act.Fori(0, CHUNKS // 2 - 1) as g:
                    two_chunks(g * 2, True)
                two_chunks(CHUNKS - 2, False)

            @block.vector
            def _(dve):
                def quantise(c):
                    o = up[:, :, ds(c * CH, CH)]
                    dve.wait_ge(o_scaled, c + 1)
                    nc.vector.tensor_scalar(o, o, -RNE, o_step, ALU.add, ALU.mult).then_inc(o_quantised, 1)

                def two_chunks(c, more):
                    for u in range(2):
                        if more:
                            quantise(c + (2 + u))
                        dve.wait_ge(turned, c + (u + 3))
                        xc = k.x[:, ds((c + u) * CH, CH)]
                        nc.vector.tensor_tensor(xc, turn_ps[u][:], xc, ALU.add).then_inc(added, 1)
                    wait_apart(k, dve, added, c + 3)
                    for j in range(8):
                        last = tile_stats(k, c * 4 + j)
                    last.then_inc(x_stats_ready, 1)

                dve.sem_inc(added, 1)
                quantise(0)
                quantise(1)
                with dve.Fori(0, CHUNKS // 2 - 1) as g:
                    two_chunks(g * 2, True)
                two_chunks(CHUNKS - 2, False)
                dve.wait_ge(x_stats_ready, CHUNKS // 2)

            @block.tensor
            def _(pe):
                def down(c, u):
                    pe.wait_ge(o_quantised, c + (u + 1))
                    pe.wait_ge(down_copied, c + 1)
                    for j in range(FB0):
                        last = nc.tensor.matmul(down_ps[u][:], k.f_down[:, j, :], up[:, j, ds((c + u) * CH, CH)],
                                                start=(j == 0), stop=(j == FB0 - 1))
                    last.then_inc(down_done, 1)

                with pe.Fori(0, CHUNKS // 2) as g:
                    c = g * 2
                    down(c, 0)
                    down(c, 1)
                    for u in range(2):
                        pe.wait_ge(down_copied, c + (u + 2))
                        pe.wait_ge(added, c + 1)
                        for j in range(4):
                            last = nc.tensor.transpose(turn_ps[u][:, j * P:(j + 1) * P], part[:, u, j * P:(j + 1) * P], k.ident[:])
                        last.then_inc(turned, 1)


def xattn1(k, io):
    nc = k.nc
    sem = k.sem
    with ExitStack() as stack:
        sb = lambda name, shape, dt=F32: stack.enter_context(nc.sbuf_tensor(name, shape, dt))
        q_all = sb("b_q", [P, 2, TOK], F32R)
        tailT = sb("b_tailT", [P, B])
        with ExitStack() as st:
            yT = st.enter_context(nc.sbuf_tensor("b_yT", [P, TOK], F32))
            layer_norm_T(k, "b_ln", yT)
            tail, v_tail = (st.enter_context(nc.sbuf_tensor(n, [B, D], F32)) for n in ("b_tail", "b_v_tail"))
            q_ps = [st.enter_context(nc.psum_tensor(f"b_q_ps{u}", [P, CH], F32)) for u in range(2)]
            tail_ps, v_ps = (st.enter_context(nc.psum_tensor(n, [P, P], F32)) for n in ("b_tail_ps", "b_v_tail_ps"))
            projected, copied, split, tail_loaded, tail_turned, tail_ready, v_done, v_copied, v_stored = (
                sem(f"b_pre_{n}") for n in ("projected", "copied", "split", "tail_loaded", "tail_turned", "tail_ready", "v_done",
                                            "v_copied", "v_stored"))
            with nc.Block() as block:

                @block.sync
                def _(sp):
                    sp.dma_start(tail[:], io["ctx_1024"][:, N_CTX - 1, :]).then_inc(tail_loaded, 16)
                    sp.wait_ge(v_copied, 1)
                    sp.dma_start(k.v_tail_dram, v_tail[:]).then_inc(v_stored, 16)
                    sp.wait_ge(v_stored, 16)

                @block.tensor
                def _(pe):
                    def queries(c):
                        for u in range(2):
                            pe.wait_ge(copied, c + (u + 1))
                            nc.tensor.matmul(q_ps[u][:], k.wq1[:], yT[:, ds((c + u) * CH, CH)], start=True, stop=True)\
                                .then_inc(projected, 1)

                    queries(0)
                    queries(2)
                    pe.wait_ge(tail_loaded, 16)
                    nc.tensor.transpose(tail_ps[:], tail[:], k.ident[:]).then_inc(tail_turned, 1)
                    pe.wait_ge(tail_ready, 1)
                    nc.tensor.matmul(v_ps[:], tailT[:], k.wv1[:], start=True, stop=True).then_inc(v_done, 1)
                    with pe.Fori(2, CHUNKS // 2) as g:
                        queries(g * 2)

                @block.scalar
                def _(act):
                    act.sem_inc(copied, 2)
                    with act.Fori(0, CHUNKS // 2) as g:
                        c = g * 2
                        for u in range(2):
                            act.wait_ge(projected, c + (u + 1))
                            cols = ds((c + u) * CH, CH)
                            for target in (q_all[:, HI, cols], yT[:, cols]):
                                last = nc.scalar.activation(target, q_ps[u][:], ACT.Identity, bias=k.bq1)
                            last.then_inc(copied, 1)
                    act.wait_ge(copied, CHUNKS + 2)

                @block.vector
                def _(dve):
                    dve.wait_ge(tail_turned, 1)
                    nc.vector.tensor_copy(tailT[:], tail_ps[:]).then_inc(tail_ready, 1)
                    dve.wait_ge(v_done, 1)
                    nc.vector.tensor_copy(v_tail[:], v_ps[:]).then_inc(v_copied, 1)
                    for c in range(0, CHUNKS, 2):
                        cols = slice(c * CH, (c + 2) * CH)
                        dve.wait_ge(copied, c + 4)
                        nc.vector.tensor_tensor(q_all[:, LO, cols], yT[:, cols], q_all[:, HI, cols], ALU.subtract).then_inc(split, 1)
                    dve.wait_ge(split, CHUNKS // 2)

        raw = sb("b_raw", [P, 8, 2, D])
        ctxT = sb("b_ctxT", [P, 8, N_CTX])
        kept = sb("b_kept", [P, 2, BPT, N_CTX], BF16)
        bias = sb("b_bias", [P, 8, N_CTX])
        v_row = sb("b_v_row", [GROUPS, 2, BPT, D])
        v_last = sb("b_v_last", [GROUPS, 8, D])
        qbd = sb("b_qbd", [P, 2, 4, H, L], F32R)
        k_whole = sb("b_k_whole", [P, 2, N_CTX])
        kT = sb("b_kT", [P, 2, 4, even(N_CTX)], F32R)
        v = sb("b_v", [P, 4, 2, D])
        neg = sb("b_neg", [P, GROUPS, N_CTX])
        nmax = sb("b_nmax", [P, 2, GROUPS])
        prob = sb("b_prob", [P, 2, GROUPS, N_CTX])
        rsum, rinv = sb("b_rsum", [P, 2, GROUPS]), sb("b_rinv", [P, 2, GROUPS])
        probT, lastT = sb("b_probT", [P, 2, CH]), sb("b_lastT", [GROUPS, P])
        weight = sb("b_weight", [P, 2, D])
        weightT = sb("b_weightT", [P, P])
        own = sb("b_own", [P, BPT, HG, L])
        oT_sum, oT = sb("b_oT_sum", [P, P]), sb("b_oT", [P, P])
        psum = lambda name: stack.enter_context(nc.psum_tensor(name, [P, CH], F32))
        score_ps, turn_ps = [psum("b_score0"), psum("b_score1")], [psum("b_turn0"), psum("b_turn1")]
        out_ps, ctx_ps, k_ps, v_ps = psum("b_out"), psum("b_ctx"), psum("b_k"), psum("b_v_ps")
        weight_ps, last_ps, proj_ps = ctx_ps[:, 2 * P:3 * P], ctx_ps[0:GROUPS, 3 * P:4 * P], out_ps[:, P:2 * P]
        raw_loaded = [sem(f"b_raw_loaded{j}") for j in range(8)]
        kept_loaded, v_row_loaded = ([sem(f"b_{n}_loaded{u}") for u in range(2)] for n in ("kept", "v_row"))
        ctx_turned, ctxT_ready, keys_ready, q_ready = sem("b_ctx_turned"), sem("b_ctxT_ready"), sem("b_tile_keys_ready"), sem("b_q_ready")
        k_done, k_taken, k_hi, k_ready, v_done, v_ready = (sem(f"b_{n}") for n in ("k_done", "k_taken", "k_hi", "k_ready", "v_done", "v_ready"))
        scored, masked, exped, rinv_ready = (sem(f"b_{n}") for n in ("scored", "masked", "exped", "rinv_ready"))
        turned, probT_ready = [sem(f"b_turned{n}") for n in range(3)], [sem(f"b_probT_ready{n}") for n in range(3)]
        out_ready, weight_ready, weight_turned, weightT_ready, own_ready, sum_ready, oT_ready, proj_ready, x_added = (
            sem(f"b_{n}") for n in ("out_ready", "weight_ready", "weight_turned", "weightT_ready", "own_ready", "sum_ready", "oT_ready",
                                    "proj_ready", "x_added"))
        x_stats_ready, biased = sem("b_x_stats_ready"), sem("b_biased")
        LEAD, LAG = 5, 1

        def tile_of(g, j, ahead=0):
            return g * 2 + (j + ahead) // 4

        with nc.Block() as block:

            @block.sync
            def _(sp):
                def load_raw(g, j):
                    sp.dma_start(raw[:, j % 8], io["ctx_1024"][ds(g * 8 + j, 1), 0:2 * P, :].rearrange(
                        "b (t p) d -> p (b t) d", p=P)).then_inc(raw_loaded[j % 8], 16)

                def load_rows(t, u):
                    batches = ds(t * BPT, BPT)
                    sp.dma_start(kept[:, u], k.keep1[batches, :].unsqueeze(0).broadcast_to([P, BPT, N_CTX])).then_inc(kept_loaded[u], 16)
                    sp.dma_start(v_row[:, u], k.v_tail_dram[batches, :].unsqueeze(0).broadcast_to([GROUPS, BPT, D]))\
                        .then_inc(v_row_loaded[u], 16)

                def step(g, j):
                    s, t, u, b = g * 8 + j, tile_of(g, j), j // 4, j % 4
                    if live(g, j, 8):
                        wait(sp, ctx_turned, s + 1)
                        load_raw(g + 1, j)
                    if b == 1 and live(g, j, 8):
                        wait(sp, k_taken, s + 3)
                        wait(sp, keys_ready, t + 1)
                        load_rows(t + 2, u)

                load_rows(0, 0)
                for j in range(3):
                    load_raw(0, j)
                run_steps(sp, step, LEAD)

            @block.gpsimd
            def _(pool):
                def step(g, j):
                    s, t, u, b = g * 8 + j, tile_of(g, j), j // 4, j % 4
                    if b == 2 and live(g, j, 0):
                        xt = k.x[:, ds(t * D, D)]
                        nc.gpsimd.tensor_tensor(xt, xt, k.bo[:], ALU.add).then_inc(biased, 1)
                    if live(g, j, 3):
                        wait(pool, scored, s * 4)
                        for half in (HI, LO):
                            last = nc.gpsimd.tensor_tensor(
                                qbd[:, half, (j + 3) % 4], q_all[:, half, ds((s + 3) * L, L)].unsqueeze(1).broadcast_to([P, H, L]),
                                k.head_of_feature[:].unsqueeze(2).broadcast_to([P, H, L]), ALU.mult)
                        last.then_inc(q_ready, 1)
                    if live(g, j, 3):
                        n = (j + 3) % 4
                        pool.wait_ge(k_hi, s + 4)
                        nc.gpsimd.tensor_tensor(kT[:, LO, n, 0:N_CTX], k_whole[:, n % 2, :], kT[:, HI, n, 0:N_CTX], ALU.subtract).then_inc(k_ready, 1)
                    if live(g, j, 1):
                        par = (j + 1) % 2
                        pool.wait_ge(rinv_ready, s + 2)
                        wait(pool, weight_turned, s)
                        nc.gpsimd.tensor_tensor(weight[:, par].rearrange("p (g f) -> p g f", g=GROUPS),
                                                k.own_value[:].rearrange("p (g f) -> p g f", g=GROUPS),
                                                rinv[:, par, :].unsqueeze(2).broadcast_to([P, GROUPS, L]), ALU.mult).then_inc(weight_ready, 1)
                    if b == 3 and live(g, j, 8):
                        slots = slice(4 * u, 4 * u + 4)
                        wait(pool, out_ready, s + 1)
                        nc.gpsimd.tensor_copy(ctxT[:, slots, N_CTX - 1:N_CTX], tailT[:, ds((t + 2) * BPT, BPT)].unsqueeze(2))
                        pool.wait_ge(v_row_loaded[u], (g + 2) * 16)
                        nc.gpsimd.tensor_tensor(v_last[:, slots, :], v_row[:, u],
                                                k.group_of_feature[:].unsqueeze(1).broadcast_to([GROUPS, BPT, D]), ALU.mult)
                        wait_apart(k, pool, kept_loaded[u], (g + 2) * 16)
                        nc.gpsimd.tensor_scalar(bias[:, slots, :], kept[:, u], NEG1, -NEG1, ALU.mult, ALU.add).then_inc(keys_ready, 1)

                for half in (HI, LO):
                    nc.gpsimd.tensor_copy(kT[:, half, :, N_CTX:], k.zero[:].unsqueeze(1).broadcast_to([P, 4, even(N_CTX) - N_CTX]))
                run_steps(pool, step, LEAD)

            @block.vector
            def _(dve):
                def mask(g, j, grp):
                    s, n, par = g * 8 + j, (j + 1) % 8, (j + 1) % 2
                    if n % 4 == 0 and grp == 0:
                        dve.wait_ge(keys_ready, tile_of(g, j, 1) + 1)
                    wait_apart(k, dve, scored, s * 4 + (5 + grp))
                    nc.vector.tensor_tensor_reduce(
                        out=neg[:, grp, :], in0=score_ps[grp % 2][:, 0:N_CTX], in1=bias[:, n, :], scale=-DH1 ** -0.5,
                        scalar=3.4e38, op0=ALU.add, op1=ALU.min, accum_out=nmax[:, par, grp:grp + 1]).then_inc(masked, 1)

                def step(g, j):
                    s, t, u, b = g * 8 + j, tile_of(g, j), j // 4, j % 4
                    if live(g, j, 1):
                        mask(g, j, 0)
                        mask(g, j, 1)
                    if live(g, j, 0):
                        dve.wait_ge(turned[0], s + 1)
                        nc.vector.tensor_copy(probT[:, 0, :], turn_ps[0][:]).then_inc(probT_ready[0], 1)
                    if live(g, j, 1):
                        mask(g, j, 2)
                        mask(g, j, 3)
                    if live(g, j, 3):
                        dve.wait_ge(k_done, s + 4)
                        dve.wait_ge(kept_loaded[(j + 3) // 4 % 2], (g + (j + 3) // 8 + 1) * 16)
                        wait(dve, k_ready, s + 2)
                        nc.vector.scalar_tensor_tensor(k_whole[:, (j + 3) % 2, :], k_ps[:, 0:N_CTX], k.bk1,
                                                       kept[:, (j + 3) // 4 % 2, (j + 3) % 4, :], ALU.add, ALU.mult).then_inc(k_taken, 1)
                    if live(g, j, 0):
                        dve.wait_ge(out_ready, s + 1)
                        dve.wait_ge(weightT_ready, s + 1)
                        nc.vector.tensor_tensor(own[:, b].rearrange("p h l -> p (h l)"), out_ps[:, 0:P], weightT[:], ALU.mult)\
                            .then_inc(own_ready, 1)
                    if live(g, j, 1):
                        par = (j + 1) % 2
                        dve.wait_ge(exped, s * 4 + 8)
                        wait(dve, weight_ready, s)
                        nc.vector.reciprocal(rinv[:, par, :], rsum[:, par, :]).then_inc(rinv_ready, 1)
                    if live(g, j, 4):
                        dve.wait_ge(ctx_turned, s + 5)
                        nc.vector.tensor_copy(ctxT[:, (j + 4) % 8, 0:2 * P], ctx_ps[:, 0:2 * P]).then_inc(ctxT_ready, 1)
                    if b == 0 and live(g, j, -1):
                        dve.wait_ge(biased, t)
                        dve.wait_ge(proj_ready, t)
                        xt = k.x[:, ds((t - 1) * D, D)]
                        nc.vector.tensor_tensor(xt, proj_ps, xt, ALU.add).then_inc(x_added, 1)
                        wait_apart(k, dve, x_added, t)
                        tile_stats(k, t - 1).then_inc(x_stats_ready, 1)
                    if b == 3 and live(g, j, 0):
                        dve.wait_ge(own_ready, s + 1)
                        nc.vector.tensor_reduce(oT_sum[:], own[:].rearrange("p b h l -> p b l h"), AX.X, ALU.add).then_inc(sum_ready, 1)

                run_steps(dve, step, LEAD, LAG)
                dve.wait_ge(x_stats_ready, TILES)

            @block.scalar
            def _(act):
                def exp(g, j, grp):
                    s, par = g * 8 + j, (j + 1) % 2
                    act.wait_ge(masked, s * 4 + (5 + grp))
                    nc.scalar.activation(prob[:, par, grp, :], neg[:, grp, :], ACT.Exp, bias=nmax[:, par, grp:grp + 1],
                                         scale=-1.0, accum_out=rsum[:, par, grp:grp + 1]).then_inc(exped, 1)

                def step(g, j):
                    s, t, u, b = g * 8 + j, tile_of(g, j), j // 4, j % 4
                    if live(g, j, 1):
                        exp(g, j, 0)
                        exp(g, j, 1)
                    if b == 0 and live(g, j, -1):
                        act.wait_ge(sum_ready, t)
                        nc.scalar.activation(oT[:], oT_sum[:], ACT.Identity, bias=k.bv1).then_inc(oT_ready, 1)
                    if live(g, j, 0):
                        act.wait_ge(turned[1], s + 1)
                        nc.scalar.activation(probT[:, 1, :], turn_ps[1][:], ACT.Copy).then_inc(probT_ready[1], 1)
                        act.wait_ge(weight_turned, s + 1)
                        wait(act, own_ready, s)
                        nc.scalar.activation(weightT[:], weight_ps, ACT.Copy).then_inc(weightT_ready, 1)
                        nc.scalar.activation(lastT[:], last_ps, ACT.Copy).then_inc(probT_ready[2], 1)
                    if live(g, j, 1):
                        exp(g, j, 2)
                        exp(g, j, 3)
                    if live(g, j, 3):
                        act.wait_ge(v_done, s + 4)
                        nc.scalar.activation(v[:, (j + 3) % 4], v_ps[:, 0:2 * P].rearrange("p (t d) -> p t d", d=D), ACT.Copy)\
                            .then_inc(v_ready, 1)
                        n = (j + 3) % 4
                        act.wait_ge(k_taken, s + 4)
                        nc.scalar.activation(kT[:, HI, n, 0:N_CTX], k_whole[:, n % 2, :], ACT.Copy).then_inc(k_hi, 1)

                run_steps(act, step, LEAD, LAG)

            @block.tensor
            def _(pe):
                def score(g, j, grp):
                    s, n = g * 8 + j, (j + 1) % 4
                    if grp == 0:
                        pe.wait_ge(k_ready, s + 2)
                        pe.wait_ge(q_ready, s + 2)
                    wait(pe, masked, s * 4 + (3 + grp))
                    for p, (a, c) in enumerate(PASSES):
                        last = nc.tensor.matmul(score_ps[grp % 2][:, 0:even(N_CTX)], qbd[:, a, n, 4 * grp:4 * grp + 4, :], kT[:, c, n, :],
                                                start=(p == 0), stop=(p == len(PASSES) - 1))
                    last.then_inc(scored, 1)

                def turn(g, j, kt):
                    s = g * 8 + j
                    if kt == 0:
                        pe.wait_ge(exped, s * 4 + 4)
                    if kt < 2:
                        for grp in range(GROUPS):
                            last = nc.tensor.transpose(turn_ps[kt][:, grp * P:(grp + 1) * P],
                                                       prob[:, j % 2, grp, kt * P:(kt + 1) * P], k.ident[:])
                    else:
                        last = nc.tensor.transpose(last_ps, prob[:, j % 2, :, N_CTX - 1], k.ident[:])
                    last.then_inc(turned[kt], 1)

                def values(g, j, kt):
                    s, b = g * 8 + j, j % 4
                    pe.wait_ge(probT_ready[kt], s + 1)
                    if kt == 0:
                        pe.wait_ge(v_ready, s + 1)
                        wait(pe, own_ready, s)
                        if b == 1 and live(g, j, -4):
                            pe.wait_ge(x_added, tile_of(g, j))
                    if kt < 2:
                        for grp in range(GROUPS):
                            rows = slice(grp * 32, grp * 32 + 32)
                            nc.tensor.matmul(out_ps[rows, 0:P], v[:, j % 4, kt, rows], probT[:, kt, grp * P:(grp + 1) * P],
                                             start=(kt == 0), stop=False, skip_group_check=True)
                    else:
                        nc.tensor.matmul(out_ps[:, 0:P], v_last[:, j, :], lastT[:], start=False, stop=True,
                                         skip_group_check=True).then_inc(out_ready, 1)

                def step(g, j):
                    s, t, u, b = g * 8 + j, tile_of(g, j), j // 4, j % 4
                    here, ahead = live(g, j, 0), live(g, j, 1)
                    if ahead:
                        score(g, j, 0)
                        score(g, j, 1)
                    if here:
                        turn(g, j, 0)
                        turn(g, j, 1)
                    if here:
                        pe.wait_ge(ctxT_ready, s + 4 if live(g, j, 3) else B)
                        turn(g, j, 2)
                        pe.wait_ge(weight_ready, s + 1)
                        nc.tensor.transpose(weight_ps, weight[:, j % 2], k.ident[:]).then_inc(weight_turned, 1)
                    if ahead:
                        score(g, j, 2)
                        score(g, j, 3)
                    if live(g, j, 3):
                        n = (j + 3) % 8
                        pe.wait_ge(ctxT_ready, s + 4)
                        if n % 4 == 0:
                            pe.wait_ge(keys_ready, tile_of(g, j, 3) + 1)
                        wait(pe, k_taken, s + 3)
                        nc.tensor.matmul(k_ps[:, 0:N_CTX], k.wk1[:], ctxT[:, n, :], start=True, stop=True).then_inc(k_done, 1)
                    if here:
                        values(g, j, 0)
                    if live(g, j, 3):
                        n = (j + 3) % 8
                        wait(pe, v_ready, s + 3)
                        for kt in range(2):
                            last = nc.tensor.matmul(v_ps[:, kt * D:(kt + 1) * D], ctxT[:, n, kt * P:(kt + 1) * P], k.wv1[:],
                                                    start=True, stop=True)
                        last.then_inc(v_done, 1)
                    if here:
                        values(g, j, 1)
                    if b == 0 and live(g, j, -1):
                        pe.wait_ge(oT_ready, t)
                        nc.tensor.matmul(proj_ps, oT[:], k.wo1[:], start=not here, stop=True, skip_group_check=True).then_inc(proj_ready, 1)
                    if here:
                        values(g, j, 2)
                    if live(g, j, 4):
                        n = (j + 4) % 8
                        pe.wait_ge(raw_loaded[n], (g + (j + 4) // 8 + 1) * 16)
                        wait(pe, ctxT_ready, s + 4)
                        if here:
                            pe.wait_ge(weightT_ready, s + 1)
                        for kt in range(2):
                            last = nc.tensor.transpose(ctx_ps[:, kt * P:(kt + 1) * P], raw[:, n, kt, :], k.ident[:])
                        last.then_inc(ctx_turned, 1)

                run_steps(pe, step, LEAD, LAG)


def run_tiles(eng, step, lead, lag):
    for t in range(-lead, 4):
        step(t // 4, t % 4)
    with eng.Fori(1, TILES // 4 - 2) as g:
        for u in range(4):
            step(g, u)
    for t in range(TILES - 8, TILES + lag):
        step(t // 4, t % 4)


def live_tile(g, u, ahead):
    return not isinstance(g, int) or 0 <= 4 * g + u + ahead < TILES


def attn1(k, io):
    nc = k.nc
    sem = k.sem
    POOL_HEADS = 12
    with ExitStack() as stack:
        sb = lambda name, shape, dt=F32: stack.enter_context(nc.sbuf_tensor(name, shape, dt))
        psum = lambda name: stack.enter_context(nc.psum_tensor(name, [P, CH], F32))
        mean, rstd = ln_stats(k, stack, "s_ln")
        z, y = sb("s_z", [P, 2, D]), sb("s_y", [P, 4, BPT, HG, L])
        q, keys = sb("s_q", [P, 2, P]), sb("s_keys", [P, 2, P])
        spread = sb("s_spread", [P, 2, BPT, H, L])
        v = sb("s_v", [P, 4, BPT, D])
        shifted, expd = sb("s_shifted", [P, 2, H, L]), sb("s_expd", [P, 2, H, L])
        rmax, rsum, rinv = sb("s_rmax", [P, H]), sb("s_rsum", [P, H]), sb("s_rinv", [P, 2, H])
        probT, out, oT = sb("s_probT", [P, GROUPS, P]), sb("s_out", [P, 2, D]), sb("s_oT", [P, P])
        query_row, mask_row = sb("s_query_row", [L, P], BF16), sb("s_mask_row", [L, H, L], BF16)
        y_ps, qk_ps, v_ps, turn_ps, out_ps, proj_ps = (psum(f"s_{n}_ps") for n in ("y", "qk", "v", "turn", "out", "proj"))
        score_ps = [psum("s_score0"), psum("s_score1")]
        rows_ready, z_ready, y_turned, y_ready, qk_done, q_ready, keys_ready, spread_pool, spread_act, v_done, v_ready, biased = (
            sem(f"s_{n}") for n in ("rows_ready", "z_ready", "y_turned", "y_ready", "qk_done", "q_ready", "keys_ready", "spread_pool",
                                    "spread_act", "v_done", "v_ready", "biased"))
        scored, max_ready, shift_ready, exped, sum_ready, rinv_ready, turned, probT_ready = (
            sem(f"s_{n}") for n in ("scored", "max_ready", "shift_ready", "exped", "sum_ready", "rinv_ready", "turned", "probT_ready"))
        out_done, out_ready, out_turned, oT_ready, proj_done, x_added = (
            sem(f"s_{n}") for n in ("out_done", "out_ready", "out_turned", "oT_ready", "proj_done", "x_added"))
        x_stats_ready = sem("s_x_stats_ready")
        LEAD, LAG = 5, 2
        row_wide = lambda a, n: a.unsqueeze(2).broadcast_to([P, H, n])
        with nc.Block() as block:

            @block.gpsimd
            def _(pool):
                def step(g, u):
                    t = g * 4 + u
                    if live_tile(g, u, 2):
                        n = u % 2
                        wait(pool, keys_ready, t + 3)
                        wait(pool, scored, t + 1)
                        nc.gpsimd.tensor_tensor(
                            spread[:, n, :, 0:POOL_HEADS, :],
                            keys[:, n].rearrange("p (b l) -> p b l", l=L).unsqueeze(2).broadcast_to([P, BPT, POOL_HEADS, L]),
                            k.head_of_feature[:, 0:POOL_HEADS].unsqueeze(1).unsqueeze(3).broadcast_to([P, BPT, POOL_HEADS, L]),
                            ALU.mult).then_inc(spread_pool, 1)
                    if live_tile(g, u, 4):
                        xt = k.x[:, ds((t + 4) * D, D)]
                        wait(pool, z_ready, t + 5)
                        nc.gpsimd.tensor_tensor(xt, xt, k.bproj[:], ALU.add).then_inc(biased, 1)

                run_tiles(pool, step, LEAD, LAG)

            @block.vector
            def _(dve):
                def step(g, u):
                    t = g * 4 + u
                    if live_tile(g, u, 1):
                        n = (u + 1) % 2
                        dve.wait_ge(scored, t + 2)
                        scores = score_ps[n][:].rearrange("p (h l) -> p h l", l=L)
                        nc.vector.tensor_reduce(rmax[:], scores, AX.X, ALU.max).then_inc(max_ready, 1)
                        dve.wait_ge(max_ready, t + 2)
                        wait(dve, exped, t)
                        nc.vector.tensor_tensor(shifted[:, n], scores, row_wide(rmax[:], L), ALU.subtract).then_inc(shift_ready, 1)
                    if live_tile(g, u, -2):
                        dve.wait_ge(proj_done, t - 1)
                        dve.wait_ge(biased, t - 1)
                        xt = k.x[:, ds((t - 2) * D, D)]
                        nc.vector.tensor_tensor(xt, proj_ps[:, D:2 * D], xt, ALU.add).then_inc(x_added, 1)
                    if live_tile(g, u, 5):
                        wait(dve, y_turned, t + 4)
                        nc.vector.tensor_scalar(z[:, (u + 1) % 2], k.x[:, ds((t + 5) * D, D)], mean[:, ds(t + 5, 1)],
                                                rstd[:, ds(t + 5, 1)], ALU.subtract, ALU.mult).then_inc(z_ready, 1)
                    if live_tile(g, u, 3):
                        dve.wait_ge(v_done, t + 4)
                        nc.vector.tensor_tensor(v[:, (u + 3) % 4], v_ps[:].rearrange("p (b d) -> p b d", d=D),
                                                k.own_value[:].unsqueeze(1).broadcast_to([P, BPT, D]), ALU.mult).then_inc(v_ready, 1)
                    if live_tile(g, u, -2):
                        wait_apart(k, dve, x_added, t - 1)
                        tile_stats(k, t - 2).then_inc(x_stats_ready, 1)
                    if live_tile(g, u, 1):
                        n = (u + 1) % 2
                        dve.wait_ge(exped, t + 2)
                        nc.vector.tensor_reduce(rsum[:], expd[:, n], AX.X, ALU.add).then_inc(sum_ready, 1)
                        dve.wait_ge(sum_ready, t + 2)
                        nc.vector.reciprocal(rinv[:, n], rsum[:]).then_inc(rinv_ready, 1)
                    if live_tile(g, u, 0):
                        dve.wait_ge(out_done, t + 1)
                        dve.wait_ge(rinv_ready, t + 1)
                        wait(dve, out_turned, t - 1)
                        nc.vector.tensor_tensor(out[:, u % 2].rearrange("p (h e) -> p h e", e=DH1),
                                                out_ps[:, 0:D].rearrange("p (h e) -> p h e", e=DH1),
                                                row_wide(rinv[:, u % 2], DH1), ALU.mult).then_inc(out_ready, 1)

                nc.vector.tensor_copy(query_row[:].rearrange("p (b l) -> p b l", l=L),
                                      k.ident[0:L, 0:L].unsqueeze(1).broadcast_to([L, BPT, L])).then_inc(rows_ready, 1)
                nc.vector.tensor_copy(mask_row[:], k.fenwick[0:L, :].unsqueeze(1).broadcast_to([L, H, L])).then_inc(rows_ready, 1)
                run_tiles(dve, step, LEAD, LAG)
                dve.wait_ge(x_stats_ready, TILES)

            @block.scalar
            def _(act):
                def step(g, u):
                    t = g * 4 + u
                    if live_tile(g, u, 4):
                        act.wait_ge(y_turned, t + 5)
                        nc.scalar.activation(y[:, u], y_ps[:, 0:P].rearrange("p (b l) -> p b l", l=L).unsqueeze(2).broadcast_to([P, BPT, HG, L]),
                                             ACT.Copy).then_inc(y_ready, 1)
                    if live_tile(g, u, 2):
                        n = u % 2
                        act.wait_ge(keys_ready, t + 3)
                        wait(act, scored, t + 1)
                        for h in range(POOL_HEADS, H):
                            last = nc.scalar.activation(spread[:, n, :, h, :], keys[:, n].rearrange("p (b l) -> p b l", l=L), ACT.Copy,
                                                        scale=k.head_of_feature[:, h:h + 1])
                        last.then_inc(spread_act, 1)
                    if live_tile(g, u, 0):
                        act.wait_ge(turned, t + 1)
                        nc.scalar.activation(probT[:].rearrange("p g q -> p (g q)"), turn_ps[:], ACT.Copy).then_inc(probT_ready, 1)
                    if live_tile(g, u, 1):
                        n = (u + 1) % 2
                        act.wait_ge(shift_ready, t + 2)
                        wait(act, turned, t)
                        nc.scalar.activation(expd[:, n], shifted[:, n], ACT.Exp, scale=DH1 ** -0.5).then_inc(exped, 1)
                    if live_tile(g, u, 3):
                        n = (u + 3) % 2
                        act.wait_ge(qk_done, t + 4)
                        wait(act, scored, t + 2)
                        wait(act, spread_pool, t + 2)
                        nc.scalar.activation(q[:, n], qk_ps[:, 0:P], ACT.Identity, bias=k.bq2).then_inc(q_ready, 1)
                        nc.scalar.activation(keys[:, n], qk_ps[:, P:2 * P], ACT.Identity, bias=k.bk2).then_inc(keys_ready, 1)
                    if live_tile(g, u, -1):
                        act.wait_ge(out_turned, t)
                        nc.scalar.activation(oT[:], proj_ps[:, 0:P], ACT.Identity, bias=k.bv2).then_inc(oT_ready, 1)

                run_tiles(act, step, LEAD, LAG)

            @block.tensor
            def _(pe):
                def step(g, u):
                    t = g * 4 + u
                    if live_tile(g, u, 4):
                        pe.wait_ge(z_ready, t + 5)
                        wait(pe, y_ready, t + 4)
                        nc.tensor.transpose(y_ps[:, 0:P], z[:, u % 2], k.ident[:]).then_inc(y_turned, 1)
                    if live_tile(g, u, 1):
                        n = (u + 1) % 2
                        wait(pe, shift_ready, t)
                        pe.wait_ge(q_ready, t + 2)
                        pe.wait_ge(spread_pool, t + 2)
                        pe.wait_ge(spread_act, t + 2)
                        nc.tensor.matmul(score_ps[n][:], query_row[:], mask_row[:].rearrange("p h l -> p (h l)"), start=True, stop=False,
                                         skip_group_check=True)
                        for b in range(BPT):
                            rows = slice(b * L, (b + 1) * L)
                            last = nc.tensor.matmul(score_ps[n][rows, :], q[:, n, rows], spread[:, n, b].rearrange("p h l -> p (h l)"),
                                                    start=False, stop=True, skip_group_check=True)
                        last.then_inc(scored, 1)
                    if live_tile(g, u, -2):
                        pe.wait_ge(oT_ready, t - 1)
                        nc.tensor.matmul(proj_ps[:, D:2 * D], oT[:], k.wproj[:], start=True, stop=True).then_inc(proj_done, 1)
                    if live_tile(g, u, 0):
                        pe.wait_ge(exped, t + 1)
                        wait(pe, probT_ready, t)
                        for grp in range(GROUPS):
                            last = nc.tensor.transpose(turn_ps[:, grp * P:(grp + 1) * P], expd[:, u % 2, 4 * grp:4 * grp + 4, :], k.ident[:])
                        last.then_inc(turned, 1)
                    if live_tile(g, u, 3):
                        n = (u + 3) % 4
                        pe.wait_ge(y_ready, t + 4)
                        wait(pe, keys_ready, t + 3)
                        nc.tensor.matmul(qk_ps[:, 0:P], k.wqkv[:, 0:D], y[:, n, :, 0, :], start=True, stop=True)
                        nc.tensor.matmul(qk_ps[:, P:2 * P], k.wqkv[:, D:2 * D], y[:, n, :, 0, :], start=True, stop=True).then_inc(qk_done, 1)
                        wait(pe, v_ready, t + 3)
                        for b in range(BPT):
                            last = nc.tensor.matmul(v_ps[:, b * D:(b + 1) * D], y[:, n, b].rearrange("p r l -> p (r l)"),
                                                    k.wqkv[:, 2 * D:3 * D], start=True, stop=True)
                        last.then_inc(v_done, 1)
                    if live_tile(g, u, -1):
                        pe.wait_ge(out_ready, t)
                        wait(pe, x_added, t - 1)
                        nc.tensor.transpose(proj_ps[:, 0:P], out[:, (u - 1) % 2], k.ident[:]).then_inc(out_turned, 1)
                    if live_tile(g, u, 0):
                        pe.wait_ge(probT_ready, t + 1)
                        pe.wait_ge(v_ready, t + 1)
                        wait(pe, out_ready, t)
                        for grp in range(GROUPS):
                            for b in range(BPT):
                                rows = slice(b * L, (b + 1) * L)
                                cols = slice(grp * HG * DH1, (grp + 1) * HG * DH1)
                                last = nc.tensor.matmul(out_ps[rows, cols], probT[:, grp, rows], v[:, u, b, cols], start=True, stop=True,
                                                        skip_group_check=True)
                        last.then_inc(out_done, 1)

                pe.wait_ge(rows_ready, 2)
                run_tiles(pe, step, LEAD, LAG)


def product(nc, out, w, x, start=True, stop=True):
    for n, (a, b) in enumerate(PASSES):
        last = nc.tensor.matmul(out, w(a), x(b), start=(start and n == 0), stop=(stop and n == len(PASSES) - 1))
    return last


def moe_routing(k, yT, y, combT, share, sh_row, weights, loads):
    nc = k.nc
    sem = k.sem
    GRP = CH // P
    with ExitStack() as stack:
        sb = lambda name, shape, dt=F32: stack.enter_context(nc.sbuf_tensor(name, shape, dt))
        psum = lambda name: stack.enter_context(nc.psum_tensor(name, [P, CH], F32))
        logitT = sb("mr_logitT", [E_N, 2, CH])
        logits, rest, marked, first, second = (sb(f"mr_{n}", [P, TILES, E_N]) for n in ("logits", "rest", "marked", "first", "second"))
        best, next_best, best_rank, next_rank, ratio, w1, w2 = (
            sb(f"mr_{n}", [P, TILES]) for n in ("best", "next_best", "best_rank", "next_rank", "ratio", "w1", "w2"))
        parts = sb("mr_parts", [P, TILES, PARTS, E_N], BF16)
        comb = sb("mr_comb", [P, 2, GRP, PARTS * E_N])
        logit_ps, comb_ps = ([psum(f"mr_{n}{u}") for u in range(2)] for n in ("logit", "comb_ps"))
        token_ps = [psum(f"mr_token{u}") for u in range(2)]
        routed, copied, turned, gathered, y_hi, y_lo, loaded, w_hi, w_lo = (
            sem(f"mr_{n}") for n in ("routed", "copied", "turned", "gathered", "y_hi", "y_lo", "loaded", "w_hi", "w_lo"))
        wide = lambda a: a.unsqueeze(2).broadcast_to([P, TILES, E_N])
        ranks = k.rank[:].unsqueeze(1).broadcast_to([P, TILES, E_N])
        with nc.Block() as block:

            @block.sync
            def _(sp):
                for target, source in loads:
                    sp.dma_start(target, source).then_inc(loaded, 16)

            @block.tensor
            def _(pe):
                def turn(c, u):
                    pe.wait_ge(gathered, c + (u + 1))
                    wait_apart(k, pe, copied, c + (u + 3))
                    for j in range(GRP):
                        last = nc.tensor.transpose(token_ps[u][:, j * E_N:(j + 1) * E_N], logitT[:, u, j * P:(j + 1) * P],
                                                   k.ident[0:E_N, 0:E_N])
                    last.then_inc(turned, 1)

                with pe.Fori(0, CHUNKS // 2) as g:
                    c = g * 2
                    for u in range(2):
                        pe.wait_ge(copied, c + (u + 1))
                        nc.tensor.matmul(logit_ps[u][0:E_N, :], k.router[:], yT[:, ds((c + u) * CH, CH)],
                                         start=True, stop=True).then_inc(routed, 1)
                    for u in range(2):
                        turn(c, u)

            @block.scalar
            def _(act):
                act.sem_inc(copied, 2)
                act.sem_inc(turned, 2)
                with act.Fori(0, CHUNKS // 2) as g:
                    c = g * 2
                    for u in range(2):
                        act.wait_ge(routed, c + (u + 1))
                        act.wait_ge(turned, c + (u + 1))
                        nc.scalar.activation(logitT[:, u, :], logit_ps[u][0:E_N, :], ACT.Copy).then_inc(copied, 1)
                        cols = ds((c + u) * CH, CH)
                        nc.scalar.activation(y[:, HI, cols], yT[:, cols], ACT.Copy).then_inc(y_hi, 1)
                act.wait_ge(loaded, 16 * len(loads))
                for halves, w in weights:
                    nc.scalar.activation(halves[:, HI], w, ACT.Copy).then_inc(w_hi, 1)
                act.wait_ge(w_hi, len(weights))

            @block.gpsimd
            def _(pool):
                with pool.Fori(0, CHUNKS) as c:
                    cols = ds(c * CH, CH)
                    wait_apart(k, pool, y_hi, c + 1)
                    nc.gpsimd.tensor_tensor(y[:, LO, cols], yT[:, cols], y[:, HI, cols], ALU.subtract).then_inc(y_lo, 1)
                pool.wait_ge(y_lo, CHUNKS)

            @block.vector
            def _(dve):
                dve.sem_inc(gathered, 2)
                with dve.Fori(0, CHUNKS // 2) as g:
                    c = g * 2
                    for u in range(2):
                        dve.wait_ge(turned, c + (u + 3))
                        nc.vector.tensor_copy(logits[:, ds((c + u) * GRP, GRP), :],
                                              token_ps[u][:, 0:GRP * E_N].rearrange("p (t e) -> p t e", e=E_N)).then_inc(gathered, 1)
                dve.wait_ge(gathered, CHUNKS + 2)
        chain, ratio_ready, share_done, share_ready = (sem(f"mr_{n}") for n in ("chain", "ratio_ready", "share_done", "share_ready"))
        with nc.Block() as block:

            @block.vector
            def _(dve):
                def mark(n, x, top, top_rank, one):
                    nc.vector.tensor_reduce(top[:], x[:], AX.X, ALU.max).then_inc(chain, 1)
                    dve.wait_ge(chain, n + 1)
                    nc.vector.tensor_tensor(marked[:], x[:], wide(top[:]), ALU.is_ge).then_inc(chain, 1)
                    dve.wait_ge(chain, n + 2)
                    nc.vector.tensor_tensor(marked[:], marked[:], ranks, ALU.mult).then_inc(chain, 1)
                    dve.wait_ge(chain, n + 3)
                    nc.vector.tensor_reduce(top_rank[:], marked[:], AX.X, ALU.max).then_inc(chain, 1)
                    dve.wait_ge(chain, n + 4)
                    nc.vector.tensor_tensor(one[:], marked[:], wide(top_rank[:]), ALU.is_equal).then_inc(chain, 1)
                    dve.wait_ge(chain, n + 5)
                    return n + 5

                n = mark(0, logits, best, best_rank, first)
                nc.vector.scalar_tensor_tensor(rest[:], first[:], -NEG0, logits[:], ALU.mult, ALU.add).then_inc(chain, 1)
                dve.wait_ge(chain, n + 1)
                n = mark(n + 1, rest, next_best, next_rank, second)
                nc.vector.tensor_tensor(w2[:], next_best[:], best[:], ALU.subtract).then_inc(chain, 1)
                n += 1
                dve.wait_ge(ratio_ready, 1)
                nc.vector.tensor_scalar(w1[:], ratio[:], 1.0, None, ALU.add).then_inc(chain, 1)
                dve.wait_ge(chain, n + 1)
                nc.vector.reciprocal(w1[:], w1[:]).then_inc(chain, 1)
                dve.wait_ge(chain, n + 2)
                nc.vector.tensor_tensor(w2[:], w1[:], ratio[:], ALU.mult).then_inc(chain, 1)
                nc.vector.tensor_tensor(first[:], first[:], wide(w1[:]), ALU.mult).then_inc(chain, 1)
                dve.wait_ge(chain, n + 4)
                nc.vector.tensor_tensor(second[:], second[:], wide(w2[:]), ALU.mult).then_inc(chain, 1)
                dve.wait_ge(chain, n + 5)
                nc.vector.tensor_tensor(first[:], first[:], second[:], ALU.add).then_inc(chain, 1)
                dve.wait_ge(chain, n + 6)
                n += 6
                for part in range(PARTS):
                    nc.vector.tensor_copy(parts[:, :, part, :], first[:]).then_inc(chain, 1)
                    dve.wait_ge(chain, n + 1)
                    if part < PARTS - 1:
                        nc.vector.tensor_tensor(first[:], first[:], parts[:, :, part, :], ALU.subtract).then_inc(chain, 1)
                        dve.wait_ge(chain, n + 2)
                    n += 2

            @block.tensor
            def _(pe):
                pe.sem_inc(share_ready, 2)
                pe.wait_ge(w_lo, 1)
                with pe.Fori(0, CHUNKS // 2) as g:
                    c = g * 2
                    for u in range(2):
                        pe.wait_ge(share_ready, c + (u + 1))
                        product(nc, logit_ps[u][:], lambda half: sh_row[:, half, :], lambda half: y[:, half, ds((c + u) * CH, CH)])\
                            .then_inc(share_done, 1)

            @block.scalar
            def _(act):
                def gates(c):
                    for u in range(2):
                        act.wait_ge(share_done, c + (u + 1))
                        nc.scalar.activation(share[:, ds((c + u) * CH, CH)], logit_ps[u][:], ACT.Sigmoid).then_inc(share_ready, 1)

                act.wait_ge(chain, 12)
                nc.scalar.activation(ratio[:], w2[:], ACT.Exp).then_inc(ratio_ready, 1)
                gates(0)
                with act.Fori(1, CHUNKS // 2) as g:
                    gates(g * 2)
                act.wait_ge(share_ready, CHUNKS + 2)

            @block.gpsimd
            def _(pool):
                for halves, w in weights:
                    nc.gpsimd.tensor_tensor(halves[:, LO], w, halves[:, HI], ALU.subtract).then_inc(w_lo, 1)
                pool.wait_ge(w_lo, len(weights))
        staged, comb_turned, comb_copied = sem("mr_staged"), sem("mr_comb_turned"), sem("mr_comb_copied")
        with nc.Block() as block:

            @block.vector
            def _(dve):
                with dve.Fori(0, CHUNKS // 2) as g:
                    c = g * 2
                    for u in range(2):
                        dve.wait_ge(comb_turned, c + (u + 1))
                        nc.vector.tensor_copy(comb[:, u], parts[:, ds((c + u) * GRP, GRP), :, :].rearrange("p t n e -> p t (n e)"))\
                            .then_inc(staged, 1)

            @block.tensor
            def _(pe):
                pe.sem_inc(comb_turned, 2)
                with pe.Fori(0, CHUNKS // 2) as g:
                    c = g * 2
                    for u in range(2):
                        pe.wait_ge(comb_copied, c + (u + 1))
                        wait_apart(k, pe, staged, c + (u + 1))
                        for j in range(GRP):
                            last = nc.tensor.transpose(comb_ps[u][0:PARTS * E_N, j * P:(j + 1) * P], comb[:, u, j, :], k.ident[:])
                        last.then_inc(comb_turned, 1)

            @block.scalar
            def _(act):
                act.sem_inc(comb_copied, 2)
                with act.Fori(0, CHUNKS // 2) as g:
                    c = g * 2
                    for u in range(2):
                        act.wait_ge(comb_turned, c + (u + 3))
                        nc.scalar.activation(combT[:, ds((c + u) * CH, CH)], comb_ps[u][0:PARTS * E_N, :], ACT.Copy).then_inc(comb_copied, 1)
                act.wait_ge(comb_copied, CHUNKS + 2)


def moe1(k, io):
    nc = k.nc
    sem = k.sem
    ITEMS = PAIRS + len(SH_BLOCKS)
    LAST = CHUNKS // 2
    with ExitStack() as stack:
        sb = lambda name, shape: stack.enter_context(nc.sbuf_tensor(name, shape, F32))
        yT = sb("m_yT", [P, TOK])
        layer_norm_T(k, "m_ln", yT)
        share = sb("m_share", [P, TOK])
        combT = stack.enter_context(nc.sbuf_tensor("m_combT", [PARTS * E_N, TOK], BF16))
        halves = lambda name, n, rows=P: stack.enter_context(nc.sbuf_tensor(f"m_{name}", [rows, 2, n], F32R))
        y = halves("y", TOK)
        w_gu, w_dn = halves("w_gu", 2 * E_N * E_FF), halves("w_dn", PAIRS * D)
        sh_gate, sh_up, sh_down, sh_row = halves("sh_gate", SH_FF), halves("sh_up", SH_FF), halves("sh_down", 3 * D), halves("sh_row", P)
        with ExitStack() as whole:
            w_gu_raw = whole.enter_context(nc.sbuf_tensor("m_w_gu_raw", [P, 2, E_N, E_FF], F32))
            w_dn_raw = whole.enter_context(nc.sbuf_tensor("m_w_dn_raw", [P, PAIRS, D], F32))
            gate_up = io["L1_ffn_w_gate_up"].rearrange("e d f -> d e f")
            moe_routing(k, yT, y, combT, share, sh_row, [
                (sh_row, k.sh_gate_row[:]),
                (w_gu, w_gu_raw[:].rearrange("p a e f -> p (a e f)")), (w_dn, w_dn_raw[:].rearrange("p n d -> p (n d)")),
                (sh_gate, k.sh_gate[:]), (sh_up, k.sh_up[:]),
                (sh_down[:, :, 0:2 * D], k.sh_down[:, 0:2].rearrange("p j d -> p (j d)")),
                (sh_down[0:SH_BLOCKS[2][1], :, 2 * D:3 * D], k.sh_down[0:SH_BLOCKS[2][1], 2])], [
                (w_gu_raw[:, 0], gate_up[:, :, 0:E_FF]), (w_gu_raw[:, 1], gate_up[:, :, E_FF:2 * E_FF]),
                (w_dn_raw[:], io["L1_ffn_w_down"].rearrange("(p e) f d -> (e f) p d", e=2))])
        psum = lambda name: stack.enter_context(nc.psum_tensor(name, [P, CH], F32))
        act_in, mul_in = ([psum(f"m_{n}{u}") for u in range(2)] for n in ("g", "h"))
        wide_ps, expert_ps, shared_ps, turn_ps = (psum(f"m_{n}") for n in ("wide", "expert", "shared", "turn"))
        silu, gated, full = sb("m_silu", [P, 2, CH]), sb("m_gated", [P, CH]), sb("m_full", [P, 2, CH])
        hidden = [halves(f"hidden{n}", CH) for n in range(4)]
        experts, shared, total = (sb(f"m_{n}", [P, CH]) for n in ("experts", "shared_out", "total"))
        g_done, h_done, wide_done, down_done, silu_ready, gated_ready, wide_used, full_ready, hi_ready, lo_ready = (
            sem(f"m_{n}") for n in ("g_done", "h_done", "wide_done", "down_done", "silu_ready", "gated_ready", "wide_used",
                                    "full_ready", "hi_ready", "lo_ready"))
        experts_copied, shared_taken, total_ready, turned, x_added = (
            sem(f"m_{n}") for n in ("experts_copied", "shared_taken", "total_ready", "turned", "x_added"))
        rows = lambda j: P if j < PAIRS else SH_BLOCKS[j - PAIRS][1]

        def place(g, i):
            return g * (2 * ITEMS) + i, g * 2 + i // ITEMS, i % ITEMS

        def slot(i):
            i %= 2 * ITEMS
            return 3 if i == 2 * ITEMS - 1 else i % 3

        def current(g):
            return not isinstance(g, int) or g < LAST

        def after(g, i, items):
            return not isinstance(g, int) or 0 <= g * 2 * ITEMS + i - items < CHUNKS * ITEMS

        def run(eng, step):
            for i in range(2 * ITEMS):
                step(0, i)
            with eng.Fori(1, LAST) as g:
                for i in range(2 * ITEMS):
                    step(g, i)
            for i in range(6):
                step(LAST, i)

        with nc.Block() as block:

            @block.tensor
            def _(pe):
                def step(g, i):
                    n, c, j = place(g, i)
                    u = i % 2
                    y_half = lambda half: y[:, half, ds(c * CH, CH)]
                    if current(g):
                        r = rows(j)
                        if j < PAIRS:
                            wg, wh = ((lambda half, a=a: w_gu[:, half, (a * E_N + 2 * j) * E_FF:(a * E_N + 2 * j + 2) * E_FF]) for a in range(2))
                        else:
                            first = SH_BLOCKS[j - PAIRS][0]
                            wg, wh = ((lambda half, w=w: w[:, half, first:first + r]) for w in (sh_gate, sh_up))
                        wait(pe, silu_ready, n - 1)
                        product(nc, act_in[u][0:r, :], wg, y_half).then_inc(g_done, 1)
                        if after(g, i, 2):
                            j2 = (j - 2) % ITEMS
                            if j2 < PAIRS:
                                pe.wait_ge(gated_ready, (c - (1 if j < 2 else 0)) * PAIRS + (j2 + 1))
                            else:
                                pe.wait_ge(full_ready, n - 1)
                        product(nc, mul_in[u][0:r, :], wh, y_half).then_inc(h_done, 1)
                    if current(g) and j < PAIRS:
                        if not isinstance(n, int) or c * PAIRS + j > 0:
                            wait_apart(k, pe, wide_used, c * PAIRS + j)
                        nc.tensor.matmul(wide_ps[:], k.pair_select[:, j, :], combT[:, ds(c * CH, CH)], start=True, stop=True)\
                            .then_inc(wide_done, 1)
                    if after(g, i, 2):
                        j2 = (j - 2) % ITEMS
                        pe.wait_ge(lo_ready, n - 1)
                        if j2 == 0:
                            wait(pe, experts_copied, c)
                        if j2 == PAIRS:
                            wait(pe, shared_taken, c)
                        h = hidden[slot(i - 2)]
                        if j2 < PAIRS:
                            product(nc, expert_ps[:], lambda half: w_dn[:, half, j2 * D:(j2 + 1) * D], lambda half: h[:, half, :],
                                    start=(j2 == 0), stop=(j2 == PAIRS - 1)).then_inc(down_done, 1)
                        else:
                            r = rows(j2)
                            b = j2 - PAIRS
                            product(nc, shared_ps[:], lambda half: sh_down[0:r, half, b * D:(b + 1) * D], lambda half: h[0:r, half, :],
                                    start=(j2 == PAIRS), stop=(j2 == ITEMS - 1)).then_inc(down_done, 1)
                    if j == 4 and after(g, i, ITEMS):
                        pe.wait_ge(total_ready, c)
                        wait(pe, x_added, c - 1)
                        for t in range(CH // P):
                            last = nc.tensor.transpose(turn_ps[:, t * P:(t + 1) * P], total[:, t * P:(t + 1) * P], k.ident[:])
                        last.then_inc(turned, 1)

                run(pe, step)

            @block.scalar
            def _(act):
                def step(g, i):
                    n, c, j = place(g, i)
                    if current(g):
                        u, r = i % 2, rows(j)
                        act.wait_ge(g_done, n + 1)
                        if after(g, i, 2):
                            j2 = (j - 2) % ITEMS
                            if j2 < PAIRS:
                                act.wait_ge(gated_ready, (c - (1 if j < 2 else 0)) * PAIRS + (j2 + 1))
                            else:
                                act.wait_ge(full_ready, n - 1)
                        nc.scalar.activation(silu[0:r, u, :], act_in[u][0:r, :], ACT.Silu).then_inc(silu_ready, 1)
                    if after(g, i, 1):
                        r1 = rows((j - 1) % ITEMS)
                        act.wait_ge(full_ready, n)
                        wait(act, down_done, n - 3)
                        nc.scalar.activation(hidden[slot(i - 1)][0:r1, HI, :], full[0:r1, (i - 1) % 2, :], ACT.Copy).then_inc(hi_ready, 1)
                    if not current(g):
                        return
                    if j == ITEMS - 1:
                        act.wait_ge(down_done, c * ITEMS + PAIRS)
                        wait(act, total_ready, c)
                        nc.scalar.activation(experts[:], expert_ps[:], ACT.Copy).then_inc(experts_copied, 1)

                run(act, step)

            @block.gpsimd
            def _(pool):
                def step(g, i):
                    n, c, j = place(g, i)
                    u = i % 2
                    if after(g, i, 1):
                        r1 = rows((j - 1) % ITEMS)
                        h = hidden[slot(i - 1)]
                        pool.wait_ge(hi_ready, n)
                        nc.gpsimd.tensor_tensor(h[0:r1, LO, :], full[0:r1, 1 - u, :], h[0:r1, HI, :], ALU.subtract).then_inc(lo_ready, 1)

                run(pool, step)

            @block.vector
            def _(dve):
                def step(g, i):
                    n, c, j = place(g, i)
                    u = i % 2
                    if current(g):
                        r = rows(j)
                        dve.wait_ge(silu_ready, n + 1)
                        dve.wait_ge(h_done, n + 1)
                        if j < PAIRS:
                            wait(dve, full_ready, n)
                            nc.vector.tensor_tensor(gated[:], silu[:, u, :], mul_in[u][:], ALU.mult).then_inc(gated_ready, 1)
                            dve.wait_ge(gated_ready, c * PAIRS + (j + 1))
                            dve.wait_ge(wide_done, c * PAIRS + (j + 1))
                            wait(dve, lo_ready, n - 1)
                            nc.vector.tensor_tensor(full[:, u, :], gated[:], wide_ps[:], ALU.mult).then_inc(full_ready, 1)
                            dve.wait_ge(full_ready, n + 1)
                            dve.sem_inc(wide_used, 1)
                        else:
                            wait(dve, lo_ready, n - 1)
                            nc.vector.tensor_tensor(full[0:r, u, :], silu[0:r, u, :], mul_in[u][0:r, :], ALU.mult).then_inc(full_ready, 1)
                    if j == 2 and after(g, i, ITEMS):
                        dve.wait_ge(down_done, c * ITEMS)
                        nc.vector.tensor_tensor(shared[:], share[:, ds((c - 1) * CH, CH)], shared_ps[:], ALU.mult).then_inc(shared_taken, 1)
                        dve.wait_ge(shared_taken, c)
                        dve.wait_ge(experts_copied, c)
                        wait(dve, turned, c - 1)
                        nc.vector.tensor_tensor(total[:], shared[:], experts[:], ALU.add).then_inc(total_ready, 1)
                    if j == 5 and after(g, i, ITEMS):
                        dve.wait_ge(turned, c)
                        xc = k.x[:, ds((c - 1) * CH, CH)]
                        nc.vector.tensor_tensor(xc, turn_ps[:], xc, ALU.add).then_inc(x_added, 1)

                run(dve, step)
                dve.wait_ge(x_added, CHUNKS)


STAGES = [xattn0, rglru0, ffn0, xattn1, attn1, moe1]




def build(nc, io, out):
    k = Core()
    k.nc = nc
    k.keep = ExitStack()
    k.in_use = []

    def sem(name):
        k.in_use.append(nc.alloc_semaphore(name=name))
        return k.in_use[-1]

    k.sem = sem
    k.keep0 = nc.dram_tensor("keep0", [B, N_CTX], BF16, kind="Internal").ap()
    k.keep1 = nc.dram_tensor("keep1", [B, N_CTX], BF16, kind="Internal").ap()
    k.lat_dram = nc.dram_tensor("latents_normalised", [TOK, D], F32, kind="Internal").ap()
    k.ctx_tail_dram = nc.dram_tensor("ctx_tail_normalised", [B, D], F32, kind="Internal").ap()
    k.v_tail_dram = nc.dram_tensor("ctx_tail_values", [B, D], F32, kind="Internal").ap()
    with k.keep:
        setup(k, io)
        for stage in STAGES:
            k.passed = k.sem(f"passed_{stage.__name__}")
            stage(k, io)
            recycle(k)
        store(k, out)


def recycle(k):
    k.nc.clear_and_free_semaphores(k.in_use)
    k.nc.all_engine_barrier()
    k.in_use = []


def store(k, out):
    nc = k.nc
    stored = k.sem("out_stored")
    with nc.Block() as block:

        @block.sync
        def _(sp):
            sp.dma_start(out.rearrange("(t b) l d -> (b l) t d", b=BPT),
                         k.x[:].rearrange("p (t d) -> p t d", d=D)).then_inc(stored, 16)
            sp.wait_ge(stored, 16)


def constants():
    p = np.arange(P)
    c = {}
    c["c_head_of_feature"] = (p[:, None] // DH1 == np.arange(H)).astype(np.float32)
    c["c_head_in_group4"] = (p[:, None] % L // DH1 == np.arange(BPT * HG) % HG).astype(np.float32)
    c["c_group_of_feature"] = (np.arange(GROUPS)[:, None] == p // L).astype(np.float32)
    c["c_own_value"] = (p[:, None] // L == p % L // DH1).astype(np.float32)
    c["c_batch_in_tile"] = (p[:, None] // L == np.arange(BPT)).astype(np.float32)
    fenwick = np.zeros((L, L), bool)
    for i in range(L):
        j = i + 1
        while j <= L:
            fenwick[i, j - 1] = True
            j += j & -j
        step = 1
        while i - step >= 0:
            fenwick[i, i - step] = True
            step *= 2
    fenwick &= np.tril(np.ones((L, L), bool))
    c["c_fenwick"] = np.tile(np.where(fenwick, 0.0, -NEG0), (HG, 1)).astype(np.float32)
    e = np.tile(np.arange(E_N), PARTS)
    c["c_rank"] = np.tile(E_N - np.arange(E_N), (P, 1)).astype(np.float32)
    c["c_pair_select"] = (e[:, None, None] == 2 * np.arange(PAIRS)[None, :, None] + p[None, None, :] // E_FF).astype(np.float32)
    return c


def kernel(**inputs):
    import numpy as _np
    import concourse.bacc as _bacc
    from concourse import mybir as _mybir
    from concourse.bass_utils import run_bass_kernel_spmd as _run

    nc = _bacc.Bacc("TRN2", target_bir_lowering=False, num_devices=1)
    arrays, io = {}, {}
    for name, a in {**inputs, **constants()}.items():
        a = _np.ascontiguousarray(a)
        if a.dtype == bool:
            a = a.reshape(-1).view(_np.int32)
        arrays[f"in_{name}"] = a
        io[name] = nc.dram_tensor(f"in_{name}", a.shape, _mybir.dt.from_np(a.dtype), kind="ExternalInput").ap()
    out = nc.dram_tensor("out_0", (B, L, D), F32, kind="ExternalOutput").ap()
    build(nc, io, out)
    r = _run(nc, [arrays], core_ids=[0])
    return r.results[0]["out_0"]
```
